# Optimizing a Trainium2 kernel written in Bass

```python
import numpy as np
import jax
import jax.numpy as jnp

def _softmax(x, axis=-1):
    return jax.nn.softmax(x, axis=axis)

def _gelu(x):
    return jax.nn.gelu(x, approximate=True)

def _silu(x):
    return jax.nn.silu(x)

def _sigmoid(x):
    return jax.nn.sigmoid(x)

def _layernorm(x, axis=-1, eps=1e-05):
    m = jnp.mean(x, axis=axis, keepdims=True)
    v = jnp.var(x, axis=axis, keepdims=True)
    return (x - m) / jnp.sqrt(v + eps)

def _scatter_add(tgt, idx, src, axis=0):
    return tgt.at[idx].add(src)

def _segment_sum(src, seg, n):
    return jax.ops.segment_sum(src, seg, n)
kernel_name = 'mk_decoder_preln_d2_seqx_r8_dc4670'

def setup_inputs(seed: int=0):
    np.random.seed(seed)
    _w = jnp.asarray

    def _rec_inputs():
        import jax
        import jax.numpy as jnp
        _rk = jax.random.key(seed)
        x = -0.0002928 + 1 * jax.random.normal(jax.random.fold_in(_rk, 1), (32, 64, 256), jnp.float32)
        _lenS = 64 - jax.random.randint(jax.random.fold_in(_rk, 7), (32,), 0, max(1, 64 // 4) + 1, jnp.int32)
        _lenS2 = 64 - jax.random.randint(jax.random.fold_in(_rk, 8), (32,), 0, max(1, 64 // 4) + 1, jnp.int32)
        _ctx_2048P = jax.random.normal(jax.random.fold_in(_rk, 11), (32, 16, 256), jnp.float32)
        _ctx_2048c = jax.random.dirichlet(jax.random.fold_in(_rk, 511), 0.3 * jnp.ones((16,), jnp.float32), (32, 64))
        _ctx_2048t = jnp.einsum('bsk,bkd->bsd', _ctx_2048c, _ctx_2048P)
        _ctx_2048t = _ctx_2048t * jax.lax.rsqrt(jnp.mean(jnp.square(_ctx_2048t)) + 1e-12) * 0.953939
        ctx_2048 = -1.39393e-06 + 0.999914 * (_ctx_2048t + 0.3 * jax.random.normal(jax.random.fold_in(_rk, 611), (32, 64, 256), jnp.float32))
        _validS = jnp.arange(64)[None, :] < _lenS[:, None]
        _validS2 = jnp.arange(64)[None, :] < _lenS2[:, None]
        _causal = jnp.tril(jnp.ones((64, 64), dtype=bool))
        mask_1xSxS2_ff0 = jnp.where(jnp.ones((1, 64, 64), dtype=bool), 0.0, -1000000000.0).astype(jnp.float32)
        return (x, ctx_2048, mask_1xSxS2_ff0)
    x, ctx_2048, mask_1xSxS2_ff0 = _rec_inputs()

    def _L0_attn_setup():
        import jax, jax.numpy as jnp
        import numpy as np
        import math
        E = 256
        H = 16
        HKV = 8
        NREP = H // HKV
        HD = E // H // 2
        DEPTH = 12
        LAMBDA_INIT = 0.8 - 0.6 * math.exp(-0.3 * DEPTH)
        EPS = 1e-06

        def _rotary(x, cos, sin):
            d = x.shape[-1] // 2
            x1, x2 = (x[..., :d], x[..., d:])
            c = cos[None, :, None, :]
            si = sin[None, :, None, :]
            return jnp.concatenate([x1 * c + x2 * si, -x1 * si + x2 * c], axis=-1)
        key = jax.random.key(seed)
        ks = jax.random.split(key, 10)
        s = lambda fan_in: 1.0 / np.sqrt(fan_in)
        return {'x': jax.random.normal(ks[0], (2, 256, E), jnp.float32), 'Wq': jax.random.normal(ks[1], (E, E), jnp.float32) * s(E), 'Wk': jax.random.normal(ks[2], (E, E // NREP), jnp.float32) * s(E), 'Wv': jax.random.normal(ks[3], (E, E // NREP), jnp.float32) * s(E), 'Wo': jax.random.normal(ks[4], (E, E), jnp.float32) * s(E), 'lam_q1': jax.random.normal(ks[5], (HD,), jnp.float32) * 0.1, 'lam_k1': jax.random.normal(ks[6], (HD,), jnp.float32) * 0.1, 'lam_q2': jax.random.normal(ks[7], (HD,), jnp.float32) * 0.1, 'lam_k2': jax.random.normal(ks[8], (HD,), jnp.float32) * 0.1, 'g': jnp.ones((2 * HD,), jnp.float32)}
    _L0_attn_all = _L0_attn_setup()
    _L0_attn_in = {k: v for k, v in _L0_attn_all.items() if k in ('Wq', 'Wk', 'Wv', 'Wo', 'lam_q1', 'lam_k1', 'lam_q2', 'lam_k2', 'g')}
    del _L0_attn_all

    def _L0_xattn_setup():
        import jax, jax.numpy as jnp
        import numpy as np
        B, C, T = (4, 64, 256)
        H = 8
        D = C // H
        SCALE = D ** (-0.5)
        key = jax.random.key(seed)
        kq, kk, kv, kw = jax.random.split(key, 4)
        q = jax.random.normal(kq, (B, C, T), dtype=jnp.float32)
        k = jax.random.normal(kk, (B, C, T), dtype=jnp.float32)
        v = jax.random.normal(kv, (B, C, T), dtype=jnp.float32)
        W = jax.random.normal(kw, (C, C), dtype=jnp.float32) * C ** (-0.5)
        return {'q': q, 'k': k, 'v': v, 'W': W}
    _L0_xattn_all = _L0_xattn_setup()
    _L0_xattn_in = {k: v for k, v in _L0_xattn_all.items() if k in ('W',)}
    del _L0_xattn_all

    def _L0_ffn_setup():
        import jax, jax.numpy as jnp
        import numpy as np
        B, T, D = (4, 128, 256)
        N, S, H = (8, 8, 8)
        ETA = 1.0
        key = jax.random.key(seed)
        ks = jax.random.split(key, 9)
        return {'x': jax.random.normal(ks[0], (B, T, D), jnp.float32), 'select_weight': jax.random.normal(ks[1], (N, D, S), jnp.float32) / D, 'select_mean_diff': jax.random.normal(ks[2], (N, D), jnp.float32) / D, 'imp_center': jax.random.normal(ks[3], (N,), jnp.float32), 'imp_slope': jax.random.normal(ks[4], (N,), jnp.float32) * 5.0, 'lora_update': jax.random.normal(ks[5], (N, D, H), jnp.float32) * 0.02, 'lora_degen': jax.random.normal(ks[6], (N, D, H), jnp.float32) * 0.02, 'bias_w': jax.random.normal(ks[7], (N, D), jnp.float32) * 0.02, 'debias_w': jax.random.normal(ks[8], (N, D), jnp.float32) * 0.02}
    _L0_ffn_all = _L0_ffn_setup()
    _L0_ffn_in = {k: v for k, v in _L0_ffn_all.items() if k in ('select_weight', 'select_mean_diff', 'imp_center', 'imp_slope', 'lora_update', 'lora_degen', 'bias_w', 'debias_w')}
    del _L0_ffn_all

    def _L1_attn_setup():
        import jax, jax.numpy as jnp
        import numpy as np
        D_MODEL, N_HEADS, D_STATE, N_GROUPS, CHUNK = (256, 32, 64, 1, 32)
        BATCH, SEQLEN = (2, 512)

        def segsum(v):
            cs = jnp.cumsum(v, axis=-1)
            seg = cs[..., :, None] - cs[..., None, :]
            T = v.shape[-1]
            mask = jnp.tril(jnp.ones((T, T), bool))
            return jnp.where(mask, seg, -jnp.inf)

        def _ssd(x, A_log, D, B_w, B_b, C_w, C_b, dt_w, dt_b, out_w, out_b):
            b, t, d = x.shape
            h = A_log.shape[0]
            n = B_w.shape[0] // N_GROUPS
            p = d // h
            l = CHUNK
            c = t // l
            A = -jnp.exp(A_log.astype(jnp.float32))
            B = (x @ B_w.T + B_b).reshape(b, t, N_GROUPS, n)
            C = (x @ C_w.T + C_b).reshape(b, t, N_GROUPS, n)
            B = jnp.broadcast_to(B, (b, t, h, n))
            C = jnp.broadcast_to(C, (b, t, h, n))
            dt = jax.nn.softplus(x @ dt_w.T + dt_b)
            xh = x.reshape(b, t, h, p)
            xc = xh.reshape(b, c, l, h, p)
            Bc = B.reshape(b, c, l, h, n)
            Cc = C.reshape(b, c, l, h, n)
            dtc = dt.reshape(b, c, l, h)
            dA = jnp.transpose(dtc * A, (0, 3, 1, 2))
            A_cumsum = jnp.cumsum(dA, axis=-1)
            L = jnp.exp(segsum(dA))
            xdt = xc * dtc[..., None]
            Y_diag = jnp.einsum('bclhn,bcshn,bhcls,bcshp->bclhp', Cc, Bc, L, xdt)
            decay_states = jnp.exp(A_cumsum[..., -1:] - A_cumsum)
            states = jnp.einsum('bclhn,bhcl,bclhp->bchpn', Bc, decay_states, xdt)
            states = jnp.concatenate([jnp.zeros_like(states[:, :1]), states], axis=1)
            dA_last = jnp.pad(A_cumsum[..., -1], ((0, 0), (0, 0), (1, 0)))
            decay_chunk = jnp.exp(segsum(dA_last))
            new_states = jnp.einsum('bhzc,bchpn->bzhpn', decay_chunk, states)
            prev_states = new_states[:, :-1]
            state_decay_out = jnp.exp(A_cumsum)
            Y_off = jnp.einsum('bclhn,bchpn,bhcl->bclhp', Cc, prev_states, state_decay_out)
            Y = (Y_diag + Y_off).reshape(b, t, h, p) + D[None, None, :, None] * xh
            return Y.reshape(b, t, d) @ out_w.T + out_b
        key = jax.random.key(seed)
        ks = jax.random.split(key, 8)
        s = 0.02
        d, h, n, g = (D_MODEL, N_HEADS, D_STATE, N_GROUPS)
        return {'x': jax.random.normal(ks[0], (BATCH, SEQLEN, d), jnp.float32), 'A_log': jnp.log(jnp.arange(1, h + 1, dtype=jnp.float32)), 'D': jnp.ones((h,), jnp.float32), 'B_w': jax.random.normal(ks[1], (g * n, d), jnp.float32) * s, 'B_b': jnp.zeros((g * n,), jnp.float32), 'C_w': jax.random.normal(ks[2], (g * n, d), jnp.float32) * s, 'C_b': jnp.zeros((g * n,), jnp.float32), 'dt_w': jax.random.normal(ks[3], (h, d), jnp.float32) * s, 'dt_b': jnp.zeros((h,), jnp.float32), 'out_w': jax.random.normal(ks[4], (d, d), jnp.float32) * s, 'out_b': jnp.zeros((d,), jnp.float32)}
    _L1_attn_all = _L1_attn_setup()
    _L1_attn_in = {k: v for k, v in _L1_attn_all.items() if k in ('A_log', 'D', 'B_w', 'B_b', 'C_w', 'C_b', 'dt_w', 'dt_b', 'out_w', 'out_b')}
    del _L1_attn_all

    def _L1_xattn_setup():
        import jax, jax.numpy as jnp
        import numpy as np
        H = 256
        NH = 16
        NKV = 4
        HD = 128
        GROUPS = NH // NKV
        EPS = 1e-06
        B, S, SE = (1, 256, 512)

        def _rmsnorm(x, w, eps=EPS):
            xf = x.astype(jnp.float32)
            var = jnp.mean(xf * xf, axis=-1, keepdims=True)
            return (xf * jax.lax.rsqrt(var + eps)).astype(x.dtype) * w
        key = jax.random.key(seed)
        ks = jax.random.split(key, 12)
        sc = 0.02
        return {'hidden_states': jax.random.normal(ks[0], (B, S, H), jnp.float32), 'encoder_hidden_states': jax.random.normal(ks[1], (B, SE, H), jnp.float32), 'attention_mask': jnp.zeros((B, S, SE), jnp.float32), 'Wq': jax.random.normal(ks[2], (H, NH * HD), jnp.float32) * sc, 'bq': jax.random.normal(ks[3], (NH * HD,), jnp.float32) * sc, 'Wk': jax.random.normal(ks[4], (H, NKV * HD), jnp.float32) * sc, 'bk': jax.random.normal(ks[5], (NKV * HD,), jnp.float32) * sc, 'Wv': jax.random.normal(ks[6], (H, NKV * HD), jnp.float32) * sc, 'bv': jax.random.normal(ks[7], (NKV * HD,), jnp.float32) * sc, 'Wo': jax.random.normal(ks[8], (NH * HD, H), jnp.float32) * sc, 'qn_w': jnp.ones((HD,), jnp.float32), 'kn_w': jnp.ones((HD,), jnp.float32)}
    _L1_xattn_all = _L1_xattn_setup()
    _L1_xattn_in = {k: v for k, v in _L1_xattn_all.items() if k in ('Wq', 'bq', 'Wk', 'bk', 'Wv', 'bv', 'Wo', 'qn_w', 'kn_w')}
    del _L1_xattn_all

    def _L1_ffn_setup():
        import jax, jax.numpy as jnp
        import numpy as np
        import math
        GOLDEN_CENTER = 1.0 / math.e
        GOLDEN_LOWER = 0.5 - math.log(4.0 / 3.0)
        GOLDEN_UPPER = 0.5
        B, T, D = (4, 128, 256)
        E = 8
        F = 1024 // (E // 2)
        R = 64
        NL = 2

        def _router_weights(x, Wr, temperature):
            logits = jnp.einsum('btd,de->bte', x, Wr)
            inhibition = jax.nn.sigmoid(logits / temperature)
            in_zone = (inhibition >= GOLDEN_LOWER) & (inhibition <= GOLDEN_UPPER)
            distance = jnp.abs(inhibition - GOLDEN_CENTER)
            w = jnp.exp(-distance / 0.1) * in_zone.astype(x.dtype)
            wsum = w.sum(axis=-1, keepdims=True)
            no_expert = wsum < 1e-08
            fb = jnp.exp(-distance / 0.3)
            _, top2 = jax.lax.top_k(fb, 2)
            fb_mask = jax.nn.one_hot(top2, E, dtype=x.dtype).sum(axis=-2)
            fb_w = fb * fb_mask
            fb_w = fb_w / jnp.clip(fb_w.sum(axis=-1, keepdims=True), 1e-08)
            w = jnp.where(no_expert, fb_w, w)
            return w / jnp.clip(w.sum(axis=-1, keepdims=True), 1e-08)
        key = jax.random.key(seed)
        ks = jax.random.split(key, 13)
        s = 0.02
        x = jax.random.normal(ks[0], (B, T, D), dtype=jnp.float32)
        Wg = jax.random.normal(ks[1], (E, D, F), dtype=jnp.float32) * s
        Wu = jax.random.normal(ks[2], (E, D, F), dtype=jnp.float32) * s
        Wd = jax.random.normal(ks[3], (E, F, D), dtype=jnp.float32) * s
        Ga = jax.random.normal(ks[4], (NL, D, R), dtype=jnp.float32) * s
        Gb = jax.random.normal(ks[5], (NL, R, F), dtype=jnp.float32) * s
        Ua = jax.random.normal(ks[6], (NL, D, R), dtype=jnp.float32) * s
        Ub = jax.random.normal(ks[7], (NL, R, F), dtype=jnp.float32) * s
        Da = jax.random.normal(ks[8], (NL, F, R), dtype=jnp.float32) * s
        Db = jax.random.normal(ks[9], (NL, R, D), dtype=jnp.float32) * s
        Wr = jax.random.normal(ks[10], (D, E), dtype=jnp.float32) * s
        temperature = jnp.ones((1,), dtype=jnp.float32)
        return {'x': x, 'Wg': Wg, 'Wu': Wu, 'Wd': Wd, 'Ga': Ga, 'Gb': Gb, 'Ua': Ua, 'Ub': Ub, 'Da': Da, 'Db': Db, 'Wr': Wr, 'temperature': temperature}
    _L1_ffn_all = _L1_ffn_setup()
    _L1_ffn_in = {k: v for k, v in _L1_ffn_all.items() if k in ('Wg', 'Wu', 'Wd', 'Ga', 'Gb', 'Ua', 'Ub', 'Da', 'Db', 'Wr', 'temperature')}
    del _L1_ffn_all
    return {'x': x, 'ctx_2048': ctx_2048, 'mask_1xSxS2_ff0': mask_1xSxS2_ff0, 'L0_attn_Wq': _L0_attn_in['Wq'], 'L0_attn_Wk': _L0_attn_in['Wk'], 'L0_attn_Wv': _L0_attn_in['Wv'], 'L0_attn_Wo': _L0_attn_in['Wo'], 'L0_attn_lam_q1': _L0_attn_in['lam_q1'], 'L0_attn_lam_k1': _L0_attn_in['lam_k1'], 'L0_attn_lam_q2': _L0_attn_in['lam_q2'], 'L0_attn_lam_k2': _L0_attn_in['lam_k2'], 'L0_attn_g': _L0_attn_in['g'], 'L0_xattn_W': _L0_xattn_in['W'], 'L0_ffn_select_weight': _L0_ffn_in['select_weight'], 'L0_ffn_select_mean_diff': _L0_ffn_in['select_mean_diff'], 'L0_ffn_imp_center': _L0_ffn_in['imp_center'], 'L0_ffn_imp_slope': _L0_ffn_in['imp_slope'], 'L0_ffn_lora_update': _L0_ffn_in['lora_update'], 'L0_ffn_lora_degen': _L0_ffn_in['lora_degen'], 'L0_ffn_bias_w': _L0_ffn_in['bias_w'], 'L0_ffn_debias_w': _L0_ffn_in['debias_w'], 'L1_attn_A_log': _L1_attn_in['A_log'], 'L1_attn_D': _L1_attn_in['D'], 'L1_attn_B_w': _L1_attn_in['B_w'], 'L1_attn_B_b': _L1_attn_in['B_b'], 'L1_attn_C_w': _L1_attn_in['C_w'], 'L1_attn_C_b': _L1_attn_in['C_b'], 'L1_attn_dt_w': _L1_attn_in['dt_w'], 'L1_attn_dt_b': _L1_attn_in['dt_b'], 'L1_attn_out_w': _L1_attn_in['out_w'], 'L1_attn_out_b': _L1_attn_in['out_b'], 'L1_xattn_Wq': _L1_xattn_in['Wq'], 'L1_xattn_bq': _L1_xattn_in['bq'], 'L1_xattn_Wk': _L1_xattn_in['Wk'], 'L1_xattn_bk': _L1_xattn_in['bk'], 'L1_xattn_Wv': _L1_xattn_in['Wv'], 'L1_xattn_bv': _L1_xattn_in['bv'], 'L1_xattn_Wo': _L1_xattn_in['Wo'], 'L1_xattn_qn_w': _L1_xattn_in['qn_w'], 'L1_xattn_kn_w': _L1_xattn_in['kn_w'], 'L1_ffn_Wg': _L1_ffn_in['Wg'], 'L1_ffn_Wu': _L1_ffn_in['Wu'], 'L1_ffn_Wd': _L1_ffn_in['Wd'], 'L1_ffn_Ga': _L1_ffn_in['Ga'], 'L1_ffn_Gb': _L1_ffn_in['Gb'], 'L1_ffn_Ua': _L1_ffn_in['Ua'], 'L1_ffn_Ub': _L1_ffn_in['Ub'], 'L1_ffn_Da': _L1_ffn_in['Da'], 'L1_ffn_Db': _L1_ffn_in['Db'], 'L1_ffn_Wr': _L1_ffn_in['Wr'], 'L1_ffn_temperature': _L1_ffn_in['temperature']}

def reference(x, ctx_2048, mask_1xSxS2_ff0, L0_attn_Wq, L0_attn_Wk, L0_attn_Wv, L0_attn_Wo, L0_attn_lam_q1, L0_attn_lam_k1, L0_attn_lam_q2, L0_attn_lam_k2, L0_attn_g, L0_xattn_W, L0_ffn_select_weight, L0_ffn_select_mean_diff, L0_ffn_imp_center, L0_ffn_imp_slope, L0_ffn_lora_update, L0_ffn_lora_degen, L0_ffn_bias_w, L0_ffn_debias_w, L1_attn_A_log, L1_attn_D, L1_attn_B_w, L1_attn_B_b, L1_attn_C_w, L1_attn_C_b, L1_attn_dt_w, L1_attn_dt_b, L1_attn_out_w, L1_attn_out_b, L1_xattn_Wq, L1_xattn_bq, L1_xattn_Wk, L1_xattn_bk, L1_xattn_Wv, L1_xattn_bv, L1_xattn_Wo, L1_xattn_qn_w, L1_xattn_kn_w, L1_ffn_Wg, L1_ffn_Wu, L1_ffn_Wd, L1_ffn_Ga, L1_ffn_Gb, L1_ffn_Ua, L1_ffn_Ub, L1_ffn_Da, L1_ffn_Db, L1_ffn_Wr, L1_ffn_temperature):
    import jax
    import jax.numpy as jnp

    def _L0_attn_ref(x, Wq, Wk, Wv, Wo, lam_q1, lam_k1, lam_q2, lam_k2, g):
        import jax, jax.numpy as jnp
        import numpy as np
        import math
        E = 256
        H = 16
        HKV = 8
        NREP = H // HKV
        HD = E // H // 2
        DEPTH = 12
        LAMBDA_INIT = 0.8 - 0.6 * math.exp(-0.3 * DEPTH)
        EPS = 1e-06

        def _rotary(x, cos, sin):
            d = x.shape[-1] // 2
            x1, x2 = (x[..., :d], x[..., d:])
            c = cos[None, :, None, :]
            si = sin[None, :, None, :]
            return jnp.concatenate([x1 * c + x2 * si, -x1 * si + x2 * c], axis=-1)
        B, T, _ = x.shape
        q = (x @ Wq).reshape(B, T, 2 * H, HD)
        k = (x @ Wk).reshape(B, T, 2 * HKV, HD)
        v = (x @ Wv).reshape(B, T, HKV, 2 * HD)
        inv_freq = 1.0 / 10000.0 ** (jnp.arange(0, HD, 2, dtype=jnp.float32) / HD)
        freqs = jnp.arange(T, dtype=jnp.float32)[:, None] * inv_freq[None, :]
        cos, sin = (jnp.cos(freqs), jnp.sin(freqs))
        q = _rotary(q, cos, sin)
        k = _rotary(k, cos, sin)
        q = jnp.transpose(q, (0, 2, 1, 3)) * HD ** (-0.5)
        k = jnp.repeat(jnp.transpose(k, (0, 2, 1, 3)), NREP, axis=1)
        v = jnp.repeat(jnp.transpose(v, (0, 2, 1, 3)), NREP, axis=1)
        scores = jnp.einsum('bhtd,bhsd->bhts', q, k)
        scores = jnp.nan_to_num(scores)
        mask = jnp.triu(jnp.full((T, T), -jnp.inf, scores.dtype), 1)
        scores = scores + mask
        p = jax.nn.softmax(scores.astype(jnp.float32), axis=-1).astype(scores.dtype)
        lam1 = jnp.exp(jnp.sum(lam_q1 * lam_k1))
        lam2 = jnp.exp(jnp.sum(lam_q2 * lam_k2))
        lam = lam1 - lam2 + LAMBDA_INIT
        p = p.reshape(B, H, 2, T, T)
        diff = p[:, :, 0] - lam * p[:, :, 1]
        attn = jnp.einsum('bhts,bhsd->bhtd', diff, v)
        attn = attn * jax.lax.rsqrt(jnp.mean(attn * attn, axis=-1, keepdims=True) + EPS) * g
        attn = attn * (1.0 - LAMBDA_INIT)
        attn = jnp.transpose(attn, (0, 2, 1, 3)).reshape(B, T, E)
        return attn @ Wo

    def _L0_xattn_ref(q, k, v, W):
        import jax, jax.numpy as jnp
        import numpy as np
        B, C, T = (4, 64, 256)
        H = 8
        D = C // H
        SCALE = D ** (-0.5)
        Bq, Cq, Tq = q.shape
        Tk = k.shape[2]
        qh = q.reshape(Bq, H, D, Tq)
        kh = k.reshape(Bq, H, D, Tk)
        vh = v.reshape(Bq, H, D, Tk)
        a = jnp.einsum('bhdq,bhdk->bhqk', qh, kh) * SCALE
        p = jax.nn.softmax(a, axis=-1)
        y = jnp.einsum('bhqk,bhdk->bhdq', p, vh).reshape(Bq, Cq, Tq)
        out = jnp.einsum('oc,bct->bot', W, y)
        return jax.nn.selu(out)

    def _L0_ffn_ref(x, select_weight, select_mean_diff, imp_center, imp_slope, lora_update, lora_degen, bias_w, debias_w):
        import jax, jax.numpy as jnp
        import numpy as np
        B, T, D = (4, 128, 256)
        N, S, H = (8, 8, 8)
        ETA = 1.0
        x_diff = x[:, None, :, :] - select_mean_diff[None, :, None, :]
        x_diff = x_diff / jnp.linalg.norm(x_diff, axis=3, keepdims=True)
        cont = jnp.einsum('nds,bntd->bnts', select_weight, x_diff) ** 2
        score = cont.sum(axis=-1)
        gate = jax.nn.sigmoid(imp_slope[None, :, None] * (score - imp_center[None, :, None]))
        sel_scale = gate.max(axis=1)[..., None]
        sel_idx = gate.argmax(axis=1)
        debias = jnp.take(debias_w, sel_idx, axis=0)
        bias = jnp.take(bias_w, sel_idx, axis=0)
        upd = jnp.take(lora_update, sel_idx, axis=0)
        dgn = jnp.take(lora_degen, sel_idx, axis=0)
        x_debias = x - debias
        mod_x = jnp.einsum('btdh,btd->bth', upd, x_debias)
        degen_up = jnp.einsum('btdh,bth->btd', dgn, mod_x)
        mod_x_bias = ETA * (bias + degen_up)
        return (1.0 - sel_scale) * x + sel_scale * mod_x_bias

    def _L1_attn_ref(x, A_log, D, B_w, B_b, C_w, C_b, dt_w, dt_b, out_w, out_b):
        import jax, jax.numpy as jnp
        import numpy as np
        D_MODEL, N_HEADS, D_STATE, N_GROUPS, CHUNK = (256, 32, 64, 1, 32)
        BATCH, SEQLEN = (2, 512)

        def segsum(v):
            cs = jnp.cumsum(v, axis=-1)
            seg = cs[..., :, None] - cs[..., None, :]
            T = v.shape[-1]
            mask = jnp.tril(jnp.ones((T, T), bool))
            return jnp.where(mask, seg, -jnp.inf)

        def _ssd(x, A_log, D, B_w, B_b, C_w, C_b, dt_w, dt_b, out_w, out_b):
            b, t, d = x.shape
            h = A_log.shape[0]
            n = B_w.shape[0] // N_GROUPS
            p = d // h
            l = CHUNK
            c = t // l
            A = -jnp.exp(A_log.astype(jnp.float32))
            B = (x @ B_w.T + B_b).reshape(b, t, N_GROUPS, n)
            C = (x @ C_w.T + C_b).reshape(b, t, N_GROUPS, n)
            B = jnp.broadcast_to(B, (b, t, h, n))
            C = jnp.broadcast_to(C, (b, t, h, n))
            dt = jax.nn.softplus(x @ dt_w.T + dt_b)
            xh = x.reshape(b, t, h, p)
            xc = xh.reshape(b, c, l, h, p)
            Bc = B.reshape(b, c, l, h, n)
            Cc = C.reshape(b, c, l, h, n)
            dtc = dt.reshape(b, c, l, h)
            dA = jnp.transpose(dtc * A, (0, 3, 1, 2))
            A_cumsum = jnp.cumsum(dA, axis=-1)
            L = jnp.exp(segsum(dA))
            xdt = xc * dtc[..., None]
            Y_diag = jnp.einsum('bclhn,bcshn,bhcls,bcshp->bclhp', Cc, Bc, L, xdt)
            decay_states = jnp.exp(A_cumsum[..., -1:] - A_cumsum)
            states = jnp.einsum('bclhn,bhcl,bclhp->bchpn', Bc, decay_states, xdt)
            states = jnp.concatenate([jnp.zeros_like(states[:, :1]), states], axis=1)
            dA_last = jnp.pad(A_cumsum[..., -1], ((0, 0), (0, 0), (1, 0)))
            decay_chunk = jnp.exp(segsum(dA_last))
            new_states = jnp.einsum('bhzc,bchpn->bzhpn', decay_chunk, states)
            prev_states = new_states[:, :-1]
            state_decay_out = jnp.exp(A_cumsum)
            Y_off = jnp.einsum('bclhn,bchpn,bhcl->bclhp', Cc, prev_states, state_decay_out)
            Y = (Y_diag + Y_off).reshape(b, t, h, p) + D[None, None, :, None] * xh
            return Y.reshape(b, t, d) @ out_w.T + out_b
        return _ssd(x, A_log, D, B_w, B_b, C_w, C_b, dt_w, dt_b, out_w, out_b)

    def _L1_xattn_ref(hidden_states, encoder_hidden_states, attention_mask, Wq, bq, Wk, bk, Wv, bv, Wo, qn_w, kn_w):
        import jax, jax.numpy as jnp
        import numpy as np
        H = 256
        NH = 16
        NKV = 4
        HD = 128
        GROUPS = NH // NKV
        EPS = 1e-06
        B, S, SE = (1, 256, 512)

        def _rmsnorm(x, w, eps=EPS):
            xf = x.astype(jnp.float32)
            var = jnp.mean(xf * xf, axis=-1, keepdims=True)
            return (xf * jax.lax.rsqrt(var + eps)).astype(x.dtype) * w
        b, s, _ = hidden_states.shape
        se = encoder_hidden_states.shape[1]
        q = (hidden_states @ Wq + bq).reshape(b, s, NH, HD).transpose(0, 2, 1, 3)
        k = (encoder_hidden_states @ Wk + bk).reshape(b, se, NKV, HD).transpose(0, 2, 1, 3)
        v = (encoder_hidden_states @ Wv + bv).reshape(b, se, NKV, HD).transpose(0, 2, 1, 3)
        k = jnp.repeat(k, GROUPS, axis=1)
        v = jnp.repeat(v, GROUPS, axis=1)
        q = _rmsnorm(q, qn_w)
        k = _rmsnorm(k, kn_w)
        scale = 1.0 / np.sqrt(HD).astype(np.float32)
        scores = jnp.einsum('bhsd,bhed->bhse', q, k) * scale
        scores = scores + attention_mask[:, None, :, :]
        probs = jax.nn.softmax(scores.astype(jnp.float32), axis=-1).astype(q.dtype)
        out = jnp.einsum('bhse,bhed->bhsd', probs, v)
        out = out.transpose(0, 2, 1, 3).reshape(b, s, NH * HD)
        return out @ Wo

    def _L1_ffn_ref(x, Wg, Wu, Wd, Ga, Gb, Ua, Ub, Da, Db, Wr, temperature):
        import jax, jax.numpy as jnp
        import numpy as np
        import math
        GOLDEN_CENTER = 1.0 / math.e
        GOLDEN_LOWER = 0.5 - math.log(4.0 / 3.0)
        GOLDEN_UPPER = 0.5
        B, T, D = (4, 128, 256)
        E = 8
        F = 1024 // (E // 2)
        R = 64
        NL = 2

        def _router_weights(x, Wr, temperature):
            logits = jnp.einsum('btd,de->bte', x, Wr)
            inhibition = jax.nn.sigmoid(logits / temperature)
            in_zone = (inhibition >= GOLDEN_LOWER) & (inhibition <= GOLDEN_UPPER)
            distance = jnp.abs(inhibition - GOLDEN_CENTER)
            w = jnp.exp(-distance / 0.1) * in_zone.astype(x.dtype)
            wsum = w.sum(axis=-1, keepdims=True)
            no_expert = wsum < 1e-08
            fb = jnp.exp(-distance / 0.3)
            _, top2 = jax.lax.top_k(fb, 2)
            fb_mask = jax.nn.one_hot(top2, E, dtype=x.dtype).sum(axis=-2)
            fb_w = fb * fb_mask
            fb_w = fb_w / jnp.clip(fb_w.sum(axis=-1, keepdims=True), 1e-08)
            w = jnp.where(no_expert, fb_w, w)
            return w / jnp.clip(w.sum(axis=-1, keepdims=True), 1e-08)
        weights = _router_weights(x, Wr, temperature)
        gate = jnp.einsum('btd,edf->ebtf', x, Wg)
        up = jnp.einsum('btd,edf->ebtf', x, Wu)
        gate = gate.at[:NL].add(jnp.einsum('btd,edr,erf->ebtf', x, Ga, Gb))
        up = up.at[:NL].add(jnp.einsum('btd,edr,erf->ebtf', x, Ua, Ub))
        mid = jax.nn.silu(gate) * up
        out = jnp.einsum('ebtf,efd->ebtd', mid, Wd)
        out = out.at[:NL].add(jnp.einsum('ebtf,efr,erd->ebtd', mid[:NL], Da, Db))
        return jnp.einsum('bte,ebtd->btd', weights, out)
    x = x + _L0_attn_ref(_layernorm(x, axis=-1), L0_attn_Wq, L0_attn_Wk, L0_attn_Wv, L0_attn_Wo, L0_attn_lam_q1, L0_attn_lam_k1, L0_attn_lam_q2, L0_attn_lam_k2, L0_attn_g)
    x = x + _L0_xattn_ref(_layernorm(x, axis=-1), ctx_2048, ctx_2048, L0_xattn_W)
    x = x + _L0_ffn_ref(_layernorm(x, axis=-1), L0_ffn_select_weight, L0_ffn_select_mean_diff, L0_ffn_imp_center, L0_ffn_imp_slope, L0_ffn_lora_update, L0_ffn_lora_degen, L0_ffn_bias_w, L0_ffn_debias_w)
    x = x + _L1_attn_ref(_layernorm(x, axis=-1), L1_attn_A_log, L1_attn_D, L1_attn_B_w, L1_attn_B_b, L1_attn_C_w, L1_attn_C_b, L1_attn_dt_w, L1_attn_dt_b, L1_attn_out_w, L1_attn_out_b)
    x = x + _L1_xattn_ref(_layernorm(x, axis=-1), ctx_2048, mask_1xSxS2_ff0, L1_xattn_Wq, L1_xattn_bq, L1_xattn_Wk, L1_xattn_bk, L1_xattn_Wv, L1_xattn_bv, L1_xattn_Wo, L1_xattn_qn_w, L1_xattn_kn_w)
    x = x + _L1_ffn_ref(_layernorm(x, axis=-1), L1_ffn_Wg, L1_ffn_Wu, L1_ffn_Wd, L1_ffn_Ga, L1_ffn_Gb, L1_ffn_Ua, L1_ffn_Ub, L1_ffn_Da, L1_ffn_Db, L1_ffn_Wr, L1_ffn_temperature)
    return x

_drawn_inputs = setup_inputs


def setup_inputs(seed=0):
    import zlib

    import numpy as np

    out = dict(_drawn_inputs(seed))
    spreads = {'L0_attn_g': (1.0, 0.2),
     'L1_attn_D': (1.0, 0.2),
     'L1_attn_B_b': (0.0, 0.1),
     'L1_attn_C_b': (0.0, 0.1),
     'L1_attn_dt_b': (0.0, 0.683),
     'L1_attn_out_b': (0.0, 0.1),
     'L1_xattn_qn_w': (1.0, 0.6),
     'L1_xattn_kn_w': (1.0, 0.6)}
    factors = {'L0_attn_lam_q1': 8.0,
     'L0_attn_lam_k1': 6.008,
     'L0_attn_lam_q2': 3.495,
     'L0_attn_lam_k2': 3.162,
     'L0_ffn_select_weight': 64.0,
     'L0_ffn_lora_update': 3.548,
     'L0_ffn_lora_degen': 3.503,
     'L0_ffn_bias_w': 3.368,
     'L0_ffn_debias_w': 8.0,
     'L1_xattn_bq': 8.0,
     'L1_xattn_bk': 8.0,
     'L1_xattn_bv': 4.063,
     'L1_ffn_Wg': 7.288,
     'L1_ffn_Wu': 7.209,
     'L1_ffn_Wd': 7.227,
     'L1_ffn_Ga': 8.0,
     'L1_ffn_Gb': 8.0,
     'L1_ffn_Ua': 8.0,
     'L1_ffn_Ub': 8.0,
     'L1_ffn_Da': 8.0,
     'L1_ffn_Db': 8.0,
     'L1_ffn_Wr': 8.0,
     'L0_ffn_select_mean_diff': 8.0}
    for name, (base, spread) in spreads.items():
        noise = np.random.default_rng([zlib.crc32(name.encode()), seed]).standard_normal(out[name].shape)
        drawn = base * np.exp(spread * noise) if base else spread * noise
        out[name] = jnp.asarray(drawn.astype(out[name].dtype))
    for name, factor in factors.items():
        out[name] = (out[name] * factor).astype(out[name].dtype)
    return out
```

```python
import math
from contextlib import ExitStack

import numpy as np

import concourse.bass as bass
from concourse import mybir

F32 = mybir.dt.float32
BF16 = mybir.dt.bfloat16
ALU = mybir.AluOpType
ACT = mybir.ActivationFunctionType
AX = mybir.AxisListType

P = 128
BATCH, SEQ, E = 32, 64, 256
TILES = BATCH * SEQ // P
PAIRS = TILES // 2
KC = E // P
LN_EPS = 1e-5
FLT_MAX = 3.4028235e38
MASKED = -1.0e30
EXP_LN = "natural_log_exp_and_others"


class Core:

    def __init__(self, nc, ctx, dram):
        self.nc, self.ctx, self.dram = nc, ctx, dram
        self.psum = ctx.enter_context(nc.psum_tensor("psum", [P, 8, 512], F32))
        self.x = self.sb("x", [P, TILES, E])
        self.context = self.sb("context", [P, TILES, E])
        self.row_stats = self.sb("row_stats", [P, TILES, 6])
        self.ident = self.sb("ident", [P, P])
        self.context_loaded = ctx.enter_context(nc.semaphore("context_loaded"))
        self.semaphores = []

    def sb(self, name, shape, dtype=F32):
        return self.ctx.enter_context(self.nc.sbuf_tensor(name, shape, dtype))

    def sem(self, name):
        self.semaphores.append(self.nc.alloc_semaphore(name=name))
        return self.semaphores[-1]

    def end_sublayer(self):
        self.nc.clear_and_free_semaphores(self.semaphores)
        self.nc.all_engine_barrier()
        self.semaphores = []

    def sems(self, name, count):
        return [self.sem(f"{name}{j}") for j in range(count)]


def chunked(weight):
    return weight.rearrange("(c p) o -> p c o", p=P)


class RowNorm:

    def __init__(self, core, stage, scope):
        nc = core.nc
        sb = lambda name, shape: scope.enter_context(nc.sbuf_tensor(f"{stage}_{name}", shape, F32))
        self.core = core
        self.sum2, self.half = sb("sum2", [P, TILES]), sb("half", [P, TILES])
        self.spread, self.mean = sb("spread", [P, TILES]), sb("mean", [P, TILES])
        self.var, self.log_var = sb("var", [P, TILES]), sb("log_var", [P, TILES])
        self.rstd = sb("rstd", [P, TILES])
        self.eps = sb("ln_eps", [P, 1])
        self.moments = core.sem(f"{stage}_ln_moments")
        self.var_ready = core.sem(f"{stage}_ln_var")
        self.log_ready = core.sem(f"{stage}_ln_log")
        self.ready = core.sem(f"{stage}_ln_ready")

    def on_vector(self, dve):
        nc, stats = self.core.nc, self.core.row_stats
        nc.vector.memset(self.eps[:], LN_EPS)
        nc.vector.tensor_tensor(self.sum2[:], stats[:, :, 1], stats[:, :, 4], ALU.add).then_inc(self.moments, 1)
        nc.vector.tensor_tensor(self.half[:], stats[:, :, 1], stats[:, :, 4], ALU.subtract).then_inc(self.moments, 1)
        nc.vector.tensor_tensor(self.spread[:], stats[:, :, 2], stats[:, :, 5], ALU.add).then_inc(self.moments, 1)
        dve.wait_ge(self.moments, 3)
        nc.vector.tensor_scalar(self.mean[:], self.sum2[:], 0.5, None, ALU.mult).then_inc(self.moments, 1)
        nc.vector.scalar_tensor_tensor(self.half[:], self.half[:], 0.25, self.half[:], ALU.mult, ALU.mult).then_inc(self.moments, 1)
        dve.wait_ge(self.moments, 5)
        nc.vector.scalar_tensor_tensor(self.var[:], self.spread[:], 1.0 / E, self.half[:], ALU.mult, ALU.add).then_inc(self.var_ready, 1)

    def on_scalar(self, act):
        nc = self.core.nc
        act.wait_ge(self.var_ready, 1)
        nc.scalar.activation(self.log_var[:], self.var[:], ACT.Ln, bias=self.eps[:]).then_inc(self.log_ready, 1)
        act.wait_ge(self.log_ready, 1)
        nc.scalar.activation(self.rstd[:], self.log_var[:], ACT.Exp, scale=-0.5).then_inc(self.ready, 1)

    def normalise(self, out, t):
        return self.core.nc.vector.tensor_scalar(
            out, self.core.x[:, t, :], self.mean[:, bass.ts(t, 1)], self.rstd[:, bass.ts(t, 1)],
            ALU.subtract, ALU.mult)

def load_inputs(core):
    nc, dram = core.nc, core.dram
    parts = 4
    per = TILES // parts
    x_loaded = core.sems("x_loaded", parts)
    ident_loaded = core.sem("ident_loaded")
    stats_done = core.sem("first_stats_done")
    with nc.Block() as block:

        @block.sync
        def _(sp):
            for g in range(parts):
                sp.dma_start(core.x[:, g * per:(g + 1) * per, :],
                             dram["x"].rearrange("(t p) e -> p t e", p=P)[:, g * per:(g + 1) * per, :]).then_inc(x_loaded[g], 16)
            sp.dma_start(core.ident[:], dram["ident"]).then_inc(ident_loaded, 16)
            sp.dma_start(core.context[:], dram["ctx"].rearrange("(t p) e -> p t e", p=P)).then_inc(core.context_loaded, 16)
            sp.wait_ge(ident_loaded, 16)
            sp.wait_ge(stats_done, TILES)

        @block.vector
        def _(dve):
            for g in range(parts):
                dve.wait_ge(x_loaded[g], 16)
                for t in range(g * per, (g + 1) * per):
                    nc.vector.bn_stats(core.row_stats[:, t, :], core.x[:, t, :]).then_inc(stats_done, 1)


D_HEADS, D_KV_HEADS, D_HD = 16, 8, 8
D_DV = 2 * D_HD
LAMBDA_INIT = 0.8 - 0.6 * math.exp(-0.3 * 12)
RMS_EPS = 1e-6


def differential_attention(core):
    nc, dram, ps, ident = core.nc, core.dram, core.psum, core.ident
    with ExitStack() as scope:
        sb = lambda name, shape, dt=F32: scope.enter_context(nc.sbuf_tensor(f"da_{name}", shape, dt))
        sem = lambda name: core.sem(f"da_{name}")
        ln = RowNorm(core, "da", scope)
        w_qk = sb("w_qk", [P, KC, 6 * P])
        w_v = sb("w_v", [P, KC, P])
        w_o = sb("w_o", [P, KC, E])
        gain = sb("gain", [P, 1])
        rotary = sb("rotary", [P, 2, 3 * P])
        head_mask = sb("head_mask", [P, D_HEADS])
        causal = sb("causal", [P, 8 * SEQ], BF16)
        ident_bf = sb("ident_bf", [P, P], BF16)
        lam_in = sb("lam_in", [P, 4, D_HD])
        lam_prod, lam_dot, lam_exp, lam = sb("lam_prod", [P, 2, D_HD]), sb("lam_dot", [P, 2]), sb("lam_exp", [P, 2]), sb("lam", [P, 1])
        rms_eps = sb("rms_eps", [P, 1])
        xn = sb("xn", [P, 2, E])
        xT = sb("xT", [P, 2, E])
        rot_a, rot_b, rot = sb("rot_a", [P, 2, 3 * P]), sb("rot_b", [P, 2, 3 * P]), sb("rot", [P, 2, 3 * P])
        keys = sb("keys", [P, 2, D_HEADS, P])
        values = sb("values", [P, 2, 2, D_KV_HEADS, 64])
        top = sb("top", [P, 2, 2, D_HEADS])
        probs = sb("probs", [P, 2, 2, D_HEADS * SEQ])
        probsT = sb("probsT", [P, 2, 2, D_HEADS * SEQ])
        headsT = sb("headsT", [P, 2, 1024])
        inv = sb("inv", [P, 2, 2, D_HEADS])
        part0, part1 = sb("part0", [P, 2, E]), sb("part1", [P, 2, E])
        attn, squares, scaled = sb("attn", [P, 2, E]), sb("squares", [P, 2, E]), sb("scaled", [P, 2, E])
        square_sum, rms_log, rms_inv = sb("square_sum", [P, 2, D_HEADS]), sb("rms_log", [P, 2, D_HEADS]), sb("rms_inv", [P, 2, D_HEADS])
        attnT = sb("attnT", [P, 2, E])

        loaded = sem("loaded")
        consts_set, lam_ready, lam_dots, lam_exps, wo_scaled = sem("consts_set"), sem("lam_ready"), sem("lam_dots"), sem("lam_exps"), sem("wo_scaled")
        lam_steps = sem("lam_steps")
        xn_ready, xT_psum, xT_ready = sem("xn_ready"), sem("xT_psum"), sem("xT_ready")
        projected, rot_parts, rot_ready, values_ready, keys_ready = sem("projected"), sem("rot_parts"), sem("rot_ready"), sem("values_ready"), sem("keys_ready")
        scored, top_raw, top_ready = core.sems("da_scored", 2), sem("top_raw"), sem("top_ready")
        shifted, exp_done = core.sems("da_shifted", 2), core.sems("da_exp_done", 2)
        probsT_psum, probsT_ready = core.sems("da_probsT_psum", 2), core.sems("da_probsT_ready", 2)
        heads_psum, headsT_ready, heads_rows = sem("heads_psum"), sem("headsT_ready"), sem("heads_rows")
        inv_ready, inv_lam, parts_ready, attn_ready, squares_ready, square_sums = sem("inv_ready"), sem("inv_lam"), sem("parts_ready"), sem("attn_ready"), sem("squares_ready"), sem("square_sums")
        rms_logs, rms_ready, scaled_ready = sem("rms_logs"), sem("rms_ready"), sem("scaled_ready")
        attnT_psum, attnT_ready, out_psum, x_ready, stats_done = sem("attnT_psum"), sem("attnT_ready"), sem("out_psum"), sem("x_ready"), sem("stats_done")
        LOADS = 9 * 16

        block = scope.enter_context(nc.Block())

        @block.sync
        def _(sp):
            for out, src in ((w_qk[:], chunked(dram["da_w_qk"])), (w_v[:], chunked(dram["da_w_v"])), (rotary[:], dram["rotary"]),
                             (head_mask[:], dram["da_head_mask"]), (causal[:], dram["causal"]), (ident_bf[:], dram["ident_bf"]),
                             (lam_in[:], dram["da_lam"]), (w_o[:], chunked(dram["da_w_o"])), (gain[:], dram["da_gain"]),
                             ):
                sp.dma_start(out, src).then_inc(loaded, 16)
            sp.wait_ge(loaded, LOADS)

        @block.gpsimd
        def _(pool):
            nc.gpsimd.memset(values[:], 0.0).then_inc(consts_set, 1)
            pool.wait_ge(consts_set, 1)
            for half in range(2):
                ones = values[64 * half:64 * half + 64, :, :, :, half * 17 + D_DV:half * 17 + D_DV + 1]
                nc.gpsimd.memset(ones, 1.0).then_inc(consts_set, 1)
            with pool.Fori(0, PAIRS) as i:
                for u in range(2):
                    n = pool.snap(2 * i + (u + 1))
                    pool.wait_ge(rot_ready, n)
                    nc.gpsimd.tensor_tensor(
                        keys[:, u], rot[:, u, None, 2 * P:3 * P].to_broadcast([P, D_HEADS, P]),
                        head_mask[:, :, None].to_broadcast([P, D_HEADS, P]), ALU.mult).then_inc(keys_ready, 1)

        @block.scalar
        def _(act):
            act.preload_act_table_set(EXP_LN)
            ln.on_scalar(act)
            act.wait_ge(lam_dots, 1)
            nc.scalar.activation(lam_exp[:], lam_dot[:], ACT.Exp).then_inc(lam_exps, 1)
            act.wait_ge(consts_set, 3)
            with act.Fori(0, PAIRS) as i:
                ns = [act.snap(2 * i + (u + 1)) for u in range(2)]
                for u, n in enumerate(ns):
                    act.wait_ge(xT_psum, n)
                    nc.scalar.copy(xT[:, u], ps[:, 6 + u, 0:E]).then_inc(xT_ready, 1)
                for u, n in enumerate(ns):
                    act.wait_ge(projected, n)
                    for b in range(2):
                        for half in range(2):
                            copied = nc.scalar.copy(
                                values[64 * half:64 * half + 64, u, b, :, half * 17:half * 17 + D_DV],
                                ps[64 * b:64 * b + 64, 6 + u, E:E + P].rearrange("p (h d) -> p h d", d=D_DV))
                    copied.then_inc(values_ready, 1)
                for u, n in enumerate(ns):
                    for r in range(2):
                        act.wait_ge(shifted[r], n)
                        nc.scalar.activation(probs[:, u, r], probs[:, u, r], ACT.Exp).then_inc(exp_done[r], 1)
                for u, n in enumerate(ns):
                    for r in range(2):
                        act.wait_ge(probsT_psum[r], n)
                        nc.scalar.copy(probsT[:, u, r].rearrange("p (b c) -> p b c", b=2), ps[:, 6:8, :]).then_inc(probsT_ready[r], 1)
                for u, n in enumerate(ns):
                    act.wait_ge(heads_psum, n)
                    nc.scalar.copy(headsT[:, u].rearrange("p (b c) -> p b c", b=2), ps[:, 0:2, :]).then_inc(headsT_ready, 1)
                for u, n in enumerate(ns):
                    act.wait_ge(square_sums, n)
                    nc.scalar.activation(rms_log[:, u], square_sum[:, u], ACT.Ln, bias=rms_eps[:], scale=1.0 / D_DV).then_inc(rms_logs, 1)
                    act.wait_ge(rms_logs, n)
                    nc.scalar.activation(rms_inv[:, u], rms_log[:, u], ACT.Exp, scale=-0.5).then_inc(rms_ready, 1)
                for u, n in enumerate(ns):
                    act.wait_ge(attnT_psum, n)
                    nc.scalar.copy(attnT[:, u], ps[:, 6 + u, 0:E]).then_inc(attnT_ready, 1)

        @block.vector
        def _(dve):
            ln.on_vector(dve)
            nc.vector.memset(rms_eps[:], RMS_EPS)
            dve.wait_ge(loaded, LOADS)
            nc.vector.tensor_tensor(lam_prod[:], lam_in[:, 0:2], lam_in[:, 2:4], ALU.mult).then_inc(lam_steps, 1)
            dve.wait_ge(lam_steps, 1)
            nc.vector.tensor_reduce(lam_dot[:], lam_prod[:], AX.X, ALU.add).then_inc(lam_dots, 1)
            for c in range(KC):
                nc.vector.tensor_scalar(w_o[:, c], w_o[:, c], gain[:], 1.0 - LAMBDA_INIT, ALU.mult, ALU.mult).then_inc(wo_scaled, 1)
            dve.wait_ge(lam_exps, 1)
            nc.vector.tensor_tensor(lam[:], lam_exp[:, 0:1], lam_exp[:, 1:2], ALU.subtract).then_inc(lam_steps, 1)
            dve.wait_ge(lam_steps, 2)
            nc.vector.tensor_scalar(lam[:], lam[:], LAMBDA_INIT, None, ALU.add).then_inc(lam_ready, 1)
            dve.wait_ge(lam_ready, 1)
            dve.wait_ge(ln.ready, 1)
            with dve.Fori(0, PAIRS) as i:
                ns = [dve.snap(2 * i + (u + 1)) for u in range(2)]
                for u, n in enumerate(ns):
                    ln.normalise(xn[:, u], 2 * i + u).then_inc(xn_ready, 1)
                for u, n in enumerate(ns):
                    dve.wait_ge(projected, n)
                    nc.vector.tensor_tensor(rot_a[:, u], ps[:, 0, 0:3 * P], rotary[:, 0], ALU.mult)
                    nc.vector.tensor_tensor(rot_b[:, u], ps[:, 1, 0:3 * P], rotary[:, 1], ALU.mult).then_inc(rot_parts, 1)
                    dve.wait_ge(rot_parts, n)
                    nc.vector.tensor_tensor(rot[:, u], rot_a[:, u], rot_b[:, u], ALU.add).then_inc(rot_ready, 1)
                for u, n in enumerate(ns):
                    score = [ps[:, 2 + 2 * r:4 + 2 * r, :].rearrange("p b (h s) -> p (b h) s", s=SEQ) for r in range(2)]
                    for r in range(2):
                        dve.wait_ge(scored[r], n)
                        nc.vector.tensor_reduce(top[:, u, r], score[r], AX.X, ALU.max).then_inc(top_raw, 1)
                    dve.wait_ge(top_raw, 2 * n)
                    nc.vector.tensor_scalar(top[:, u], top[:, u], FLT_MAX, -FLT_MAX, ALU.min, ALU.max).then_inc(top_ready, 1)
                    dve.wait_ge(top_ready, n)
                    for r in range(2):
                        nc.vector.scalar_tensor_tensor(
                            probs[:, u, r].rearrange("p (h s) -> p h s", s=SEQ), score[r], FLT_MAX,
                            top[:, u, r, :, None].to_broadcast([P, D_HEADS, SEQ]), ALU.min, ALU.subtract).then_inc(shifted[r], 1)
                for u, n in enumerate(ns):
                    dve.wait_ge(heads_rows, n)
                    heads = ps[:, 2:4, :].rearrange("p r (g c) -> p r g c", c=64)
                    sums = [heads[:, r, :, 0:34].rearrange("p g (h d) -> p g h d", d=17)[:, :, :, D_DV] for r in range(2)]
                    weighted = [heads[:, r, :, 0:34].rearrange("p g (h d) -> p g h d", d=17)[:, :, :, 0:D_DV] for r in range(2)]
                    pair = lambda a: a.rearrange("p (g h) -> p g h", h=2)
                    quad = lambda a: a.rearrange("p (g h d) -> p g h d", h=2, d=D_DV)
                    spread = lambda a: pair(a)[:, :, :, None].to_broadcast([P, D_HEADS // 2, 2, D_DV])
                    for r in range(2):
                        nc.vector.reciprocal(pair(inv[:, u, r]), sums[r]).then_inc(inv_ready, 1)
                    dve.wait_ge(inv_ready, 2 * n)
                    nc.vector.tensor_scalar(inv[:, u, 1], inv[:, u, 1], lam[:], None, ALU.mult).then_inc(inv_lam, 1)
                    nc.vector.tensor_tensor(quad(part0[:, u]), weighted[0], spread(inv[:, u, 0]), ALU.mult)
                    dve.wait_ge(inv_lam, n)
                    nc.vector.tensor_tensor(quad(part1[:, u]), weighted[1], spread(inv[:, u, 1]), ALU.mult).then_inc(parts_ready, 1)
                    dve.wait_ge(parts_ready, n)
                    nc.vector.tensor_tensor(attn[:, u], part0[:, u], part1[:, u], ALU.subtract).then_inc(attn_ready, 1)
                    dve.wait_ge(attn_ready, n)
                    nc.vector.tensor_tensor(squares[:, u], attn[:, u], attn[:, u], ALU.mult).then_inc(squares_ready, 1)
                    dve.wait_ge(squares_ready, n)
                    nc.vector.tensor_reduce(square_sum[:, u], squares[:, u].rearrange("p (h d) -> p h d", d=D_DV), AX.X, ALU.add).then_inc(square_sums, 1)
                for u, n in enumerate(ns):
                    dve.wait_ge(rms_ready, n)
                    nc.vector.tensor_tensor(
                        scaled[:, u].rearrange("p (h d) -> p h d", d=D_DV), attn[:, u].rearrange("p (h d) -> p h d", d=D_DV),
                        rms_inv[:, u, :, None].to_broadcast([P, D_HEADS, D_DV]), ALU.mult).then_inc(scaled_ready, 1)
                for u, n in enumerate(ns):
                    dve.wait_ge(out_psum, n)
                    nc.vector.tensor_tensor(core.x[:, 2 * i + u, :], core.x[:, 2 * i + u, :], ps[:, 4 + u, 0:E], ALU.add).then_inc(x_ready, 1)
                    dve.wait_ge(x_ready, n)
                    nc.vector.bn_stats(core.row_stats[:, 2 * i + u, :], core.x[:, 2 * i + u, :]).then_inc(stats_done, 1)
            dve.wait_ge(stats_done, TILES)

        @block.tensor
        def _(pe):
            pe.wait_ge(loaded, LOADS)
            pe.wait_ge(wo_scaled, KC)
            with pe.Fori(0, PAIRS) as i:
                ns = [pe.snap(2 * i + (u + 1)) for u in range(2)]
                for u, n in enumerate(ns):
                    pe.wait_ge(xn_ready, n)
                    for c in range(KC):
                        done = nc.tensor.transpose(ps[:, 6 + u, c * P:(c + 1) * P], xn[:, u, c * P:(c + 1) * P], ident[:])
                    done.then_inc(xT_psum, 1)
                for u, n in enumerate(ns):
                    pe.wait_ge(xT_ready, n)
                    if u == 1:
                        pe.wait_ge(rot_ready, ns[0])
                    for m in range(6):
                        for c in range(KC):
                            nc.tensor.matmul(ps[:, m // 3, (m % 3) * P:(m % 3 + 1) * P], w_qk[:, c, m * P:(m + 1) * P],
                                             xT[:, u, c * P:(c + 1) * P], start=(c == 0), stop=(c == KC - 1))
                    for c in range(KC):
                        done = nc.tensor.matmul(ps[:, 6 + u, E:E + P], xT[:, u, c * P:(c + 1) * P], w_v[:, c],
                                                start=(c == 0), stop=(c == KC - 1))
                    done.then_inc(projected, 1)
                for u, n in enumerate(ns):
                    pe.wait_ge(keys_ready, n)
                    for r in range(2):
                        if u == 1:
                            pe.wait_ge(shifted[r], ns[0])
                        for half in range(2):
                            nc.tensor.matmul(ps[:, 2 + 2 * r + half, :], ident_bf[:], causal[:], start=True, stop=False, skip_group_check=True)
                            for b in range(2):
                                done = nc.tensor.matmul(
                                    ps[64 * b:64 * b + 64, 2 + 2 * r + half, :], rot[:, u, r * P + 64 * b:r * P + 64 * b + 64],
                                    keys[:, u, 8 * half:8 * half + 8, 64 * b:64 * b + 64], start=False, stop=(b == 1), skip_group_check=True)
                        done.then_inc(scored[r], 1)
                for u, n in enumerate(ns):
                    for r in range(2):
                        pe.wait_ge(exp_done[r], n)
                        if (u, r) == (0, 0):
                            pe.wait_ge(values_ready, ns[1])
                        else:
                            pe.wait_ge(probsT_ready[1 - r], ns[0] if (u, r) != (1, 1) else ns[1])
                        for j in range(D_KV_HEADS):
                            done = nc.tensor.transpose(ps[:, 6 + j // 4, (j % 4) * P:(j % 4 + 1) * P], probs[:, u, r, j * P:(j + 1) * P], ident[:])
                        done.then_inc(probsT_psum[r], 1)
                    pe.wait_ge(probsT_ready[0], n)
                    pe.wait_ge(probsT_ready[1], n)
                    if u == 0:
                        pe.wait_ge(rot_ready, ns[1])
                    else:
                        pe.wait_ge(headsT_ready, ns[0])
                    for b in range(2):
                        for j in range(D_KV_HEADS):
                            weights = probsT[:, u].rearrange("p r (j t) -> p r j t", t=P)[:, :, j, 64 * b:64 * b + 64]
                            out = ps[64 * (j % 2):64 * (j % 2) + 64, 0:2, :].rearrange("p k (g r b t) -> p (k g) r b t", g=2, r=2, b=2)[:, j // 2, :, b, :]
                            done = nc.tensor.matmul(out, values[:, u, b, j, :], weights, start=True, stop=True)
                    done.then_inc(heads_psum, 1)
                for u, n in enumerate(ns):
                    pe.wait_ge(headsT_ready, n)
                    if u == 1:
                        pe.wait_ge(parts_ready, ns[0])
                    for r in range(2):
                        for g in range(4):
                            done = nc.tensor.transpose(ps[:, 2 + r, g * P:(g + 1) * P],
                                                       headsT[:, u].rearrange("p (g r t) -> p g r t", g=4, r=2)[:, g, r, :], ident[:])
                    done.then_inc(heads_rows, 1)
                for u, n in enumerate(ns):
                    pe.wait_ge(scaled_ready, n)
                    for c in range(KC):
                        done = nc.tensor.transpose(ps[:, 6 + u, c * P:(c + 1) * P], scaled[:, u, c * P:(c + 1) * P], ident[:])
                    done.then_inc(attnT_psum, 1)
                for u, n in enumerate(ns):
                    pe.wait_ge(attnT_ready, n)
                    for c in range(KC):
                        done = nc.tensor.matmul(ps[:, 4 + u, 0:E], attnT[:, u, c * P:(c + 1) * P], w_o[:, c],
                                                start=(c == 0), stop=(c == KC - 1))
                    done.then_inc(out_psum, 1)

C_HEADS, C_HD = 8, 8
PARTS = 3
STACK = PARTS * C_HD
MAX_ROW = 96
STACK_ROWS = MAX_ROW + PARTS
RING = 3
V_COLS = 32
SELU_SCALE, SELU_ALPHA = 1.0507009873554805, 1.6732632423543772


def split_parts(core):
    nc, dram = core.nc, core.dram
    with ExitStack() as scope:
        sb = lambda name, shape, dt=F32: scope.enter_context(nc.sbuf_tensor(f"sp_{name}", shape, dt))
        sem = lambda name: core.sem(f"sp_{name}")
        ln = RowNorm(core, "sp", scope)
        rows = sb("rows", [P, 2, E])
        rest = sb("rest", [P, 2, 2, E])
        parts = sb("parts", [P, 2, 2, PARTS, E], BF16)
        rows_ready, high_ready, rest_ready, mid_ready, low_ready = (
            sem("rows_ready"), sem("high_ready"), sem("rest_ready"), sem("mid_ready"), sem("low_ready"))
        stored = core.sems("sp_stored", 2)
        scaled_ready = sem("scaled_ready")
        STORES = 2 * PARTS * 16
        block = scope.enter_context(nc.Block())

        def source(kind, u, t):
            return rows[:, u, :] if kind == 0 else core.context[:, t, :]

        @block.vector
        def _(dve):
            ln.on_vector(dve)
            dve.wait_ge(ln.ready, 1)
            nc.vector.tensor_scalar(ln.rstd[:], ln.rstd[:], C_HD ** -0.5, None, ALU.mult).then_inc(scaled_ready, 1)
            dve.wait_ge(scaled_ready, 1)
            with dve.Fori(0, PAIRS) as i:
                for u in range(2):
                    dve.wait_ge(low_ready, 2 * (2 * i + u) + 1)
                    ln.normalise(rows[:, u], 2 * i + u).then_inc(rows_ready, 1)

        @block.scalar
        def _(act):
            ln.on_scalar(act)
            act.wait_ge(core.context_loaded, 16)
            with act.Fori(0, PAIRS) as i:
                for u in range(2):
                    t = 2 * i + u
                    act.wait_ge(stored[u], STORES * i + STORES)
                    act.wait_ge(rows_ready, t + 1)
                    for kind in range(2):
                        nc.scalar.copy(parts[:, u, kind, 0], source(kind, u, t)).then_inc(high_ready, 1)
                    for kind in range(2):
                        act.wait_ge(rest_ready, 2 * t + (kind + 1))
                        nc.scalar.copy(parts[:, u, kind, 1], rest[:, u, kind]).then_inc(mid_ready, 1)

        @block.gpsimd
        def _(pool):
            pool.sem_inc(low_ready, 2 * 2 - 1)
            with pool.Fori(0, PAIRS) as i:
                for u in range(2):
                    t = 2 * i + u
                    for kind in range(2):
                        pool.wait_ge(high_ready, 2 * t + (kind + 1))
                        nc.gpsimd.tensor_tensor(rest[:, u, kind], source(kind, u, t), parts[:, u, kind, 0], ALU.subtract).then_inc(rest_ready, 1)
                    for kind in range(2):
                        pool.wait_ge(mid_ready, 2 * t + (kind + 1))
                        pool.wait_ge(rest_ready, 2 * t + (kind + 1))
                        nc.gpsimd.tensor_tensor(parts[:, u, kind, 2], rest[:, u, kind], parts[:, u, kind, 1], ALU.subtract).then_inc(low_ready, 1)

        @block.sync
        def _(sp):
            for u in range(2):
                sp.sem_inc(stored[u], STORES)
            with sp.Fori(0, PAIRS) as i:
                for u in range(2):
                    t = 2 * i + u
                    sp.wait_ge(low_ready, 2 * t + (2 + 3))
                    for kind, name in enumerate(("q_parts", "k_parts")):
                        for part in range(PARTS):
                            to = dram[name].rearrange("(a d) g f -> a g d f", d=C_HD)[part, bass.ts(t, 2 * C_HEADS)]
                            sp.dma_start(to, parts[:, u, kind, part]).then_inc(stored[u], 16)
            for u in range(2):
                sp.wait_ge(stored[u], STORES * (PAIRS + 1))


def feature_attention(core):
    nc, dram, ps, ident = core.nc, core.dram, core.psum, core.ident
    split_parts(core)
    with ExitStack() as scope:
        sb = lambda name, shape, dt=F32: scope.enter_context(nc.sbuf_tensor(f"fa_{name}", shape, dt))
        sem = lambda name: core.sem(f"fa_{name}")
        ident_bf = sb("ident_bf", [P, P], BF16)
        w_out = sb("w_out", [P, P])
        q_stack = sb("q_stack", [P, RING, 2, C_HEADS, E], BF16)
        k_stack = sb("k_stack", [P, RING, 2, C_HEADS, E], BF16)
        values = sb("values", [P, RING, 2, 2 * C_HEADS, V_COLS])
        neg_max = sb("neg_max", [P, 2, 2, C_HEADS])
        ctx_now = sb("ctx_now", [P, RING, E])
        max_rest = sb("max_rest", [P, 2, 2, C_HEADS])
        max_parts = sb("max_parts", [P, 2, 2, PARTS, C_HEADS], BF16)
        max_rows = sb("max_rows", [P, 2, E], BF16)
        probs = sb("probs", [P, 4, 2, 2, E])
        mixedT = sb("mixedT", [P, 2, E])
        inv = sb("inv", [P, 2 * C_HEADS])
        mixed = sb("mixed", [P, 2, 2, C_HEADS * C_HD])
        mixed_c = sb("mixed_c", [P, E])
        below, above, exp_below, selu = sb("below", [P, E]), sb("above", [P, E]), sb("exp_below", [P, E]), sb("selu", [P, E])

        loaded, q_cleared, cleared, zeroed, cleared_values = sem("loaded"), sem("q_cleared"), sem("cleared"), sem("zeroed"), sem("cleared_values")
        ctx_copied = sem("ctx_copied")
        stacked = core.sems("fa_stacked", RING)
        values_psum, values_ready = sem("values_psum"), sem("values_ready")
        max_scored, max_taken = sem("max_scored"), sem("max_taken")
        max_high, max_left, max_mid, max_split = sem("max_high"), sem("max_left"), sem("max_mid"), sem("max_split")
        max_turned, max_rows_ready, max_stacked = sem("max_turned"), sem("max_rows_ready"), core.sems("fa_max_stacked", 2)
        scored, exp_done, mixed_done, mixedT_ready = sem("scored"), sem("exp_done"), sem("mixed_done"), sem("mixedT_ready")
        mixed_rows, inv_ready, mixed_ready = sem("mixed_rows"), sem("inv_ready"), sem("mixed_ready")
        mixed_turned, mixed_c_ready, projected = sem("mixed_turned"), sem("mixed_c_ready"), sem("projected")
        below_ready, above_ready, exp_below_ready, selu_ready = sem("below_ready"), sem("above_ready"), sem("exp_below_ready"), sem("selu_ready")
        x_ready, stats_done = sem("x_ready"), sem("stats_done")
        LOADS = 2 * PARTS * 16
        EXP_CREDIT = 2
        MIX_CREDIT = 2

        block = scope.enter_context(nc.Block())

        def each_tile(eng, step):
            with eng.Fori(0, (TILES - 1) // RING) as i:
                for r in range(RING):
                    step(i, r, True)
            step((TILES - 1) // RING, 0, False)

        @block.sync
        def _(sp):
            sp.dma_start(ident_bf[:], dram["ident_bf"]).then_inc(loaded, 16)
            sp.dma_start(w_out[:], dram["fa_w_out"]).then_inc(loaded, 16)

            def load(t, slot):
                for k in range(PARTS):
                    of = dram["q_parts"][:, bass.ts(t, 2 * C_HEADS), :].rearrange("r g f -> r (g f)")
                    to = q_stack[k * STACK:(k + 1) * STACK, slot].rearrange("p b h f -> p (b h f)")
                    sp.dma_start(to, of).then_inc(stacked[slot], 16)
                for k in range(PARTS):
                    of = dram["k_parts"][k * C_HD:(k + 1) * C_HD, bass.ts(t, 2 * C_HEADS), :].rearrange("d g f -> d (g f)")
                    to = k_stack[k * STACK:(k + 1) * STACK, slot].rearrange("p b h f -> p (b h f)")
                    sp.dma_start(to, of[None].to_broadcast([PARTS, C_HD, 2 * C_HEADS * E])).then_inc(stacked[slot], 16)

            def max_to_stack(t, slot):
                for b in range(2):
                    sp.wait_ge(max_rows_ready, 2 * t + (b + 1))
                    sp.dma_start(q_stack[MAX_ROW:MAX_ROW + PARTS, slot, b], max_rows[0:PARTS * C_HEADS, b]).then_inc(max_stacked[b], 16)

            def step(i, r, more):
                t = RING * i + r
                if more:
                    sp.wait_ge(scored, 8 * t + 1)
                    load(t + 2, (r + 2) % RING)
                max_to_stack(t + 1, (r + 1) % RING)

            sp.wait_ge(q_cleared, 1)
            sp.wait_ge(cleared, 1)
            for t in range(2):
                load(t, t)
            max_to_stack(0, 0)
            rounds = (TILES - 2) // RING
            with sp.Fori(0, rounds) as i:
                for r in range(RING):
                    step(i, r, True)
            for t in range(RING * rounds, TILES - 1):
                step(t // RING, t % RING, t + 2 < TILES)

        @block.vector
        def _(dve):
            nc.vector.memset(k_stack[64:P].rearrange("p s b h f -> p (s b h f)").bitcast(F32), 0.0).then_inc(zeroed, 1)
            dve.wait_ge(zeroed, 1)
            nc.vector.memset(k_stack[MAX_ROW:MAX_ROW + PARTS], 1.0).then_inc(cleared, 1)

            def maxima(t, b):
                for h in range(C_HEADS):
                    dve.wait_ge(max_scored, 16 * t + (8 * b + h + 1))
                    nc.vector.tensor_reduce(neg_max[:, b, :, h], ps[:, h % 2, :].rearrange("p (q k) -> p q k", q=2),
                                            AX.X, ALU.max, negate=True).then_inc(max_taken, 1)
                dve.wait_ge(max_taken, 16 * t + (8 * b + 8))
                k = 2 * t + (b + 1)
                nc.vector.tensor_copy(max_parts[:, b, :, 0], neg_max[:, b]).then_inc(max_high, 1)
                dve.wait_ge(max_high, k)
                nc.vector.tensor_tensor(max_rest[:, b], neg_max[:, b], max_parts[:, b, :, 0], ALU.subtract).then_inc(max_left, 1)
                dve.wait_ge(max_left, k)
                nc.vector.tensor_copy(max_parts[:, b, :, 1], max_rest[:, b]).then_inc(max_mid, 1)
                dve.wait_ge(max_mid, k)
                nc.vector.tensor_tensor(max_parts[:, b, :, 2], max_rest[:, b], max_parts[:, b, :, 1], ALU.subtract).then_inc(max_split, 1)

            def divide(t, b):
                k = 2 * t + (b + 1)
                dve.wait_ge(mixed_rows, k)
                view = ps[:, 6, :].rearrange("p (g c) -> p g c", c=V_COLS)
                nc.vector.reciprocal(inv[:], view[:, :, C_HD]).then_inc(inv_ready, 1)
                dve.wait_ge(inv_ready, k)
                out = mixed[:, :, b].rearrange("p q (h d) -> p q h d", d=C_HD)
                nc.vector.tensor_tensor(out, view[:, :, 0:C_HD].rearrange("p (q h) d -> p q h d", q=2),
                                        inv[:].rearrange("p (q h) -> p q h", q=2)[:, :, :, None].to_broadcast([P, 2, C_HEADS, C_HD]),
                                        ALU.mult).then_inc(mixed_ready, 1)

            def activate(t):
                n = t + 1
                dve.wait_ge(projected, n)
                nc.vector.tensor_scalar(below[:], ps[:, 7, E:2 * E], 0.0, None, ALU.min).then_inc(below_ready, 1)
                nc.vector.tensor_scalar(above[:], ps[:, 7, E:2 * E], 0.0, SELU_SCALE, ALU.max, ALU.mult).then_inc(above_ready, 1)
                dve.wait_ge(exp_below_ready, n)
                dve.wait_ge(above_ready, n + 1)
                nc.vector.scalar_tensor_tensor(selu[:], exp_below[:], SELU_SCALE * SELU_ALPHA, above[:], ALU.mult, ALU.add).then_inc(selu_ready, 1)
                dve.wait_ge(selu_ready, n)
                nc.vector.scalar_tensor_tensor(core.x[:, t, :], selu[:], -SELU_SCALE * SELU_ALPHA, core.x[:, t, :], ALU.add, ALU.add).then_inc(x_ready, 1)
                dve.wait_ge(x_ready, n)
                nc.vector.bn_stats(core.row_stats[:, t, :], core.x[:, t, :]).then_inc(stats_done, 1)

            for b in range(2):
                maxima(0, b)

            def step(i, r, ahead):
                t = RING * i + r
                for b in range(2):
                    if ahead:
                        maxima(t + 1, b)
                    divide(t, b)
                activate(t)

            each_tile(dve, step)
            dve.wait_ge(stats_done, TILES)

        @block.scalar
        def _(act):
            act.sem_inc(exp_done, EXP_CREDIT)

            def values_of(t, slot):
                act.wait_ge(values_psum, t + 1)
                nc.scalar.copy(values[:, slot, :, :, 0:C_HD],
                               ps[:, 7, 0:E].rearrange("p (k g d) -> p k g d", k=2, d=C_HD)).then_inc(values_ready, 1)

            def max_to_rows(t, b):
                act.wait_ge(max_turned, 2 * t + (b + 1))
                nc.scalar.copy(max_rows[0:PARTS * C_HEADS, b], ps[0:PARTS * C_HEADS, 7, 0:E]).then_inc(max_rows_ready, 1)

            def exponentials(t, b, g):
                act.wait_ge(scored, 8 * t + (4 * b + g + 1))
                act.wait_ge(mixed_done, 4 * t + (2 * b + g // 2 + 1))
                nc.scalar.activation(probs[:, g].rearrange("p h k q -> p h (k q)"), ps[:, 2 + 2 * (g % 2):4 + 2 * (g % 2), :], ACT.Exp).then_inc(exp_done, 1)

            act.wait_ge(cleared_values, 3)
            values_of(0, 0)
            for b in range(2):
                max_to_rows(0, b)

            def step(i, r, ahead):
                t = RING * i + r
                if ahead:
                    values_of(t + 1, (r + 1) % RING)
                for b in range(2):
                    for g in range(4):
                        exponentials(t, b, g)
                    if ahead:
                        max_to_rows(t + 1, b)
                    act.wait_ge(mixed_done, 4 * t + (2 * b + 2 + MIX_CREDIT))
                    nc.scalar.copy(mixedT[:], ps[:, 6, :].rearrange("p (k q) -> p k q", k=2)).then_inc(mixedT_ready, 1)
                act.wait_ge(mixed_turned, t + 1)
                nc.scalar.copy(mixed_c[:], ps[:, 7, 0:E]).then_inc(mixed_c_ready, 1)
                act.wait_ge(below_ready, t + 1)
                nc.scalar.activation(exp_below[:], below[:], ACT.Exp).then_inc(exp_below_ready, 1)

            each_tile(act, step)

        @block.gpsimd
        def _(pool):
            nc.gpsimd.memset(values[:], 0.0).then_inc(cleared_values, 1)
            pool.wait_ge(cleared_values, 1)
            nc.gpsimd.memset(values[:, :, :, :, C_HD:C_HD + 1], 1.0).then_inc(cleared_values, 2)
            pool.wait_ge(cleared_values, 3)
            nc.gpsimd.memset(q_stack[64:P].rearrange("p s b h f -> p (s b h f)").bitcast(F32), 0.0).then_inc(q_cleared, 1)
            pool.wait_ge(q_cleared, 1)
            nc.gpsimd.tensor_copy(ctx_now[:, 0], core.context[:, 0, :]).then_inc(ctx_copied, 1)
            with pool.Fori(0, (TILES - 1) // RING) as i:
                for r in range(RING):
                    t = RING * i + r
                    pool.wait_ge(values_psum, t + 1)
                    nc.gpsimd.tensor_copy(ctx_now[:, (r + 1) % RING], core.context[:, t + 1, :]).then_inc(ctx_copied, 1)

        @block.tensor
        def _(pe):
            pe.sem_inc(mixed_done, MIX_CREDIT)
            pe.sem_inc(mixed_ready, 1)
            pe.sem_inc(above_ready, 1)
            pe.wait_ge(loaded, 32)

            def turn_values(t, parity):
                pe.wait_ge(ctx_copied, t + 1)
                if not isinstance(t, int):
                    pe.wait_ge(above_ready, t)
                    pe.wait_ge(max_rows_ready, 2 * t)
                for k in range(2):
                    done = nc.tensor.transpose(ps[:, 7, k * P:(k + 1) * P], ctx_now[:, parity, k * P:(k + 1) * P], ident[:])
                done.then_inc(values_psum, 1)

            def score_for_max(t, slot, b, h):
                head = 8 * b + h
                if not isinstance(t, int) or head >= 2:
                    pe.wait_ge(max_taken, 16 * t + (head - 1))
                for q in range(2):
                    done = nc.tensor.matmul(ps[:, h % 2, q * E:(q + 1) * E], q_stack[0:MAX_ROW, slot, b, h, q * P:(q + 1) * P],
                                            k_stack[0:MAX_ROW, slot, b, h, :], start=True, stop=True)
                done.then_inc(max_scored, 1)

            def turn_max(t, b):
                pe.wait_ge(max_split, 2 * t + (b + 1))
                if b == 0:
                    pe.wait_ge(values_ready, t + 1)
                else:
                    pe.wait_ge(max_rows_ready, 2 * t + 1)
                for q in range(2):
                    done = nc.tensor.matmul(ps[0:PARTS * C_HEADS, 7, q * P:(q + 1) * P],
                                            max_parts[:, b, q].rearrange("p a h -> p (a h)"), ident_bf[:], start=True, stop=True)
                done.then_inc(max_turned, 1)

            def score(t, slot, b, g):
                pe.wait_ge(exp_done, 8 * t + (4 * b + g + 1))
                for h in range(2):
                    for k in range(2):
                        done = nc.tensor.matmul(ps[:, 2 + 2 * (g % 2) + h, k * E:(k + 1) * E],
                                                k_stack[0:STACK_ROWS, slot, b, 2 * g + h, k * P:(k + 1) * P],
                                                q_stack[0:STACK_ROWS, slot, b, 2 * g + h, :], start=True, stop=True)
                done.then_inc(scored, 1)

            def mix(t, slot, b, half):
                pe.wait_ge(exp_done, 8 * t + (4 * b + 2 * half + 2 + EXP_CREDIT))
                if half == 0:
                    pe.wait_ge(mixed_ready, 2 * t + (b + 1))
                    pe.wait_ge(values_ready, t + 1)
                for k in range(2):
                    for c in range(4):
                        h = 4 * half + c
                        done = nc.tensor.matmul(ps[32 * c:32 * c + 32, 6, half * E:(half + 1) * E], values[:, slot, k, 8 * b + h, :],
                                                probs[:, h // 2, h % 2, k, :], start=(k == 0), stop=(k == 1), skip_group_check=True)
                done.then_inc(mixed_done, 1)

            def turn_mixed(t, b):
                pe.wait_ge(mixedT_ready, 2 * t + (b + 1))
                for q in range(2):
                    for half in range(2):
                        done = nc.tensor.transpose(ps[:, 6, (2 * q + half) * P:(2 * q + half + 1) * P],
                                                   mixedT[:, half, q * P:(q + 1) * P], ident[:])
                done.then_inc(mixed_rows, 1)

            def project(t, ahead):
                pe.wait_ge(mixed_ready, 2 * t + (2 + 1))
                if ahead:
                    pe.wait_ge(max_rows_ready, 2 * t + 4)
                else:
                    pe.wait_ge(above_ready, t + 1)
                for q in range(2):
                    done = nc.tensor.transpose(ps[:, 7, q * P:(q + 1) * P], mixed[:, q].rearrange("p b c -> p (b c)"), ident[:])
                done.then_inc(mixed_turned, 1)
                pe.wait_ge(mixed_c_ready, t + 1)
                nc.tensor.matmul(ps[:, 7, E:2 * E], w_out[:], mixed_c[:], start=True, stop=True).then_inc(projected, 1)

            def step(i, r, ahead):
                t, slot, nxt = RING * i + r, r, (r + 1) % RING
                if ahead:
                    turn_values(t + 1, nxt)
                    pe.wait_ge(stacked[nxt], LOADS * i + LOADS * (2 if nxt == 0 else 1))
                for b in range(2):
                    pe.wait_ge(max_stacked[b], 16 * t + 16)
                    for g in range(4):
                        if ahead:
                            score_for_max(t + 1, nxt, b, 2 * g)
                            score_for_max(t + 1, nxt, b, 2 * g + 1)
                        score(t, slot, b, g)
                    for half in range(2):
                        mix(t, slot, b, half)
                    if ahead:
                        turn_max(t + 1, b)
                    turn_mixed(t, b)
                project(t, ahead)

            turn_values(0, 0)
            pe.wait_ge(stacked[0], LOADS)
            for b in range(2):
                for h in range(C_HEADS):
                    score_for_max(0, 0, b, h)
                turn_max(0, b)
            each_tile(pe, step)


F_N, F_S, F_H = 8, 8, 8
F_SEL, F_UPD = F_N * F_S, F_N * F_H
F_IN = F_SEL + F_N + F_UPD
F_MEAN, F_UPD_AT = F_SEL, F_SEL + F_N
F_ROWS = 96
WIDE = 4
EXP_LIMIT = 87.0


def selected_update(core):
    nc, dram, ps, ident = core.nc, core.dram, core.psum, core.ident
    with ExitStack() as scope:
        sb = lambda name, shape, dt=F32: scope.enter_context(nc.sbuf_tensor(f"ff_{name}", shape, dt))
        sem = lambda name: core.sem(f"ff_{name}")
        ln = RowNorm(core, "ff", scope)
        w_in = sb("w_in", [P, KC, F_IN])
        debias = sb("debias", [P, KC, F_N])
        w_back = sb("w_back", [P, E])
        center, slope, first = sb("center", [P, F_N]), sb("slope", [P, F_N]), sb("first", [P, F_N])
        ones = sb("ones", [P, P])
        shift_parts, shift = sb("shift_parts", [P, KC, F_IN]), sb("shift", [P, F_IN])
        xn, xT = sb("xn", [P, WIDE, E]), sb("xT", [P, WIDE, E])
        proj = sb("proj", [P, TILES, F_IN])
        squares = sb("squares", [P, TILES, F_SEL])
        raw, dist, gate, hot = (sb(name, [P, TILES, F_N]) for name in ("raw", "dist", "gate", "hot"))
        length, best, pick, keep, move = (sb(name, [P, TILES]) for name in ("length", "best", "pick", "keep", "move"))
        chosen = sb("chosen", [P, WIDE, F_ROWS])
        chosenT = sb("chosenT", [P, WIDE, P])
        moved = sb("moved", [P, WIDE, E])

        loaded, zeroed, shift_step, shift_psum, shift_ready = (sem(n) for n in ("loaded", "zeroed", "shift_step", "shift_psum", "shift_ready"))
        xn_ready, xT_psum, xT_ready, projected, proj_ready = (sem(n) for n in ("xn_ready", "xT_psum", "xT_ready", "projected", "proj_ready"))
        squares_ready, gate_step, z_ready, gate_exp, hot_ready = (sem(n) for n in ("squares_ready", "gate_step", "z_ready", "gate_exp", "hot_ready"))
        chosen_ready, bias_ready, turned, chosenT_ready, moved_ready, back, x_ready, stats_done = (
            sem(n) for n in ("chosen_ready", "bias_ready", "turned", "chosenT_ready", "moved_ready", "back", "x_ready", "stats_done"))
        LOADS = 6 * 16
        by_update = lambda a, width: a.rearrange("p (n s) -> p n s", s=width)

        block = scope.enter_context(nc.Block())

        @block.sync
        def _(sp):
            for out, src in ((w_in[:], chunked(dram["ff_w_in"])), (debias[:], chunked(dram["ff_debias"])), (w_back[0:F_ROWS], dram["ff_w_back"]),
                             (center[:], dram["ff_center"]), (slope[:], dram["ff_slope"]), (first[:], dram["ff_first"])):
                sp.dma_start(out, src).then_inc(loaded, 16)
            sp.wait_ge(loaded, LOADS)

        @block.gpsimd
        def _(pool):
            nc.gpsimd.memset(chosen[:], 0.0).then_inc(zeroed, 1)
            pool.wait_ge(zeroed, 1)
            pool.wait_ge(hot_ready, 1)
            pool.sem_inc(turned, WIDE)
            with pool.Fori(0, TILES // WIDE) as i:
                for u in range(WIDE):
                    t = WIDE * i + u
                    pool.wait_ge(turned, t + 1)
                    nc.gpsimd.tensor_copy(chosen[:, u, F_UPD:F_UPD + F_N], hot[:, t, :]).then_inc(bias_ready, 1)

        @block.scalar
        def _(act):
            act.preload_act_table_set(EXP_LN)
            ln.on_scalar(act)
            act.wait_ge(shift_psum, 1)
            nc.scalar.copy(shift[:], ps[:, 7, 0:F_IN]).then_inc(shift_ready, 1)
            with act.Fori(0, TILES // WIDE) as i:
                for u in range(WIDE):
                    act.wait_ge(xT_psum, WIDE * i + u + 1)
                    nc.scalar.copy(xT[:, u], ps[:, u, 0:E]).then_inc(xT_ready, 1)
            act.wait_ge(proj_ready, TILES)
            nc.scalar.activation(squares[:], proj[:, :, 0:F_SEL], ACT.Square).then_inc(squares_ready, 1)
            act.wait_ge(z_ready, 1)
            nc.scalar.activation(gate[:], raw[:], ACT.Exp).then_inc(gate_exp, 1)
            with act.Fori(0, TILES // WIDE) as i:
                for u in range(WIDE):
                    act.wait_ge(turned, WIDE * i + u + 1 + WIDE)
                    nc.scalar.copy(chosenT[0:F_ROWS, u], ps[0:F_ROWS, u, 0:P]).then_inc(chosenT_ready, 1)

        @block.vector
        def _(dve):
            ln.on_vector(dve)
            nc.vector.memset(ones[:], 1.0).then_inc(shift_step, 1)
            dve.wait_ge(loaded, LOADS)
            for c in range(KC):
                mean = w_in[:, c, F_MEAN:F_MEAN + F_N]
                nc.vector.tensor_tensor(by_update(shift_parts[:, c, 0:F_SEL], F_S), by_update(w_in[:, c, 0:F_SEL], F_S),
                                        mean[:, :, None].to_broadcast([P, F_N, F_S]), ALU.mult).then_inc(shift_step, 1)
                nc.vector.scalar_tensor_tensor(shift_parts[:, c, F_MEAN:F_MEAN + F_N], mean, 0.5, mean, ALU.mult, ALU.mult).then_inc(shift_step, 1)
                nc.vector.tensor_tensor(by_update(shift_parts[:, c, F_UPD_AT:], F_H), by_update(w_in[:, c, F_UPD_AT:], F_H),
                                        debias[:, c, :, None].to_broadcast([P, F_N, F_H]), ALU.mult).then_inc(shift_step, 1)
            dve.wait_ge(ln.ready, 1)
            dve.wait_ge(shift_ready, 1)
            with dve.Fori(0, TILES // WIDE) as i:
                for u in range(WIDE):
                    ln.normalise(xn[:, u], WIDE * i + u).then_inc(xn_ready, 1)
                for u in range(WIDE):
                    t = WIDE * i + u
                    dve.wait_ge(projected, t + 1)
                    nc.vector.tensor_tensor(proj[:, t, :], ps[:, WIDE + u, 0:F_IN], shift[:], ALU.subtract).then_inc(proj_ready, 1)
            across = lambda a: a[:, :, None].to_broadcast([P, TILES, F_N])
            every = lambda a: a[:, None, :].to_broadcast([P, TILES, F_N])
            nc.vector.tensor_tensor(length[:], ln.rstd[:], ln.rstd[:], ALU.mult).then_inc(gate_step, 1)
            dve.wait_ge(gate_step, 1)
            nc.vector.scalar_tensor_tensor(length[:], length[:], float(E), ln.var[:], ALU.mult, ALU.mult).then_inc(gate_step, 1)
            dve.wait_ge(gate_step, 2)
            dve.wait_ge(proj_ready, TILES)
            nc.vector.scalar_tensor_tensor(dist[:], proj[:, :, F_MEAN:F_MEAN + F_N], -2.0, across(length), ALU.mult, ALU.add).then_inc(gate_step, 1)
            dve.wait_ge(gate_step, 3)
            nc.vector.reciprocal(dist[:], dist[:]).then_inc(gate_step, 1)
            dve.wait_ge(squares_ready, 1)
            nc.vector.tensor_reduce(raw[:], squares[:].rearrange("p t (n s) -> p t n s", s=F_S), AX.X, ALU.add).then_inc(gate_step, 1)
            dve.wait_ge(gate_step, 5)
            nc.vector.tensor_tensor(raw[:], raw[:], dist[:], ALU.mult).then_inc(gate_step, 1)
            dve.wait_ge(gate_step, 6)
            nc.vector.tensor_tensor(raw[:], every(center), raw[:], ALU.subtract).then_inc(gate_step, 1)
            dve.wait_ge(gate_step, 7)
            nc.vector.tensor_tensor(raw[:], raw[:], every(slope), ALU.mult).then_inc(gate_step, 1)
            dve.wait_ge(gate_step, 8)
            nc.vector.tensor_scalar(raw[:], raw[:], EXP_LIMIT, None, ALU.min).then_inc(z_ready, 1)
            dve.wait_ge(gate_exp, 1)
            nc.vector.tensor_scalar(gate[:], gate[:], 1.0, None, ALU.add).then_inc(gate_step, 1)
            dve.wait_ge(gate_step, 9)
            nc.vector.reciprocal(gate[:], gate[:]).then_inc(gate_step, 1)
            dve.wait_ge(gate_step, 10)
            nc.vector.tensor_reduce(best[:], gate[:], AX.X, ALU.max).then_inc(gate_step, 1)
            dve.wait_ge(gate_step, 11)
            nc.vector.tensor_tensor(gate[:], gate[:], across(best), ALU.is_ge).then_inc(gate_step, 1)
            nc.vector.tensor_scalar(keep[:], best[:], -1.0, 1.0, ALU.mult, ALU.add).then_inc(gate_step, 1)
            dve.wait_ge(gate_step, 13)
            nc.vector.tensor_tensor(gate[:], gate[:], every(first), ALU.mult).then_inc(gate_step, 1)
            nc.vector.tensor_tensor(keep[:], keep[:], ln.rstd[:], ALU.mult).then_inc(gate_step, 1)
            dve.wait_ge(gate_step, 15)
            nc.vector.tensor_reduce(pick[:], gate[:], AX.X, ALU.max).then_inc(gate_step, 1)
            nc.vector.tensor_tensor(move[:], ln.mean[:], keep[:], ALU.mult).then_inc(gate_step, 1)
            dve.wait_ge(gate_step, 17)
            nc.vector.tensor_tensor(hot[:], gate[:], across(pick), ALU.is_equal).then_inc(gate_step, 1)
            nc.vector.tensor_scalar(keep[:], keep[:], 1.0, None, ALU.add).then_inc(gate_step, 1)
            dve.wait_ge(gate_step, 19)
            nc.vector.tensor_tensor(hot[:], hot[:], across(best), ALU.mult).then_inc(hot_ready, 1)
            dve.wait_ge(hot_ready, 1)
            dve.wait_ge(zeroed, 1)
            with dve.Fori(0, TILES // WIDE) as i:
                for u in range(WIDE):
                    t = WIDE * i + u
                    nc.vector.tensor_tensor(by_update(chosen[:, u, 0:F_UPD], F_H), by_update(proj[:, t, F_UPD_AT:], F_H),
                                            hot[:, t, :, None].to_broadcast([P, F_N, F_H]), ALU.mult).then_inc(chosen_ready, 1)
                for u in range(WIDE):
                    t = WIDE * i + u
                    nc.vector.tensor_scalar(moved[:, u], core.x[:, t, :], keep[:, bass.ts(t, 1)], move[:, bass.ts(t, 1)],
                                            ALU.mult, ALU.subtract).then_inc(moved_ready, 1)
                for u in range(WIDE):
                    t = WIDE * i + u
                    dve.wait_ge(back, t + 1)
                    dve.wait_ge(moved_ready, t + 1)
                    nc.vector.tensor_tensor(core.x[:, t, :], moved[:, u], ps[:, WIDE + u, 0:E], ALU.add).then_inc(x_ready, 1)
                for u in range(WIDE):
                    t = WIDE * i + u
                    dve.wait_ge(x_ready, t + 1)
                    nc.vector.bn_stats(core.row_stats[:, t, :], core.x[:, t, :]).then_inc(stats_done, 1)
            dve.wait_ge(stats_done, TILES)

        @block.tensor
        def _(pe):
            pe.wait_ge(loaded, LOADS)
            pe.wait_ge(shift_step, 1 + 3 * KC)
            for c in range(KC):
                done = nc.tensor.matmul(ps[:, 7, 0:F_IN], ones[:], shift_parts[:, c], start=(c == 0), stop=(c == KC - 1))
            done.then_inc(shift_psum, 1)
            pe.wait_ge(shift_ready, 1)
            with pe.Fori(0, TILES // WIDE) as i:
                for u in range(WIDE):
                    pe.wait_ge(xn_ready, WIDE * i + u + 1)
                    for c in range(KC):
                        done = nc.tensor.transpose(ps[:, u, c * P:(c + 1) * P], xn[:, u, c * P:(c + 1) * P], ident[:])
                    done.then_inc(xT_psum, 1)
                for u in range(WIDE):
                    pe.wait_ge(xT_ready, WIDE * i + u + 1)
                    for c in range(KC):
                        done = nc.tensor.matmul(ps[:, WIDE + u, 0:F_IN], xT[:, u, c * P:(c + 1) * P], w_in[:, c],
                                                start=(c == 0), stop=(c == KC - 1))
                    done.then_inc(projected, 1)
            with pe.Fori(0, TILES // WIDE) as i:
                for u in range(WIDE):
                    pe.wait_ge(chosen_ready, WIDE * i + u + 1)
                    pe.wait_ge(bias_ready, WIDE * i + u + 1)
                    nc.tensor.transpose(ps[0:F_ROWS, u, 0:P], chosen[:, u], ident[:]).then_inc(turned, 1)
                for u in range(WIDE):
                    pe.wait_ge(chosenT_ready, WIDE * i + u + 1)
                    nc.tensor.matmul(ps[:, WIDE + u, 0:E], chosenT[0:F_ROWS, u], w_back[0:F_ROWS], start=True, stop=True).then_inc(back, 1)

S_HEADS, S_STATE = 32, 64
S_HD = E // S_HEADS
LEVELS = SEQ.bit_length() - 1


def state_space(core):
    nc, dram, ps, ident = core.nc, core.dram, core.psum, core.ident
    with ExitStack() as scope:
        sb = lambda name, shape, dt=F32: scope.enter_context(nc.sbuf_tensor(f"ss_{name}", shape, dt))
        sem = lambda name: core.sem(f"ss_{name}")
        ln = RowNorm(core, "ss", scope)
        w_bc = sb("w_bc", [P, KC, 2 * S_STATE])
        w_dt, w_out = sb("w_dt", [P, KC, S_HEADS]), sb("w_out", [P, KC, E])
        bias_bc = sb("bias_bc", [S_STATE, 2])
        bias_dt, skip, rate, bias_out = sb("bias_dt", [P, S_HEADS]), sb("skip", [P, S_HEADS]), sb("rate", [P, S_HEADS]), sb("bias_out", [P, E])
        spans = sb("spans", [P, LEVELS, P])
        pairs = sb("pairs", [P, LEVELS, P])
        xn, xT = sb("xn", [P, 2, E]), sb("xT", [P, 2, E])
        bcT = sb("bcT", [S_STATE, 2, 2, P])
        dt, dt_tail, dA = (sb(name, [P, TILES, S_HEADS]) for name in ("dt", "dt_tail", "dA"))
        scoresT = sb("scoresT", [P, TILES, P])
        same, same_dot = sb("same", [P, TILES, P]), sb("same_dot", [P, TILES])
        own = sb("own", [P, TILES, S_HEADS])
        decay = sb("decay", [P, TILES, LEVELS, S_HEADS])
        level_scores = sb("level_scores", [P, 2, LEVELS, P])
        xdt, inputs = sb("xdt", [P, 2, E]), sb("inputs", [P, 2, LEVELS, E])
        own_rows, outputs = sb("own_rows", [P, 2, E]), sb("outputs", [P, 2, LEVELS, E])
        yT = sb("yT", [P, 2, E])

        loaded = sem("loaded")
        xn_ready, xT_psum, xT_ready, projected, bc_ready, dt_raw, scored, scores_ready = (
            sem(n) for n in ("xn_ready", "xT_psum", "xT_ready", "projected", "bc_ready", "dt_raw", "scored", "scores_ready"))
        soft_step, tail_exp, tail_log, rate_ready, dA_ready, spans_psum, decay_ready, own_step = (
            sem(n) for n in ("soft_step", "tail_exp", "tail_log", "rate_ready", "dA_ready", "spans_psum", "decay_ready", "own_step"))
        pool_step, inputs_ready, own_ready, biased, level_ready, level_psum, outputs_ready, y_psum, yT_ready, out_psum, x_ready, stats_done = (
            sem(n) for n in ("pool_step", "inputs_ready", "own_ready", "biased", "level_ready", "level_psum", "outputs_ready",
                             "y_psum", "yT_ready", "out_psum", "x_ready", "stats_done"))
        LOADS = 10 * 16
        by_head = lambda a: a.rearrange("p (h d) -> p h d", d=S_HD)
        per_head = lambda a: a[:, :, None].to_broadcast([P, S_HEADS, S_HD])

        block = scope.enter_context(nc.Block())

        @block.sync
        def _(sp):
            for out, src in ((w_bc[:], chunked(dram["ss_w_bc"])), (w_dt[:], chunked(dram["ss_w_dt"])), (w_out[:], chunked(dram["ss_w_out"])),
                             (bias_bc[:], dram["ss_bias_bc"]), (bias_dt[:], dram["ss_bias_dt"]), (skip[:], dram["ss_skip"]),
                             (rate[:], dram["ss_A_log"]), (bias_out[:], dram["ss_bias_out"]), (spans[:], dram["ss_spans"]),
                             (pairs[:], dram["ss_pairs"])):
                sp.dma_start(out, src).then_inc(loaded, 16)
            sp.wait_ge(loaded, LOADS)

        @block.gpsimd
        def _(pool):
            pool.wait_ge(own_step, 4)
            pool.wait_ge(decay_ready, LEVELS)
            with pool.Fori(0, PAIRS) as i:
                for u in range(2):
                    t = 2 * i + u
                    pool.wait_ge(xn_ready, t + (TILES + 1))
                    nc.gpsimd.tensor_tensor(by_head(xdt[:, u]), by_head(xn[:, u]), per_head(dt[:, t, :]), ALU.mult).then_inc(pool_step, 1)
                    pool.wait_ge(pool_step, t + 1)
                    nc.gpsimd.tensor_tensor(inputs[:, u].rearrange("p m (h d) -> p m h d", d=S_HD),
                                            by_head(xdt[:, u])[:, None].to_broadcast([P, LEVELS, S_HEADS, S_HD]),
                                            decay[:, t, :, :, None].to_broadcast([P, LEVELS, S_HEADS, S_HD]), ALU.mult).then_inc(inputs_ready, 1)
                for u in range(2):
                    t = 2 * i + u
                    nc.gpsimd.tensor_tensor(by_head(own_rows[:, u]), by_head(xn[:, u]), per_head(own[:, t, :]), ALU.mult).then_inc(own_ready, 1)
                    nc.gpsimd.tensor_tensor(core.x[:, t, :], core.x[:, t, :], bias_out[:], ALU.add).then_inc(biased, 1)

        @block.scalar
        def _(act):
            act.preload_act_table_set(EXP_LN)
            ln.on_scalar(act)
            act.wait_ge(loaded, LOADS)
            nc.scalar.activation(rate[:], rate[:], ACT.Exp).then_inc(rate_ready, 1)
            with act.Fori(0, PAIRS) as i:
                ns = [act.snap(2 * i + (u + 1)) for u in range(2)]
                for u, n in enumerate(ns):
                    act.wait_ge(xT_psum, n)
                    nc.scalar.copy(xT[:, u], ps[:, u, 0:E]).then_inc(xT_ready, 1)
                for u, n in enumerate(ns):
                    act.wait_ge(projected, n)
                    for k in range(2):
                        done = nc.scalar.activation(bcT[:, u, k], ps[0:S_STATE, 2 + u, k * P:(k + 1) * P], ACT.Identity, bias=bias_bc[:, k:k + 1])
                    done.then_inc(bc_ready, 1)
                for u, n in enumerate(ns):
                    act.wait_ge(scored, n)
                    nc.scalar.copy(scoresT[:, 2 * i + u, :], ps[:, 6 + u, 0:P]).then_inc(scores_ready, 1)
            act.wait_ge(soft_step, 1)
            nc.scalar.activation(dt_tail[:], dt_tail[:], ACT.Exp, scale=-1.0).then_inc(tail_exp, 1)
            act.wait_ge(tail_exp, 1)
            nc.scalar.activation(dt_tail[:], dt_tail[:], ACT.Ln, bias=1.0).then_inc(tail_log, 1)
            for m in range(LEVELS):
                act.wait_ge(spans_psum, m + 1)
                nc.scalar.activation(decay[:, :, m, :], ps[:, m, :].rearrange("p (t h) -> p t h", h=S_HEADS), ACT.Exp).then_inc(decay_ready, 1)
            with act.Fori(0, PAIRS) as i:
                for u in range(2):
                    act.wait_ge(y_psum, 2 * i + (u + 1))
                    nc.scalar.copy(yT[:, u], ps[:, 6 + u, 0:E]).then_inc(yT_ready, 1)

        @block.vector
        def _(dve):
            ln.on_vector(dve)
            dve.wait_ge(ln.ready, 1)
            dve.wait_ge(loaded, LOADS)
            with dve.Fori(0, PAIRS) as i:
                for u in range(2):
                    ln.normalise(xn[:, u], 2 * i + u).then_inc(xn_ready, 1)
                for u in range(2):
                    dve.wait_ge(projected, 2 * i + (u + 1))
                    nc.vector.tensor_tensor(dt[:, 2 * i + u, :], ps[:, 4 + u, 0:S_HEADS], bias_dt[:], ALU.add).then_inc(dt_raw, 1)
            every = lambda a: a[:, None, :].to_broadcast([P, TILES, S_HEADS])
            dve.wait_ge(dt_raw, TILES)
            nc.vector.scalar_tensor_tensor(dt_tail[:], dt[:], -1.0, dt[:], ALU.mult, ALU.max).then_inc(soft_step, 1)
            dve.wait_ge(tail_log, 1)
            nc.vector.scalar_tensor_tensor(dt[:], dt[:], 0.0, dt_tail[:], ALU.max, ALU.add).then_inc(soft_step, 1)
            dve.wait_ge(soft_step, 2)
            dve.wait_ge(rate_ready, 1)
            nc.vector.scalar_tensor_tensor(dA[:], dt[:], -1.0, every(rate), ALU.mult, ALU.mult).then_inc(dA_ready, 1)
            dve.wait_ge(scores_ready, TILES)
            nc.vector.tensor_tensor(same[:], scoresT[:], ident[:, None, :].to_broadcast([P, TILES, P]), ALU.mult).then_inc(own_step, 1)
            dve.wait_ge(own_step, 1)
            nc.vector.tensor_reduce(same_dot[:], same[:], AX.X, ALU.add).then_inc(own_step, 1)
            dve.wait_ge(own_step, 2)
            nc.vector.tensor_tensor(own[:], dt[:], same_dot[:, :, None].to_broadcast([P, TILES, S_HEADS]), ALU.mult).then_inc(own_step, 1)
            dve.wait_ge(own_step, 3)
            nc.vector.tensor_tensor(own[:], own[:], every(skip), ALU.add).then_inc(own_step, 1)
            dve.wait_ge(decay_ready, LEVELS)
            with dve.Fori(0, PAIRS) as i:
                for u in range(2):
                    ln.normalise(xn[:, u], 2 * i + u).then_inc(xn_ready, 1)
                for u in range(2):
                    nc.vector.tensor_tensor(level_scores[:, u], pairs[:], scoresT[:, 2 * i + u, None, :].to_broadcast([P, LEVELS, P]),
                                            ALU.mult).then_inc(level_ready, 1)
                for u in range(2):
                    t = 2 * i + u
                    dve.wait_ge(level_psum, t + 1)
                    nc.vector.tensor_tensor(outputs[:, u].rearrange("p m (h d) -> p m h d", d=S_HD),
                                            ps[:, 3 * u:3 * u + 3, :].rearrange("p k (m h d) -> p (k m) h d", m=2, d=S_HD),
                                            decay[:, t, :, :, None].to_broadcast([P, LEVELS, S_HEADS, S_HD]), ALU.mult).then_inc(outputs_ready, 1)
                for u in range(2):
                    t = 2 * i + u
                    dve.wait_ge(out_psum, t + 1)
                    dve.wait_ge(biased, t + 1)
                    nc.vector.tensor_tensor(core.x[:, t, :], core.x[:, t, :], ps[:, 6 + u, E:2 * E], ALU.add).then_inc(x_ready, 1)
                    dve.wait_ge(x_ready, t + 1)
                    nc.vector.bn_stats(core.row_stats[:, t, :], core.x[:, t, :]).then_inc(stats_done, 1)
            dve.wait_ge(stats_done, TILES)

        @block.tensor
        def _(pe):
            pe.wait_ge(loaded, LOADS)
            with pe.Fori(0, PAIRS) as i:
                ns = [pe.snap(2 * i + (u + 1)) for u in range(2)]
                for u, n in enumerate(ns):
                    pe.wait_ge(xn_ready, n)
                    for c in range(KC):
                        done = nc.tensor.transpose(ps[:, u, c * P:(c + 1) * P], xn[:, u, c * P:(c + 1) * P], ident[:])
                    done.then_inc(xT_psum, 1)
                for u, n in enumerate(ns):
                    pe.wait_ge(xT_ready, n)
                    rows = lambda c: xT[:, u, c * P:(c + 1) * P]
                    for k in range(2):
                        for c in range(KC):
                            nc.tensor.matmul(ps[0:S_STATE, 2 + u, k * P:(k + 1) * P], w_bc[:, c, k * S_STATE:(k + 1) * S_STATE], rows(c),
                                             start=(c == 0), stop=(c == KC - 1))
                    for c in range(KC):
                        done = nc.tensor.matmul(ps[:, 4 + u, 0:S_HEADS], rows(c), w_dt[:, c], start=(c == 0), stop=(c == KC - 1))
                    done.then_inc(projected, 1)
                for u, n in enumerate(ns):
                    pe.wait_ge(bc_ready, n)
                    nc.tensor.matmul(ps[:, 6 + u, 0:P], bcT[:, u, 0], bcT[:, u, 1], start=True, stop=True).then_inc(scored, 1)
            pe.wait_ge(dA_ready, 1)
            pe.wait_ge(bc_ready, TILES)
            for m in range(LEVELS):
                nc.tensor.matmul(ps[:, m, :], spans[:, m], dA[:].rearrange("p t h -> p (t h)"), start=True, stop=True).then_inc(spans_psum, 1)
            with pe.Fori(0, PAIRS) as i:
                ns = [pe.snap(2 * i + (u + 1)) for u in range(2)]
                for u, n in enumerate(ns):
                    pe.wait_ge(level_ready, n)
                    pe.wait_ge(inputs_ready, n)
                    for m in range(LEVELS):
                        done = nc.tensor.matmul(ps[:, 3 * u + m // 2, (m % 2) * E:(m % 2 + 1) * E], level_scores[:, u, m], inputs[:, u, m],
                                                start=True, stop=True)
                    done.then_inc(level_psum, 1)
                for u, n in enumerate(ns):
                    pe.wait_ge(own_ready, n)
                    pe.wait_ge(outputs_ready, n)
                    for c in range(KC):
                        y = ps[:, 6 + u, c * P:(c + 1) * P]
                        nc.tensor.matmul(y, own_rows[:, u, c * P:(c + 1) * P], ident[:], start=True, stop=False)
                        for m in range(LEVELS):
                            done = nc.tensor.matmul(y, outputs[:, u, m, c * P:(c + 1) * P], ident[:], start=False, stop=(m == LEVELS - 1))
                    done.then_inc(y_psum, 1)
                for u, n in enumerate(ns):
                    pe.wait_ge(yT_ready, n)
                    for c in range(KC):
                        done = nc.tensor.matmul(ps[:, 6 + u, E:2 * E], yT[:, u, c * P:(c + 1) * P], w_out[:, c],
                                                start=(c == 0), stop=(c == KC - 1))
                    done.then_inc(out_psum, 1)

G_HEADS, G_KV, G_HD = 16, 4, 128
G_GROUP = G_HEADS // G_KV
Q_COLS, KV_COLS = G_HEADS * G_HD, G_KV * G_HD
G_CHUNK = Q_COLS // G_KV


def grouped_attention(core):
    nc, dram, ps, ident = core.nc, core.dram, core.psum, core.ident
    with ExitStack() as scope:
        sb = lambda name, shape, dt=F32: scope.enter_context(nc.sbuf_tensor(f"ga_{name}", shape, dt))
        sem = lambda name: core.sem(f"ga_{name}")
        ln = RowNorm(core, "ga", scope)
        w_q, w_k, w_v = sb("w_q", [P, KC, Q_COLS]), sb("w_k", [P, KC, KV_COLS]), sb("w_v", [P, KC, KV_COLS])
        w_o = sb("w_o", [P, G_HEADS, E])
        bias_q, bias_v, bias_k = sb("bias_q", [P, Q_COLS]), sb("bias_v", [P, KV_COLS]), sb("bias_k", [P, G_KV])
        gain_q, gain_k, gain = sb("gain_q", [P, 1]), sb("gain_k", [P, 1]), sb("gain", [P, 1])
        mask = sb("mask", [P, SEQ])
        ones, rms_eps = sb("ones", [P, P]), sb("rms_eps", [P, 1])
        xn, xT, ctxT = sb("xn", [P, E]), sb("xT", [P, E]), sb("ctxT", [P, KC, P])
        q, squares = sb("q", [P, Q_COLS]), sb("squares", [P, Q_COLS])
        q_sum, q_log, q_inv = sb("q_sum", [P, G_HEADS]), sb("q_log", [P, G_HEADS]), sb("q_inv", [P, G_HEADS])
        diag = sb("diag", [P, G_HEADS, P])
        qT = sb("qT", [P, G_HEADS, P])
        k_raw, k_squares, k_log, k_inv, kT = (sb(name, [P, KV_COLS]) for name in ("k_raw", "k_squares", "k_log", "k_inv", "kT"))
        values = sb("values", [P, 2, KV_COLS])
        scoresT = sb("scoresT", [P, G_HEADS * SEQ])
        probs = sb("probs", [P, G_HEADS, SEQ])
        top, total, inv = sb("top", [P, G_HEADS]), sb("total", [P, G_HEADS]), sb("inv", [P, G_HEADS])
        probsT = sb("probsT", [P, G_HEADS * SEQ])
        mixedT = sb("mixedT", [P, G_HEADS, P])

        loaded, consts_set, zeroed, ctx_ready = sem("loaded"), sem("consts_set"), sem("zeroed"), sem("ctx_ready")
        xn_ready, xT_psum, xT_ready, q_psum, q_ready, squares_ready, q_sums, q_logs, q_invs, diag_ready, qT_psum, qT_ready = (
            sem(n) for n in ("xn_ready", "xT_psum", "xT_ready", "q_psum", "q_ready", "squares_ready", "q_sums", "q_logs", "q_invs",
                             "diag_ready", "qT_psum", "qT_ready"))
        k_psum, k_ready, k_squared, k_sums, k_logs, k_invs, kT_ready, v_psum, v_ready = (
            sem(n) for n in ("k_psum", "k_ready", "k_squared", "k_sums", "k_logs", "k_invs", "kT_ready", "v_psum", "v_ready"))
        scored, scoresT_ready, turned, masked, top_ready, shifted, exp_done, totals, inv_ready, probs_ready = (
            sem(n) for n in ("scored", "scoresT_ready", "turned", "masked", "top_ready", "shifted", "exp_done", "totals", "inv_ready", "probs_ready"))
        probsT_psum, probsT_ready, mixed_psum, mixed_ready, out_psum, x_ready, stats_done = (
            sem(n) for n in ("probsT_psum", "probsT_ready", "mixed_psum", "mixed_ready", "out_psum", "x_ready", "stats_done"))
        LOADS = 11 * 16

        block = scope.enter_context(nc.Block())

        def pipeline(eng, project, step):
            project(0)
            with eng.Fori(0, TILES - 1) as t:
                step(t, True)
            step(TILES - 1, False)

        @block.sync
        def _(sp):
            for out, src in ((w_q[:], chunked(dram["ga_w_q"])), (bias_q[:], dram["ga_bias_q"].to_broadcast([P, Q_COLS])),
                             (w_k[:], chunked(dram["ga_w_k"])), (w_v[:], chunked(dram["ga_w_v"])), (w_o[:], chunked(dram["ga_w_o"])),
                             (bias_v[:], dram["ga_bias_v"].to_broadcast([P, KV_COLS])), (bias_k[:], dram["ga_bias_k"]),
                             (gain_q[:], dram["ga_gain_q"]), (gain_k[:], dram["ga_gain_k"]),
                             (mask[0:SEQ], dram["mask"]), (mask[SEQ:P], dram["mask"])):
                sp.dma_start(out, src).then_inc(loaded, 16)
            ctx_rows = chunked(dram["ctxT"])
            sp.dma_start(ctxT[:], ctx_rows[:, :, 0:P]).then_inc(ctx_ready, 16)
            with sp.Fori(0, TILES - 1) as t:
                sp.wait_ge(v_psum, t + 1)
                sp.dma_start(ctxT[:], ctx_rows[:, :, bass.ts(t + 1, P)]).then_inc(ctx_ready, 16)
            sp.wait_ge(ctx_ready, 16 * TILES)
            sp.wait_ge(loaded, LOADS)

        @block.gpsimd
        def _(pool):
            nc.gpsimd.memset(values[:], 0.0).then_inc(zeroed, 1)
            pool.wait_ge(zeroed, 1)

            def squared_keys(n):
                pool.wait_ge(k_ready, n + 1)
                nc.gpsimd.tensor_tensor(k_squares[:], k_raw[:], k_raw[:], ALU.mult).then_inc(k_squared, 1)

            def diagonals(n):
                pool.wait_ge(q_invs, n + 1)
                nc.gpsimd.tensor_tensor(diag[:], ident[:, None, :].to_broadcast([P, G_HEADS, P]),
                                        q_inv[:, :, None].to_broadcast([P, G_HEADS, P]), ALU.mult).then_inc(diag_ready, 1)

            def project(n):
                squared_keys(n)
                diagonals(n)

            def step(t, ahead):
                if ahead:
                    project(t + 1)

            pipeline(pool, project, step)

        @block.scalar
        def _(act):
            act.preload_act_table_set(EXP_LN)
            ln.on_scalar(act)
            act.wait_ge(loaded, LOADS)
            act.wait_ge(consts_set, 1)
            act.sem_inc(mixed_ready, G_KV)

            def rows(n):
                act.wait_ge(xT_psum, n + 1)
                nc.scalar.copy(xT[:], ps[:, 2, 0:E]).then_inc(xT_ready, 1)

            def square(n, g):
                act.wait_ge(q_ready, 4 * n + (g + 1))
                nc.scalar.activation(squares[:, g * G_CHUNK:(g + 1) * G_CHUNK], q[:, g * G_CHUNK:(g + 1) * G_CHUNK], ACT.Square).then_inc(squares_ready, 1)

            def keys(n):
                act.wait_ge(k_psum, n + 1)
                for j in range(G_KV):
                    done = nc.scalar.activation(k_raw[:, j * P:(j + 1) * P], ps[:, 2, j * P:(j + 1) * P], ACT.Identity, bias=bias_k[:, j:j + 1])
                done.then_inc(k_ready, 1)

            def query_rms(n):
                act.wait_ge(q_sums, n + 1)
                nc.scalar.activation(q_log[:], q_sum[:], ACT.Ln, bias=rms_eps[:], scale=1.0 / G_HD).then_inc(q_logs, 1)
                act.wait_ge(q_logs, n + 1)
                nc.scalar.activation(q_inv[:], q_log[:], ACT.Exp, scale=-0.5).then_inc(q_invs, 1)

            def key_rms(n):
                act.wait_ge(k_sums, n + 1)
                nc.scalar.activation(k_log[:], ps[:, 2, :], ACT.Ln, bias=rms_eps[:], scale=1.0 / G_HD).then_inc(k_logs, 1)
                act.wait_ge(k_logs, n + 1)
                nc.scalar.activation(k_inv[:], k_log[:], ACT.Exp, scale=-0.5).then_inc(k_invs, 1)

            def queries(n):
                for g in range(G_KV):
                    act.wait_ge(qT_psum, 4 * n + (g + 1))
                    nc.scalar.copy(qT[:, 4 * g:4 * g + 4].rearrange("p h t -> p (h t)"), ps[:, g % 2, :]).then_inc(qT_ready, 1)

            def project(n):
                rows(n)
                for g in range(G_KV):
                    square(n, g)
                keys(n)
                query_rms(n)
                key_rms(n)
                queries(n)

            def step(t, ahead):
                if ahead:
                    rows(t + 1)
                act.wait_ge(scored, t + 1)
                nc.scalar.copy(scoresT[:].rearrange("p (b c) -> p b c", b=2), ps[:, 4:6, :]).then_inc(scoresT_ready, 1)
                if ahead:
                    square(t + 1, 0)
                    square(t + 1, 1)
                act.wait_ge(shifted, t + 1)
                nc.scalar.activation(probs[:], probs[:], ACT.Exp).then_inc(exp_done, 1)
                if ahead:
                    square(t + 1, 2)
                    square(t + 1, 3)
                    keys(t + 1)
                act.wait_ge(probsT_psum, t + 1)
                nc.scalar.copy(probsT[:].rearrange("p (b c) -> p b c", b=2), ps[:, 4:6, :]).then_inc(probsT_ready, 1)
                if ahead:
                    query_rms(t + 1)
                    key_rms(t + 1)
                for j in range(G_KV):
                    act.wait_ge(mixed_psum, 4 * t + (j + 1))
                    nc.scalar.copy(mixedT[:, 4 * j:4 * j + 4].rearrange("p h (b t) -> p b h t", b=2),
                                   ps[:, 4 + j % 2, :].rearrange("p (b h t) -> p b h t", b=2, h=G_GROUP)).then_inc(mixed_ready, 1)
                if ahead:
                    queries(t + 1)

            pipeline(act, project, step)

        @block.vector
        def _(dve):
            ln.on_vector(dve)
            nc.vector.memset(ones[:], 1.0)
            nc.vector.memset(rms_eps[:], RMS_EPS).then_inc(consts_set, 1)
            dve.wait_ge(loaded, LOADS)
            nc.vector.scalar_tensor_tensor(gain[:], gain_q[:], float(np.float32(1.0) / np.sqrt(np.float32(G_HD))), gain_k[:],
                                           ALU.mult, ALU.mult).then_inc(consts_set, 1)
            dve.wait_ge(consts_set, 2)
            dve.wait_ge(zeroed, 1)
            dve.wait_ge(ln.ready, 1)

            def rows(n):
                ln.normalise(xn[:], n).then_inc(xn_ready, 1)

            def biased(n, g):
                dve.wait_ge(q_psum, 4 * n + (g + 1))
                nc.vector.tensor_tensor(q[:, g * G_CHUNK:(g + 1) * G_CHUNK], ps[:, g % 2, :], bias_q[:, g * G_CHUNK:(g + 1) * G_CHUNK],
                                        ALU.add).then_inc(q_ready, 1)

            def query_sums(n):
                dve.wait_ge(squares_ready, 4 * n + 4)
                nc.vector.tensor_reduce(q_sum[:], squares[:].rearrange("p (h d) -> p h d", d=G_HD), AX.X, ALU.add).then_inc(q_sums, 1)

            def keys(n):
                dve.wait_ge(k_invs, n + 1)
                nc.vector.scalar_tensor_tensor(kT[:], k_raw[:], gain[:], k_inv[:], ALU.mult, ALU.mult).then_inc(kT_ready, 1)

            def value_rows(n):
                dve.wait_ge(v_psum, n + 1)
                for b in range(2):
                    half = slice(SEQ * b, SEQ * b + SEQ)
                    done = nc.vector.tensor_tensor(values[half, b, :], ps[half, 3, :], bias_v[half], ALU.add)
                done.then_inc(v_ready, 1)

            def project(n):
                rows(n)
                for g in range(G_KV):
                    biased(n, g)
                query_sums(n)
                keys(n)
                value_rows(n)

            def step(t, ahead):
                if ahead:
                    rows(t + 1)
                    biased(t + 1, 0)
                    biased(t + 1, 1)
                across = lambda a: a[:, :, None].to_broadcast([P, G_HEADS, SEQ])
                dve.wait_ge(turned, t + 1)
                nc.vector.tensor_tensor(probs[:], ps[:, 6:8, :].rearrange("p k (h s) -> p (k h) s", s=SEQ),
                                        mask[:, None, :].to_broadcast([P, G_HEADS, SEQ]), ALU.add).then_inc(masked, 1)
                dve.wait_ge(masked, t + 1)
                nc.vector.tensor_reduce(top[:], probs[:], AX.X, ALU.max).then_inc(top_ready, 1)
                dve.wait_ge(top_ready, t + 1)
                nc.vector.tensor_tensor(probs[:], probs[:], across(top), ALU.subtract).then_inc(shifted, 1)
                if ahead:
                    biased(t + 1, 2)
                    biased(t + 1, 3)
                dve.wait_ge(exp_done, t + 1)
                nc.vector.tensor_reduce(total[:], probs[:], AX.X, ALU.add).then_inc(totals, 1)
                dve.wait_ge(totals, t + 1)
                nc.vector.reciprocal(inv[:], total[:]).then_inc(inv_ready, 1)
                dve.wait_ge(inv_ready, t + 1)
                nc.vector.tensor_tensor(probs[:], probs[:], across(inv), ALU.mult).then_inc(probs_ready, 1)
                if ahead:
                    query_sums(t + 1)
                    keys(t + 1)
                dve.wait_ge(out_psum, t + 1)
                nc.vector.tensor_tensor(core.x[:, t, :], core.x[:, t, :], ps[:, 6, 0:E], ALU.add).then_inc(x_ready, 1)
                dve.wait_ge(x_ready, t + 2)
                nc.vector.bn_stats(core.row_stats[:, t, :], core.x[:, t, :]).then_inc(stats_done, 1)
                if ahead:
                    value_rows(t + 1)

            dve.sem_inc(x_ready, 1)
            pipeline(dve, project, step)
            dve.wait_ge(stats_done, TILES)

        @block.tensor
        def _(pe):
            pe.wait_ge(loaded, LOADS)
            pe.wait_ge(consts_set, 2)

            def rows(n):
                pe.wait_ge(xn_ready, n + 1)
                if not isinstance(n, int):
                    pe.wait_ge(k_logs, n)
                for c in range(KC):
                    done = nc.tensor.transpose(ps[:, 2, c * P:(c + 1) * P], xn[:, c * P:(c + 1) * P], ident[:])
                done.then_inc(xT_psum, 1)

            def query(n, g):
                if g == 0:
                    pe.wait_ge(xT_ready, n + 1)
                if g >= 2:
                    pe.wait_ge(q_ready, 4 * n + (g - 1))
                elif not isinstance(n, int):
                    pe.wait_ge(qT_ready, 4 * n - 1 + g)
                for c in range(KC):
                    done = nc.tensor.matmul(ps[:, g % 2, :], xT[:, c * P:(c + 1) * P], w_q[:, c, g * G_CHUNK:(g + 1) * G_CHUNK],
                                            start=(c == 0), stop=(c == KC - 1))
                done.then_inc(q_psum, 1)

            def keys(n):
                pe.wait_ge(ctx_ready, 16 * n + 16)
                pe.wait_ge(xT_ready, n + 1)
                for j in range(G_KV):
                    for c in range(KC):
                        done = nc.tensor.matmul(ps[:, 2, j * P:(j + 1) * P], w_k[:, c, j * P:(j + 1) * P], ctxT[:, c],
                                                start=(c == 0), stop=(c == KC - 1))
                done.then_inc(k_psum, 1)

            def key_sums(n):
                pe.wait_ge(k_squared, n + 1)
                nc.tensor.matmul(ps[:, 2, :], ones[:], k_squares[:], start=True, stop=True).then_inc(k_sums, 1)

            def turn_queries(n):
                pe.wait_ge(diag_ready, n + 1)
                for g in range(G_KV):
                    if g >= 2:
                        pe.wait_ge(qT_ready, 4 * n + (g - 1))
                    else:
                        pe.wait_ge(q_ready, 4 * n + (g + 3))
                    for h in range(4 * g, 4 * g + 4):
                        done = nc.tensor.matmul(ps[:, g % 2, (h % 4) * P:(h % 4 + 1) * P], q[:, h * G_HD:(h + 1) * G_HD], diag[:, h],
                                                start=True, stop=True)
                    done.then_inc(qT_psum, 1)

            def value_rows(n):
                if not isinstance(n, int):
                    pe.wait_ge(v_ready, n)
                for c in range(KC):
                    done = nc.tensor.matmul(ps[:, 3, :], ctxT[:, c], w_v[:, c], start=(c == 0), stop=(c == KC - 1))
                done.then_inc(v_psum, 1)

            def project(n):
                rows(n)
                for g in range(G_KV):
                    query(n, g)
                keys(n)
                key_sums(n)
                turn_queries(n)
                value_rows(n)

            def step(t, ahead):
                if ahead:
                    rows(t + 1)
                pe.wait_ge(qT_ready, 4 * t + 4)
                pe.wait_ge(kT_ready, t + 1)
                pe.wait_ge(mixed_ready, 4 * t + 4)
                for j in range(G_KV):
                    for b in range(2):
                        half = slice(SEQ * b, SEQ * b + SEQ)
                        done = nc.tensor.matmul(ps[half, 4 + j // 2, (j % 2) * E:(j % 2 + 1) * E], kT[:, j * P + SEQ * b:j * P + SEQ * b + SEQ],
                                                qT[:, 4 * j:4 * j + 4, SEQ * b:SEQ * b + SEQ], start=True, stop=True)
                done.then_inc(scored, 1)
                if ahead:
                    query(t + 1, 0)
                    query(t + 1, 1)
                pe.wait_ge(scoresT_ready, t + 1)
                pe.wait_ge(x_ready, t + 1)
                for j in range(G_HEADS // 2):
                    done = nc.tensor.transpose(ps[:, 6 + j // 4, (j % 4) * P:(j % 4 + 1) * P], scoresT[:, j * P:(j + 1) * P], ident[:])
                done.then_inc(turned, 1)
                if ahead:
                    query(t + 1, 2)
                    query(t + 1, 3)
                    keys(t + 1)
                pe.wait_ge(probs_ready, t + 1)
                for j in range(G_HEADS // 2):
                    done = nc.tensor.transpose(ps[:, 4 + j // 4, (j % 4) * P:(j % 4 + 1) * P],
                                               probs[:, 2 * j:2 * j + 2].rearrange("p b s -> p (b s)"), ident[:])
                done.then_inc(probsT_psum, 1)
                if ahead:
                    key_sums(t + 1)
                pe.wait_ge(v_ready, t + 1)
                pe.wait_ge(probsT_ready, t + 1)

                def mix(j):
                    if j >= 2:
                        pe.wait_ge(mixed_ready, 4 * t + (j - 1 + G_KV))
                    for b in range(2):
                        done = nc.tensor.matmul(ps[:, 4 + j % 2, b * E:(b + 1) * E], values[:, b, j * G_HD:(j + 1) * G_HD],
                                                probsT[:, j * E:(j + 1) * E], start=True, stop=True)
                    done.then_inc(mixed_psum, 1)

                mix(0)
                for j in range(G_KV):
                    if j + 1 < G_KV:
                        mix(j + 1)
                    pe.wait_ge(mixed_ready, 4 * t + (j + 1 + G_KV))
                    for h in range(4 * j, 4 * j + 4):
                        done = nc.tensor.matmul(ps[:, 6, 0:E], mixedT[:, h], w_o[:, h], start=(h == 0), stop=(h == G_HEADS - 1))
                done.then_inc(out_psum, 1)
                if ahead:
                    turn_queries(t + 1)
                    value_rows(t + 1)

            pipeline(pe, project, step)

M_EXPERTS, M_FF = 8, 256
M_RANK, M_LORA = 64, 2
FT = M_FF // P
ZONE_CENTER, ZONE_LOW, ZONE_HIGH = 1.0 / math.e, 0.5 - math.log(4.0 / 3.0), 0.5
ZONE_WIDTH, FALLBACK_WIDTH, TINY = 0.1, 0.3, 1e-8


def mixture(core):
    nc, dram, ps, ident = core.nc, core.dram, core.psum, core.ident
    with ExitStack() as scope:
        sb = lambda name, shape, dt=F32: scope.enter_context(nc.sbuf_tensor(f"mo_{name}", shape, dt))
        sem = lambda name: core.sem(f"mo_{name}")
        ln = RowNorm(core, "mo", scope)
        weights = [sb(name, [P, M_EXPERTS, KC, M_FF]) for name in ("w_gate", "w_up", "w_down")]
        w_gate, w_up, w_down = weights
        lora_a = sb("lora_a", [M_RANK, 3, M_LORA, E])
        lora_b = sb("lora_b", [M_RANK, 3, M_LORA, M_FF])
        w_route = sb("w_route", [P, KC, M_EXPERTS])
        temperature, first = sb("temperature", [P, 1]), sb("first", [P, M_EXPERTS])
        xn, xT_now, xT = sb("xn", [P, 2, E]), sb("xT_now", [P, 2, E]), sb("xT", [P, KC, TILES * P])
        logits, gate, dist, zone, near, rank, hot1, hot2 = (
            sb(name, [P, TILES, M_EXPERTS]) for name in ("logits", "gate", "dist", "zone", "near", "rank", "hot1", "hot2"))
        total, nobody, best = (sb(name, [P, TILES]) for name in ("total", "nobody", "best"))
        silu, mid = sb("silu", [P, 4, 2 * P]), sb("mid", [P, 2, FT, 2 * P])

        loaded, folded_psum, folded, xn_ready, xT_psum, xT_ready, xT_kept, routed, logits_ready, route_step, inverted = (
            sem(n) for n in ("loaded", "folded_psum", "folded", "xn_ready", "xT_psum", "xT_ready", "xT_kept", "routed", "logits_ready", "route_step", "inverted"))
        gate_arg, gate_exp, dists, near_exp, zone_exp, mix_ready = (
            sem(n) for n in ("gate_arg", "gate_exp", "dists", "near_exp", "zone_exp", "mix_ready"))
        wide_psum, silu_ready, mid_ready, down_psum, added, stored = (
            sem(n) for n in ("wide_psum", "silu_ready", "mid_ready", "down_psum", "added", "stored"))
        LOADS = 8 * 16
        MIDS = M_EXPERTS * FT
        ADDS = 2 * M_EXPERTS
        ADD_CREDIT = 4
        FOLDS = 3 * M_LORA

        block = scope.enter_context(nc.Block())

        @block.sync
        def _(sp):
            for out, src in ((w_route[:], chunked(dram["mo_w_route"])), (temperature[:], dram["mo_temperature"].to_broadcast([P, 1])),
                             (first[:], dram["ff_first"]), (lora_a[:], dram["mo_lora_a"]), (lora_b[:], dram["mo_lora_b"]),
                             (w_gate[:].rearrange("p e c f -> p (e c) f"), dram["mo_w_gate"].rearrange("e (c p) f -> p (e c) f", p=P)),
                             (w_up[:].rearrange("p e c f -> p (e c) f"), dram["mo_w_up"].rearrange("e (c p) f -> p (e c) f", p=P)),
                             (w_down[:].rearrange("p e c f -> p (e c) f"), dram["mo_w_down"].rearrange("e (c p) f -> p (e c) f", p=P))):
                sp.dma_start(out, src).then_inc(loaded, 16)
            sp.wait_ge(loaded, LOADS)
            rows = dram["out"].rearrange("(t p) e -> p t e", p=P)
            with sp.Fori(0, PAIRS) as i:
                sp.wait_ge(added, ADDS * i + (ADDS + ADD_CREDIT))
                sp.dma_start(rows[:, bass.ts(i, 2), :], core.x[:, bass.ts(i, 2), :]).then_inc(stored, 16)
            sp.wait_ge(stored, 16 * PAIRS)

        @block.gpsimd
        def _(pool):
            with pool.Fori(0, PAIRS) as i:
                for u in range(2):
                    t = 2 * i + u
                    pool.wait_ge(xT_ready, t + 1)
                    nc.gpsimd.tensor_copy(xT[:, :, bass.ts(t, P)], xT_now[:, u].rearrange("p (c t) -> p c t", c=KC)).then_inc(xT_kept, 1)

        @block.scalar
        def _(act):
            act.preload_act_table_set(EXP_LN)
            ln.on_scalar(act)
            act.sem_inc(xT_kept, 2)
            with act.Fori(0, PAIRS) as i:
                for u in range(2):
                    t = 2 * i + u
                    act.wait_ge(xT_kept, t + 1)
                    act.wait_ge(xT_psum, t + 1)
                    nc.scalar.copy(xT_now[:, u], ps[:, u, 0:E]).then_inc(xT_ready, 1)
                for u in range(2):
                    t = 2 * i + u
                    act.wait_ge(routed, t + 1)
                    nc.scalar.copy(logits[:, t, :], ps[:, 2 + u, 0:M_EXPERTS]).then_inc(logits_ready, 1)
            act.wait_ge(gate_arg, 1)
            nc.scalar.activation(gate[:], logits[:], ACT.Exp).then_inc(gate_exp, 1)
            act.wait_ge(dists, 1)
            nc.scalar.activation(near[:], dist[:], ACT.Exp, scale=-1.0 / FALLBACK_WIDTH).then_inc(near_exp, 1)
            nc.scalar.activation(dist[:], dist[:], ACT.Exp, scale=-1.0 / ZONE_WIDTH).then_inc(zone_exp, 1)
            act.preload_act_table_set("silu_and_others")
            with act.Fori(0, PAIRS) as i:
                for j in range(MIDS):
                    act.wait_ge(wide_psum, MIDS * i + (j + 1))
                    nc.scalar.activation(silu[:, j % 4], ps[:, j % 4, 0:2 * P], ACT.Silu).then_inc(silu_ready, 1)

        @block.vector
        def _(dve):
            ln.on_vector(dve)
            dve.wait_ge(ln.ready, 1)
            dve.wait_ge(loaded, LOADS)
            nc.vector.reciprocal(temperature[:], temperature[:]).then_inc(inverted, 1)
            dve.wait_ge(inverted, 1)
            with dve.Fori(0, PAIRS) as i:
                for u in range(2):
                    t = 2 * i + u
                    ln.normalise(xn[:, u], t).then_inc(xn_ready, 1)
                for u in range(2):
                    dve.wait_ge(xT_ready, 2 * i + (u + 1))
            for k in range(3):
                for e in range(M_LORA):
                    j = M_LORA * k + e
                    dve.wait_ge(folded_psum, j + 1)
                    nc.vector.tensor_tensor(weights[k][:, e], weights[k][:, e],
                                            ps[:, 4 + j % 4, :].rearrange("p (c f) -> p c f", c=KC), ALU.add).then_inc(folded, 1)
            across = lambda a: a[:, :, None].to_broadcast([P, TILES, M_EXPERTS])
            every = lambda a: a[:, None, :].to_broadcast([P, TILES, M_EXPERTS])
            dve.wait_ge(logits_ready, TILES)
            nc.vector.tensor_scalar(logits[:], logits[:], temperature[:], -1.0, ALU.mult, ALU.mult).then_inc(route_step, 1)
            dve.wait_ge(route_step, 1)
            nc.vector.tensor_scalar(logits[:], logits[:], EXP_LIMIT, None, ALU.min).then_inc(gate_arg, 1)
            dve.wait_ge(gate_exp, 1)
            nc.vector.tensor_scalar(gate[:], gate[:], 1.0, None, ALU.add).then_inc(route_step, 1)
            dve.wait_ge(route_step, 2)
            nc.vector.reciprocal(gate[:], gate[:]).then_inc(route_step, 1)
            dve.wait_ge(route_step, 3)
            nc.vector.tensor_scalar(dist[:], gate[:], ZONE_CENTER, None, ALU.subtract).then_inc(route_step, 1)
            dve.wait_ge(route_step, 4)
            nc.vector.scalar_tensor_tensor(dist[:], dist[:], -1.0, dist[:], ALU.mult, ALU.max).then_inc(dists, 1)
            nc.vector.tensor_scalar(zone[:], gate[:], ZONE_LOW, None, ALU.is_ge).then_inc(route_step, 1)
            dve.wait_ge(route_step, 5)
            nc.vector.scalar_tensor_tensor(zone[:], gate[:], ZONE_HIGH, zone[:], ALU.is_le, ALU.mult).then_inc(route_step, 1)
            dve.wait_ge(route_step, 6)
            dve.wait_ge(zone_exp, 1)
            nc.vector.tensor_tensor(zone[:], zone[:], dist[:], ALU.mult).then_inc(route_step, 1)
            dve.wait_ge(route_step, 7)
            nc.vector.tensor_reduce(total[:], zone[:], AX.X, ALU.add).then_inc(route_step, 1)
            dve.wait_ge(route_step, 8)
            nc.vector.tensor_scalar(nobody[:], total[:], TINY, None, ALU.is_lt).then_inc(route_step, 1)
            dve.wait_ge(route_step, 9)
            nc.vector.tensor_reduce(best[:], near[:], AX.X, ALU.max).then_inc(route_step, 1)
            dve.wait_ge(route_step, 10)
            nc.vector.tensor_tensor(rank[:], near[:], across(best), ALU.is_ge).then_inc(route_step, 1)
            dve.wait_ge(route_step, 11)
            nc.vector.tensor_tensor(rank[:], rank[:], every(first), ALU.mult).then_inc(route_step, 1)
            dve.wait_ge(route_step, 12)
            nc.vector.tensor_reduce(best[:], rank[:], AX.X, ALU.max).then_inc(route_step, 1)
            dve.wait_ge(route_step, 13)
            nc.vector.tensor_tensor(hot1[:], rank[:], across(best), ALU.is_equal).then_inc(route_step, 1)
            dve.wait_ge(route_step, 14)
            nc.vector.scalar_tensor_tensor(gate[:], hot1[:], -2.0, near[:], ALU.mult, ALU.add).then_inc(route_step, 1)
            dve.wait_ge(route_step, 15)
            nc.vector.tensor_reduce(best[:], gate[:], AX.X, ALU.max).then_inc(route_step, 1)
            dve.wait_ge(route_step, 16)
            nc.vector.tensor_tensor(rank[:], gate[:], across(best), ALU.is_ge).then_inc(route_step, 1)
            dve.wait_ge(route_step, 17)
            nc.vector.tensor_tensor(rank[:], rank[:], every(first), ALU.mult).then_inc(route_step, 1)
            dve.wait_ge(route_step, 18)
            nc.vector.tensor_reduce(best[:], rank[:], AX.X, ALU.max).then_inc(route_step, 1)
            dve.wait_ge(route_step, 19)
            nc.vector.tensor_tensor(hot2[:], rank[:], across(best), ALU.is_equal).then_inc(route_step, 1)
            dve.wait_ge(route_step, 20)
            nc.vector.tensor_tensor(hot1[:], hot1[:], hot2[:], ALU.add).then_inc(route_step, 1)
            dve.wait_ge(route_step, 21)
            nc.vector.tensor_tensor(near[:], near[:], hot1[:], ALU.mult).then_inc(route_step, 1)
            dve.wait_ge(route_step, 22)
            nc.vector.tensor_reduce(best[:], near[:], AX.X, ALU.add).then_inc(route_step, 1)
            dve.wait_ge(route_step, 23)
            nc.vector.tensor_scalar(best[:], best[:], TINY, None, ALU.max).then_inc(route_step, 1)
            dve.wait_ge(route_step, 24)
            nc.vector.reciprocal(best[:], best[:]).then_inc(route_step, 1)
            dve.wait_ge(route_step, 25)
            nc.vector.tensor_tensor(best[:], best[:], nobody[:], ALU.mult).then_inc(route_step, 1)
            dve.wait_ge(route_step, 26)
            nc.vector.tensor_tensor(near[:], near[:], across(best), ALU.mult).then_inc(route_step, 1)
            dve.wait_ge(route_step, 27)
            nc.vector.tensor_scalar(nobody[:], nobody[:], -1.0, 1.0, ALU.mult, ALU.add).then_inc(route_step, 1)
            dve.wait_ge(route_step, 28)
            nc.vector.tensor_tensor(zone[:], zone[:], across(nobody), ALU.mult).then_inc(route_step, 1)
            dve.wait_ge(route_step, 29)
            nc.vector.tensor_tensor(zone[:], zone[:], near[:], ALU.add).then_inc(route_step, 1)
            dve.wait_ge(route_step, 30)
            nc.vector.tensor_reduce(total[:], zone[:], AX.X, ALU.add).then_inc(route_step, 1)
            dve.wait_ge(route_step, 31)
            nc.vector.tensor_scalar(total[:], total[:], TINY, None, ALU.max).then_inc(route_step, 1)
            dve.wait_ge(route_step, 32)
            nc.vector.reciprocal(total[:], total[:]).then_inc(route_step, 1)
            dve.wait_ge(route_step, 33)
            nc.vector.tensor_tensor(zone[:], zone[:], across(total), ALU.mult).then_inc(mix_ready, 1)
            dve.wait_ge(mix_ready, 1)

            dve.sem_inc(added, ADD_CREDIT)
            with dve.Fori(0, PAIRS) as i:
                def middles(e):
                    for f in range(FT):
                        j = FT * e + f
                        dve.wait_ge(silu_ready, MIDS * i + (j + 1))
                        nc.vector.tensor_tensor(mid[:, e % 2, f], silu[:, j % 4], ps[:, j % 4, 2 * P:4 * P], ALU.mult).then_inc(mid_ready, 1)

                def add(e):
                    dve.wait_ge(down_psum, M_EXPERTS * i + (e + 1))
                    for u in range(2):
                        t = 2 * i + u
                        dve.wait_ge(added, ADDS * i + (2 * e + u + ADD_CREDIT - 1))
                        nc.vector.scalar_tensor_tensor(core.x[:, t, :], ps[:, 4 + e % 2, u * E:(u + 1) * E], zone[:, t, e:e + 1],
                                                       core.x[:, t, :], ALU.mult, ALU.add).then_inc(added, 1)

                for e in range(M_EXPERTS):
                    middles(e)
                    if e:
                        add(e - 1)
                add(M_EXPERTS - 1)

        @block.tensor
        def _(pe):
            pe.wait_ge(loaded, LOADS)
            with pe.Fori(0, PAIRS) as i:
                for u in range(2):
                    t = 2 * i + u
                    pe.wait_ge(xn_ready, t + 1)
                    for c in range(KC):
                        done = nc.tensor.transpose(ps[:, u, c * P:(c + 1) * P], xn[:, u, c * P:(c + 1) * P], ident[:])
                    done.then_inc(xT_psum, 1)
                for u in range(2):
                    t = 2 * i + u
                    pe.wait_ge(xT_ready, t + 1)
                    for c in range(KC):
                        done = nc.tensor.matmul(ps[:, 2 + u, 0:M_EXPERTS], xT_now[:, u, c * P:(c + 1) * P], w_route[:, c],
                                                start=(c == 0), stop=(c == KC - 1))
                    done.then_inc(routed, 1)
            for k in range(3):
                for e in range(M_LORA):
                    j = M_LORA * k + e
                    if j >= 4:
                        pe.wait_ge(folded, j - 3)
                    for c in range(KC):
                        done = nc.tensor.matmul(ps[:, 4 + j % 4, c * M_FF:(c + 1) * M_FF], lora_a[:, k, e, c * P:(c + 1) * P], lora_b[:, k, e],
                                                start=True, stop=True)
                    done.then_inc(folded_psum, 1)
            pe.wait_ge(folded, FOLDS)
            pe.wait_ge(xT_kept, TILES + 2)
            pe.wait_ge(logits_ready, TILES)
            pe.sem_inc(mid_ready, 4)
            with pe.Fori(0, PAIRS) as i:
                def widen(e):
                    for f in range(FT):
                        j = FT * e + f
                        pe.wait_ge(mid_ready, MIDS * i + (j + 1))
                        for k in range(2):
                            for c in range(KC):
                                done = nc.tensor.matmul(ps[:, j % 4, 2 * P * k:2 * P * (k + 1)], weights[k][:, e, c, f * P:(f + 1) * P],
                                                        xT[:, c, bass.ts(i, 2 * P)], start=(c == 0), stop=(c == KC - 1))
                        done.then_inc(wide_psum, 1)

                def narrow(e):
                    pe.wait_ge(mid_ready, MIDS * i + (FT * e + FT + 4))
                    pe.wait_ge(added, ADDS * i + (2 * e + ADD_CREDIT - 2))
                    for u in range(2):
                        for f in range(FT):
                            done = nc.tensor.matmul(ps[:, 4 + e % 2, u * E:(u + 1) * E], mid[:, e % 2, f, u * P:(u + 1) * P], w_down[:, e, f],
                                                    start=(f == 0), stop=(f == FT - 1))
                    done.then_inc(down_psum, 1)

                for e in range(M_EXPERTS):
                    widen(e)
                    if e:
                        narrow(e - 1)
                narrow(M_EXPERTS - 1)
SUBLAYERS = (differential_attention, feature_attention, selected_update, state_space, grouped_attention, mixture)

def decoder(nc, dram):
    with ExitStack() as ctx:
        for name in ("q_parts", "k_parts"):
            dram[name] = nc.dram_tensor(name, (STACK, BATCH * C_HEADS, E), BF16, kind="Internal").ap()
        core = Core(nc, ctx, dram)
        load_inputs(core)
        core.end_sublayer()
        for sublayer in SUBLAYERS:
            sublayer(core)
            core.end_sublayer()

def rotary_tables():
    inv_freq = 1.0 / 10000.0 ** (np.arange(0, D_HD, 2, dtype=np.float32) / np.float32(D_HD))
    angle = np.arange(SEQ, dtype=np.float32)[None, :] * inv_freq.astype(np.float32)[:, None]
    cos = np.tile(np.cos(angle), (P // (D_HD // 2), 2))
    sin = np.tile(np.concatenate([np.sin(angle), -np.sin(angle)]), (P // D_HD, 2))
    scale = np.float32(D_HD ** -0.5)
    return np.stack([np.concatenate([t * scale, t * scale, t], axis=1) for t in (cos, sin)], axis=1).astype(np.float32)


def swapped(w):
    rows = w.shape[0]
    return w.reshape(rows, -1, 2, D_HD // 2)[:, :, ::-1].reshape(rows, -1)


def layout(inputs):
    a = {k: np.asarray(v) for k, v in inputs.items()}
    f32 = np.float32
    halves = a["L0_attn_Wq"].reshape(E, D_HEADS, 2, D_HD)
    q0, q1 = halves[:, :, 0].reshape(E, P), halves[:, :, 1].reshape(E, P)
    k = a["L0_attn_Wk"]
    rows = np.arange(P)
    tri = np.where(np.arange(SEQ)[None, :] <= np.arange(SEQ)[:, None], 0.0, MASKED).astype(f32)
    out = {
        "x": a["x"].reshape(BATCH * SEQ, E),
        "ctx": a["ctx_2048"].reshape(BATCH * SEQ, E),
        "ident": np.eye(P, dtype=f32),
        "ident_bf": np.eye(P, dtype=f32),
        "da_w_qk": np.concatenate([q0, q1, k, swapped(q0), swapped(q1), swapped(k)], axis=1),
        "da_w_v": a["L0_attn_Wv"],
        "da_w_o": a["L0_attn_Wo"],
        "da_gain": np.tile(a["L0_attn_g"], P // D_DV)[:, None],
        "rotary": rotary_tables(),
        "da_head_mask": (rows[:, None] // D_HD == np.arange(D_HEADS)[None, :]).astype(f32),
        "causal": np.tile(tri, (2, 8)),
        "da_lam": np.broadcast_to(np.stack([a["L0_attn_lam_" + v] for v in ("q1", "q2", "k1", "k2")])[None], (P, 4, D_HD)),
    }
    w_out = np.zeros((2, SEQ, 2, SEQ), f32)
    for b in range(2):
        w_out[b, :, b] = a["L0_xattn_W"].T
    out["fa_w_out"] = w_out.reshape(P, P)
    spread = lambda v: np.broadcast_to(v[None], (P, v.shape[0]))
    out["ff_w_in"] = np.concatenate([a["L0_ffn_select_weight"].transpose(1, 0, 2).reshape(E, F_SEL), a["L0_ffn_select_mean_diff"].T,
                                     a["L0_ffn_lora_update"].transpose(1, 0, 2).reshape(E, F_UPD)], axis=1)
    out["ff_debias"] = a["L0_ffn_debias_w"].T
    out["ff_w_back"] = np.concatenate([a["L0_ffn_lora_degen"].transpose(0, 2, 1).reshape(F_UPD, E), a["L0_ffn_bias_w"],
                                       np.zeros((F_ROWS - F_UPD - F_N, E), f32)], axis=0)
    out["ff_center"], out["ff_slope"] = spread(a["L0_ffn_imp_center"]), spread(a["L0_ffn_imp_slope"])
    out["ff_first"] = spread(np.arange(F_N, 0, -1).astype(f32))
    out["ss_w_bc"] = np.concatenate([a["L1_attn_B_w"].T, a["L1_attn_C_w"].T], axis=1)
    out["ss_bias_bc"] = np.stack([a["L1_attn_B_b"], a["L1_attn_C_b"]], axis=1)
    out["ss_w_dt"], out["ss_w_out"] = a["L1_attn_dt_w"].T, a["L1_attn_out_w"].T
    out["ss_bias_dt"], out["ss_skip"] = spread(a["L1_attn_dt_b"]), spread(a["L1_attn_D"])
    out["ss_A_log"], out["ss_bias_out"] = spread(a["L1_attn_A_log"]), spread(a["L1_attn_out_b"])
    row, col = rows[:, None], rows[None, :]
    spans, pairs = [], []
    for level in range(LEVELS):
        half = 1 << level
        pivot = col // (2 * half) * (2 * half) + half - 1
        spans.append(((col <= pivot) & (row > col) & (row <= pivot)) | ((col > pivot) & (row > pivot) & (row <= col)))
        pairs.append((row // (2 * half) == col // (2 * half)) & (row <= pivot) & (col > pivot))
    out["ss_spans"], out["ss_pairs"] = np.stack(spans, axis=1).astype(f32), np.stack(pairs, axis=1).astype(f32)
    out["ctxT"] = out["ctx"].T
    for name in ("q", "k", "v", "o"):
        out["ga_w_" + name] = a["L1_xattn_W" + name]
    out["ga_bias_q"], out["ga_bias_v"] = a["L1_xattn_bq"][None], a["L1_xattn_bv"][None]
    out["ga_bias_k"] = a["L1_xattn_bk"].reshape(G_KV, G_HD).T
    out["ga_gain_q"], out["ga_gain_k"] = a["L1_xattn_qn_w"][:, None], a["L1_xattn_kn_w"][:, None]
    out["mask"] = a["mask_1xSxS2_ff0"][0]
    out["mo_w_route"], out["mo_temperature"] = a["L1_ffn_Wr"], a["L1_ffn_temperature"][None]
    out["mo_w_gate"], out["mo_w_up"], out["mo_w_down"] = a["L1_ffn_Wg"], a["L1_ffn_Wu"], a["L1_ffn_Wd"]
    out["mo_lora_a"] = np.stack([a["L1_ffn_" + n].transpose(2, 0, 1) for n in ("Ga", "Ua", "Da")], axis=1)
    out["mo_lora_b"] = np.stack([a["L1_ffn_" + n].transpose(1, 0, 2) for n in ("Gb", "Ub", "Db")], axis=1)
    bf16 = mybir.dt.np(BF16)
    for name in ("ident_bf", "causal"):
        out[name] = out[name].astype(bf16)
    return {n: np.ascontiguousarray(v) for n, v in out.items()}


def kernel(**inputs):
    import concourse.bacc as bacc
    from concourse.bass_utils import run_bass_kernel_spmd

    nc = bacc.Bacc("TRN2", target_bir_lowering=False, num_devices=1)
    arrays = layout(inputs)
    dram = {n: nc.dram_tensor(f"in_{n}", v.shape, mybir.dt.from_np(v.dtype), kind="ExternalInput").ap() for n, v in arrays.items()}
    dram["out"] = nc.dram_tensor("out", (BATCH * SEQ, E), F32, kind="ExternalOutput").ap()
    decoder(nc, dram)
    result = run_bass_kernel_spmd(nc, [{f"in_{n}": v for n, v in arrays.items()}], core_ids=[0])
    return result.results[0]["out"].reshape(BATCH, SEQ, E)
```

```python
import math
from contextlib import ExitStack

import numpy as np

import concourse.bass as bass
from concourse import mybir

F32 = mybir.dt.float32
F32R = mybir.dt.float32r
BF16 = mybir.dt.bfloat16
ALU = mybir.AluOpType
ACT = mybir.ActivationFunctionType
AX = mybir.AxisListType

P = 128
BATCH, SEQ, E = 32, 64, 256
TILES = BATCH * SEQ // P
PAIRS = TILES // 2
KC = E // P
LN_EPS = 1e-5
FLT_MAX = 3.4028235e38
MASKED = -1.0e30
EXP_LN = "natural_log_exp_and_others"


class Core:

    def __init__(self, nc, ctx, dram):
        self.nc, self.ctx, self.dram = nc, ctx, dram
        self.psum = ctx.enter_context(nc.psum_tensor("psum", [P, 8, 512], F32))
        self.x = self.sb("x", [P, TILES, E])
        self.row_stats = self.sb("row_stats", [P, TILES, 6])
        self.ident = self.sb("ident", [P, P])
        self.semaphores = []

    def sb(self, name, shape, dtype=F32):
        return self.ctx.enter_context(self.nc.sbuf_tensor(name, shape, dtype))

    def sem(self, name):
        self.semaphores.append(self.nc.alloc_semaphore(name=name))
        return self.semaphores[-1]

    def end_sublayer(self):
        self.nc.clear_and_free_semaphores(self.semaphores)
        self.nc.all_engine_barrier()
        self.semaphores = []

    def sems(self, name, count):
        return [self.sem(f"{name}{j}") for j in range(count)]


def chunked(weight):
    return weight.rearrange("(c p) o -> p c o", p=P)


class RowNorm:

    def __init__(self, core, stage, scope):
        nc = core.nc
        sb = lambda name, shape: scope.enter_context(nc.sbuf_tensor(f"{stage}_{name}", shape, F32))
        self.core = core
        self.sum2, self.half = sb("sum2", [P, TILES]), sb("half", [P, TILES])
        self.spread, self.mean = sb("spread", [P, TILES]), sb("mean", [P, TILES])
        self.var, self.log_var = sb("var", [P, TILES]), sb("log_var", [P, TILES])
        self.rstd = sb("rstd", [P, TILES])
        self.eps = sb("ln_eps", [P, 1])
        self.moments = core.sem(f"{stage}_ln_moments")
        self.var_ready = core.sem(f"{stage}_ln_var")
        self.log_ready = core.sem(f"{stage}_ln_log")
        self.ready = core.sem(f"{stage}_ln_ready")

    def on_vector(self, dve):
        nc, stats = self.core.nc, self.core.row_stats
        nc.vector.memset(self.eps[:], LN_EPS)
        nc.vector.tensor_tensor(self.sum2[:], stats[:, :, 1], stats[:, :, 4], ALU.add).then_inc(self.moments, 1)
        nc.vector.tensor_tensor(self.half[:], stats[:, :, 1], stats[:, :, 4], ALU.subtract).then_inc(self.moments, 1)
        nc.vector.tensor_tensor(self.spread[:], stats[:, :, 2], stats[:, :, 5], ALU.add).then_inc(self.moments, 1)
        dve.wait_ge(self.moments, 3)
        nc.vector.tensor_scalar(self.mean[:], self.sum2[:], 0.5, None, ALU.mult).then_inc(self.moments, 1)
        nc.vector.scalar_tensor_tensor(self.half[:], self.half[:], 0.25, self.half[:], ALU.mult, ALU.mult).then_inc(self.moments, 1)
        dve.wait_ge(self.moments, 5)
        nc.vector.scalar_tensor_tensor(self.var[:], self.spread[:], 1.0 / E, self.half[:], ALU.mult, ALU.add).then_inc(self.var_ready, 1)

    def on_scalar(self, act):
        nc = self.core.nc
        act.wait_ge(self.var_ready, 1)
        nc.scalar.activation(self.log_var[:], self.var[:], ACT.Ln, bias=self.eps[:]).then_inc(self.log_ready, 1)
        act.wait_ge(self.log_ready, 1)
        nc.scalar.activation(self.rstd[:], self.log_var[:], ACT.Exp, scale=-0.5).then_inc(self.ready, 1)

    def normalise(self, out, t):
        return self.core.nc.vector.tensor_scalar(
            out, self.core.x[:, t, :], self.mean[:, bass.ts(t, 1)], self.rstd[:, bass.ts(t, 1)],
            ALU.subtract, ALU.mult)

def load_inputs(core):
    nc, dram = core.nc, core.dram
    parts = 4
    per = TILES // parts
    x_loaded = core.sems("x_loaded", parts)
    ident_loaded = core.sem("ident_loaded")
    stats_done = core.sem("first_stats_done")
    with nc.Block() as block:

        @block.sync
        def _(sp):
            for g in range(parts):
                sp.dma_start(core.x[:, g * per:(g + 1) * per, :],
                             dram["x"].rearrange("(t p) e -> p t e", p=P)[:, g * per:(g + 1) * per, :]).then_inc(x_loaded[g], 16)
            sp.dma_start(core.ident[:], dram["ident"]).then_inc(ident_loaded, 16)
            sp.wait_ge(ident_loaded, 16)
            sp.wait_ge(stats_done, TILES)

        @block.vector
        def _(dve):
            for g in range(parts):
                dve.wait_ge(x_loaded[g], 16)
                for t in range(g * per, (g + 1) * per):
                    nc.vector.bn_stats(core.row_stats[:, t, :], core.x[:, t, :]).then_inc(stats_done, 1)


D_HEADS, D_KV_HEADS, D_HD = 16, 8, 8
D_DV = 2 * D_HD
LAMBDA_INIT = 0.8 - 0.6 * math.exp(-0.3 * 12)
RMS_EPS = 1e-6


def differential_attention(core):
    nc, dram, ps, ident = core.nc, core.dram, core.psum, core.ident
    with ExitStack() as scope:
        sb = lambda name, shape, dt=F32: scope.enter_context(nc.sbuf_tensor(f"da_{name}", shape, dt))
        sem = lambda name: core.sem(f"da_{name}")
        ln = RowNorm(core, "da", scope)
        w_qk = sb("w_qk", [P, KC, 6 * P])
        w_v = sb("w_v", [P, KC, P])
        w_o = sb("w_o", [P, KC, E])
        gain = sb("gain", [P, 1])
        rotary = sb("rotary", [P, 2, 3 * P])
        head_mask = sb("head_mask", [P, D_HEADS])
        causal = sb("causal", [P, 8 * SEQ], BF16)
        ident_bf = sb("ident_bf", [P, P], BF16)
        lam_in = sb("lam_in", [P, 4, D_HD])
        lam_prod, lam_dot, lam_exp, lam = sb("lam_prod", [P, 2, D_HD]), sb("lam_dot", [P, 2]), sb("lam_exp", [P, 2]), sb("lam", [P, 1])
        rms_eps = sb("rms_eps", [P, 1])
        xn, xT = sb("xn", [P, E]), sb("xT", [P, E])
        rot_a, rot_b, rot = sb("rot_a", [P, 3 * P]), sb("rot_b", [P, 3 * P]), sb("rot", [P, 3 * P])
        keys = sb("keys", [P, D_HEADS, P])
        kept = sb("kept", [P, TILES, 2, P])
        values = sb("values", [P, 2, D_KV_HEADS, 64])
        top = sb("top", [P, 2, D_HEADS])
        probs = sb("probs", [P, 2, D_HEADS * SEQ])
        probsT = sb("probsT", [P, 2, D_HEADS * SEQ])
        headsT = sb("headsT", [P, 1024])
        inv = sb("inv", [P, 2, D_HEADS])
        part0, part1 = sb("part0", [P, E]), sb("part1", [P, E])
        attn, squares, scaled = sb("attn", [P, E]), sb("squares", [P, E]), sb("scaled", [P, E])
        square_sum, rms_log, rms_inv = sb("square_sum", [P, D_HEADS]), sb("rms_log", [P, D_HEADS]), sb("rms_inv", [P, D_HEADS])
        attnT = sb("attnT", [P, E])

        loaded = sem("loaded")
        consts_set, lam_ready, lam_dots, lam_exps, wo_scaled, lam_steps = (
            sem(n) for n in ("consts_set", "lam_ready", "lam_dots", "lam_exps", "wo_scaled", "lam_steps"))
        xn_ready, xT_psum, xT_ready, projected, v_kept, rot_parts, rot_ready, values_ready, keys_ready = (
            sem(n) for n in ("xn_ready", "xT_psum", "xT_ready", "projected", "v_kept", "rot_parts", "rot_ready", "values_ready", "keys_ready"))
        scored, top_raw, top_ready, shifted, exp_done, probsT_psum, probsT_ready = (
            core.sems("da_" + n, 2) for n in ("scored", "top_raw", "top_ready", "shifted", "exp_done", "probsT_psum", "probsT_ready"))
        heads_psum, headsT_ready, heads_rows, inv_ready, inv_lam, parts_ready, attn_ready, squares_ready, square_sums = (
            sem(n) for n in ("heads_psum", "headsT_ready", "heads_rows", "inv_ready", "inv_lam", "parts_ready", "attn_ready", "squares_ready", "square_sums"))
        rms_logs, rms_ready, scaled_ready, attnT_psum, attnT_ready, out_psum, x_ready, stats_done = (
            sem(n) for n in ("rms_logs", "rms_ready", "scaled_ready", "attnT_psum", "attnT_ready", "out_psum", "x_ready", "stats_done"))
        LOADS = 9 * 16

        block = scope.enter_context(nc.Block())

        def pipeline(eng, turn):
            first, last = 1, TILES - 3
            for t in range(-3, first):
                turn(t, lambda k: 0 <= k < TILES)
            with eng.Fori(first, last) as t:
                turn(t, lambda k: True)
            for t in range(last, TILES + 1):
                turn(t, lambda k: 0 <= k < TILES)

        def started(t, first):
            return not isinstance(t, int) or t >= first

        @block.sync
        def _(sp):
            for out, src in ((w_qk[:], chunked(dram["da_w_qk"])), (w_v[:], chunked(dram["da_w_v"])), (rotary[:], dram["rotary"]),
                             (head_mask[:], dram["da_head_mask"]), (causal[:], dram["causal"]), (ident_bf[:], dram["ident_bf"]),
                             (lam_in[:], dram["da_lam"]), (w_o[:], chunked(dram["da_w_o"])), (gain[:], dram["da_gain"]),
                             ):
                sp.dma_start(out, src).then_inc(loaded, 16)
            sp.wait_ge(loaded, LOADS)

        @block.gpsimd
        def _(pool):
            nc.gpsimd.memset(values[:], 0.0).then_inc(consts_set, 1)
            pool.wait_ge(consts_set, 1)
            for half in range(2):
                ones = values[64 * half:64 * half + 64, :, :, half * 17 + D_DV:half * 17 + D_DV + 1]
                nc.gpsimd.memset(ones, 1.0).then_inc(consts_set, 1)
            pool.wait_ge(consts_set, 3)

            def turn(t, valid):
                if valid(t):
                    pool.wait_ge(v_kept, t + 1)
                    if started(t, 1):
                        pool.wait_ge(heads_psum, 2 * t)
                    if started(t, -1) and valid(t + 1):
                        pool.wait_ge(keys_ready, t + 2)
                    for half in range(2):
                        rows = slice(64 * half, 64 * half + 64)
                        done = nc.gpsimd.tensor_copy(values[rows, :, :, half * 17:half * 17 + D_DV],
                                                     kept[rows, t].rearrange("p b (h d) -> p b h d", d=D_DV))
                    done.then_inc(values_ready, 1)
                if valid(t + 2):
                    pool.wait_ge(rot_ready, t + 3)
                    if valid(t):
                        pool.wait_ge(values_ready, t + 1)
                    nc.gpsimd.tensor_tensor(
                        keys[:], rot[:, None, 2 * P:3 * P].to_broadcast([P, D_HEADS, P]),
                        head_mask[:, :, None].to_broadcast([P, D_HEADS, P]), ALU.mult).then_inc(keys_ready, 1)

            pipeline(pool, turn)

        @block.scalar
        def _(act):
            act.preload_act_table_set(EXP_LN)
            ln.on_scalar(act)
            act.wait_ge(lam_dots, 1)
            nc.scalar.activation(lam_exp[:], lam_dot[:], ACT.Exp).then_inc(lam_exps, 1)

            def turn(t, valid):
                if valid(t + 2):
                    act.wait_ge(projected, t + 3)
                    for b in range(2):
                        for half in range(2):
                            done = nc.scalar.copy(kept[64 * half:64 * half + 64, t + 2, b, :], ps[64 * b:64 * b + 64, 4, 3 * P:4 * P])
                    done.then_inc(v_kept, 1)
                if valid(t - 1):
                    act.wait_ge(attn_ready, t)
                    nc.scalar.activation(squares[:], attn[:], ACT.Square).then_inc(squares_ready, 1)

                def take_probsT(r):
                    for c in range(2):
                        act.wait_ge(probsT_psum[r], 2 * t + (c + 1))
                        nc.scalar.copy(probsT[:, r, c * 512:(c + 1) * 512], ps[:, 6 + c, :]).then_inc(probsT_ready[r], 1)

                def exponentials(r):
                    act.wait_ge(shifted[r], t + 2)
                    nc.scalar.activation(probs[:, r], probs[:, r], ACT.Exp).then_inc(exp_done[r], 1)

                if valid(t):
                    take_probsT(0)
                if valid(t + 1):
                    exponentials(0)
                if valid(t - 1):
                    act.wait_ge(square_sums, t)
                    nc.scalar.activation(rms_log[:], square_sum[:], ACT.Ln, bias=rms_eps[:], scale=1.0 / D_DV).then_inc(rms_logs, 1)
                    act.wait_ge(rms_logs, t)
                    nc.scalar.activation(rms_inv[:], rms_log[:], ACT.Exp, scale=-0.5).then_inc(rms_ready, 1)
                if valid(t):
                    take_probsT(1)
                    for c in range(2):
                        act.wait_ge(heads_psum, 2 * t + (c + 1))
                        nc.scalar.copy(headsT[:, c * 512:(c + 1) * 512], ps[:, c, :]).then_inc(headsT_ready, 1)
                if valid(t - 1):
                    act.wait_ge(attnT_psum, t)
                    nc.scalar.copy(attnT[:], ps[:, 2, 0:E]).then_inc(attnT_ready, 1)
                if valid(t + 3):
                    act.wait_ge(xT_psum, t + 4)
                    nc.scalar.copy(xT[:], ps[:, 3, 0:E]).then_inc(xT_ready, 1)
                if valid(t + 1):
                    exponentials(1)

            pipeline(act, turn)

        @block.vector
        def _(dve):
            ln.on_vector(dve)
            nc.vector.memset(rms_eps[:], RMS_EPS)
            dve.wait_ge(loaded, LOADS)
            nc.vector.tensor_tensor(lam_prod[:], lam_in[:, 0:2], lam_in[:, 2:4], ALU.mult).then_inc(lam_steps, 1)
            dve.wait_ge(lam_steps, 1)
            nc.vector.tensor_reduce(lam_dot[:], lam_prod[:], AX.X, ALU.add).then_inc(lam_dots, 1)
            for c in range(KC):
                nc.vector.tensor_scalar(w_o[:, c], w_o[:, c], gain[:], 1.0 - LAMBDA_INIT, ALU.mult, ALU.mult).then_inc(wo_scaled, 1)
            dve.wait_ge(lam_exps, 1)
            nc.vector.tensor_tensor(lam[:], lam_exp[:, 0:1], lam_exp[:, 1:2], ALU.subtract).then_inc(lam_steps, 1)
            dve.wait_ge(lam_steps, 2)
            nc.vector.tensor_scalar(lam[:], lam[:], LAMBDA_INIT, None, ALU.add).then_inc(lam_ready, 1)
            dve.wait_ge(lam_ready, 1)
            dve.wait_ge(ln.ready, 1)
            dve.sem_inc(x_ready, 1)
            by_head = lambda a: a.rearrange("p (h d) -> p h d", d=D_DV)
            scores = [ps[:, 2 + 2 * r:4 + 2 * r, :].rearrange("p b (h s) -> p (b h) s", s=SEQ) for r in range(2)]
            heads = ps[:, 6:8, :].rearrange("p r (g c) -> p r g c", c=64)
            sums = [heads[:, r, :, 0:34].rearrange("p g (h d) -> p g h d", d=17)[:, :, :, D_DV] for r in range(2)]
            weighted = [heads[:, r, :, 0:34].rearrange("p g (h d) -> p g h d", d=17)[:, :, :, 0:D_DV] for r in range(2)]
            pair = lambda a: a.rearrange("p (g h) -> p g h", h=2)
            quad = lambda a: a.rearrange("p (g h d) -> p g h d", h=2, d=D_DV)
            spread = lambda a: pair(a)[:, :, :, None].to_broadcast([P, D_HEADS // 2, 2, D_DV])

            def turn(t, valid):
                def maxima(r):
                    dve.wait_ge(scored[r], t + 2)
                    nc.vector.tensor_reduce(top[:, r], scores[r], AX.X, ALU.max).then_inc(top_raw[r], 1)

                def shift(r):
                    dve.wait_ge(top_raw[r], t + 2)
                    nc.vector.tensor_scalar(top[:, r], top[:, r], FLT_MAX, -FLT_MAX, ALU.min, ALU.max).then_inc(top_ready[r], 1)
                    dve.wait_ge(top_ready[r], t + 2)
                    if started(t, 0):
                        dve.wait_ge(probsT_psum[r], 2 * t + 2)
                    nc.vector.scalar_tensor_tensor(
                        probs[:, r].rearrange("p (h s) -> p h s", s=SEQ), scores[r], FLT_MAX,
                        top[:, r, :, None].to_broadcast([P, D_HEADS, SEQ]), ALU.min, ALU.subtract).then_inc(shifted[r], 1)

                if valid(t + 2):
                    dve.wait_ge(projected, t + 3)
                    nc.vector.tensor_tensor(rot_b[:], ps[:, 5, 0:3 * P], rotary[:, 1], ALU.mult)
                    dve.wait_ge(v_kept, t + 3)
                    nc.vector.tensor_tensor(rot_a[:], ps[:, 4, 0:3 * P], rotary[:, 0], ALU.mult).then_inc(rot_parts, 1)
                if valid(t + 1):
                    maxima(0)
                    shift(0)
                if valid(t - 1):
                    dve.wait_ge(squares_ready, t)
                    nc.vector.tensor_reduce(square_sum[:], by_head(squares[:]), AX.X, ALU.add).then_inc(square_sums, 1)
                if valid(t + 1):
                    maxima(1)
                if valid(t + 2):
                    dve.wait_ge(rot_parts, t + 3)
                    nc.vector.tensor_tensor(rot[:], rot_a[:], rot_b[:], ALU.add).then_inc(rot_ready, 1)
                if valid(t + 1):
                    shift(1)
                if valid(t - 1):
                    dve.wait_ge(rms_ready, t)
                    nc.vector.tensor_tensor(by_head(scaled[:]), by_head(attn[:]), rms_inv[:, :, None].to_broadcast([P, D_HEADS, D_DV]),
                                            ALU.mult).then_inc(scaled_ready, 1)
                if valid(t + 3):
                    ln.normalise(xn[:], t + 3).then_inc(xn_ready, 1)
                if valid(t):
                    dve.wait_ge(heads_rows, t + 1)
                    for r in range(2):
                        nc.vector.reciprocal(pair(inv[:, r]), sums[r]).then_inc(inv_ready, 1)
                    dve.wait_ge(inv_ready, 2 * t + 2)
                    nc.vector.tensor_scalar(inv[:, 1], inv[:, 1], lam[:], None, ALU.mult).then_inc(inv_lam, 1)
                    nc.vector.tensor_tensor(quad(part0[:]), weighted[0], spread(inv[:, 0]), ALU.mult)
                    dve.wait_ge(inv_lam, t + 1)
                    nc.vector.tensor_tensor(quad(part1[:]), weighted[1], spread(inv[:, 1]), ALU.mult).then_inc(parts_ready, 1)
                    dve.wait_ge(parts_ready, t + 1)
                    nc.vector.tensor_tensor(attn[:], part0[:], part1[:], ALU.subtract).then_inc(attn_ready, 1)
                if valid(t - 1):
                    dve.wait_ge(out_psum, t)
                    nc.vector.tensor_tensor(core.x[:, t - 1, :], core.x[:, t - 1, :], ps[:, 2, E:2 * E], ALU.add).then_inc(x_ready, 1)
                    dve.wait_ge(x_ready, t + 1)
                    nc.vector.bn_stats(core.row_stats[:, t - 1, :], core.x[:, t - 1, :]).then_inc(stats_done, 1)

            pipeline(dve, turn)
            dve.wait_ge(stats_done, TILES)

        @block.tensor
        def _(pe):
            pe.wait_ge(loaded, LOADS)
            pe.wait_ge(wo_scaled, KC)

            def turn(t, valid):
                def score(r):
                    for half in range(2):
                        bank = 2 + 2 * r + half
                        nc.tensor.matmul(ps[:, bank, :], ident_bf[:], causal[:], start=True, stop=False, skip_group_check=True)
                        for b in range(2):
                            done = nc.tensor.matmul(
                                ps[64 * b:64 * b + 64, bank, :], rot[:, r * P + 64 * b:r * P + 64 * b + 64],
                                keys[:, 8 * half:8 * half + 8, 64 * b:64 * b + 64], start=False, stop=(b == 1), skip_group_check=True)
                    done.then_inc(scored[r], 1)

                def turn_probs(r):
                    pe.wait_ge(exp_done[r], t + 1)
                    for c in range(2):
                        if r == 1:
                            pe.wait_ge(probsT_ready[0], 2 * t + (c + 1))
                        for j in range(4):
                            done = nc.tensor.transpose(ps[:, 6 + c, j * P:(j + 1) * P], probs[:, r, (4 * c + j) * P:(4 * c + j + 1) * P], ident[:])
                        done.then_inc(probsT_psum[r], 1)

                if valid(t + 1):
                    pe.wait_ge(keys_ready, t + 2)
                    if started(t, 0):
                        pe.wait_ge(shifted[0], t + 1)
                    if started(t, 1):
                        pe.wait_ge(x_ready, t)
                    score(0)
                if valid(t):
                    if started(t, 1):
                        pe.wait_ge(parts_ready, t)
                    turn_probs(0)
                if valid(t + 1):
                    if started(t, 0):
                        pe.wait_ge(shifted[1], t + 1)
                    if valid(t + 2):
                        pe.wait_ge(rot_parts, t + 3)
                    score(1)
                if valid(t):
                    turn_probs(1)
                    pe.wait_ge(values_ready, t + 1)
                    for c in range(2):
                        pe.wait_ge(probsT_ready[1], 2 * t + (c + 1))
                        if started(t, 1):
                            pe.wait_ge(headsT_ready, 2 * t - 1 + c)
                        for b in range(2):
                            for j in range(4 * c, 4 * c + 4):
                                weights = probsT[:].rearrange("p r (j t) -> p r j t", t=P)[:, :, j, 64 * b:64 * b + 64]
                                out = ps[64 * (j % 2):64 * (j % 2) + 64, c, :].rearrange("p (g r b t) -> p g r b t", g=2, r=2, b=2)[:, (j // 2) % 2, :, b, :]
                                done = nc.tensor.matmul(out, values[:, b, j, :], weights, start=True, stop=True)
                        done.then_inc(heads_psum, 1)
                if valid(t - 1):
                    pe.wait_ge(scaled_ready, t)
                    if valid(t + 1):
                        pe.wait_ge(shifted[0], t + 2)
                    else:
                        pe.wait_ge(x_ready, t)
                    for c in range(KC):
                        done = nc.tensor.transpose(ps[:, 2, c * P:(c + 1) * P], scaled[:, c * P:(c + 1) * P], ident[:])
                    done.then_inc(attnT_psum, 1)
                if valid(t + 3):
                    pe.wait_ge(xn_ready, t + 4)
                    if valid(t + 1):
                        pe.wait_ge(shifted[0], t + 2)
                    for c in range(KC):
                        done = nc.tensor.transpose(ps[:, 3, c * P:(c + 1) * P], xn[:, c * P:(c + 1) * P], ident[:])
                    done.then_inc(xT_psum, 1)
                if valid(t):
                    for c in range(2):
                        pe.wait_ge(headsT_ready, 2 * t + (c + 1))
                        for r in range(2):
                            for g in range(2 * c, 2 * c + 2):
                                done = nc.tensor.transpose(ps[:, 6 + r, g * P:(g + 1) * P],
                                                           headsT[:].rearrange("p (g r t) -> p g r t", g=4, r=2)[:, g, r, :], ident[:])
                    done.then_inc(heads_rows, 1)
                if valid(t - 1):
                    pe.wait_ge(attnT_ready, t)
                    for c in range(KC):
                        done = nc.tensor.matmul(ps[:, 2, E:2 * E], attnT[:, c * P:(c + 1) * P], w_o[:, c],
                                                start=(c == 0), stop=(c == KC - 1))
                    done.then_inc(out_psum, 1)
                if valid(t + 3):
                    pe.wait_ge(xT_ready, t + 4)
                    if valid(t + 1):
                        pe.wait_ge(shifted[1], t + 2)
                    elif valid(t + 2):
                        pe.wait_ge(rot_parts, t + 3)
                    for m in range(6):
                        for c in range(KC):
                            nc.tensor.matmul(ps[:, 4 + m // 3, (m % 3) * P:(m % 3 + 1) * P], w_qk[:, c, m * P:(m + 1) * P],
                                             xT[:, c * P:(c + 1) * P], start=(c == 0), stop=(c == KC - 1))
                    for c in range(KC):
                        done = nc.tensor.matmul(ps[:, 4, 3 * P:4 * P], xT[:, c * P:(c + 1) * P], w_v[:, c],
                                                start=(c == 0), stop=(c == KC - 1))
                    done.then_inc(projected, 1)

            pipeline(pe, turn)

C_HEADS, C_HD = 8, 8
PARTS = 3
STACK = PARTS * C_HD
MAX_ROW = 96
STACK_ROWS = MAX_ROW + PARTS
RING = 3
V_COLS = 32
SELU_SCALE, SELU_ALPHA = 1.0507009873554805, 1.6732632423543772


def feature_attention(core):
    nc, dram, ps, ident = core.nc, core.dram, core.psum, core.ident
    with ExitStack() as scope:
        sb = lambda name, shape, dt=F32: scope.enter_context(nc.sbuf_tensor(f"fa_{name}", shape, dt))
        sem = lambda name: core.sem(f"fa_{name}")
        ln = RowNorm(core, "fa", scope)
        ident_bf = sb("ident_bf", [P, P], BF16)
        w_out = sb("w_out", [P, P])
        rows = sb("rows", [P, E])
        zeros = sb("zeros", [P, E])
        context = sb("context", [P, RING, E])
        rest = sb("rest", [P, 2, E])
        parts = sb("parts", [P, RING, 2, PARTS, E], BF16)
        q_stack = sb("q_stack", [P, RING, 2, C_HEADS, E], BF16)
        k_stack = sb("k_stack", [P, RING, 2, C_HEADS, E], BF16)
        values = sb("values", [P, RING, 2, 2 * C_HEADS, V_COLS])
        neg_max = sb("neg_max", [P, 2, 2, C_HEADS])
        max_rest = sb("max_rest", [P, 2, 2, C_HEADS])
        max_parts = sb("max_parts", [P, 2, 2, PARTS, C_HEADS], BF16)
        max_rows = sb("max_rows", [P, 2, E], BF16)
        probs = sb("probs", [P, 4, 2, 2, E])
        mixedT = sb("mixedT", [P, 2, E])
        inv = sb("inv", [P, 2 * C_HEADS])
        mixed = sb("mixed", [P, 2, 2, C_HEADS * C_HD])
        mixed_c = sb("mixed_c", [P, E])
        above, below, exp_below, negative, selu = (sb(n, [P, E]) for n in ("above", "below", "exp_below", "negative", "selu"))
        minus_one = sb("minus_one", [P, 1])

        loaded, padded, consts_set, cleared_values, scaled_rstd = (sem(n) for n in ("loaded", "padded", "consts_set", "cleared_values", "scaled_rstd"))
        rows_ready, high_ready, split_step, split_done = (sem(n) for n in ("rows_ready", "high_ready", "split_step", "split_done"))
        context_ready = core.sems("fa_context_ready", RING)
        stored, stacked, max_stacked = core.sems("fa_stored", RING), core.sems("fa_stacked", RING), core.sems("fa_max_stacked", 2)
        values_psum, values_ready, max_scored, max_taken = (sem(n) for n in ("values_psum", "values_ready", "max_scored", "max_taken"))
        max_high, max_left, max_mid, max_split, max_turned, max_rows_ready = (
            sem(n) for n in ("max_high", "max_left", "max_mid", "max_split", "max_turned", "max_rows_ready"))
        scored, exp_done, mixed_done, mixedT_ready, mixed_rows, inv_ready, mixed_ready = (
            sem(n) for n in ("scored", "exp_done", "mixed_done", "mixedT_ready", "mixed_rows", "inv_ready", "mixed_ready"))
        mixed_turned, mixed_c_ready, projected, channels_read = (sem(n) for n in ("mixed_turned", "mixed_c_ready", "projected", "channels_read"))
        exp_below_ready, selu_parts, selu_ready, selu_sum, x_ready, stats_done = (
            sem(n) for n in ("exp_below_ready", "selu_parts", "selu_ready", "selu_sum", "x_ready", "stats_done"))
        LOADS, STORES = 2 * PARTS * 16, 2 * PARTS * 16

        block = scope.enter_context(nc.Block())

        def pipeline(eng, turn):
            first, last = 1, TILES - RING
            exists = lambda k: 0 <= k < TILES
            for t in range(-RING, first):
                turn(t, lambda d: (t + d) % RING, lambda d: (t + d) // RING, exists)
            with eng.Fori(0, (last - first) // RING) as i:
                for r in range(RING):
                    turn(RING * i + (first + r), lambda d: (first + r + d) % RING, lambda d: i + (first + r + d) // RING, lambda k: True)
            for t in range(last, TILES + 1):
                turn(t, lambda d: (t + d) % RING, lambda d: (t + d) // RING, exists)

        assert (TILES - RING - 1) % RING == 0

        def started(t, first):
            return not isinstance(t, int) or t >= first

        @block.sync
        def _(sp):
            sp.dma_start(ident_bf[:], dram["ident_bf"]).then_inc(loaded, 16)
            sp.dma_start(w_out[:], dram["fa_w_out"]).then_inc(loaded, 16)

            def max_to_stack(tile, slot, b):
                sp.wait_ge(max_rows_ready, 2 * tile + (b + 1))
                sp.dma_start(q_stack[MAX_ROW:MAX_ROW + PARTS, slot, b], max_rows[0:PARTS * C_HEADS, b]).then_inc(max_stacked[b], 16)

            def load(t, slot, round):
                if started(t, 1):
                    sp.wait_ge(scored, 8 * t)
                sp.wait_ge(stored[slot], STORES * round + STORES)
                groups = bass.ts(t + 2, 2 * C_HEADS)
                for k in range(PARTS):
                    of = dram["q_parts"][:, groups, :].rearrange("r g f -> r (g f)")
                    sp.dma_start(q_stack[k * STACK:(k + 1) * STACK, slot].rearrange("p b h f -> p (b h f)"), of).then_inc(stacked[slot], 16)
                for k in range(PARTS):
                    of = dram["k_parts"][k * C_HD:(k + 1) * C_HD, groups, :].rearrange("d g f -> d (g f)")
                    sp.dma_start(k_stack[k * STACK:(k + 1) * STACK, slot].rearrange("p b h f -> p (b h f)"),
                                 of[None].to_broadcast([PARTS, C_HD, 2 * C_HEADS * E])).then_inc(stacked[slot], 16)

            def store(t, slot):
                sp.wait_ge(split_done, t + 4)
                for kind, name in enumerate(("q_parts", "k_parts")):
                    for part in range(PARTS):
                        to = dram[name].rearrange("(a d) g f -> a g d f", d=C_HD)[part, bass.ts(t + 3, 2 * C_HEADS)]
                        sp.dma_start(to, parts[:, slot, kind, part]).then_inc(stored[slot], 16)

            def load_context(tile, slot):
                sp.dma_start(context[:, slot], dram["ctx"][bass.ts(tile, P), :]).then_inc(context_ready[slot], 16)

            def turn(t, ring, rounds, valid):
                if valid(t + 3):
                    if started(t, 0):
                        sp.wait_ge(values_psum, t + 1)
                    load_context(t + 3, ring(3))
                if valid(t):
                    max_to_stack(t, ring(0), 1)
                if valid(t + 2):
                    load(t, ring(2), rounds(2))
                if valid(t + 3):
                    store(t, ring(3))
                if valid(t + 1):
                    max_to_stack(t + 1, ring(1), 0)

            pipeline(sp, turn)

        @block.vector
        def _(dve):
            ln.on_vector(dve)
            nc.vector.memset(minus_one[:], -SELU_SCALE * SELU_ALPHA).then_inc(consts_set, 1)
            dve.wait_ge(ln.ready, 1)
            nc.vector.tensor_scalar(ln.rstd[:], ln.rstd[:], C_HD ** -0.5, None, ALU.mult).then_inc(scaled_rstd, 1)
            dve.wait_ge(scaled_rstd, 1)
            ln.normalise(rows[:], 0).then_inc(rows_ready, 1)

            def maximum(tile, b, h):
                dve.wait_ge(max_scored, 16 * tile + (8 * b + h + 1))
                nc.vector.tensor_reduce(neg_max[:, b, :, h], ps[:, h % 2, :].rearrange("p (q k) -> p q k", q=2),
                                        AX.X, ALU.max, negate=True).then_inc(max_taken, 1)

            def divide(tile, b):
                count = 2 * tile + (b + 1)
                dve.wait_ge(mixed_rows, count)
                view = ps[:, 6, :].rearrange("p (g c) -> p g c", c=V_COLS)
                nc.vector.reciprocal(inv[:], view[:, :, C_HD]).then_inc(inv_ready, 1)
                dve.wait_ge(inv_ready, count)
                out = mixed[:, :, b].rearrange("p q (h d) -> p q h d", d=C_HD)
                nc.vector.tensor_tensor(out, view[:, :, 0:C_HD].rearrange("p (q h) d -> p q h d", q=2),
                                        inv[:].rearrange("p (q h) -> p q h", q=2)[:, :, :, None].to_broadcast([P, 2, C_HEADS, C_HD]),
                                        ALU.mult).then_inc(mixed_ready, 1)

            def turn(t, ring, rounds, valid):
                if valid(t + 3) and started(t, -2):
                    dve.wait_ge(split_done, t + 3)
                    ln.normalise(rows[:], t + 3).then_inc(rows_ready, 1)
                for b in range(2):
                    for g in range(4):
                        if valid(t + 1):
                            maximum(t + 1, b, 2 * g)
                            maximum(t + 1, b, 2 * g + 1)
                        if g == 1 and b == 0 and valid(t - 1):
                            divide(t - 1, 1)
                        if g == 1 and b == 1 and valid(t):
                            divide(t, 0)
                if valid(t - 1):
                    dve.wait_ge(x_ready, t)
                    nc.vector.bn_stats(core.row_stats[:, t - 1, :], core.x[:, t - 1, :]).then_inc(stats_done, 1)

            pipeline(dve, turn)
            dve.wait_ge(stats_done, TILES)

        @block.scalar
        def _(act):
            for slot in range(RING):
                for stack, rows_of in ((q_stack, MAX_ROW), (k_stack, STACK_ROWS)):
                    act.dma_start(stack[PARTS * STACK:rows_of, slot].rearrange("p b h f -> p (b h f)"),
                                  dram["fa_padding"][0:rows_of - PARTS * STACK]).then_inc(padded, 16)
            ln.on_scalar(act)
            act.wait_ge(cleared_values, 2)
            act.wait_ge(consts_set, 1)

            def split_high(n, slot, round):
                act.wait_ge(rows_ready, n + 1)
                act.wait_ge(context_ready[slot], 16 * round + 16)
                if started(n, RING):
                    act.wait_ge(stored[slot], STORES * round)
                for kind, source in enumerate((rows[:], context[:, slot])):
                    nc.scalar.copy(parts[:, slot, kind, 0], source).then_inc(high_ready, 1)

            def values_of(tile, slot):
                act.wait_ge(values_psum, tile + 1)
                nc.scalar.copy(values[:, slot, :, :, 0:C_HD],
                               ps[:, 7, 0:E].rearrange("p (k g d) -> p k g d", k=2, d=C_HD)).then_inc(values_ready, 1)

            def max_to_rows(tile, b):
                act.wait_ge(max_turned, 2 * tile + (b + 1))
                nc.scalar.copy(max_rows[0:PARTS * C_HEADS, b], ps[0:PARTS * C_HEADS, 7, 0:E]).then_inc(max_rows_ready, 1)

            def exponentials(t, b, g):
                act.wait_ge(scored, 8 * t + (4 * b + g + 1))
                if b or started(t, 1):
                    act.wait_ge(mixed_done, 4 * t + (2 * b + g // 2 - 1))
                nc.scalar.activation(probs[:, g].rearrange("p h k q -> p h (k q)"), ps[:, 2 + 2 * (g % 2):4 + 2 * (g % 2), :], ACT.Exp).then_inc(exp_done, 1)

            def take_mixed(tile, b):
                act.wait_ge(mixed_done, 4 * tile + (2 * b + 2))
                nc.scalar.copy(mixedT[:], ps[:, 6, :].rearrange("p (k q) -> p k q", k=2)).then_inc(mixedT_ready, 1)

            def turn(t, ring, rounds, valid):
                if valid(t):
                    exponentials(t, 0, 0)
                if valid(t - 1):
                    take_mixed(t - 1, 1)
                if valid(t):
                    exponentials(t, 0, 1)
                if valid(t + 3):
                    split_high(t + 3, ring(3), rounds(3))
                if valid(t):
                    max_to_rows(t, 1)
                    exponentials(t, 0, 2)
                if valid(t - 1):
                    act.wait_ge(mixed_turned, t)
                    nc.scalar.copy(mixed_c[:], ps[:, 7, 0:E]).then_inc(mixed_c_ready, 1)
                if valid(t):
                    exponentials(t, 0, 3)
                    exponentials(t, 1, 0)
                    take_mixed(t, 0)
                if valid(t - 1):
                    act.wait_ge(projected, t)
                    nc.scalar.activation(below[:], ps[:, 7, E:2 * E], ACT.Relu, scale=-1.0).then_inc(selu_parts, 1)
                    nc.scalar.activation(above[:], ps[:, 7, E:2 * E], ACT.Relu, scale=SELU_SCALE).then_inc(channels_read, 1)
                if valid(t):
                    exponentials(t, 1, 1)
                if valid(t - 1):
                    act.wait_ge(selu_parts, t)
                    nc.scalar.activation(exp_below[:], below[:], ACT.Exp, scale=-1.0).then_inc(exp_below_ready, 1)
                if valid(t + 1):
                    max_to_rows(t + 1, 0)
                if valid(t - 1):
                    act.wait_ge(exp_below_ready, t)
                    nc.scalar.activation(negative[:], exp_below[:], ACT.Identity, scale=SELU_SCALE * SELU_ALPHA, bias=minus_one[:]).then_inc(selu_ready, 1)
                if valid(t):
                    exponentials(t, 1, 2)
                if valid(t + 1):
                    values_of(t + 1, ring(1))
                if valid(t):
                    exponentials(t, 1, 3)

            pipeline(act, turn)

        @block.gpsimd
        def _(pool):
            nc.gpsimd.memset(values[:], 0.0).then_inc(cleared_values, 1)
            pool.wait_ge(cleared_values, 1)
            nc.gpsimd.memset(values[:, :, :, :, C_HD:C_HD + 1], 1.0).then_inc(cleared_values, 1)
            pool.wait_ge(cleared_values, 2)
            nc.gpsimd.memset(zeros[:], 0.0).then_inc(cleared_values, 1)
            pool.wait_ge(cleared_values, 3)

            few_zeros = zeros[:, 0:2 * C_HEADS].rearrange("p (q h) -> p q h", q=2)

            def split(n, slot):
                part = lambda kind, k: parts[:, slot, kind, k]
                for kind, source in enumerate((rows[:], context[:, slot])):
                    pool.wait_ge(high_ready, 2 * n + (kind + 1))
                    nc.gpsimd.tensor_tensor(rest[:, kind], source, part(kind, 0), ALU.subtract).then_inc(split_step, 1)
                for kind in range(2):
                    pool.wait_ge(split_step, 4 * n + (kind + 1))
                    nc.gpsimd.tensor_tensor(part(kind, 1), rest[:, kind], zeros[:], ALU.add).then_inc(split_step, 1)
                pool.wait_ge(split_step, 4 * n + 4)
                for kind in range(2):
                    done = nc.gpsimd.tensor_tensor(part(kind, 2), rest[:, kind], part(kind, 1), ALU.subtract)
                done.then_inc(split_done, 1)

            def split_max(tile, b):
                count = 2 * tile + (b + 1)
                pool.wait_ge(max_taken, 16 * tile + (8 * b + 8))
                nc.gpsimd.tensor_tensor(max_parts[:, b, :, 0], neg_max[:, b], few_zeros, ALU.add).then_inc(max_high, 1)
                pool.wait_ge(max_high, count)
                nc.gpsimd.tensor_tensor(max_rest[:, b], neg_max[:, b], max_parts[:, b, :, 0], ALU.subtract).then_inc(max_left, 1)
                pool.wait_ge(max_left, count)
                nc.gpsimd.tensor_tensor(max_parts[:, b, :, 1], max_rest[:, b], few_zeros, ALU.add).then_inc(max_mid, 1)
                pool.wait_ge(max_mid, count)
                nc.gpsimd.tensor_tensor(max_parts[:, b, :, 2], max_rest[:, b], max_parts[:, b, :, 1], ALU.subtract).then_inc(max_split, 1)

            def turn(t, ring, rounds, valid):
                if valid(t + 3):
                    split(t + 3, ring(3))
                if valid(t + 1):
                    split_max(t + 1, 0)
                if valid(t - 1):
                    pool.wait_ge(selu_ready, t)
                    nc.gpsimd.tensor_tensor(selu[:], above[:], negative[:], ALU.add).then_inc(selu_sum, 1)
                    pool.wait_ge(selu_sum, t)
                    nc.gpsimd.tensor_tensor(core.x[:, t - 1, :], core.x[:, t - 1, :], selu[:], ALU.add).then_inc(x_ready, 1)
                if valid(t + 1):
                    split_max(t + 1, 1)

            pipeline(pool, turn)

        @block.tensor
        def _(pe):
            pe.wait_ge(loaded, 32)
            pe.wait_ge(padded, 2 * RING * 16)

            def score_for_max(tile, slot, round, b, h):
                if (b, h) == (0, 0):
                    pe.wait_ge(stacked[slot], LOADS * round + LOADS)
                if not isinstance(tile, int) or 8 * b + h >= 2 or tile:
                    pe.wait_ge(max_taken, 16 * tile + (8 * b + h - 1))
                for q in range(2):
                    done = nc.tensor.matmul(ps[:, h % 2, q * E:(q + 1) * E], q_stack[0:MAX_ROW, slot, b, h, q * P:(q + 1) * P],
                                            k_stack[0:MAX_ROW, slot, b, h, :], start=True, stop=True)
                done.then_inc(max_scored, 1)

            def score(t, slot, b, g):
                if g == 0:
                    pe.wait_ge(max_stacked[b], 16 * t + 16)
                if not isinstance(t, int) or 8 * t + 4 * b + g >= 2:
                    pe.wait_ge(exp_done, 8 * t + (4 * b + g - 1))
                for h in range(2):
                    for k in range(2):
                        done = nc.tensor.matmul(ps[:, 2 + 2 * (g % 2) + h, k * E:(k + 1) * E],
                                                k_stack[0:STACK_ROWS, slot, b, 2 * g + h, k * P:(k + 1) * P],
                                                q_stack[0:STACK_ROWS, slot, b, 2 * g + h, :], start=True, stop=True)
                done.then_inc(scored, 1)

            def mix(tile, slot, b, half):
                pe.wait_ge(exp_done, 8 * tile + (4 * b + 2 * half + 2))
                if half == 0:
                    if b or started(tile, 1):
                        pe.wait_ge(mixed_ready, 2 * tile + b)
                    pe.wait_ge(values_ready, tile + 1)
                for k in range(2):
                    for c in range(4):
                        h = 4 * half + c
                        done = nc.tensor.matmul(ps[32 * c:32 * c + 32, 6, half * E:(half + 1) * E], values[:, slot, k, 8 * b + h, :],
                                                probs[:, h // 2, h % 2, k, :], start=(k == 0), stop=(k == 1), skip_group_check=True)
                done.then_inc(mixed_done, 1)

            def turn_mixed(tile, b):
                pe.wait_ge(mixedT_ready, 2 * tile + (b + 1))
                for q in range(2):
                    for half in range(2):
                        done = nc.tensor.transpose(ps[:, 6, (2 * q + half) * P:(2 * q + half + 1) * P],
                                                   mixedT[:, half, q * P:(q + 1) * P], ident[:])
                done.then_inc(mixed_rows, 1)

            def turn_max(tile, b):
                pe.wait_ge(max_split, 2 * tile + (b + 1))
                for q in range(2):
                    done = nc.tensor.matmul(ps[0:PARTS * C_HEADS, 7, q * P:(q + 1) * P],
                                            max_parts[:, b, q].rearrange("p a h -> p (a h)"), ident_bf[:], start=True, stop=True)
                done.then_inc(max_turned, 1)

            def turn(t, ring, rounds, valid):
                def heads(b, g):
                    if valid(t + 1):
                        score_for_max(t + 1, ring(1), rounds(1), b, 2 * g)
                        score_for_max(t + 1, ring(1), rounds(1), b, 2 * g + 1)
                    if valid(t):
                        score(t, ring(0), b, g)

                heads(0, 0)
                if valid(t - 1):
                    mix(t - 1, ring(-1), 1, 1)
                heads(0, 1)
                if valid(t):
                    pe.wait_ge(values_ready, t + 1)
                    turn_max(t, 1)
                if valid(t - 1):
                    turn_mixed(t - 1, 1)
                heads(0, 2)
                if valid(t - 1):
                    if valid(t):
                        pe.wait_ge(max_rows_ready, 2 * t + 2)
                    else:
                        pe.wait_ge(channels_read, t - 1)
                    pe.wait_ge(mixed_ready, 2 * t)
                    for q in range(2):
                        done = nc.tensor.transpose(ps[:, 7, q * P:(q + 1) * P], mixed[:, q].rearrange("p b c -> p (b c)"), ident[:])
                    done.then_inc(mixed_turned, 1)
                heads(0, 3)
                if valid(t):
                    mix(t, ring(0), 0, 0)
                if valid(t - 1):
                    pe.wait_ge(mixed_c_ready, t)
                    nc.tensor.matmul(ps[:, 7, E:2 * E], w_out[:], mixed_c[:], start=True, stop=True).then_inc(projected, 1)
                heads(1, 0)
                if valid(t):
                    mix(t, ring(0), 0, 1)
                heads(1, 1)
                if valid(t + 1):
                    if valid(t - 1):
                        pe.wait_ge(channels_read, t)
                    elif valid(t):
                        pe.wait_ge(max_rows_ready, 2 * t + 2)
                    turn_max(t + 1, 0)
                if valid(t):
                    turn_mixed(t, 0)
                heads(1, 2)
                if valid(t + 1):
                    pe.wait_ge(context_ready[ring(1)], 16 * rounds(1) + 16)
                    pe.wait_ge(max_rows_ready, 2 * t + 3)
                    for k in range(2):
                        done = nc.tensor.transpose(ps[:, 7, k * P:(k + 1) * P], context[:, ring(1), k * P:(k + 1) * P], ident[:])
                    done.then_inc(values_psum, 1)
                heads(1, 3)
                if valid(t):
                    mix(t, ring(0), 1, 0)

            pipeline(pe, turn)

F_N, F_S, F_H = 8, 8, 8
F_SEL, F_UPD = F_N * F_S, F_N * F_H
F_IN = F_SEL + F_N + F_UPD
F_MEAN, F_UPD_AT = F_SEL, F_SEL + F_N
F_ROWS = 96
WIDE = 4
EXP_LIMIT = 87.0


def selected_update(core):
    nc, dram, ps, ident = core.nc, core.dram, core.psum, core.ident
    with ExitStack() as scope:
        sb = lambda name, shape, dt=F32: scope.enter_context(nc.sbuf_tensor(f"ff_{name}", shape, dt))
        sem = lambda name: core.sem(f"ff_{name}")
        ln = RowNorm(core, "ff", scope)
        w_in = sb("w_in", [P, KC, F_IN])
        debias = sb("debias", [P, KC, F_N])
        w_back = sb("w_back", [P, E])
        center, slope, first = sb("center", [P, F_N]), sb("slope", [P, F_N]), sb("first", [P, F_N])
        ones = sb("ones", [P, P])
        shift_parts, shift = sb("shift_parts", [P, KC, F_IN]), sb("shift", [P, F_IN])
        xn, xT = sb("xn", [P, WIDE, E]), sb("xT", [P, WIDE, E])
        proj = sb("proj", [P, TILES, F_IN])
        squares = sb("squares", [P, TILES, F_SEL])
        raw, dist, gate, hot = (sb(name, [P, TILES, F_N]) for name in ("raw", "dist", "gate", "hot"))
        length, best, pick, keep, move = (sb(name, [P, TILES]) for name in ("length", "best", "pick", "keep", "move"))
        chosen = sb("chosen", [P, WIDE, F_ROWS])
        chosenT = sb("chosenT", [P, WIDE, P])
        moved = sb("moved", [P, WIDE, E])

        loaded, zeroed, shift_step, shift_psum, shift_ready = (sem(n) for n in ("loaded", "zeroed", "shift_step", "shift_psum", "shift_ready"))
        xn_ready, xT_psum, xT_ready, projected, proj_ready = (sem(n) for n in ("xn_ready", "xT_psum", "xT_ready", "projected", "proj_ready"))
        squares_ready, gate_step, z_ready, gate_exp, hot_ready = (sem(n) for n in ("squares_ready", "gate_step", "z_ready", "gate_exp", "hot_ready"))
        chosen_ready, bias_ready, turned, chosenT_ready, moved_ready, back, x_ready, stats_done = (
            sem(n) for n in ("chosen_ready", "bias_ready", "turned", "chosenT_ready", "moved_ready", "back", "x_ready", "stats_done"))
        LOADS = 6 * 16
        by_update = lambda a, width: a.rearrange("p (n s) -> p n s", s=width)

        block = scope.enter_context(nc.Block())

        @block.sync
        def _(sp):
            for out, src in ((w_in[:], chunked(dram["ff_w_in"])), (debias[:], chunked(dram["ff_debias"])), (w_back[0:F_ROWS], dram["ff_w_back"]),
                             (center[:], dram["ff_center"]), (slope[:], dram["ff_slope"]), (first[:], dram["ff_first"])):
                sp.dma_start(out, src).then_inc(loaded, 16)
            sp.wait_ge(loaded, LOADS)

        @block.gpsimd
        def _(pool):
            nc.gpsimd.memset(chosen[:], 0.0).then_inc(zeroed, 1)
            pool.wait_ge(zeroed, 1)
            pool.wait_ge(hot_ready, 1)
            pool.sem_inc(turned, WIDE)
            with pool.Fori(0, TILES // WIDE) as i:
                for u in range(WIDE):
                    t = WIDE * i + u
                    pool.wait_ge(turned, t + 1)
                    nc.gpsimd.tensor_copy(chosen[:, u, F_UPD:F_UPD + F_N], hot[:, t, :]).then_inc(bias_ready, 1)

        @block.scalar
        def _(act):
            act.preload_act_table_set(EXP_LN)
            ln.on_scalar(act)
            act.wait_ge(shift_psum, 1)
            nc.scalar.copy(shift[:], ps[:, 7, 0:F_IN]).then_inc(shift_ready, 1)
            with act.Fori(0, TILES // WIDE) as i:
                for u in range(WIDE):
                    act.wait_ge(xT_psum, WIDE * i + u + 1)
                    nc.scalar.copy(xT[:, u], ps[:, u, 0:E]).then_inc(xT_ready, 1)
            act.wait_ge(proj_ready, TILES)
            nc.scalar.activation(squares[:], proj[:, :, 0:F_SEL], ACT.Square).then_inc(squares_ready, 1)
            act.wait_ge(z_ready, 1)
            nc.scalar.activation(gate[:], raw[:], ACT.Exp).then_inc(gate_exp, 1)
            with act.Fori(0, TILES // WIDE) as i:
                for u in range(WIDE):
                    act.wait_ge(turned, WIDE * i + u + 1 + WIDE)
                    nc.scalar.copy(chosenT[0:F_ROWS, u], ps[0:F_ROWS, u, 0:P]).then_inc(chosenT_ready, 1)

        @block.vector
        def _(dve):
            ln.on_vector(dve)
            nc.vector.memset(ones[:], 1.0).then_inc(shift_step, 1)
            dve.wait_ge(loaded, LOADS)
            for c in range(KC):
                mean = w_in[:, c, F_MEAN:F_MEAN + F_N]
                nc.vector.tensor_tensor(by_update(shift_parts[:, c, 0:F_SEL], F_S), by_update(w_in[:, c, 0:F_SEL], F_S),
                                        mean[:, :, None].to_broadcast([P, F_N, F_S]), ALU.mult).then_inc(shift_step, 1)
                nc.vector.scalar_tensor_tensor(shift_parts[:, c, F_MEAN:F_MEAN + F_N], mean, 0.5, mean, ALU.mult, ALU.mult).then_inc(shift_step, 1)
                nc.vector.tensor_tensor(by_update(shift_parts[:, c, F_UPD_AT:], F_H), by_update(w_in[:, c, F_UPD_AT:], F_H),
                                        debias[:, c, :, None].to_broadcast([P, F_N, F_H]), ALU.mult).then_inc(shift_step, 1)
            dve.wait_ge(ln.ready, 1)
            dve.wait_ge(shift_ready, 1)
            with dve.Fori(0, TILES // WIDE) as i:
                for u in range(WIDE):
                    ln.normalise(xn[:, u], WIDE * i + u).then_inc(xn_ready, 1)
                for u in range(WIDE):
                    t = WIDE * i + u
                    dve.wait_ge(projected, t + 1)
                    nc.vector.tensor_tensor(proj[:, t, :], ps[:, WIDE + u, 0:F_IN], shift[:], ALU.subtract).then_inc(proj_ready, 1)
            across = lambda a: a[:, :, None].to_broadcast([P, TILES, F_N])
            every = lambda a: a[:, None, :].to_broadcast([P, TILES, F_N])
            nc.vector.tensor_tensor(length[:], ln.rstd[:], ln.rstd[:], ALU.mult).then_inc(gate_step, 1)
            dve.wait_ge(gate_step, 1)
            nc.vector.scalar_tensor_tensor(length[:], length[:], float(E), ln.var[:], ALU.mult, ALU.mult).then_inc(gate_step, 1)
            dve.wait_ge(gate_step, 2)
            dve.wait_ge(proj_ready, TILES)
            nc.vector.scalar_tensor_tensor(dist[:], proj[:, :, F_MEAN:F_MEAN + F_N], -2.0, across(length), ALU.mult, ALU.add).then_inc(gate_step, 1)
            dve.wait_ge(gate_step, 3)
            nc.vector.reciprocal(dist[:], dist[:]).then_inc(gate_step, 1)
            dve.wait_ge(squares_ready, 1)
            nc.vector.tensor_reduce(raw[:], squares[:].rearrange("p t (n s) -> p t n s", s=F_S), AX.X, ALU.add).then_inc(gate_step, 1)
            dve.wait_ge(gate_step, 5)
            nc.vector.tensor_tensor(raw[:], raw[:], dist[:], ALU.mult).then_inc(gate_step, 1)
            dve.wait_ge(gate_step, 6)
            nc.vector.tensor_tensor(raw[:], every(center), raw[:], ALU.subtract).then_inc(gate_step, 1)
            dve.wait_ge(gate_step, 7)
            nc.vector.tensor_tensor(raw[:], raw[:], every(slope), ALU.mult).then_inc(gate_step, 1)
            dve.wait_ge(gate_step, 8)
            nc.vector.tensor_scalar(raw[:], raw[:], EXP_LIMIT, None, ALU.min).then_inc(z_ready, 1)
            dve.wait_ge(gate_exp, 1)
            nc.vector.tensor_scalar(gate[:], gate[:], 1.0, None, ALU.add).then_inc(gate_step, 1)
            dve.wait_ge(gate_step, 9)
            nc.vector.reciprocal(gate[:], gate[:]).then_inc(gate_step, 1)
            dve.wait_ge(gate_step, 10)
            nc.vector.tensor_reduce(best[:], gate[:], AX.X, ALU.max).then_inc(gate_step, 1)
            dve.wait_ge(gate_step, 11)
            nc.vector.tensor_tensor(gate[:], gate[:], across(best), ALU.is_ge).then_inc(gate_step, 1)
            nc.vector.tensor_scalar(keep[:], best[:], -1.0, 1.0, ALU.mult, ALU.add).then_inc(gate_step, 1)
            dve.wait_ge(gate_step, 13)
            nc.vector.tensor_tensor(gate[:], gate[:], every(first), ALU.mult).then_inc(gate_step, 1)
            nc.vector.tensor_tensor(keep[:], keep[:], ln.rstd[:], ALU.mult).then_inc(gate_step, 1)
            dve.wait_ge(gate_step, 15)
            nc.vector.tensor_reduce(pick[:], gate[:], AX.X, ALU.max).then_inc(gate_step, 1)
            nc.vector.tensor_tensor(move[:], ln.mean[:], keep[:], ALU.mult).then_inc(gate_step, 1)
            dve.wait_ge(gate_step, 17)
            nc.vector.tensor_tensor(hot[:], gate[:], across(pick), ALU.is_equal).then_inc(gate_step, 1)
            nc.vector.tensor_scalar(keep[:], keep[:], 1.0, None, ALU.add).then_inc(gate_step, 1)
            dve.wait_ge(gate_step, 19)
            nc.vector.tensor_tensor(hot[:], hot[:], across(best), ALU.mult).then_inc(hot_ready, 1)
            dve.wait_ge(hot_ready, 1)
            dve.wait_ge(zeroed, 1)
            with dve.Fori(0, TILES // WIDE) as i:
                for u in range(WIDE):
                    t = WIDE * i + u
                    nc.vector.tensor_tensor(by_update(chosen[:, u, 0:F_UPD], F_H), by_update(proj[:, t, F_UPD_AT:], F_H),
                                            hot[:, t, :, None].to_broadcast([P, F_N, F_H]), ALU.mult).then_inc(chosen_ready, 1)
                for u in range(WIDE):
                    t = WIDE * i + u
                    nc.vector.tensor_scalar(moved[:, u], core.x[:, t, :], keep[:, bass.ts(t, 1)], move[:, bass.ts(t, 1)],
                                            ALU.mult, ALU.subtract).then_inc(moved_ready, 1)
                for u in range(WIDE):
                    t = WIDE * i + u
                    dve.wait_ge(back, t + 1)
                    dve.wait_ge(moved_ready, t + 1)
                    nc.vector.tensor_tensor(core.x[:, t, :], moved[:, u], ps[:, WIDE + u, 0:E], ALU.add).then_inc(x_ready, 1)
                for u in range(WIDE):
                    t = WIDE * i + u
                    dve.wait_ge(x_ready, t + 1)
                    nc.vector.bn_stats(core.row_stats[:, t, :], core.x[:, t, :]).then_inc(stats_done, 1)
            dve.wait_ge(stats_done, TILES)

        @block.tensor
        def _(pe):
            pe.wait_ge(loaded, LOADS)
            pe.wait_ge(shift_step, 1 + 3 * KC)
            for c in range(KC):
                done = nc.tensor.matmul(ps[:, 7, 0:F_IN], ones[:], shift_parts[:, c], start=(c == 0), stop=(c == KC - 1))
            done.then_inc(shift_psum, 1)
            pe.wait_ge(shift_ready, 1)
            with pe.Fori(0, TILES // WIDE) as i:
                for u in range(WIDE):
                    pe.wait_ge(xn_ready, WIDE * i + u + 1)
                    for c in range(KC):
                        done = nc.tensor.transpose(ps[:, u, c * P:(c + 1) * P], xn[:, u, c * P:(c + 1) * P], ident[:])
                    done.then_inc(xT_psum, 1)
                for u in range(WIDE):
                    pe.wait_ge(xT_ready, WIDE * i + u + 1)
                    for c in range(KC):
                        done = nc.tensor.matmul(ps[:, WIDE + u, 0:F_IN], xT[:, u, c * P:(c + 1) * P], w_in[:, c],
                                                start=(c == 0), stop=(c == KC - 1))
                    done.then_inc(projected, 1)
            with pe.Fori(0, TILES // WIDE) as i:
                for u in range(WIDE):
                    pe.wait_ge(chosen_ready, WIDE * i + u + 1)
                    pe.wait_ge(bias_ready, WIDE * i + u + 1)
                    nc.tensor.transpose(ps[0:F_ROWS, u, 0:P], chosen[:, u], ident[:]).then_inc(turned, 1)
                for u in range(WIDE):
                    pe.wait_ge(chosenT_ready, WIDE * i + u + 1)
                    nc.tensor.matmul(ps[:, WIDE + u, 0:E], chosenT[0:F_ROWS, u], w_back[0:F_ROWS], start=True, stop=True).then_inc(back, 1)

S_HEADS, S_STATE = 32, 64
S_HD = E // S_HEADS
LEVELS = SEQ.bit_length() - 1


def state_space(core):
    nc, dram, ps, ident = core.nc, core.dram, core.psum, core.ident
    with ExitStack() as scope:
        sb = lambda name, shape, dt=F32: scope.enter_context(nc.sbuf_tensor(f"ss_{name}", shape, dt))
        sem = lambda name: core.sem(f"ss_{name}")
        ln = RowNorm(core, "ss", scope)
        w_bc = sb("w_bc", [P, KC, 2 * S_STATE])
        w_dt, w_out = sb("w_dt", [P, KC, S_HEADS]), sb("w_out", [P, KC, E])
        bias_bc = sb("bias_bc", [S_STATE, 2])
        bias_dt, skip, rate, bias_out = sb("bias_dt", [P, S_HEADS]), sb("skip", [P, S_HEADS]), sb("rate", [P, S_HEADS]), sb("bias_out", [P, E])
        spans = sb("spans", [P, LEVELS, P])
        pairs = sb("pairs", [P, LEVELS, P])
        xn, xT = sb("xn", [P, 2, E]), sb("xT", [P, 2, E])
        bcT = sb("bcT", [S_STATE, 2, 2, P])
        dt, dt_tail, dA = (sb(name, [P, TILES, S_HEADS]) for name in ("dt", "dt_tail", "dA"))
        scoresT = sb("scoresT", [P, TILES, P])
        same, same_dot = sb("same", [P, TILES, P]), sb("same_dot", [P, TILES])
        own = sb("own", [P, TILES, S_HEADS])
        decay = sb("decay", [P, TILES, LEVELS, S_HEADS])
        level_scores = sb("level_scores", [P, 2, LEVELS, P])
        xdt, inputs = sb("xdt", [P, 2, E]), sb("inputs", [P, 2, LEVELS, E])
        own_rows, outputs = sb("own_rows", [P, 2, E]), sb("outputs", [P, 2, LEVELS, E])
        yT = sb("yT", [P, 2, E])

        loaded = sem("loaded")
        xn_ready, xT_psum, xT_ready, projected, bc_ready, dt_raw, scored, scores_ready = (
            sem(n) for n in ("xn_ready", "xT_psum", "xT_ready", "projected", "bc_ready", "dt_raw", "scored", "scores_ready"))
        soft_step, tail_exp, tail_log, rate_ready, dA_ready, spans_psum, decay_ready, own_step = (
            sem(n) for n in ("soft_step", "tail_exp", "tail_log", "rate_ready", "dA_ready", "spans_psum", "decay_ready", "own_step"))
        pool_step, inputs_ready, own_ready, biased, level_ready, level_psum, outputs_ready, y_psum, yT_ready, out_psum, x_ready, stats_done = (
            sem(n) for n in ("pool_step", "inputs_ready", "own_ready", "biased", "level_ready", "level_psum", "outputs_ready",
                             "y_psum", "yT_ready", "out_psum", "x_ready", "stats_done"))
        LOADS = 10 * 16
        by_head = lambda a: a.rearrange("p (h d) -> p h d", d=S_HD)
        per_head = lambda a: a[:, :, None].to_broadcast([P, S_HEADS, S_HD])

        block = scope.enter_context(nc.Block())

        @block.sync
        def _(sp):
            for out, src in ((w_bc[:], chunked(dram["ss_w_bc"])), (w_dt[:], chunked(dram["ss_w_dt"])), (w_out[:], chunked(dram["ss_w_out"])),
                             (bias_bc[:], dram["ss_bias_bc"]), (bias_dt[:], dram["ss_bias_dt"]), (skip[:], dram["ss_skip"]),
                             (rate[:], dram["ss_A_log"]), (bias_out[:], dram["ss_bias_out"]), (spans[:], dram["ss_spans"]),
                             (pairs[:], dram["ss_pairs"])):
                sp.dma_start(out, src).then_inc(loaded, 16)
            sp.wait_ge(loaded, LOADS)

        @block.gpsimd
        def _(pool):
            pool.wait_ge(own_step, 4)
            pool.wait_ge(decay_ready, LEVELS)
            with pool.Fori(0, PAIRS) as i:
                for u in range(2):
                    t = 2 * i + u
                    pool.wait_ge(xn_ready, t + (TILES + 1))
                    nc.gpsimd.tensor_tensor(by_head(xdt[:, u]), by_head(xn[:, u]), per_head(dt[:, t, :]), ALU.mult).then_inc(pool_step, 1)
                    pool.wait_ge(pool_step, t + 1)
                    nc.gpsimd.tensor_tensor(inputs[:, u].rearrange("p m (h d) -> p m h d", d=S_HD),
                                            by_head(xdt[:, u])[:, None].to_broadcast([P, LEVELS, S_HEADS, S_HD]),
                                            decay[:, t, :, :, None].to_broadcast([P, LEVELS, S_HEADS, S_HD]), ALU.mult).then_inc(inputs_ready, 1)
                for u in range(2):
                    t = 2 * i + u
                    nc.gpsimd.tensor_tensor(by_head(own_rows[:, u]), by_head(xn[:, u]), per_head(own[:, t, :]), ALU.mult).then_inc(own_ready, 1)
                    nc.gpsimd.tensor_tensor(core.x[:, t, :], core.x[:, t, :], bias_out[:], ALU.add).then_inc(biased, 1)

        @block.scalar
        def _(act):
            act.preload_act_table_set(EXP_LN)
            ln.on_scalar(act)
            act.wait_ge(loaded, LOADS)
            nc.scalar.activation(rate[:], rate[:], ACT.Exp).then_inc(rate_ready, 1)
            with act.Fori(0, PAIRS) as i:
                ns = [act.snap(2 * i + (u + 1)) for u in range(2)]
                for u, n in enumerate(ns):
                    act.wait_ge(xT_psum, n)
                    nc.scalar.copy(xT[:, u], ps[:, u, 0:E]).then_inc(xT_ready, 1)
                for u, n in enumerate(ns):
                    act.wait_ge(projected, n)
                    for k in range(2):
                        done = nc.scalar.activation(bcT[:, u, k], ps[0:S_STATE, 2 + u, k * P:(k + 1) * P], ACT.Identity, bias=bias_bc[:, k:k + 1])
                    done.then_inc(bc_ready, 1)
                for u, n in enumerate(ns):
                    act.wait_ge(scored, n)
                    nc.scalar.copy(scoresT[:, 2 * i + u, :], ps[:, 6 + u, 0:P]).then_inc(scores_ready, 1)
            act.wait_ge(soft_step, 1)
            nc.scalar.activation(dt_tail[:], dt_tail[:], ACT.Exp, scale=-1.0).then_inc(tail_exp, 1)
            act.wait_ge(tail_exp, 1)
            nc.scalar.activation(dt_tail[:], dt_tail[:], ACT.Ln, bias=1.0).then_inc(tail_log, 1)
            for m in range(LEVELS):
                act.wait_ge(spans_psum, m + 1)
                nc.scalar.activation(decay[:, :, m, :], ps[:, m, :].rearrange("p (t h) -> p t h", h=S_HEADS), ACT.Exp).then_inc(decay_ready, 1)
            with act.Fori(0, PAIRS) as i:
                for u in range(2):
                    act.wait_ge(y_psum, 2 * i + (u + 1))
                    nc.scalar.copy(yT[:, u], ps[:, 6 + u, 0:E]).then_inc(yT_ready, 1)

        @block.vector
        def _(dve):
            ln.on_vector(dve)
            dve.wait_ge(ln.ready, 1)
            dve.wait_ge(loaded, LOADS)
            with dve.Fori(0, PAIRS) as i:
                for u in range(2):
                    ln.normalise(xn[:, u], 2 * i + u).then_inc(xn_ready, 1)
                for u in range(2):
                    dve.wait_ge(projected, 2 * i + (u + 1))
                    nc.vector.tensor_tensor(dt[:, 2 * i + u, :], ps[:, 4 + u, 0:S_HEADS], bias_dt[:], ALU.add).then_inc(dt_raw, 1)
            every = lambda a: a[:, None, :].to_broadcast([P, TILES, S_HEADS])
            dve.wait_ge(dt_raw, TILES)
            nc.vector.scalar_tensor_tensor(dt_tail[:], dt[:], -1.0, dt[:], ALU.mult, ALU.max).then_inc(soft_step, 1)
            dve.wait_ge(tail_log, 1)
            nc.vector.scalar_tensor_tensor(dt[:], dt[:], 0.0, dt_tail[:], ALU.max, ALU.add).then_inc(soft_step, 1)
            dve.wait_ge(soft_step, 2)
            dve.wait_ge(rate_ready, 1)
            nc.vector.scalar_tensor_tensor(dA[:], dt[:], -1.0, every(rate), ALU.mult, ALU.mult).then_inc(dA_ready, 1)
            dve.wait_ge(scores_ready, TILES)
            nc.vector.tensor_tensor(same[:], scoresT[:], ident[:, None, :].to_broadcast([P, TILES, P]), ALU.mult).then_inc(own_step, 1)
            dve.wait_ge(own_step, 1)
            nc.vector.tensor_reduce(same_dot[:], same[:], AX.X, ALU.add).then_inc(own_step, 1)
            dve.wait_ge(own_step, 2)
            nc.vector.tensor_tensor(own[:], dt[:], same_dot[:, :, None].to_broadcast([P, TILES, S_HEADS]), ALU.mult).then_inc(own_step, 1)
            dve.wait_ge(own_step, 3)
            nc.vector.tensor_tensor(own[:], own[:], every(skip), ALU.add).then_inc(own_step, 1)
            dve.wait_ge(decay_ready, LEVELS)
            with dve.Fori(0, PAIRS) as i:
                for u in range(2):
                    ln.normalise(xn[:, u], 2 * i + u).then_inc(xn_ready, 1)
                for u in range(2):
                    nc.vector.tensor_tensor(level_scores[:, u], pairs[:], scoresT[:, 2 * i + u, None, :].to_broadcast([P, LEVELS, P]),
                                            ALU.mult).then_inc(level_ready, 1)
                for u in range(2):
                    t = 2 * i + u
                    dve.wait_ge(level_psum, t + 1)
                    nc.vector.tensor_tensor(outputs[:, u].rearrange("p m (h d) -> p m h d", d=S_HD),
                                            ps[:, 3 * u:3 * u + 3, :].rearrange("p k (m h d) -> p (k m) h d", m=2, d=S_HD),
                                            decay[:, t, :, :, None].to_broadcast([P, LEVELS, S_HEADS, S_HD]), ALU.mult).then_inc(outputs_ready, 1)
                for u in range(2):
                    t = 2 * i + u
                    dve.wait_ge(out_psum, t + 1)
                    dve.wait_ge(biased, t + 1)
                    nc.vector.tensor_tensor(core.x[:, t, :], core.x[:, t, :], ps[:, 6 + u, E:2 * E], ALU.add).then_inc(x_ready, 1)
                    dve.wait_ge(x_ready, t + 1)
                    nc.vector.bn_stats(core.row_stats[:, t, :], core.x[:, t, :]).then_inc(stats_done, 1)
            dve.wait_ge(stats_done, TILES)

        @block.tensor
        def _(pe):
            pe.wait_ge(loaded, LOADS)
            with pe.Fori(0, PAIRS) as i:
                ns = [pe.snap(2 * i + (u + 1)) for u in range(2)]
                for u, n in enumerate(ns):
                    pe.wait_ge(xn_ready, n)
                    for c in range(KC):
                        done = nc.tensor.transpose(ps[:, u, c * P:(c + 1) * P], xn[:, u, c * P:(c + 1) * P], ident[:])
                    done.then_inc(xT_psum, 1)
                for u, n in enumerate(ns):
                    pe.wait_ge(xT_ready, n)
                    rows = lambda c: xT[:, u, c * P:(c + 1) * P]
                    for k in range(2):
                        for c in range(KC):
                            nc.tensor.matmul(ps[0:S_STATE, 2 + u, k * P:(k + 1) * P], w_bc[:, c, k * S_STATE:(k + 1) * S_STATE], rows(c),
                                             start=(c == 0), stop=(c == KC - 1))
                    for c in range(KC):
                        done = nc.tensor.matmul(ps[:, 4 + u, 0:S_HEADS], rows(c), w_dt[:, c], start=(c == 0), stop=(c == KC - 1))
                    done.then_inc(projected, 1)
                for u, n in enumerate(ns):
                    pe.wait_ge(bc_ready, n)
                    nc.tensor.matmul(ps[:, 6 + u, 0:P], bcT[:, u, 0], bcT[:, u, 1], start=True, stop=True).then_inc(scored, 1)
            pe.wait_ge(dA_ready, 1)
            pe.wait_ge(bc_ready, TILES)
            for m in range(LEVELS):
                nc.tensor.matmul(ps[:, m, :], spans[:, m], dA[:].rearrange("p t h -> p (t h)"), start=True, stop=True).then_inc(spans_psum, 1)
            with pe.Fori(0, PAIRS) as i:
                ns = [pe.snap(2 * i + (u + 1)) for u in range(2)]
                for u, n in enumerate(ns):
                    pe.wait_ge(level_ready, n)
                    pe.wait_ge(inputs_ready, n)
                    for m in range(LEVELS):
                        done = nc.tensor.matmul(ps[:, 3 * u + m // 2, (m % 2) * E:(m % 2 + 1) * E], level_scores[:, u, m], inputs[:, u, m],
                                                start=True, stop=True)
                    done.then_inc(level_psum, 1)
                for u, n in enumerate(ns):
                    pe.wait_ge(own_ready, n)
                    pe.wait_ge(outputs_ready, n)
                    for c in range(KC):
                        y = ps[:, 6 + u, c * P:(c + 1) * P]
                        nc.tensor.matmul(y, own_rows[:, u, c * P:(c + 1) * P], ident[:], start=True, stop=False)
                        for m in range(LEVELS):
                            done = nc.tensor.matmul(y, outputs[:, u, m, c * P:(c + 1) * P], ident[:], start=False, stop=(m == LEVELS - 1))
                    done.then_inc(y_psum, 1)
                for u, n in enumerate(ns):
                    pe.wait_ge(yT_ready, n)
                    for c in range(KC):
                        done = nc.tensor.matmul(ps[:, 6 + u, E:2 * E], yT[:, u, c * P:(c + 1) * P], w_out[:, c],
                                                start=(c == 0), stop=(c == KC - 1))
                    done.then_inc(out_psum, 1)

G_HEADS, G_KV, G_HD = 16, 4, 128
G_GROUP = G_HEADS // G_KV
Q_COLS, KV_COLS = G_HEADS * G_HD, G_KV * G_HD
G_CHUNK = Q_COLS // G_KV



def three_passes(nc, out, lhsT, rhs, start, stop):
    for k, (i, j) in enumerate(((0, 0), (1, 0), (0, 1))):
        done = nc.tensor.matmul(out, lhsT[i], rhs[j], start=start and k == 0, stop=stop and k == 2)
    return done


def grouped_attention(core):
    nc, dram, ps, ident = core.nc, core.dram, core.psum, core.ident
    with ExitStack() as scope:
        sb = lambda name, shape, dt=F32: scope.enter_context(nc.sbuf_tensor(f"ga_{name}", shape, dt))
        sem = lambda name: core.sem(f"ga_{name}")
        ln = RowNorm(core, "ga", scope)
        raw = sb("raw", [P, KC * Q_COLS])
        w_q_high, w_q_low = sb("w_q_high", [P, KC, Q_COLS], F32R), sb("w_q_low", [P, KC, Q_COLS], F32R)
        w_o_high, w_o_low = sb("w_o_high", [P, G_HEADS, E], F32R), sb("w_o_low", [P, G_HEADS, E], F32R)
        w_k, w_v = sb("w_k", [P, KC, KV_COLS]), sb("w_v", [P, KC, KV_COLS])
        bias_q, bias_v, bias_k = sb("bias_q", [P, Q_COLS]), sb("bias_v", [P, KV_COLS]), sb("bias_k", [P, G_KV])
        gain_q, gain_k, gain = sb("gain_q", [P, 1]), sb("gain_k", [P, 1]), sb("gain", [P, 1])
        mask = sb("mask", [P, SEQ])
        ones, rms_eps = sb("ones", [P, P]), sb("rms_eps", [P, 1])
        xn, ctxT_k, ctxT_v = sb("xn", [P, E]), sb("ctxT_k", [P, KC, P]), sb("ctxT_v", [P, KC, P])
        xT_high, xT_low = sb("xT_high", [P, E], F32R), sb("xT_low", [P, E], F32R)
        q, squares, q_scaled = sb("q", [P, Q_COLS]), sb("squares", [P, Q_COLS]), sb("q_scaled", [P, Q_COLS])
        q_sum, q_log, q_inv = sb("q_sum", [P, G_HEADS]), sb("q_log", [P, G_HEADS]), sb("q_inv", [P, G_HEADS])
        qT = sb("qT", [P, G_HEADS, P])
        k_raw, k_squares, k_log, k_inv, kT = (sb(name, [P, KV_COLS]) for name in ("k_raw", "k_squares", "k_log", "k_inv", "kT"))
        values = sb("values", [P, 2, KV_COLS])
        scoresT = sb("scoresT", [P, G_HEADS * SEQ])
        probs = sb("probs", [P, G_HEADS, SEQ])
        top, total, inv = sb("top", [P, G_HEADS]), sb("total", [P, G_HEADS]), sb("inv", [P, G_HEADS])
        probsT = sb("probsT", [P, G_HEADS * SEQ])
        mixedT_high, mixedT_low = sb("mixedT_high", [P, G_HEADS, P], F32R), sb("mixedT_low", [P, G_HEADS, P], F32R)

        loaded, w_q_loaded, w_o_loaded, consts_set, zeroed = (sem(n) for n in ("loaded", "w_q_loaded", "w_o_loaded", "consts_set", "zeroed"))
        w_q_highs, w_q_split, w_o_highs, w_o_split = (sem(n) for n in ("w_q_highs", "w_q_split", "w_o_highs", "w_o_split"))
        ctx_k_ready, ctx_v_ready, xn_ready, xT_psum, xT_highs, xT_ready = (
            sem(n) for n in ("ctx_k_ready", "ctx_v_ready", "xn_ready", "xT_psum", "xT_highs", "xT_ready"))
        q_psum, q_ready, squares_ready, q_sums, q_logs, q_invs, q_scaled_ready, qT_psum, qT_ready = (
            sem(n) for n in ("q_psum", "q_ready", "squares_ready", "q_sums", "q_logs", "q_invs", "q_scaled_ready", "qT_psum", "qT_ready"))
        k_psum, k_ready, k_squared, k_sums, k_logs, k_invs, kT_ready, v_psum, v_ready = (
            sem(n) for n in ("k_psum", "k_ready", "k_squared", "k_sums", "k_logs", "k_invs", "kT_ready", "v_psum", "v_ready"))
        scored, scoresT_ready, turned, masked, top_ready, shifted, exp_done, totals, inv_ready, probs_ready = (
            sem(n) for n in ("scored", "scoresT_ready", "turned", "masked", "top_ready", "shifted", "exp_done", "totals", "inv_ready", "probs_ready"))
        probsT_psum, probsT_ready, mixed_psum, mixed_highs, mixed_lows, out_psum, x_ready, stats_done = (
            sem(n) for n in ("probsT_psum", "probsT_ready", "mixed_psum", "mixed_highs", "mixed_lows", "out_psum", "x_ready", "stats_done"))
        LOADS = 9 * 16
        HALF = G_HEADS // 2

        block = scope.enter_context(nc.Block())

        def pipeline(eng, turn):
            first, last = 1, TILES - 2
            for t in range(-2, first):
                turn(t, lambda k: 0 <= k < TILES)
            with eng.Fori(first, last) as t:
                turn(t, lambda k: True)
            for t in range(last, TILES + 1):
                turn(t, lambda k: 0 <= k < TILES)

        def started(t, first):
            return not isinstance(t, int) or t >= first

        @block.sync
        def _(sp):
            ctx_rows = chunked(dram["ctxT"])
            for g in range(G_KV):
                columns = slice(g * G_CHUNK, (g + 1) * G_CHUNK)
                sp.dma_start(raw[:].rearrange("p (c q) -> p c q", c=KC)[:, :, columns], chunked(dram["ga_w_q"])[:, :, columns]).then_inc(w_q_loaded, 16)
            for out, src in ((bias_q[:], dram["ga_bias_q"].to_broadcast([P, Q_COLS])),
                             (w_k[:], chunked(dram["ga_w_k"])), (w_v[:], chunked(dram["ga_w_v"])),
                             (bias_v[:], dram["ga_bias_v"].to_broadcast([P, KV_COLS])), (bias_k[:], dram["ga_bias_k"]),
                             (gain_q[:], dram["ga_gain_q"]), (gain_k[:], dram["ga_gain_k"]),
                             (mask[0:SEQ], dram["mask"]), (mask[SEQ:P], dram["mask"])):
                sp.dma_start(out, src).then_inc(loaded, 16)

            def turn(t, valid):
                if valid(t + 1):
                    if started(t, 0):
                        sp.wait_ge(k_psum, t + 1)
                    sp.dma_start(ctxT_k[:], ctx_rows[:, :, bass.ts(t + 1, P)]).then_inc(ctx_k_ready, 16)
                if valid(t):
                    if started(t, 1):
                        sp.wait_ge(v_psum, t)
                    sp.dma_start(ctxT_v[:], ctx_rows[:, :, bass.ts(t, P)]).then_inc(ctx_v_ready, 16)
                if isinstance(t, int) and t == -1:
                    sp.wait_ge(w_q_split, KC)
                    sp.dma_start(raw[:].rearrange("p (h e) -> p h e", e=E), chunked(dram["ga_w_o"])).then_inc(w_o_loaded, 16)

            pipeline(sp, turn)
            sp.wait_ge(ctx_v_ready, 16 * TILES)
            sp.wait_ge(loaded, LOADS)

        @block.gpsimd
        def _(pool):
            nc.gpsimd.memset(values[:], 0.0).then_inc(zeroed, 1)
            pool.wait_ge(zeroed, 1)

            def turn(t, valid):
                if valid(t + 1):
                    pool.wait_ge(k_ready, t + 2)
                    nc.gpsimd.tensor_tensor(k_squares[:], k_raw[:], k_raw[:], ALU.mult).then_inc(k_squared, 1)
                if valid(t + 1):
                    for half in range(2):
                        heads = slice(HALF * half, HALF * (half + 1))
                        columns = slice(HALF * G_HD * half, HALF * G_HD * (half + 1))
                        pool.wait_ge(q_invs, 2 * t + (half + 3))
                        nc.gpsimd.tensor_tensor(q_scaled[:, columns].rearrange("p (h d) -> p h d", d=G_HD), q[:, columns].rearrange("p (h d) -> p h d", d=G_HD),
                                                q_inv[:, heads, None].to_broadcast([P, HALF, G_HD]), ALU.mult).then_inc(q_scaled_ready, 1)
                if isinstance(t, int) and t == -1:
                    pool.wait_ge(w_o_highs, 1)
                    nc.gpsimd.tensor_tensor(w_o_low[:], raw[:].rearrange("p (h e) -> p h e", e=E), w_o_high[:].bitcast(F32), ALU.subtract).then_inc(w_o_split, 1)

            pipeline(pool, turn)

        @block.scalar
        def _(act):
            act.preload_act_table_set(EXP_LN)
            ln.on_scalar(act)
            act.wait_ge(loaded, LOADS)
            act.wait_ge(consts_set, 1)

            def square(n, g):
                act.wait_ge(q_ready, 4 * n + (g + 1))
                nc.scalar.activation(squares[:, g * G_CHUNK:(g + 1) * G_CHUNK], q[:, g * G_CHUNK:(g + 1) * G_CHUNK], ACT.Square).then_inc(squares_ready, 1)

            def query_rms(n, half):
                heads = slice(HALF * half, HALF * (half + 1))
                act.wait_ge(q_sums, 2 * n + (half + 1))
                nc.scalar.activation(q_log[:, heads], q_sum[:, heads], ACT.Ln, bias=rms_eps[:], scale=1.0 / G_HD).then_inc(q_logs, 1)
                act.wait_ge(q_logs, 2 * n + (half + 1))
                nc.scalar.activation(q_inv[:, heads], q_log[:, heads], ACT.Exp, scale=-0.5).then_inc(q_invs, 1)

            def take_mixed(n, j):
                act.wait_ge(mixed_psum, 4 * n + (j + 1))
                nc.scalar.copy(mixedT_high[:, 4 * j:4 * j + 4].rearrange("p h (b t) -> p b h t", b=2),
                               ps[:, 4 + j % 2, :].rearrange("p (b h t) -> p b h t", b=2, h=G_GROUP)).then_inc(mixed_highs, 1)

            def turn(t, valid):
                if valid(t):
                    act.wait_ge(scored, t + 1)
                    nc.scalar.copy(scoresT[:].rearrange("p (b c) -> p b c", b=2), ps[:, 4:6, :]).then_inc(scoresT_ready, 1)
                if valid(t + 1):
                    square(t + 1, 0)
                    square(t + 1, 1)
                if valid(t - 1):
                    take_mixed(t - 1, 0)
                    take_mixed(t - 1, 1)
                if valid(t):
                    act.wait_ge(shifted, t + 1)
                    nc.scalar.activation(probs[:], probs[:], ACT.Exp).then_inc(exp_done, 1)
                if valid(t + 1):
                    square(t + 1, 2)
                    square(t + 1, 3)
                if valid(t + 1):
                    query_rms(t + 1, 0)
                if valid(t - 1):
                    take_mixed(t - 1, 2)
                    take_mixed(t - 1, 3)
                if valid(t + 1):
                    act.wait_ge(k_psum, t + 2)
                    for j in range(G_KV):
                        done = nc.scalar.activation(k_raw[:, j * P:(j + 1) * P], ps[:, 2, j * P:(j + 1) * P], ACT.Identity, bias=bias_k[:, j:j + 1])
                    done.then_inc(k_ready, 1)
                    query_rms(t + 1, 1)
                    act.wait_ge(k_sums, t + 2)
                    nc.scalar.activation(k_log[:], ps[:, 2, :], ACT.Ln, bias=rms_eps[:], scale=1.0 / G_HD).then_inc(k_logs, 1)
                    act.wait_ge(k_logs, t + 2)
                    nc.scalar.activation(k_inv[:], k_log[:], ACT.Exp, scale=-0.5).then_inc(k_invs, 1)
                if valid(t):
                    act.wait_ge(probsT_psum, t + 1)
                    nc.scalar.copy(probsT[:].rearrange("p (b c) -> p b c", b=2), ps[:, 4:6, :]).then_inc(probsT_ready, 1)

                def take_queries(g):
                    act.wait_ge(qT_psum, 4 * t + (g + 5))
                    nc.scalar.copy(qT[:, 4 * g:4 * g + 4].rearrange("p h t -> p (h t)"), ps[:, g % 2, :]).then_inc(qT_ready, 1)

                if valid(t + 1):
                    take_queries(0)
                    take_queries(1)
                if valid(t + 2):
                    act.wait_ge(xT_psum, t + 3)
                    nc.scalar.copy(xT_high[:], ps[:, 2, 0:E]).then_inc(xT_highs, 1)
                if valid(t + 1):
                    take_queries(2)
                    take_queries(3)

            pipeline(act, turn)

        @block.vector
        def _(dve):
            ln.on_vector(dve)
            nc.vector.memset(ones[:], 1.0)
            nc.vector.memset(rms_eps[:], RMS_EPS).then_inc(consts_set, 1)
            dve.wait_ge(w_q_loaded, 16 * G_KV)
            for c in range(KC):
                weights = raw[:, c * Q_COLS:(c + 1) * Q_COLS]
                nc.vector.tensor_copy(w_q_high[:, c], weights).then_inc(w_q_highs, 1)
                dve.wait_ge(w_q_highs, c + 1)
                nc.vector.tensor_tensor(w_q_low[:, c], weights, w_q_high[:, c].bitcast(F32), ALU.subtract).then_inc(w_q_split, 1)
            dve.wait_ge(loaded, LOADS)
            nc.vector.scalar_tensor_tensor(gain[:], gain_q[:], float(np.float32(1.0) / np.sqrt(np.float32(G_HD))), gain_k[:],
                                           ALU.mult, ALU.mult).then_inc(consts_set, 1)
            dve.wait_ge(consts_set, 2)
            dve.wait_ge(zeroed, 1)
            dve.wait_ge(ln.ready, 1)
            dve.sem_inc(x_ready, 1)
            across = lambda a: a[:, :, None].to_broadcast([P, G_HEADS, SEQ])

            def biased(n, g):
                dve.wait_ge(q_psum, 4 * n + (g + 1))
                nc.vector.tensor_tensor(q[:, g * G_CHUNK:(g + 1) * G_CHUNK], ps[:, g % 2, :], bias_q[:, g * G_CHUNK:(g + 1) * G_CHUNK],
                                        ALU.add).then_inc(q_ready, 1)

            def query_sums(n, half):
                columns = slice(HALF * G_HD * half, HALF * G_HD * (half + 1))
                dve.wait_ge(squares_ready, 4 * n + (2 * half + 2))
                nc.vector.tensor_reduce(q_sum[:, HALF * half:HALF * (half + 1)], squares[:, columns].rearrange("p (h d) -> p h d", d=G_HD),
                                        AX.X, ALU.add).then_inc(q_sums, 1)

            def mixed_low(n, j):
                dve.wait_ge(mixed_highs, 4 * n + (j + 1))
                halves = [half[:, G_GROUP * j:G_GROUP * (j + 1)].rearrange("p h (b t) -> p b h t", b=2) for half in (mixedT_high, mixedT_low)]
                nc.vector.tensor_tensor(halves[1], ps[:, 4 + j % 2, :].rearrange("p (b h t) -> p b h t", b=2, h=G_GROUP),
                                        halves[0].bitcast(F32), ALU.subtract).then_inc(mixed_lows, 1)

            def turn(t, valid):
                if valid(t + 1):
                    biased(t + 1, 0)
                    biased(t + 1, 1)
                if valid(t + 2):
                    ln.normalise(xn[:], t + 2).then_inc(xn_ready, 1)
                if valid(t):
                    dve.wait_ge(turned, t + 1)
                    nc.vector.tensor_tensor(probs[:], ps[:, 6:8, :].rearrange("p k (h s) -> p (k h) s", s=SEQ),
                                            mask[:, None, :].to_broadcast([P, G_HEADS, SEQ]), ALU.add).then_inc(masked, 1)
                    dve.wait_ge(masked, t + 1)
                    nc.vector.tensor_reduce(top[:], probs[:], AX.X, ALU.max).then_inc(top_ready, 1)
                    dve.wait_ge(top_ready, t + 1)
                    nc.vector.tensor_tensor(probs[:], probs[:], across(top), ALU.subtract).then_inc(shifted, 1)
                if valid(t - 1):
                    mixed_low(t - 1, 0)
                    mixed_low(t - 1, 1)
                if valid(t + 1):
                    biased(t + 1, 2)
                    biased(t + 1, 3)
                    query_sums(t + 1, 0)
                if isinstance(t, int) and t == -1:
                    dve.wait_ge(w_o_loaded, 16)
                    nc.vector.tensor_copy(w_o_high[:], raw[:].rearrange("p (h e) -> p h e", e=E)).then_inc(w_o_highs, 1)
                if valid(t - 1):
                    mixed_low(t - 1, 2)
                    mixed_low(t - 1, 3)
                if valid(t):
                    dve.wait_ge(exp_done, t + 1)
                    nc.vector.tensor_reduce(total[:], probs[:], AX.X, ALU.add).then_inc(totals, 1)
                    dve.wait_ge(totals, t + 1)
                    nc.vector.reciprocal(inv[:], total[:]).then_inc(inv_ready, 1)
                    dve.wait_ge(inv_ready, t + 1)
                    nc.vector.tensor_tensor(probs[:], probs[:], across(inv), ALU.mult).then_inc(probs_ready, 1)
                if valid(t + 1):
                    query_sums(t + 1, 1)
                if valid(t - 1):
                    dve.wait_ge(out_psum, t)
                    nc.vector.tensor_tensor(core.x[:, t - 1, :], core.x[:, t - 1, :], ps[:, 6, 0:E], ALU.add).then_inc(x_ready, 1)
                if valid(t + 1):
                    dve.wait_ge(k_invs, t + 2)
                    nc.vector.scalar_tensor_tensor(kT[:], k_raw[:], gain[:], k_inv[:], ALU.mult, ALU.mult).then_inc(kT_ready, 1)
                if valid(t - 1):
                    dve.wait_ge(x_ready, t + 1)
                    nc.vector.bn_stats(core.row_stats[:, t - 1, :], core.x[:, t - 1, :]).then_inc(stats_done, 1)
                if valid(t + 2):
                    dve.wait_ge(xT_highs, t + 3)
                    nc.vector.tensor_tensor(xT_low[:], ps[:, 2, 0:E], xT_high[:].bitcast(F32), ALU.subtract).then_inc(xT_ready, 1)
                if valid(t):
                    dve.wait_ge(v_psum, t + 1)
                    for b in range(2):
                        half = slice(SEQ * b, SEQ * b + SEQ)
                        done = nc.vector.tensor_tensor(values[half, b, :], ps[half, 3, :], bias_v[half], ALU.add)
                    done.then_inc(v_ready, 1)

            pipeline(dve, turn)
            dve.wait_ge(stats_done, TILES)

        @block.tensor
        def _(pe):
            pe.wait_ge(loaded, LOADS)
            pe.wait_ge(consts_set, 2)
            pe.wait_ge(w_q_split, KC)

            def query(n, g):
                if g >= 2:
                    pe.wait_ge(q_ready, 4 * n + (g - 1))
                for c in range(KC):
                    rows, columns = slice(c * P, (c + 1) * P), slice(g * G_CHUNK, (g + 1) * G_CHUNK)
                    done = three_passes(nc, ps[:, g % 2, :], (xT_high[:, rows], xT_low[:, rows]), (w_q_high[:, c, columns], w_q_low[:, c, columns]),
                                        start=(c == 0), stop=(c == KC - 1))
                done.then_inc(q_psum, 1)

            def mix(n, j):
                if j >= 2:
                    pe.wait_ge(mixed_lows, 4 * n + (j - 1))
                for b in range(2):
                    done = nc.tensor.matmul(ps[:, 4 + j % 2, b * E:(b + 1) * E], values[:, b, j * G_HD:(j + 1) * G_HD],
                                            probsT[:, j * E:(j + 1) * E], start=True, stop=True)
                done.then_inc(mixed_psum, 1)

            def turn(t, valid):
                if valid(t):
                    pe.wait_ge(kT_ready, t + 1)
                    if started(t, 1):
                        pe.wait_ge(probsT_ready, t)
                    for j in range(G_KV):
                        pe.wait_ge(qT_ready, 4 * t + (j + 1))
                        for b in range(2):
                            half = slice(SEQ * b, SEQ * b + SEQ)
                            done = nc.tensor.matmul(ps[half, 4 + j // 2, (j % 2) * E:(j % 2 + 1) * E], kT[:, j * P + SEQ * b:j * P + SEQ * b + SEQ],
                                                    qT[:, 4 * j:4 * j + 4, SEQ * b:SEQ * b + SEQ], start=True, stop=True)
                    done.then_inc(scored, 1)
                if valid(t + 1):
                    pe.wait_ge(xT_ready, t + 2)
                    query(t + 1, 0)
                    query(t + 1, 1)
                if valid(t):
                    pe.wait_ge(scoresT_ready, t + 1)
                    if started(t, 1):
                        pe.wait_ge(x_ready, t)
                    for j in range(G_HEADS // 2):
                        done = nc.tensor.transpose(ps[:, 6 + j // 4, (j % 4) * P:(j % 4 + 1) * P], scoresT[:, j * P:(j + 1) * P], ident[:])
                    done.then_inc(turned, 1)
                if valid(t + 1):
                    query(t + 1, 2)
                    query(t + 1, 3)
                if valid(t - 1):
                    pe.wait_ge(v_ready, t)
                    pe.wait_ge(probsT_ready, t)
                    if valid(t):
                        pe.wait_ge(scoresT_ready, t + 1)
                        pe.wait_ge(masked, t + 1)
                    mix(t - 1, 0)
                    mix(t - 1, 1)
                if valid(t + 1):
                    pe.wait_ge(ctx_k_ready, 16 * t + 32)
                    for j in range(G_KV):
                        for c in range(KC):
                            done = nc.tensor.matmul(ps[:, 2, j * P:(j + 1) * P], w_k[:, c, j * P:(j + 1) * P], ctxT_k[:, c],
                                                    start=(c == 0), stop=(c == KC - 1))
                    done.then_inc(k_psum, 1)
                if valid(t - 1):
                    mix(t - 1, 2)
                    mix(t - 1, 3)
                if valid(t - 1):
                    if isinstance(t, int) and t == 1 or not isinstance(t, int):
                        pe.wait_ge(w_o_split, 1)
                    for j in range(G_KV):
                        pe.wait_ge(mixed_highs, 4 * t + (j - 3))
                        for h in range(4 * j, 4 * j + 4):
                            for weight in (w_o_high, w_o_low):
                                nc.tensor.matmul(ps[:, 6, 0:E], mixedT_high[:, h], weight[:, h], start=(h == 0 and weight is w_o_high), stop=False)
                    for j in range(G_KV):
                        pe.wait_ge(mixed_lows, 4 * t + (j - 3))
                        for h in range(4 * j, 4 * j + 4):
                            done = nc.tensor.matmul(ps[:, 6, 0:E], mixedT_low[:, h], w_o_high[:, h], start=False, stop=(h == G_HEADS - 1))
                    done.then_inc(out_psum, 1)
                if valid(t + 1):
                    pe.wait_ge(k_squared, t + 2)
                    nc.tensor.matmul(ps[:, 2, :], ones[:], k_squares[:], start=True, stop=True).then_inc(k_sums, 1)
                if valid(t):
                    pe.wait_ge(probs_ready, t + 1)
                    if started(t, 1):
                        pe.wait_ge(mixed_lows, 4 * t)
                    for j in range(G_HEADS // 2):
                        done = nc.tensor.transpose(ps[:, 4 + j // 4, (j % 4) * P:(j % 4 + 1) * P],
                                                   probs[:, 2 * j:2 * j + 2].rearrange("p b s -> p (b s)"), ident[:])
                    done.then_inc(probsT_psum, 1)

                def turn_queries(g):
                    if g >= 2:
                        pe.wait_ge(qT_ready, 4 * t + (g + 3))
                    else:
                        pe.wait_ge(q_ready, 4 * t + (g + 7))
                    pe.wait_ge(q_scaled_ready, 2 * t + (g // 2 + 3))
                    for h in range(4 * g, 4 * g + 4):
                        done = nc.tensor.transpose(ps[:, g % 2, (h % 4) * P:(h % 4 + 1) * P], q_scaled[:, h * G_HD:(h + 1) * G_HD], ident[:])
                    done.then_inc(qT_psum, 1)

                if valid(t + 1):
                    turn_queries(0)
                    turn_queries(1)
                if valid(t + 2):
                    pe.wait_ge(xn_ready, t + 3)
                    if valid(t + 1):
                        pe.wait_ge(k_logs, t + 2)
                    for c in range(KC):
                        done = nc.tensor.transpose(ps[:, 2, c * P:(c + 1) * P], xn[:, c * P:(c + 1) * P], ident[:])
                    done.then_inc(xT_psum, 1)
                if valid(t):
                    pe.wait_ge(ctx_v_ready, 16 * t + 16)
                    if started(t, 1):
                        pe.wait_ge(v_ready, t)
                    for c in range(KC):
                        done = nc.tensor.matmul(ps[:, 3, :], ctxT_v[:, c], w_v[:, c], start=(c == 0), stop=(c == KC - 1))
                    done.then_inc(v_psum, 1)
                if valid(t + 1):
                    turn_queries(2)
                    turn_queries(3)

            pipeline(pe, turn)

M_EXPERTS, M_FF = 8, 256
M_RANK, M_LORA = 64, 2
FT = M_FF // P
ZONE_CENTER, ZONE_LOW, ZONE_HIGH = 1.0 / math.e, 0.5 - math.log(4.0 / 3.0), 0.5
ZONE_WIDTH, FALLBACK_WIDTH, TINY = 0.1, 0.3, 1e-8


def mixture(core):
    nc, dram, ps, ident = core.nc, core.dram, core.psum, core.ident
    with ExitStack() as scope:
        sb = lambda name, shape, dt=F32: scope.enter_context(nc.sbuf_tensor(f"mo_{name}", shape, dt))
        sem = lambda name: core.sem(f"mo_{name}")
        ln = RowNorm(core, "mo", scope)
        weights = [sb(name, [P, M_EXPERTS, KC, M_FF]) for name in ("w_gate", "w_up", "w_down")]
        w_gate, w_up, w_down = weights
        lora_a = sb("lora_a", [M_RANK, 3, M_LORA, E])
        lora_b = sb("lora_b", [M_RANK, 3, M_LORA, M_FF])
        w_route = sb("w_route", [P, KC, M_EXPERTS])
        temperature, first = sb("temperature", [P, 1]), sb("first", [P, M_EXPERTS])
        xn, xT_now, xT = sb("xn", [P, 2, E]), sb("xT_now", [P, 2, E]), sb("xT", [P, KC, TILES * P])
        logits, gate, dist, zone, near, rank, hot1, hot2 = (
            sb(name, [P, TILES, M_EXPERTS]) for name in ("logits", "gate", "dist", "zone", "near", "rank", "hot1", "hot2"))
        total, nobody, best = (sb(name, [P, TILES]) for name in ("total", "nobody", "best"))
        silu, mid = sb("silu", [P, 4, 2 * P]), sb("mid", [P, 2, FT, 2 * P])

        loaded, folded_psum, folded, xn_ready, xT_psum, xT_ready, xT_kept, routed, logits_ready, route_step, inverted = (
            sem(n) for n in ("loaded", "folded_psum", "folded", "xn_ready", "xT_psum", "xT_ready", "xT_kept", "routed", "logits_ready", "route_step", "inverted"))
        gate_arg, gate_exp, dists, near_exp, zone_exp, mix_ready = (
            sem(n) for n in ("gate_arg", "gate_exp", "dists", "near_exp", "zone_exp", "mix_ready"))
        wide_psum, silu_ready, mid_ready, down_psum, added, stored = (
            sem(n) for n in ("wide_psum", "silu_ready", "mid_ready", "down_psum", "added", "stored"))
        LOADS = 8 * 16
        MIDS = M_EXPERTS * FT
        ADDS = 2 * M_EXPERTS
        ADD_CREDIT = 4
        FOLDS = 3 * M_LORA

        block = scope.enter_context(nc.Block())

        @block.sync
        def _(sp):
            for out, src in ((w_route[:], chunked(dram["mo_w_route"])), (temperature[:], dram["mo_temperature"].to_broadcast([P, 1])),
                             (first[:], dram["ff_first"]), (lora_a[:], dram["mo_lora_a"]), (lora_b[:], dram["mo_lora_b"]),
                             (w_gate[:].rearrange("p e c f -> p (e c) f"), dram["mo_w_gate"].rearrange("e (c p) f -> p (e c) f", p=P)),
                             (w_up[:].rearrange("p e c f -> p (e c) f"), dram["mo_w_up"].rearrange("e (c p) f -> p (e c) f", p=P)),
                             (w_down[:].rearrange("p e c f -> p (e c) f"), dram["mo_w_down"].rearrange("e (c p) f -> p (e c) f", p=P))):
                sp.dma_start(out, src).then_inc(loaded, 16)
            sp.wait_ge(loaded, LOADS)
            rows = dram["out"].rearrange("(t p) e -> p t e", p=P)
            with sp.Fori(0, PAIRS) as i:
                sp.wait_ge(added, ADDS * i + (ADDS + ADD_CREDIT))
                sp.dma_start(rows[:, bass.ts(i, 2), :], core.x[:, bass.ts(i, 2), :]).then_inc(stored, 16)
            sp.wait_ge(stored, 16 * PAIRS)

        @block.gpsimd
        def _(pool):
            with pool.Fori(0, PAIRS) as i:
                for u in range(2):
                    t = 2 * i + u
                    pool.wait_ge(xT_ready, t + 1)
                    nc.gpsimd.tensor_copy(xT[:, :, bass.ts(t, P)], xT_now[:, u].rearrange("p (c t) -> p c t", c=KC)).then_inc(xT_kept, 1)

        @block.scalar
        def _(act):
            act.preload_act_table_set(EXP_LN)
            ln.on_scalar(act)
            act.sem_inc(xT_kept, 2)
            with act.Fori(0, PAIRS) as i:
                for u in range(2):
                    t = 2 * i + u
                    act.wait_ge(xT_kept, t + 1)
                    act.wait_ge(xT_psum, t + 1)
                    nc.scalar.copy(xT_now[:, u], ps[:, u, 0:E]).then_inc(xT_ready, 1)
                for u in range(2):
                    t = 2 * i + u
                    act.wait_ge(routed, t + 1)
                    nc.scalar.copy(logits[:, t, :], ps[:, 2 + u, 0:M_EXPERTS]).then_inc(logits_ready, 1)
            act.wait_ge(gate_arg, 1)
            nc.scalar.activation(gate[:], logits[:], ACT.Exp).then_inc(gate_exp, 1)
            act.wait_ge(dists, 1)
            nc.scalar.activation(near[:], dist[:], ACT.Exp, scale=-1.0 / FALLBACK_WIDTH).then_inc(near_exp, 1)
            nc.scalar.activation(dist[:], dist[:], ACT.Exp, scale=-1.0 / ZONE_WIDTH).then_inc(zone_exp, 1)
            act.preload_act_table_set("silu_and_others")
            with act.Fori(0, PAIRS) as i:
                for j in range(MIDS):
                    act.wait_ge(wide_psum, MIDS * i + (j + 1))
                    nc.scalar.activation(silu[:, j % 4], ps[:, j % 4, 0:2 * P], ACT.Silu).then_inc(silu_ready, 1)

        @block.vector
        def _(dve):
            ln.on_vector(dve)
            dve.wait_ge(ln.ready, 1)
            dve.wait_ge(loaded, LOADS)
            nc.vector.reciprocal(temperature[:], temperature[:]).then_inc(inverted, 1)
            dve.wait_ge(inverted, 1)
            with dve.Fori(0, PAIRS) as i:
                for u in range(2):
                    t = 2 * i + u
                    ln.normalise(xn[:, u], t).then_inc(xn_ready, 1)
                for u in range(2):
                    dve.wait_ge(xT_ready, 2 * i + (u + 1))
            for k in range(3):
                for e in range(M_LORA):
                    j = M_LORA * k + e
                    dve.wait_ge(folded_psum, j + 1)
                    nc.vector.tensor_tensor(weights[k][:, e], weights[k][:, e],
                                            ps[:, 4 + j % 4, :].rearrange("p (c f) -> p c f", c=KC), ALU.add).then_inc(folded, 1)
            across = lambda a: a[:, :, None].to_broadcast([P, TILES, M_EXPERTS])
            every = lambda a: a[:, None, :].to_broadcast([P, TILES, M_EXPERTS])
            dve.wait_ge(logits_ready, TILES)
            nc.vector.tensor_scalar(logits[:], logits[:], temperature[:], -1.0, ALU.mult, ALU.mult).then_inc(route_step, 1)
            dve.wait_ge(route_step, 1)
            nc.vector.tensor_scalar(logits[:], logits[:], EXP_LIMIT, None, ALU.min).then_inc(gate_arg, 1)
            dve.wait_ge(gate_exp, 1)
            nc.vector.tensor_scalar(gate[:], gate[:], 1.0, None, ALU.add).then_inc(route_step, 1)
            dve.wait_ge(route_step, 2)
            nc.vector.reciprocal(gate[:], gate[:]).then_inc(route_step, 1)
            dve.wait_ge(route_step, 3)
            nc.vector.tensor_scalar(dist[:], gate[:], ZONE_CENTER, None, ALU.subtract).then_inc(route_step, 1)
            dve.wait_ge(route_step, 4)
            nc.vector.scalar_tensor_tensor(dist[:], dist[:], -1.0, dist[:], ALU.mult, ALU.max).then_inc(dists, 1)
            nc.vector.tensor_scalar(zone[:], gate[:], ZONE_LOW, None, ALU.is_ge).then_inc(route_step, 1)
            dve.wait_ge(route_step, 5)
            nc.vector.scalar_tensor_tensor(zone[:], gate[:], ZONE_HIGH, zone[:], ALU.is_le, ALU.mult).then_inc(route_step, 1)
            dve.wait_ge(route_step, 6)
            dve.wait_ge(zone_exp, 1)
            nc.vector.tensor_tensor(zone[:], zone[:], dist[:], ALU.mult).then_inc(route_step, 1)
            dve.wait_ge(route_step, 7)
            nc.vector.tensor_reduce(total[:], zone[:], AX.X, ALU.add).then_inc(route_step, 1)
            dve.wait_ge(route_step, 8)
            nc.vector.tensor_scalar(nobody[:], total[:], TINY, None, ALU.is_lt).then_inc(route_step, 1)
            dve.wait_ge(route_step, 9)
            nc.vector.tensor_reduce(best[:], near[:], AX.X, ALU.max).then_inc(route_step, 1)
            dve.wait_ge(route_step, 10)
            nc.vector.tensor_tensor(rank[:], near[:], across(best), ALU.is_ge).then_inc(route_step, 1)
            dve.wait_ge(route_step, 11)
            nc.vector.tensor_tensor(rank[:], rank[:], every(first), ALU.mult).then_inc(route_step, 1)
            dve.wait_ge(route_step, 12)
            nc.vector.tensor_reduce(best[:], rank[:], AX.X, ALU.max).then_inc(route_step, 1)
            dve.wait_ge(route_step, 13)
            nc.vector.tensor_tensor(hot1[:], rank[:], across(best), ALU.is_equal).then_inc(route_step, 1)
            dve.wait_ge(route_step, 14)
            nc.vector.scalar_tensor_tensor(gate[:], hot1[:], -2.0, near[:], ALU.mult, ALU.add).then_inc(route_step, 1)
            dve.wait_ge(route_step, 15)
            nc.vector.tensor_reduce(best[:], gate[:], AX.X, ALU.max).then_inc(route_step, 1)
            dve.wait_ge(route_step, 16)
            nc.vector.tensor_tensor(rank[:], gate[:], across(best), ALU.is_ge).then_inc(route_step, 1)
            dve.wait_ge(route_step, 17)
            nc.vector.tensor_tensor(rank[:], rank[:], every(first), ALU.mult).then_inc(route_step, 1)
            dve.wait_ge(route_step, 18)
            nc.vector.tensor_reduce(best[:], rank[:], AX.X, ALU.max).then_inc(route_step, 1)
            dve.wait_ge(route_step, 19)
            nc.vector.tensor_tensor(hot2[:], rank[:], across(best), ALU.is_equal).then_inc(route_step, 1)
            dve.wait_ge(route_step, 20)
            nc.vector.tensor_tensor(hot1[:], hot1[:], hot2[:], ALU.add).then_inc(route_step, 1)
            dve.wait_ge(route_step, 21)
            nc.vector.tensor_tensor(near[:], near[:], hot1[:], ALU.mult).then_inc(route_step, 1)
            dve.wait_ge(route_step, 22)
            nc.vector.tensor_reduce(best[:], near[:], AX.X, ALU.add).then_inc(route_step, 1)
            dve.wait_ge(route_step, 23)
            nc.vector.tensor_scalar(best[:], best[:], TINY, None, ALU.max).then_inc(route_step, 1)
            dve.wait_ge(route_step, 24)
            nc.vector.reciprocal(best[:], best[:]).then_inc(route_step, 1)
            dve.wait_ge(route_step, 25)
            nc.vector.tensor_tensor(best[:], best[:], nobody[:], ALU.mult).then_inc(route_step, 1)
            dve.wait_ge(route_step, 26)
            nc.vector.tensor_tensor(near[:], near[:], across(best), ALU.mult).then_inc(route_step, 1)
            dve.wait_ge(route_step, 27)
            nc.vector.tensor_scalar(nobody[:], nobody[:], -1.0, 1.0, ALU.mult, ALU.add).then_inc(route_step, 1)
            dve.wait_ge(route_step, 28)
            nc.vector.tensor_tensor(zone[:], zone[:], across(nobody), ALU.mult).then_inc(route_step, 1)
            dve.wait_ge(route_step, 29)
            nc.vector.tensor_tensor(zone[:], zone[:], near[:], ALU.add).then_inc(route_step, 1)
            dve.wait_ge(route_step, 30)
            nc.vector.tensor_reduce(total[:], zone[:], AX.X, ALU.add).then_inc(route_step, 1)
            dve.wait_ge(route_step, 31)
            nc.vector.tensor_scalar(total[:], total[:], TINY, None, ALU.max).then_inc(route_step, 1)
            dve.wait_ge(route_step, 32)
            nc.vector.reciprocal(total[:], total[:]).then_inc(route_step, 1)
            dve.wait_ge(route_step, 33)
            nc.vector.tensor_tensor(zone[:], zone[:], across(total), ALU.mult).then_inc(mix_ready, 1)
            dve.wait_ge(mix_ready, 1)

            dve.sem_inc(added, ADD_CREDIT)
            with dve.Fori(0, PAIRS) as i:
                def middles(e):
                    for f in range(FT):
                        j = FT * e + f
                        dve.wait_ge(silu_ready, MIDS * i + (j + 1))
                        nc.vector.tensor_tensor(mid[:, e % 2, f], silu[:, j % 4], ps[:, j % 4, 2 * P:4 * P], ALU.mult).then_inc(mid_ready, 1)

                def add(e):
                    dve.wait_ge(down_psum, M_EXPERTS * i + (e + 1))
                    for u in range(2):
                        t = 2 * i + u
                        dve.wait_ge(added, ADDS * i + (2 * e + u + ADD_CREDIT - 1))
                        nc.vector.scalar_tensor_tensor(core.x[:, t, :], ps[:, 4 + e % 2, u * E:(u + 1) * E], zone[:, t, e:e + 1],
                                                       core.x[:, t, :], ALU.mult, ALU.add).then_inc(added, 1)

                for e in range(M_EXPERTS):
                    middles(e)
                    if e:
                        add(e - 1)
                add(M_EXPERTS - 1)

        @block.tensor
        def _(pe):
            pe.wait_ge(loaded, LOADS)
            with pe.Fori(0, PAIRS) as i:
                for u in range(2):
                    t = 2 * i + u
                    pe.wait_ge(xn_ready, t + 1)
                    for c in range(KC):
                        done = nc.tensor.transpose(ps[:, u, c * P:(c + 1) * P], xn[:, u, c * P:(c + 1) * P], ident[:])
                    done.then_inc(xT_psum, 1)
                for u in range(2):
                    t = 2 * i + u
                    pe.wait_ge(xT_ready, t + 1)
                    for c in range(KC):
                        done = nc.tensor.matmul(ps[:, 2 + u, 0:M_EXPERTS], xT_now[:, u, c * P:(c + 1) * P], w_route[:, c],
                                                start=(c == 0), stop=(c == KC - 1))
                    done.then_inc(routed, 1)
            for k in range(3):
                for e in range(M_LORA):
                    j = M_LORA * k + e
                    if j >= 4:
                        pe.wait_ge(folded, j - 3)
                    for c in range(KC):
                        done = nc.tensor.matmul(ps[:, 4 + j % 4, c * M_FF:(c + 1) * M_FF], lora_a[:, k, e, c * P:(c + 1) * P], lora_b[:, k, e],
                                                start=True, stop=True)
                    done.then_inc(folded_psum, 1)
            pe.wait_ge(folded, FOLDS)
            pe.wait_ge(xT_kept, TILES + 2)
            pe.wait_ge(logits_ready, TILES)
            pe.sem_inc(mid_ready, 4)
            with pe.Fori(0, PAIRS) as i:
                def widen(e):
                    for f in range(FT):
                        j = FT * e + f
                        pe.wait_ge(mid_ready, MIDS * i + (j + 1))
                        for k in range(2):
                            for c in range(KC):
                                done = nc.tensor.matmul(ps[:, j % 4, 2 * P * k:2 * P * (k + 1)], weights[k][:, e, c, f * P:(f + 1) * P],
                                                        xT[:, c, bass.ts(i, 2 * P)], start=(c == 0), stop=(c == KC - 1))
                        done.then_inc(wide_psum, 1)

                def narrow(e):
                    pe.wait_ge(mid_ready, MIDS * i + (FT * e + FT + 4))
                    pe.wait_ge(added, ADDS * i + (2 * e + ADD_CREDIT - 2))
                    for u in range(2):
                        for f in range(FT):
                            done = nc.tensor.matmul(ps[:, 4 + e % 2, u * E:(u + 1) * E], mid[:, e % 2, f, u * P:(u + 1) * P], w_down[:, e, f],
                                                    start=(f == 0), stop=(f == FT - 1))
                    done.then_inc(down_psum, 1)

                for e in range(M_EXPERTS):
                    widen(e)
                    if e:
                        narrow(e - 1)
                narrow(M_EXPERTS - 1)
SUBLAYERS = (differential_attention, feature_attention, selected_update, state_space, grouped_attention, mixture)

def decoder(nc, dram):
    with ExitStack() as ctx:
        for name in ("q_parts", "k_parts"):
            dram[name] = nc.dram_tensor(name, (STACK, BATCH * C_HEADS, E), BF16, kind="Internal").ap()
        core = Core(nc, ctx, dram)
        load_inputs(core)
        core.end_sublayer()
        for sublayer in SUBLAYERS:
            sublayer(core)
            core.end_sublayer()

def rotary_tables():
    inv_freq = 1.0 / 10000.0 ** (np.arange(0, D_HD, 2, dtype=np.float32) / np.float32(D_HD))
    angle = np.arange(SEQ, dtype=np.float32)[None, :] * inv_freq.astype(np.float32)[:, None]
    cos = np.tile(np.cos(angle), (P // (D_HD // 2), 2))
    sin = np.tile(np.concatenate([np.sin(angle), -np.sin(angle)]), (P // D_HD, 2))
    scale = np.float32(D_HD ** -0.5)
    return np.stack([np.concatenate([t * scale, t * scale, t], axis=1) for t in (cos, sin)], axis=1).astype(np.float32)


def swapped(w):
    rows = w.shape[0]
    return w.reshape(rows, -1, 2, D_HD // 2)[:, :, ::-1].reshape(rows, -1)


def layout(inputs):
    a = {k: np.asarray(v) for k, v in inputs.items()}
    f32 = np.float32
    halves = a["L0_attn_Wq"].reshape(E, D_HEADS, 2, D_HD)
    q0, q1 = halves[:, :, 0].reshape(E, P), halves[:, :, 1].reshape(E, P)
    k = a["L0_attn_Wk"]
    rows = np.arange(P)
    tri = np.where(np.arange(SEQ)[None, :] <= np.arange(SEQ)[:, None], 0.0, MASKED).astype(f32)
    out = {
        "x": a["x"].reshape(BATCH * SEQ, E),
        "ctx": a["ctx_2048"].reshape(BATCH * SEQ, E),
        "ident": np.eye(P, dtype=f32),
        "ident_bf": np.eye(P, dtype=f32),
        "da_w_qk": np.concatenate([q0, q1, k, swapped(q0), swapped(q1), swapped(k)], axis=1),
        "da_w_v": a["L0_attn_Wv"],
        "da_w_o": a["L0_attn_Wo"],
        "da_gain": np.tile(a["L0_attn_g"], P // D_DV)[:, None],
        "rotary": rotary_tables(),
        "da_head_mask": (rows[:, None] // D_HD == np.arange(D_HEADS)[None, :]).astype(f32),
        "causal": np.tile(tri, (2, 8)),
        "da_lam": np.broadcast_to(np.stack([a["L0_attn_lam_" + v] for v in ("q1", "q2", "k1", "k2")])[None], (P, 4, D_HD)),
    }
    w_out = np.zeros((2, SEQ, 2, SEQ), f32)
    for b in range(2):
        w_out[b, :, b] = a["L0_xattn_W"].T
    out["fa_w_out"] = w_out.reshape(P, P)
    out["fa_padding"] = np.repeat(np.arange(STACK_ROWS - PARTS * STACK) >= MAX_ROW - PARTS * STACK, 2 * C_HEADS * E).reshape(-1, 2 * C_HEADS * E).astype(f32)
    spread = lambda v: np.broadcast_to(v[None], (P, v.shape[0]))
    out["ff_w_in"] = np.concatenate([a["L0_ffn_select_weight"].transpose(1, 0, 2).reshape(E, F_SEL), a["L0_ffn_select_mean_diff"].T,
                                     a["L0_ffn_lora_update"].transpose(1, 0, 2).reshape(E, F_UPD)], axis=1)
    out["ff_debias"] = a["L0_ffn_debias_w"].T
    out["ff_w_back"] = np.concatenate([a["L0_ffn_lora_degen"].transpose(0, 2, 1).reshape(F_UPD, E), a["L0_ffn_bias_w"],
                                       np.zeros((F_ROWS - F_UPD - F_N, E), f32)], axis=0)
    out["ff_center"], out["ff_slope"] = spread(a["L0_ffn_imp_center"]), spread(a["L0_ffn_imp_slope"])
    out["ff_first"] = spread(np.arange(F_N, 0, -1).astype(f32))
    out["ss_w_bc"] = np.concatenate([a["L1_attn_B_w"].T, a["L1_attn_C_w"].T], axis=1)
    out["ss_bias_bc"] = np.stack([a["L1_attn_B_b"], a["L1_attn_C_b"]], axis=1)
    out["ss_w_dt"], out["ss_w_out"] = a["L1_attn_dt_w"].T, a["L1_attn_out_w"].T
    out["ss_bias_dt"], out["ss_skip"] = spread(a["L1_attn_dt_b"]), spread(a["L1_attn_D"])
    out["ss_A_log"], out["ss_bias_out"] = spread(a["L1_attn_A_log"]), spread(a["L1_attn_out_b"])
    row, col = rows[:, None], rows[None, :]
    spans, pairs = [], []
    for level in range(LEVELS):
        half = 1 << level
        pivot = col // (2 * half) * (2 * half) + half - 1
        spans.append(((col <= pivot) & (row > col) & (row <= pivot)) | ((col > pivot) & (row > pivot) & (row <= col)))
        pairs.append((row // (2 * half) == col // (2 * half)) & (row <= pivot) & (col > pivot))
    out["ss_spans"], out["ss_pairs"] = np.stack(spans, axis=1).astype(f32), np.stack(pairs, axis=1).astype(f32)
    out["ctxT"] = out["ctx"].T
    for name in ("q", "k", "v", "o"):
        out["ga_w_" + name] = a["L1_xattn_W" + name]
    out["ga_bias_q"], out["ga_bias_v"] = a["L1_xattn_bq"][None], a["L1_xattn_bv"][None]
    out["ga_bias_k"] = a["L1_xattn_bk"].reshape(G_KV, G_HD).T
    out["ga_gain_q"], out["ga_gain_k"] = a["L1_xattn_qn_w"][:, None], a["L1_xattn_kn_w"][:, None]
    out["mask"] = a["mask_1xSxS2_ff0"][0]
    out["mo_w_route"], out["mo_temperature"] = a["L1_ffn_Wr"], a["L1_ffn_temperature"][None]
    out["mo_w_gate"], out["mo_w_up"], out["mo_w_down"] = a["L1_ffn_Wg"], a["L1_ffn_Wu"], a["L1_ffn_Wd"]
    out["mo_lora_a"] = np.stack([a["L1_ffn_" + n].transpose(2, 0, 1) for n in ("Ga", "Ua", "Da")], axis=1)
    out["mo_lora_b"] = np.stack([a["L1_ffn_" + n].transpose(1, 0, 2) for n in ("Gb", "Ub", "Db")], axis=1)
    bf16 = mybir.dt.np(BF16)
    for name in ("ident_bf", "causal", "fa_padding"):
        out[name] = out[name].astype(bf16)
    return {n: np.ascontiguousarray(v) for n, v in out.items()}


def kernel(**inputs):
    import concourse.bacc as bacc
    from concourse.bass_utils import run_bass_kernel_spmd

    nc = bacc.Bacc("TRN2", target_bir_lowering=False, num_devices=1)
    arrays = layout(inputs)
    dram = {n: nc.dram_tensor(f"in_{n}", v.shape, mybir.dt.from_np(v.dtype), kind="ExternalInput").ap() for n, v in arrays.items()}
    dram["out"] = nc.dram_tensor("out", (BATCH * SEQ, E), F32, kind="ExternalOutput").ap()
    decoder(nc, dram)
    result = run_bass_kernel_spmd(nc, [{f"in_{n}": v for n, v in arrays.items()}], core_ids=[0])
    return result.results[0]["out"].reshape(BATCH, SEQ, E)
```

```python
import math
from contextlib import ExitStack

import numpy as np

import concourse.bass as bass
from concourse import mybir

F32 = mybir.dt.float32
F32R = mybir.dt.float32r
BF16 = mybir.dt.bfloat16
ALU = mybir.AluOpType
ACT = mybir.ActivationFunctionType
AX = mybir.AxisListType

P = 128
BATCH, SEQ, E = 32, 64, 256
TILES = BATCH * SEQ // P
PAIRS = TILES // 2
KC = E // P
LN_EPS = 1e-5
FLT_MAX = 3.4028235e38
MASKED = -1.0e30
EXP_LN = "natural_log_exp_and_others"


class Core:

    def __init__(self, nc, ctx, dram):
        self.nc, self.ctx, self.dram = nc, ctx, dram
        self.psum = ctx.enter_context(nc.psum_tensor("psum", [P, 8, 512], F32))
        self.x = self.sb("x", [P, TILES, E])
        self.row_stats = self.sb("row_stats", [P, TILES, 6])
        self.ident = self.sb("ident", [P, P])
        self.semaphores = []

    def sb(self, name, shape, dtype=F32):
        return self.ctx.enter_context(self.nc.sbuf_tensor(name, shape, dtype))

    def sem(self, name):
        self.semaphores.append(self.nc.alloc_semaphore(name=name))
        return self.semaphores[-1]

    def end_sublayer(self):
        self.nc.clear_and_free_semaphores(self.semaphores)
        self.nc.all_engine_barrier()
        self.semaphores = []

    def sems(self, name, count):
        return [self.sem(f"{name}{j}") for j in range(count)]


def chunked(weight):
    return weight.rearrange("(c p) o -> p c o", p=P)


class RowNorm:

    def __init__(self, core, stage, scope):
        nc = core.nc
        sb = lambda name, shape: scope.enter_context(nc.sbuf_tensor(f"{stage}_{name}", shape, F32))
        self.core = core
        self.sum2, self.half = sb("sum2", [P, TILES]), sb("half", [P, TILES])
        self.spread, self.mean = sb("spread", [P, TILES]), sb("mean", [P, TILES])
        self.var, self.log_var = sb("var", [P, TILES]), sb("log_var", [P, TILES])
        self.rstd = sb("rstd", [P, TILES])
        self.eps = sb("ln_eps", [P, 1])
        self.moments = core.sem(f"{stage}_ln_moments")
        self.var_ready = core.sem(f"{stage}_ln_var")
        self.log_ready = core.sem(f"{stage}_ln_log")
        self.ready = core.sem(f"{stage}_ln_ready")

    def on_vector(self, dve):
        nc, stats = self.core.nc, self.core.row_stats
        nc.vector.memset(self.eps[:], LN_EPS)
        nc.vector.tensor_tensor(self.sum2[:], stats[:, :, 1], stats[:, :, 4], ALU.add).then_inc(self.moments, 1)
        nc.vector.tensor_tensor(self.half[:], stats[:, :, 1], stats[:, :, 4], ALU.subtract).then_inc(self.moments, 1)
        nc.vector.tensor_tensor(self.spread[:], stats[:, :, 2], stats[:, :, 5], ALU.add).then_inc(self.moments, 1)
        dve.wait_ge(self.moments, 3)
        nc.vector.tensor_scalar(self.mean[:], self.sum2[:], 0.5, None, ALU.mult).then_inc(self.moments, 1)
        nc.vector.scalar_tensor_tensor(self.half[:], self.half[:], 0.25, self.half[:], ALU.mult, ALU.mult).then_inc(self.moments, 1)
        dve.wait_ge(self.moments, 5)
        nc.vector.scalar_tensor_tensor(self.var[:], self.spread[:], 1.0 / E, self.half[:], ALU.mult, ALU.add).then_inc(self.var_ready, 1)

    def on_scalar(self, act):
        nc = self.core.nc
        act.wait_ge(self.var_ready, 1)
        nc.scalar.activation(self.log_var[:], self.var[:], ACT.Ln, bias=self.eps[:]).then_inc(self.log_ready, 1)
        act.wait_ge(self.log_ready, 1)
        nc.scalar.activation(self.rstd[:], self.log_var[:], ACT.Exp, scale=-0.5).then_inc(self.ready, 1)

    def normalise(self, out, t):
        return self.core.nc.vector.tensor_scalar(
            out, self.core.x[:, t, :], self.mean[:, bass.ts(t, 1)], self.rstd[:, bass.ts(t, 1)],
            ALU.subtract, ALU.mult)

class FirstRows:
    PARTS = 4

    def __init__(self, core):
        self.core = core
        self.x_loaded = core.sems("x_loaded", self.PARTS)
        self.ident_loaded = core.sem("ident_loaded")
        self.stats_done = core.sem("first_stats_done")

    def groups(self):
        per = TILES // self.PARTS
        return [slice(g * per, (g + 1) * per) for g in range(self.PARTS)]

    def on_sync(self, sp):
        core = self.core
        for g, tiles in enumerate(self.groups()):
            sp.dma_start(core.x[:, tiles, :], core.dram["x"].rearrange("(t p) e -> p t e", p=P)[:, tiles, :]).then_inc(self.x_loaded[g], 16)
        sp.dma_start(core.ident[:], core.dram["ident"]).then_inc(self.ident_loaded, 16)

    def on_vector(self, dve):
        core = self.core
        for g, tiles in enumerate(self.groups()):
            dve.wait_ge(self.x_loaded[g], 16)
            for t in range(tiles.start, tiles.stop):
                core.nc.vector.bn_stats(core.row_stats[:, t, :], core.x[:, t, :]).then_inc(self.stats_done, 1)
        dve.wait_ge(self.stats_done, TILES)


D_HEADS, D_KV_HEADS, D_HD = 16, 8, 8
D_DV = 2 * D_HD
LAMBDA_INIT = 0.8 - 0.6 * math.exp(-0.3 * 12)
RMS_EPS = 1e-6


def differential_attention(core):
    nc, dram, ps, ident = core.nc, core.dram, core.psum, core.ident
    with ExitStack() as scope:
        sb = lambda name, shape, dt=F32: scope.enter_context(nc.sbuf_tensor(f"da_{name}", shape, dt))
        sem = lambda name: core.sem(f"da_{name}")
        first_rows, ln = FirstRows(core), RowNorm(core, "da", scope)
        w_qk = sb("w_qk", [P, KC, 6 * P])
        w_v = sb("w_v", [P, KC, P])
        w_o = sb("w_o", [P, KC, E])
        gain = sb("gain", [P, 1])
        rotary = sb("rotary", [P, 2, 3 * P])
        head_mask = sb("head_mask", [P, D_HEADS // 2])
        causal = sb("causal", [P, 8 * SEQ], BF16)
        ident_bf = sb("ident_bf", [P, P], BF16)
        lam_in = sb("lam_in", [P, 4, D_HD])
        lam_prod, lam_dot, lam_exp, lam = sb("lam_prod", [P, 2, D_HD]), sb("lam_dot", [P, 2]), sb("lam_exp", [P, 2]), sb("lam", [P, 1])
        rms_eps = sb("rms_eps", [P, 1])
        xn, xT = sb("xn", [P, E]), sb("xT", [P, E])
        rot_a, rot_b, rot = sb("rot_a", [P, 3 * P]), sb("rot_b", [P, 3 * P]), sb("rot", [P, 3 * P])
        keys = sb("keys", [P, D_HEADS // 2, P])
        kept = sb("kept", [P, TILES, 2, P])
        values = sb("values", [P, 2, D_KV_HEADS, 64])
        top = sb("top", [P, 2, D_HEADS])
        probs = sb("probs", [P, 2, D_HEADS * SEQ])
        probsT = sb("probsT", [P, 2, D_HEADS * SEQ])
        headsT = sb("headsT", [P, 1024])
        inv = sb("inv", [P, 2, D_HEADS])
        part0, part1 = sb("part0", [P, E]), sb("part1", [P, E])
        attn, squares, scaled = sb("attn", [P, E]), sb("squares", [P, E]), sb("scaled", [P, E])
        square_sum, rms_log, rms_inv = sb("square_sum", [P, D_HEADS]), sb("rms_log", [P, D_HEADS]), sb("rms_inv", [P, D_HEADS])
        attnT = sb("attnT", [P, E])

        loaded = sem("loaded")
        consts_set, lam_ready, lam_dots, lam_exps, wo_scaled, lam_steps = (
            sem(n) for n in ("consts_set", "lam_ready", "lam_dots", "lam_exps", "wo_scaled", "lam_steps"))
        xn_ready, xT_psum, xT_ready, projected, v_kept, rot_parts, rot_ready, values_ready, keys_ready = (
            sem(n) for n in ("xn_ready", "xT_psum", "xT_ready", "projected", "v_kept", "rot_parts", "rot_ready", "values_ready", "keys_ready"))
        scored, top_raw, top_ready, shifted, exp_done, probsT_psum, probsT_ready = (
            core.sems("da_" + n, 2) for n in ("scored", "top_raw", "top_ready", "shifted", "exp_done", "probsT_psum", "probsT_ready"))
        heads_psum, headsT_ready, heads_rows, inv_ready, inv_lam, parts_ready, attn_ready, squares_ready, square_sums = (
            sem(n) for n in ("heads_psum", "headsT_ready", "heads_rows", "inv_ready", "inv_lam", "parts_ready", "attn_ready", "squares_ready", "square_sums"))
        rms_logs, rms_ready, scaled_ready, attnT_psum, attnT_ready, out_psum, x_ready, stats_done = (
            sem(n) for n in ("rms_logs", "rms_ready", "scaled_ready", "attnT_psum", "attnT_ready", "out_psum", "x_ready", "stats_done"))
        LOADS = 9 * 16

        block = scope.enter_context(nc.Block())

        def pipeline(eng, turn):
            first, last = 1, TILES - 3
            for t in range(-3, first):
                turn(t, lambda k: 0 <= k < TILES)
            with eng.Fori(first, last) as t:
                turn(t, lambda k: True)
            for t in range(last, TILES + 1):
                turn(t, lambda k: 0 <= k < TILES)

        def started(t, first):
            return not isinstance(t, int) or t >= first

        @block.sync
        def _(sp):
            first_rows.on_sync(sp)
            for out, src in ((w_qk[:], chunked(dram["da_w_qk"])), (w_v[:], chunked(dram["da_w_v"])), (rotary[:], dram["rotary"]),
                             (head_mask[:], dram["da_head_mask"]), (causal[:], dram["causal"]), (ident_bf[:], dram["ident_bf"]),
                             (lam_in[:], dram["da_lam"]), (w_o[:], chunked(dram["da_w_o"])), (gain[:], dram["da_gain"]),
                             ):
                sp.dma_start(out, src).then_inc(loaded, 16)
            sp.wait_ge(loaded, LOADS)
            sp.wait_ge(first_rows.ident_loaded, 16)

        @block.gpsimd
        def _(pool):
            nc.gpsimd.memset(values[:], 0.0).then_inc(consts_set, 1)
            pool.wait_ge(consts_set, 1)
            for half in range(2):
                ones = values[64 * half:64 * half + 64, :, :, half * 17 + D_DV:half * 17 + D_DV + 1]
                nc.gpsimd.memset(ones, 1.0).then_inc(consts_set, 1)
            pool.wait_ge(consts_set, 3)

            def turn(t, valid):
                if valid(t):
                    pool.wait_ge(v_kept, t + 1)
                    if started(t, 1):
                        pool.wait_ge(heads_psum, 2 * t)
                    if started(t, -1) and valid(t + 1):
                        pool.wait_ge(keys_ready, t + 2)
                    for half in range(2):
                        rows = slice(64 * half, 64 * half + 64)
                        done = nc.gpsimd.tensor_copy(values[rows, :, :, half * 17:half * 17 + D_DV],
                                                     kept[rows, t].rearrange("p b (h d) -> p b h d", d=D_DV))
                    done.then_inc(values_ready, 1)
                if valid(t + 2):
                    pool.wait_ge(rot_ready, t + 3)
                    if valid(t):
                        pool.wait_ge(values_ready, t + 1)
                    nc.gpsimd.tensor_tensor(
                        keys[:], rot[:, None, 2 * P:3 * P].to_broadcast([P, D_HEADS // 2, P]),
                        head_mask[:, :, None].to_broadcast([P, D_HEADS // 2, P]), ALU.mult).then_inc(keys_ready, 1)

            pipeline(pool, turn)

        @block.scalar
        def _(act):
            act.preload_act_table_set(EXP_LN)
            ln.on_scalar(act)

            def turn(t, valid):
                if isinstance(t, int) and t == -2:
                    act.wait_ge(lam_dots, 1)
                    nc.scalar.activation(lam_exp[:], lam_dot[:], ACT.Exp).then_inc(lam_exps, 1)
                if valid(t + 2):
                    act.wait_ge(projected, t + 3)
                    for b in range(2):
                        for half in range(2):
                            done = nc.scalar.copy(kept[64 * half:64 * half + 64, t + 2, b, :], ps[64 * b:64 * b + 64, 4, 3 * P:4 * P])
                    done.then_inc(v_kept, 1)
                if valid(t - 1):
                    act.wait_ge(attn_ready, t)
                    nc.scalar.activation(squares[:], attn[:], ACT.Square).then_inc(squares_ready, 1)

                def take_probsT(r):
                    for c in range(2):
                        act.wait_ge(probsT_psum[r], 2 * t + (c + 1))
                        nc.scalar.copy(probsT[:, r, c * 512:(c + 1) * 512], ps[:, 6 + c, :]).then_inc(probsT_ready[r], 1)

                def exponentials(r):
                    act.wait_ge(shifted[r], t + 2)
                    nc.scalar.activation(probs[:, r], probs[:, r], ACT.Exp).then_inc(exp_done[r], 1)

                if valid(t):
                    take_probsT(0)
                if valid(t + 1):
                    exponentials(0)
                if valid(t):
                    take_probsT(1)
                if valid(t - 1):
                    act.wait_ge(square_sums, t)
                    nc.scalar.activation(rms_log[:], square_sum[:], ACT.Ln, bias=rms_eps[:], scale=1.0 / D_DV).then_inc(rms_logs, 1)
                    act.wait_ge(rms_logs, t)
                    nc.scalar.activation(rms_inv[:], rms_log[:], ACT.Exp, scale=-0.5).then_inc(rms_ready, 1)
                if valid(t):
                    for c in range(2):
                        act.wait_ge(heads_psum, 2 * t + (c + 1))
                        nc.scalar.copy(headsT[:, c * 512:(c + 1) * 512], ps[:, c, :]).then_inc(headsT_ready, 1)
                if valid(t - 1):
                    act.wait_ge(attnT_psum, t)
                    nc.scalar.copy(attnT[:], ps[:, 2, 0:E]).then_inc(attnT_ready, 1)
                if valid(t + 3):
                    act.wait_ge(xT_psum, t + 4)
                    nc.scalar.copy(xT[:], ps[:, 3, 0:E]).then_inc(xT_ready, 1)
                if valid(t + 1):
                    exponentials(1)

            pipeline(act, turn)

        @block.vector
        def _(dve):
            first_rows.on_vector(dve)
            ln.on_vector(dve)
            nc.vector.memset(rms_eps[:], RMS_EPS)
            dve.wait_ge(ln.ready, 1)
            dve.sem_inc(x_ready, 1)
            by_head = lambda a: a.rearrange("p (h d) -> p h d", d=D_DV)
            scores = [ps[:, 2 + 2 * r:4 + 2 * r, :].rearrange("p b (h s) -> p (b h) s", s=SEQ) for r in range(2)]
            heads = ps[:, 6:8, :].rearrange("p r (g c) -> p r g c", c=64)
            sums = [heads[:, r, :, 0:34].rearrange("p g (h d) -> p g h d", d=17)[:, :, :, D_DV] for r in range(2)]
            weighted = [heads[:, r, :, 0:34].rearrange("p g (h d) -> p g h d", d=17)[:, :, :, 0:D_DV] for r in range(2)]
            pair = lambda a: a.rearrange("p (g h) -> p g h", h=2)
            quad = lambda a: a.rearrange("p (g h d) -> p g h d", h=2, d=D_DV)
            spread = lambda a: pair(a)[:, :, :, None].to_broadcast([P, D_HEADS // 2, 2, D_DV])

            def lambda_dots():
                dve.wait_ge(loaded, LOADS)
                nc.vector.tensor_tensor(lam_prod[:], lam_in[:, 0:2], lam_in[:, 2:4], ALU.mult).then_inc(lam_steps, 1)
                dve.wait_ge(lam_steps, 1)
                nc.vector.tensor_reduce(lam_dot[:], lam_prod[:], AX.X, ALU.add).then_inc(lam_dots, 1)
                for c in range(KC):
                    nc.vector.tensor_scalar(w_o[:, c], w_o[:, c], gain[:], 1.0 - LAMBDA_INIT, ALU.mult, ALU.mult).then_inc(wo_scaled, 1)

            def lambda_difference():
                dve.wait_ge(lam_exps, 1)
                nc.vector.tensor_tensor(lam[:], lam_exp[:, 0:1], lam_exp[:, 1:2], ALU.subtract).then_inc(lam_steps, 1)
                dve.wait_ge(lam_steps, 2)
                nc.vector.tensor_scalar(lam[:], lam[:], LAMBDA_INIT, None, ALU.add).then_inc(lam_ready, 1)

            def turn(t, valid):
                def maxima(r):
                    dve.wait_ge(scored[r], t + 2)
                    nc.vector.tensor_reduce(top[:, r], scores[r], AX.X, ALU.max).then_inc(top_raw[r], 1)

                def shift(r):
                    dve.wait_ge(top_raw[r], t + 2)
                    nc.vector.tensor_scalar(top[:, r], top[:, r], FLT_MAX, -FLT_MAX, ALU.min, ALU.max).then_inc(top_ready[r], 1)
                    dve.wait_ge(top_ready[r], t + 2)
                    if started(t, 0):
                        dve.wait_ge(probsT_psum[r], 2 * t + 2)
                    nc.vector.scalar_tensor_tensor(
                        probs[:, r].rearrange("p (h s) -> p h s", s=SEQ), scores[r], FLT_MAX,
                        top[:, r, :, None].to_broadcast([P, D_HEADS, SEQ]), ALU.min, ALU.subtract).then_inc(shifted[r], 1)

                filling = isinstance(t, int) and t in (-2, -1)
                if filling:
                    dve.wait_ge(xT_psum, t + 3)
                    ln.normalise(xn[:], t + 3).then_inc(xn_ready, 1)
                if valid(t + 2):
                    if started(t, -1):
                        dve.wait_ge(rot_ready, t + 2)
                    dve.wait_ge(projected, t + 3)
                    nc.vector.tensor_tensor(rot_b[:], ps[:, 5, 0:3 * P], rotary[:, 1], ALU.mult)
                    dve.wait_ge(v_kept, t + 3)
                    nc.vector.tensor_tensor(rot_a[:], ps[:, 4, 0:3 * P], rotary[:, 0], ALU.mult).then_inc(rot_parts, 1)
                if valid(t + 1):
                    maxima(0)
                    shift(0)
                if valid(t - 1):
                    dve.wait_ge(squares_ready, t)
                    nc.vector.tensor_reduce(square_sum[:], by_head(squares[:]), AX.X, ALU.add).then_inc(square_sums, 1)
                if valid(t + 1):
                    maxima(1)
                if valid(t + 2):
                    dve.wait_ge(rot_parts, t + 3)
                    nc.vector.tensor_tensor(rot[:], rot_a[:], rot_b[:], ALU.add).then_inc(rot_ready, 1)
                if valid(t + 1):
                    shift(1)
                if valid(t - 1):
                    dve.wait_ge(rms_ready, t)
                    nc.vector.tensor_tensor(by_head(scaled[:]), by_head(attn[:]), rms_inv[:, :, None].to_broadcast([P, D_HEADS, D_DV]),
                                            ALU.mult).then_inc(scaled_ready, 1)
                if valid(t + 3) and not filling:
                    ln.normalise(xn[:], t + 3).then_inc(xn_ready, 1)
                if valid(t):
                    dve.wait_ge(heads_rows, t + 1)
                    for r in range(2):
                        nc.vector.reciprocal(pair(inv[:, r]), sums[r]).then_inc(inv_ready, 1)
                    dve.wait_ge(inv_ready, 2 * t + 2)
                    if isinstance(t, int) and t == 0:
                        dve.wait_ge(lam_ready, 1)
                    nc.vector.tensor_scalar(inv[:, 1], inv[:, 1], lam[:], None, ALU.mult).then_inc(inv_lam, 1)
                    nc.vector.tensor_tensor(quad(part0[:]), weighted[0], spread(inv[:, 0]), ALU.mult)
                    dve.wait_ge(inv_lam, t + 1)
                    nc.vector.tensor_tensor(quad(part1[:]), weighted[1], spread(inv[:, 1]), ALU.mult).then_inc(parts_ready, 1)
                    dve.wait_ge(parts_ready, t + 1)
                    nc.vector.tensor_tensor(attn[:], part0[:], part1[:], ALU.subtract).then_inc(attn_ready, 1)
                if valid(t - 1):
                    dve.wait_ge(out_psum, t)
                    nc.vector.tensor_tensor(core.x[:, t - 1, :], core.x[:, t - 1, :], ps[:, 2, E:2 * E], ALU.add).then_inc(x_ready, 1)
                    dve.wait_ge(x_ready, t + 1)
                    nc.vector.bn_stats(core.row_stats[:, t - 1, :], core.x[:, t - 1, :]).then_inc(stats_done, 1)
                if isinstance(t, int) and t == -3:
                    lambda_dots()
                if isinstance(t, int) and t == -1:
                    lambda_difference()

            pipeline(dve, turn)
            dve.wait_ge(stats_done, TILES)

        @block.tensor
        def _(pe):
            pe.wait_ge(first_rows.ident_loaded, 16)

            def turn(t, valid):
                def score(r):
                    banks = (2 + 2 * r, 3 + 2 * r)
                    for bank in banks:
                        nc.tensor.matmul(ps[:, bank, :], ident_bf[:], causal[:], start=True, stop=False, skip_group_check=True)
                    for b in range(2):
                        for half, bank in enumerate(banks):
                            rows = slice(64 * half, 64 * half + 64)
                            done = nc.tensor.matmul(
                                ps[64 * b:64 * b + 64, bank, :], rot[rows, r * P + 64 * b:r * P + 64 * b + 64],
                                keys[rows, :, 64 * b:64 * b + 64], start=False, stop=True, skip_group_check=True)
                    done.then_inc(scored[r], 1)

                def turn_probs(r):
                    pe.wait_ge(exp_done[r], t + 1)
                    for c in range(2):
                        if r == 1:
                            pe.wait_ge(probsT_ready[0], 2 * t + (c + 1))
                        for j in range(4):
                            done = nc.tensor.transpose(ps[:, 6 + c, j * P:(j + 1) * P], probs[:, r, (4 * c + j) * P:(4 * c + j + 1) * P], ident[:])
                        done.then_inc(probsT_psum[r], 1)

                if valid(t + 1):
                    pe.wait_ge(keys_ready, t + 2)
                    if started(t, 0):
                        pe.wait_ge(shifted[0], t + 1)
                    if started(t, 1):
                        pe.wait_ge(x_ready, t)
                    score(0)
                if valid(t):
                    if started(t, 1):
                        pe.wait_ge(parts_ready, t)
                    turn_probs(0)
                if valid(t + 1):
                    if started(t, 0):
                        pe.wait_ge(shifted[1], t + 1)
                    if valid(t + 2):
                        pe.wait_ge(rot_parts, t + 3)
                    score(1)
                if valid(t):
                    turn_probs(1)
                    pe.wait_ge(values_ready, t + 1)
                    for c in range(2):
                        pe.wait_ge(probsT_ready[1], 2 * t + (c + 1))
                        if started(t, 1):
                            pe.wait_ge(headsT_ready, 2 * t - 1 + c)
                        for b in range(2):
                            for j in range(4 * c, 4 * c + 4):
                                weights = probsT[:].rearrange("p r (j t) -> p r j t", t=P)[:, :, j, 64 * b:64 * b + 64]
                                out = ps[64 * (j % 2):64 * (j % 2) + 64, c, :].rearrange("p (g r b t) -> p g r b t", g=2, r=2, b=2)[:, (j // 2) % 2, :, b, :]
                                done = nc.tensor.matmul(out, values[:, b, j, :], weights, start=True, stop=True)
                        done.then_inc(heads_psum, 1)
                if valid(t - 1):
                    pe.wait_ge(scaled_ready, t)
                    if valid(t + 1):
                        pe.wait_ge(shifted[0], t + 2)
                    else:
                        pe.wait_ge(x_ready, t)
                    for c in range(KC):
                        done = nc.tensor.transpose(ps[:, 2, c * P:(c + 1) * P], scaled[:, c * P:(c + 1) * P], ident[:])
                    done.then_inc(attnT_psum, 1)
                if valid(t + 3):
                    pe.wait_ge(xn_ready, t + 4)
                    if valid(t + 1):
                        pe.wait_ge(shifted[0], t + 2)
                    for c in range(KC):
                        done = nc.tensor.transpose(ps[:, 3, c * P:(c + 1) * P], xn[:, c * P:(c + 1) * P], ident[:])
                    done.then_inc(xT_psum, 1)
                if valid(t):
                    for c in range(2):
                        pe.wait_ge(headsT_ready, 2 * t + (c + 1))
                        for r in range(2):
                            for g in range(2 * c, 2 * c + 2):
                                done = nc.tensor.transpose(ps[:, 6 + r, g * P:(g + 1) * P],
                                                           headsT[:].rearrange("p (g r t) -> p g r t", g=4, r=2)[:, g, r, :], ident[:])
                    done.then_inc(heads_rows, 1)
                if valid(t - 1):
                    pe.wait_ge(attnT_ready, t)
                    for c in range(KC):
                        done = nc.tensor.matmul(ps[:, 2, E:2 * E], attnT[:, c * P:(c + 1) * P], w_o[:, c],
                                                start=(c == 0), stop=(c == KC - 1))
                    done.then_inc(out_psum, 1)
                if valid(t + 3):
                    pe.wait_ge(xT_ready, t + 4)
                    if valid(t + 1):
                        pe.wait_ge(shifted[1], t + 2)
                    elif valid(t + 2):
                        pe.wait_ge(rot_parts, t + 3)
                    if isinstance(t, int) and t == -3:
                        pe.wait_ge(loaded, LOADS)
                        pe.wait_ge(wo_scaled, KC)
                    for m in range(6):
                        for c in range(KC):
                            nc.tensor.matmul(ps[:, 4 + m // 3, (m % 3) * P:(m % 3 + 1) * P], w_qk[:, c, m * P:(m + 1) * P],
                                             xT[:, c * P:(c + 1) * P], start=(c == 0), stop=(c == KC - 1))
                    for c in range(KC):
                        done = nc.tensor.matmul(ps[:, 4, 3 * P:4 * P], xT[:, c * P:(c + 1) * P], w_v[:, c],
                                                start=(c == 0), stop=(c == KC - 1))
                    done.then_inc(projected, 1)

            pipeline(pe, turn)

C_HEADS, C_HD = 8, 8
PARTS = 3
STACK = PARTS * C_HD
MAX_ROW = 96
STACK_ROWS = MAX_ROW + PARTS
RING = 3
V_COLS = 32
SELU_SCALE, SELU_ALPHA = 1.0507009873554805, 1.6732632423543772


def feature_attention(core):
    nc, dram, ps, ident = core.nc, core.dram, core.psum, core.ident
    with ExitStack() as scope:
        sb = lambda name, shape, dt=F32: scope.enter_context(nc.sbuf_tensor(f"fa_{name}", shape, dt))
        sem = lambda name: core.sem(f"fa_{name}")
        ln = RowNorm(core, "fa", scope)
        ident_bf = sb("ident_bf", [P, P], BF16)
        w_out = sb("w_out", [P, P])
        rows = sb("rows", [P, E])
        zeros = sb("zeros", [P, E])
        context = sb("context", [P, RING, E])
        rest = sb("rest", [P, 2, E])
        parts = sb("parts", [P, RING, 2, PARTS, E], BF16)
        q_stack = sb("q_stack", [P, RING, 2, C_HEADS, E], BF16)
        k_stack = sb("k_stack", [P, RING, 2, C_HEADS, E], BF16)
        values = sb("values", [P, RING, 2, 2 * C_HEADS, V_COLS])
        neg_max = sb("neg_max", [P, 2, 2, C_HEADS])
        max_rest = sb("max_rest", [P, 2, 2, C_HEADS])
        max_parts = sb("max_parts", [P, 2, 2, PARTS, C_HEADS], BF16)
        max_rows = sb("max_rows", [P, 2, E], BF16)
        probs = sb("probs", [P, 4, 2, 2, E])
        mixedT = sb("mixedT", [P, 2, E])
        inv = sb("inv", [P, 2 * C_HEADS])
        mixed = sb("mixed", [P, 2, 2, C_HEADS * C_HD])
        mixed_c = sb("mixed_c", [P, E])
        above, below, exp_below, negative, selu = (sb(n, [P, E]) for n in ("above", "below", "exp_below", "negative", "selu"))
        minus_one = sb("minus_one", [P, 1])

        loaded, padded, consts_set, cleared_values, scaled_rstd = (sem(n) for n in ("loaded", "padded", "consts_set", "cleared_values", "scaled_rstd"))
        rows_ready, high_ready, split_step, split_done = (sem(n) for n in ("rows_ready", "high_ready", "split_step", "split_done"))
        context_ready = core.sems("fa_context_ready", RING)
        stored, stacked, max_stacked = core.sems("fa_stored", RING), core.sems("fa_stacked", RING), core.sems("fa_max_stacked", 2)
        values_psum, values_ready, max_scored, max_taken = (sem(n) for n in ("values_psum", "values_ready", "max_scored", "max_taken"))
        max_high, max_left, max_mid, max_split, max_turned, max_rows_ready = (
            sem(n) for n in ("max_high", "max_left", "max_mid", "max_split", "max_turned", "max_rows_ready"))
        scored, exp_done, mixed_done, mixedT_ready, mixed_rows, inv_ready, mixed_ready = (
            sem(n) for n in ("scored", "exp_done", "mixed_done", "mixedT_ready", "mixed_rows", "inv_ready", "mixed_ready"))
        mixed_turned, mixed_c_ready, projected, channels_read = (sem(n) for n in ("mixed_turned", "mixed_c_ready", "projected", "channels_read"))
        exp_below_ready, selu_parts, selu_ready, selu_sum, x_ready, stats_done = (
            sem(n) for n in ("exp_below_ready", "selu_parts", "selu_ready", "selu_sum", "x_ready", "stats_done"))
        LOADS, STORES = 2 * PARTS * 16, 2 * PARTS * 16

        block = scope.enter_context(nc.Block())

        def pipeline(eng, turn):
            first, last = 1, TILES - RING
            exists = lambda k: 0 <= k < TILES
            for t in range(-RING, first):
                turn(t, lambda d: (t + d) % RING, lambda d: (t + d) // RING, exists)
            with eng.Fori(0, (last - first) // RING) as i:
                for r in range(RING):
                    turn(RING * i + (first + r), lambda d: (first + r + d) % RING, lambda d: i + (first + r + d) // RING, lambda k: True)
            for t in range(last, TILES + 1):
                turn(t, lambda d: (t + d) % RING, lambda d: (t + d) // RING, exists)

        assert (TILES - RING - 1) % RING == 0

        def started(t, first):
            return not isinstance(t, int) or t >= first

        @block.sync
        def _(sp):
            sp.dma_start(ident_bf[:], dram["ident_bf"]).then_inc(loaded, 16)
            sp.dma_start(w_out[:], dram["fa_w_out"]).then_inc(loaded, 16)

            def pad_stacks():
                for slot in range(RING):
                    for stack, rows_of in ((q_stack, MAX_ROW), (k_stack, STACK_ROWS)):
                        sp.dma_start(stack[PARTS * STACK:rows_of, slot].rearrange("p b h f -> p (b h f)"),
                                      dram["fa_padding"][0:rows_of - PARTS * STACK]).then_inc(padded, 16)

            def max_to_stack(tile, slot, b):
                sp.wait_ge(max_rows_ready, 2 * tile + (b + 1))
                sp.dma_start(q_stack[MAX_ROW:MAX_ROW + PARTS, slot, b], max_rows[0:PARTS * C_HEADS, b]).then_inc(max_stacked[b], 16)

            def load(t, slot, round):
                if started(t, 1):
                    sp.wait_ge(scored, 8 * t)
                sp.wait_ge(stored[slot], STORES * round + STORES)
                groups = bass.ts(t + 2, 2 * C_HEADS)
                for k in range(PARTS):
                    of = dram["q_parts"][:, groups, :].rearrange("r g f -> r (g f)")
                    sp.dma_start(q_stack[k * STACK:(k + 1) * STACK, slot].rearrange("p b h f -> p (b h f)"), of).then_inc(stacked[slot], 16)
                for k in range(PARTS):
                    of = dram["k_parts"][k * C_HD:(k + 1) * C_HD, groups, :].rearrange("d g f -> d (g f)")
                    sp.dma_start(k_stack[k * STACK:(k + 1) * STACK, slot].rearrange("p b h f -> p (b h f)"),
                                 of[None].to_broadcast([PARTS, C_HD, 2 * C_HEADS * E])).then_inc(stacked[slot], 16)

            def store(t, slot, of):
                sp.wait_ge(split_done, t + 4)
                for kind, part in of:
                    to = dram[("q_parts", "k_parts")[kind]].rearrange("(a d) g f -> a g d f", d=C_HD)[part, bass.ts(t + 3, 2 * C_HEADS)]
                    sp.dma_start(to, parts[:, slot, kind, part]).then_inc(stored[slot], 16)

            all_parts = [(kind, part) for kind in range(2) for part in range(PARTS)]
            FIRST_STORES = 5

            def load_context(tile, slot):
                sp.dma_start(context[:, slot], dram["ctx"][bass.ts(tile, P), :]).then_inc(context_ready[slot], 16)

            def turn(t, ring, rounds, valid):
                if valid(t + 3):
                    if started(t, 0):
                        sp.wait_ge(values_psum, t + 1)
                    load_context(t + 3, ring(3))
                if isinstance(t, int) and t == -RING:
                    pad_stacks()
                if valid(t):
                    max_to_stack(t, ring(0), 1)
                if valid(t + 2):
                    load(t, ring(2), rounds(2))
                if valid(t + 3):
                    store(t, ring(3), all_parts[:FIRST_STORES])
                if valid(t + 1):
                    max_to_stack(t + 1, ring(1), 0)
                if valid(t + 3):
                    store(t, ring(3), all_parts[FIRST_STORES:])

            pipeline(sp, turn)

        @block.vector
        def _(dve):
            ln.on_vector(dve)
            nc.vector.memset(minus_one[:], -SELU_SCALE * SELU_ALPHA).then_inc(consts_set, 1)
            dve.wait_ge(ln.ready, 1)
            nc.vector.tensor_scalar(ln.rstd[:], ln.rstd[:], C_HD ** -0.5, None, ALU.mult).then_inc(scaled_rstd, 1)
            dve.wait_ge(scaled_rstd, 1)
            ln.normalise(rows[:], 0).then_inc(rows_ready, 1)

            def maximum(tile, b, h):
                dve.wait_ge(max_scored, 16 * tile + (8 * b + h + 1))
                nc.vector.tensor_reduce(neg_max[:, b, :, h], ps[:, h % 2, :].rearrange("p (q k) -> p q k", q=2),
                                        AX.X, ALU.max, negate=True).then_inc(max_taken, 1)

            def divide(tile, b):
                count = 2 * tile + (b + 1)
                dve.wait_ge(mixed_rows, count)
                view = ps[:, 6, :].rearrange("p (g c) -> p g c", c=V_COLS)
                nc.vector.reciprocal(inv[:], view[:, :, C_HD]).then_inc(inv_ready, 1)
                dve.wait_ge(inv_ready, count)
                out = mixed[:, :, b].rearrange("p q (h d) -> p q h d", d=C_HD)
                nc.vector.tensor_tensor(out, view[:, :, 0:C_HD].rearrange("p (q h) d -> p q h d", q=2),
                                        inv[:].rearrange("p (q h) -> p q h", q=2)[:, :, :, None].to_broadcast([P, 2, C_HEADS, C_HD]),
                                        ALU.mult).then_inc(mixed_ready, 1)

            def turn(t, ring, rounds, valid):
                if valid(t + 3) and started(t, -2):
                    dve.wait_ge(split_done, t + 3)
                    ln.normalise(rows[:], t + 3).then_inc(rows_ready, 1)
                for b in range(2):
                    for g in range(4):
                        if valid(t + 1):
                            maximum(t + 1, b, 2 * g)
                            maximum(t + 1, b, 2 * g + 1)
                        if g == 1 and b == 0 and valid(t - 1):
                            divide(t - 1, 1)
                        if g == 1 and b == 1 and valid(t):
                            divide(t, 0)
                if valid(t - 1):
                    dve.wait_ge(x_ready, t)
                    nc.vector.bn_stats(core.row_stats[:, t - 1, :], core.x[:, t - 1, :]).then_inc(stats_done, 1)

            pipeline(dve, turn)
            dve.wait_ge(stats_done, TILES)

        @block.scalar
        def _(act):
            act.preload_act_table_set(EXP_LN)
            ln.on_scalar(act)
            act.wait_ge(cleared_values, 2)
            act.wait_ge(consts_set, 1)

            def split_high(n, slot, round):
                act.wait_ge(rows_ready, n + 1)
                act.wait_ge(context_ready[slot], 16 * round + 16)
                if started(n, RING):
                    act.wait_ge(stored[slot], STORES * round)
                for kind, source in enumerate((rows[:], context[:, slot])):
                    nc.scalar.copy(parts[:, slot, kind, 0], source).then_inc(high_ready, 1)

            def values_of(tile, slot):
                act.wait_ge(values_psum, tile + 1)
                nc.scalar.copy(values[:, slot, :, :, 0:C_HD],
                               ps[:, 7, 0:E].rearrange("p (k g d) -> p k g d", k=2, d=C_HD)).then_inc(values_ready, 1)

            def max_to_rows(tile, b):
                act.wait_ge(max_turned, 2 * tile + (b + 1))
                nc.scalar.copy(max_rows[0:PARTS * C_HEADS, b], ps[0:PARTS * C_HEADS, 7, 0:E]).then_inc(max_rows_ready, 1)

            def exponentials(t, b, g):
                act.wait_ge(scored, 8 * t + (4 * b + g + 1))
                if b or started(t, 1):
                    act.wait_ge(mixed_done, 4 * t + (2 * b + g // 2 - 1))
                nc.scalar.activation(probs[:, g].rearrange("p h k q -> p h (k q)"), ps[:, 2 + 2 * (g % 2):4 + 2 * (g % 2), :], ACT.Exp).then_inc(exp_done, 1)

            def take_mixed(tile, b):
                act.wait_ge(mixed_done, 4 * tile + (2 * b + 2))
                nc.scalar.copy(mixedT[:], ps[:, 6, :].rearrange("p (k q) -> p k q", k=2)).then_inc(mixedT_ready, 1)

            def turn(t, ring, rounds, valid):
                if valid(t):
                    exponentials(t, 0, 0)
                if valid(t + 3):
                    split_high(t + 3, ring(3), rounds(3))
                if valid(t - 1):
                    take_mixed(t - 1, 1)
                if valid(t):
                    exponentials(t, 0, 1)
                if valid(t):
                    max_to_rows(t, 1)
                    exponentials(t, 0, 2)
                if valid(t - 1):
                    act.wait_ge(mixed_turned, t)
                    nc.scalar.copy(mixed_c[:], ps[:, 7, 0:E]).then_inc(mixed_c_ready, 1)
                if valid(t):
                    exponentials(t, 0, 3)
                if valid(t - 1):
                    act.wait_ge(projected, t)
                    nc.scalar.activation(below[:], ps[:, 7, E:2 * E], ACT.Relu, scale=-1.0).then_inc(selu_parts, 1)
                    nc.scalar.activation(above[:], ps[:, 7, E:2 * E], ACT.Relu, scale=SELU_SCALE).then_inc(channels_read, 1)
                if valid(t):
                    exponentials(t, 1, 0)
                    take_mixed(t, 0)
                if valid(t):
                    exponentials(t, 1, 1)
                if valid(t - 1):
                    act.wait_ge(selu_parts, t)
                    nc.scalar.activation(exp_below[:], below[:], ACT.Exp, scale=-1.0).then_inc(exp_below_ready, 1)
                if valid(t + 1):
                    max_to_rows(t + 1, 0)
                if valid(t - 1):
                    act.wait_ge(exp_below_ready, t)
                    nc.scalar.activation(negative[:], exp_below[:], ACT.Identity, scale=SELU_SCALE * SELU_ALPHA, bias=minus_one[:]).then_inc(selu_ready, 1)
                if valid(t):
                    exponentials(t, 1, 2)
                if valid(t + 1):
                    values_of(t + 1, ring(1))
                if valid(t):
                    exponentials(t, 1, 3)

            pipeline(act, turn)

        @block.gpsimd
        def _(pool):
            nc.gpsimd.memset(values[:], 0.0).then_inc(cleared_values, 1)
            pool.wait_ge(cleared_values, 1)
            nc.gpsimd.memset(values[:, :, :, :, C_HD:C_HD + 1], 1.0).then_inc(cleared_values, 1)
            pool.wait_ge(cleared_values, 2)
            nc.gpsimd.memset(zeros[:], 0.0).then_inc(cleared_values, 1)
            pool.wait_ge(cleared_values, 3)

            few_zeros = zeros[:, 0:2 * C_HEADS].rearrange("p (q h) -> p q h", q=2)

            def split(n, slot):
                part = lambda kind, k: parts[:, slot, kind, k]
                for kind, source in enumerate((rows[:], context[:, slot])):
                    pool.wait_ge(high_ready, 2 * n + (kind + 1))
                    nc.gpsimd.tensor_tensor(rest[:, kind], source, part(kind, 0), ALU.subtract).then_inc(split_step, 1)
                for kind in range(2):
                    pool.wait_ge(split_step, 4 * n + (kind + 1))
                    nc.gpsimd.tensor_tensor(part(kind, 1), rest[:, kind], zeros[:], ALU.add).then_inc(split_step, 1)
                pool.wait_ge(split_step, 4 * n + 4)
                for kind in range(2):
                    done = nc.gpsimd.tensor_tensor(part(kind, 2), rest[:, kind], part(kind, 1), ALU.subtract)
                done.then_inc(split_done, 1)

            def split_max(tile, b):
                count = 2 * tile + (b + 1)
                pool.wait_ge(max_taken, 16 * tile + (8 * b + 8))
                nc.gpsimd.tensor_tensor(max_parts[:, b, :, 0], neg_max[:, b], few_zeros, ALU.add).then_inc(max_high, 1)
                pool.wait_ge(max_high, count)
                nc.gpsimd.tensor_tensor(max_rest[:, b], neg_max[:, b], max_parts[:, b, :, 0], ALU.subtract).then_inc(max_left, 1)
                pool.wait_ge(max_left, count)
                nc.gpsimd.tensor_tensor(max_parts[:, b, :, 1], max_rest[:, b], few_zeros, ALU.add).then_inc(max_mid, 1)
                pool.wait_ge(max_mid, count)
                nc.gpsimd.tensor_tensor(max_parts[:, b, :, 2], max_rest[:, b], max_parts[:, b, :, 1], ALU.subtract).then_inc(max_split, 1)

            def turn(t, ring, rounds, valid):
                if valid(t + 3):
                    split(t + 3, ring(3))
                if valid(t + 1):
                    split_max(t + 1, 0)
                if valid(t - 1):
                    pool.wait_ge(selu_ready, t)
                    nc.gpsimd.tensor_tensor(selu[:], above[:], negative[:], ALU.add).then_inc(selu_sum, 1)
                    pool.wait_ge(selu_sum, t)
                    nc.gpsimd.tensor_tensor(core.x[:, t - 1, :], core.x[:, t - 1, :], selu[:], ALU.add).then_inc(x_ready, 1)
                if valid(t + 1):
                    split_max(t + 1, 1)

            pipeline(pool, turn)

        @block.tensor
        def _(pe):
            pe.wait_ge(loaded, 32)
            pe.wait_ge(padded, 2 * RING * 16)

            def score_for_max(tile, slot, round, b, h):
                if (b, h) == (0, 0):
                    pe.wait_ge(stacked[slot], LOADS * round + LOADS)
                if not isinstance(tile, int) or 8 * b + h >= 2 or tile:
                    pe.wait_ge(max_taken, 16 * tile + (8 * b + h - 1))
                for q in range(2):
                    done = nc.tensor.matmul(ps[:, h % 2, q * E:(q + 1) * E], q_stack[0:MAX_ROW, slot, b, h, q * P:(q + 1) * P],
                                            k_stack[0:MAX_ROW, slot, b, h, :], start=True, stop=True)
                done.then_inc(max_scored, 1)

            def score(t, slot, b, g):
                if g == 0:
                    pe.wait_ge(max_stacked[b], 16 * t + 16)
                if not isinstance(t, int) or 8 * t + 4 * b + g >= 2:
                    pe.wait_ge(exp_done, 8 * t + (4 * b + g - 1))
                for h in range(2):
                    for k in range(2):
                        done = nc.tensor.matmul(ps[:, 2 + 2 * (g % 2) + h, k * E:(k + 1) * E],
                                                k_stack[0:STACK_ROWS, slot, b, 2 * g + h, k * P:(k + 1) * P],
                                                q_stack[0:STACK_ROWS, slot, b, 2 * g + h, :], start=True, stop=True)
                done.then_inc(scored, 1)

            def mix(tile, slot, b, half):
                pe.wait_ge(exp_done, 8 * tile + (4 * b + 2 * half + 2))
                if half == 0:
                    if b or started(tile, 1):
                        pe.wait_ge(mixed_ready, 2 * tile + b)
                    pe.wait_ge(values_ready, tile + 1)
                for k in range(2):
                    for c in range(4):
                        h = 4 * half + c
                        done = nc.tensor.matmul(ps[32 * c:32 * c + 32, 6, half * E:(half + 1) * E], values[:, slot, k, 8 * b + h, :],
                                                probs[:, h // 2, h % 2, k, :], start=(k == 0), stop=(k == 1), skip_group_check=True)
                done.then_inc(mixed_done, 1)

            def turn_mixed(tile, b):
                pe.wait_ge(mixedT_ready, 2 * tile + (b + 1))
                for q in range(2):
                    for half in range(2):
                        done = nc.tensor.transpose(ps[:, 6, (2 * q + half) * P:(2 * q + half + 1) * P],
                                                   mixedT[:, half, q * P:(q + 1) * P], ident[:])
                done.then_inc(mixed_rows, 1)

            def turn_max(tile, b):
                pe.wait_ge(max_split, 2 * tile + (b + 1))
                for q in range(2):
                    done = nc.tensor.matmul(ps[0:PARTS * C_HEADS, 7, q * P:(q + 1) * P],
                                            max_parts[:, b, q].rearrange("p a h -> p (a h)"), ident_bf[:], start=True, stop=True)
                done.then_inc(max_turned, 1)

            def turn(t, ring, rounds, valid):
                def heads(b, g):
                    if valid(t + 1):
                        score_for_max(t + 1, ring(1), rounds(1), b, 2 * g)
                    if valid(t):
                        score(t, ring(0), b, g)
                    if valid(t + 1):
                        score_for_max(t + 1, ring(1), rounds(1), b, 2 * g + 1)

                heads(0, 0)
                if valid(t - 1):
                    mix(t - 1, ring(-1), 1, 1)
                heads(0, 1)
                if valid(t - 1):
                    turn_mixed(t - 1, 1)
                if valid(t):
                    pe.wait_ge(values_ready, t + 1)
                    turn_max(t, 1)
                heads(0, 2)
                if valid(t - 1):
                    if valid(t):
                        pe.wait_ge(max_rows_ready, 2 * t + 2)
                    else:
                        pe.wait_ge(channels_read, t - 1)
                    pe.wait_ge(mixed_ready, 2 * t)
                    for q in range(2):
                        done = nc.tensor.transpose(ps[:, 7, q * P:(q + 1) * P], mixed[:, q].rearrange("p b c -> p (b c)"), ident[:])
                    done.then_inc(mixed_turned, 1)
                heads(0, 3)
                if valid(t):
                    mix(t, ring(0), 0, 0)
                if valid(t - 1):
                    pe.wait_ge(mixed_c_ready, t)
                    nc.tensor.matmul(ps[:, 7, E:2 * E], w_out[:], mixed_c[:], start=True, stop=True).then_inc(projected, 1)
                heads(1, 0)
                if valid(t):
                    mix(t, ring(0), 0, 1)
                heads(1, 1)
                if valid(t):
                    turn_mixed(t, 0)
                if valid(t + 1):
                    if valid(t - 1):
                        pe.wait_ge(channels_read, t)
                    elif valid(t):
                        pe.wait_ge(max_rows_ready, 2 * t + 2)
                    turn_max(t + 1, 0)
                heads(1, 2)
                if valid(t + 1):
                    pe.wait_ge(context_ready[ring(1)], 16 * rounds(1) + 16)
                    pe.wait_ge(max_rows_ready, 2 * t + 3)
                    for k in range(2):
                        done = nc.tensor.transpose(ps[:, 7, k * P:(k + 1) * P], context[:, ring(1), k * P:(k + 1) * P], ident[:])
                    done.then_inc(values_psum, 1)
                heads(1, 3)
                if valid(t):
                    mix(t, ring(0), 1, 0)

            pipeline(pe, turn)

F_N, F_S, F_H = 8, 8, 8
F_SEL, F_UPD = F_N * F_S, F_N * F_H
F_IN = F_SEL + F_N + F_UPD
F_MEAN, F_UPD_AT = F_SEL, F_SEL + F_N
F_ROWS = 96
EXP_LIMIT = 87.0


def selected_update(core):
    nc, dram, ps, ident = core.nc, core.dram, core.psum, core.ident
    with ExitStack() as scope:
        sb = lambda name, shape, dt=F32: scope.enter_context(nc.sbuf_tensor(f"ff_{name}", shape, dt))
        sem = lambda name: core.sem(f"ff_{name}")
        ln = RowNorm(core, "ff", scope)
        w_in = sb("w_in", [P, KC, F_IN])
        debias = sb("debias", [P, KC, F_N])
        w_back = sb("w_back", [P, E])
        center, slope, first = sb("center", [P, F_N]), sb("slope", [P, F_N]), sb("first", [P, F_N])
        ones = sb("ones", [P, P])
        shift_parts, shift = sb("shift_parts", [P, KC, F_IN]), sb("shift", [P, F_IN])
        xn, xT = sb("xn", [P, 2, E]), sb("xT", [P, 2, E])
        proj = sb("proj", [P, TILES, F_IN])
        squares = sb("squares", [P, TILES, F_SEL])
        raw, dist, gate, hot = (sb(name, [P, TILES, F_N]) for name in ("raw", "dist", "gate", "hot"))
        length, best, pick, keep, move = (sb(name, [P, TILES]) for name in ("length", "best", "pick", "keep", "move"))
        chosen = sb("chosen", [P, 2, F_ROWS])
        chosenT = sb("chosenT", [P, 2, P])
        moved = sb("moved", [P, 2, E])

        loaded, zeroed, shift_step, shift_psum, shift_ready = (sem(n) for n in ("loaded", "zeroed", "shift_step", "shift_psum", "shift_ready"))
        xn_ready, xT_psum, xT_ready, projected, proj_ready = (sem(n) for n in ("xn_ready", "xT_psum", "xT_ready", "projected", "proj_ready"))
        squares_ready, gate_step, z_ready, gate_exp, hot_ready, moves = (sem(n) for n in ("squares_ready", "gate_step", "z_ready", "gate_exp", "hot_ready", "moves"))
        chosen_ready, bias_ready, turned, chosenT_ready, moved_ready, back, x_ready, stats_done = (
            sem(n) for n in ("chosen_ready", "bias_ready", "turned", "chosenT_ready", "moved_ready", "back", "x_ready", "stats_done"))
        LOADS = 6 * 16
        by_update = lambda a, width: a.rearrange("p (n s) -> p n s", s=width)

        def pipeline(eng, turn, before):
            first, last = 2, TILES - before
            exists = lambda k: 0 <= k < TILES
            for t in range(-before, first):
                turn(t, lambda d: (t + d) % 2, exists)
            rounds = (last - first) // 4
            with eng.Fori(0, rounds) as i:
                for r in range(4):
                    turn(4 * i + (first + r), lambda d: (first + r + d) % 2, lambda k: True)
            for t in range(first + 4 * rounds, TILES):
                turn(t, lambda d: (t + d) % 2, exists)

        def started(t, first):
            return not isinstance(t, int) or t >= first

        block = scope.enter_context(nc.Block())

        @block.sync
        def _(sp):
            for out, src in ((w_in[:], chunked(dram["ff_w_in"])), (debias[:], chunked(dram["ff_debias"])), (w_back[0:F_ROWS], dram["ff_w_back"]),
                             (center[:], dram["ff_center"]), (slope[:], dram["ff_slope"]), (first[:], dram["ff_first"])):
                sp.dma_start(out, src).then_inc(loaded, 16)
            sp.wait_ge(loaded, LOADS)

        @block.gpsimd
        def _(pool):
            nc.gpsimd.memset(chosen[:], 0.0).then_inc(zeroed, 1)
            pool.wait_ge(zeroed, 1)
            pool.wait_ge(hot_ready, 1)

            def turn(t, place, valid):
                if valid(t + 2):
                    if started(t, 0):
                        pool.wait_ge(turned, t + 1)
                    nc.gpsimd.tensor_copy(chosen[:, place(2), F_UPD:F_UPD + F_N], hot[:, t + 2, :]).then_inc(bias_ready, 1)

            pipeline(pool, turn, 2)

        @block.scalar
        def _(act):
            act.preload_act_table_set(EXP_LN)
            ln.on_scalar(act)

            def project(t, place, valid):
                if valid(t + 1):
                    act.wait_ge(xT_psum, t + 2)
                    nc.scalar.copy(xT[:, place(1)], ps[:, place(1), 0:E]).then_inc(xT_ready, 1)
                if isinstance(t, int) and t == -1:
                    act.wait_ge(shift_psum, 1)
                    nc.scalar.copy(shift[:], ps[:, 7, 0:F_IN]).then_inc(shift_ready, 1)

            pipeline(act, project, 1)
            act.wait_ge(proj_ready, TILES)
            nc.scalar.activation(squares[:], proj[:, :, 0:F_SEL], ACT.Square).then_inc(squares_ready, 1)
            act.wait_ge(z_ready, 1)
            nc.scalar.activation(gate[:], raw[:], ACT.Exp).then_inc(gate_exp, 1)
            act.wait_ge(moves, 2)

            def turn(t, place, valid):
                if valid(t + 1):
                    act.wait_ge(turned, t + 2)
                    nc.scalar.copy(chosenT[0:F_ROWS, place(1)], ps[0:F_ROWS, place(1), 0:P]).then_inc(chosenT_ready, 1)
                    if started(t, 1):
                        act.wait_ge(x_ready, t)
                    nc.scalar.activation(moved[:, place(1)], core.x[:, t + 1, :], ACT.Identity, bias=move[:, bass.ts(t + 1, 1)],
                                         scale=keep[:, bass.ts(t + 1, 1)]).then_inc(moved_ready, 1)

            pipeline(act, turn, 1)

        @block.vector
        def _(dve):
            ln.on_vector(dve)
            nc.vector.memset(ones[:], 1.0).then_inc(shift_step, 1)
            dve.wait_ge(ln.ready, 1)

            def project(t, place, valid):
                if valid(t + 2):
                    if started(t, 0):
                        dve.wait_ge(xT_psum, t + 1)
                    ln.normalise(xn[:, place(2)], t + 2).then_inc(xn_ready, 1)
                if isinstance(t, int) and t == -1:
                    dve.wait_ge(loaded, LOADS)
                    for c in range(KC):
                        mean = w_in[:, c, F_MEAN:F_MEAN + F_N]
                        nc.vector.tensor_tensor(by_update(shift_parts[:, c, 0:F_SEL], F_S), by_update(w_in[:, c, 0:F_SEL], F_S),
                                                mean[:, :, None].to_broadcast([P, F_N, F_S]), ALU.mult).then_inc(shift_step, 1)
                        nc.vector.scalar_tensor_tensor(shift_parts[:, c, F_MEAN:F_MEAN + F_N], mean, 0.5, mean, ALU.mult, ALU.mult).then_inc(shift_step, 1)
                        nc.vector.tensor_tensor(by_update(shift_parts[:, c, F_UPD_AT:], F_H), by_update(w_in[:, c, F_UPD_AT:], F_H),
                                                debias[:, c, :, None].to_broadcast([P, F_N, F_H]), ALU.mult).then_inc(shift_step, 1)
                if isinstance(t, int) and t == 0:
                    dve.wait_ge(shift_ready, 1)
                if valid(t):
                    dve.wait_ge(projected, t + 1)
                    nc.vector.tensor_tensor(proj[:, t, :], ps[:, 2 + place(0), 0:F_IN], shift[:], ALU.subtract).then_inc(proj_ready, 1)

            pipeline(dve, project, 2)
            across = lambda a: a[:, :, None].to_broadcast([P, TILES, F_N])
            every = lambda a: a[:, None, :].to_broadcast([P, TILES, F_N])
            nc.vector.tensor_tensor(length[:], ln.rstd[:], ln.rstd[:], ALU.mult).then_inc(gate_step, 1)
            dve.wait_ge(gate_step, 1)
            nc.vector.scalar_tensor_tensor(length[:], length[:], float(E), ln.var[:], ALU.mult, ALU.mult).then_inc(gate_step, 1)
            dve.wait_ge(gate_step, 2)
            dve.wait_ge(proj_ready, TILES)
            nc.vector.scalar_tensor_tensor(dist[:], proj[:, :, F_MEAN:F_MEAN + F_N], -2.0, across(length), ALU.mult, ALU.add).then_inc(gate_step, 1)
            dve.wait_ge(gate_step, 3)
            nc.vector.reciprocal(dist[:], dist[:]).then_inc(gate_step, 1)
            dve.wait_ge(squares_ready, 1)
            nc.vector.tensor_reduce(raw[:], squares[:].rearrange("p t (n s) -> p t n s", s=F_S), AX.X, ALU.add).then_inc(gate_step, 1)
            dve.wait_ge(gate_step, 5)
            nc.vector.tensor_tensor(raw[:], raw[:], dist[:], ALU.mult).then_inc(gate_step, 1)
            dve.wait_ge(gate_step, 6)
            nc.vector.tensor_tensor(raw[:], every(center), raw[:], ALU.subtract).then_inc(gate_step, 1)
            dve.wait_ge(gate_step, 7)
            nc.vector.tensor_tensor(raw[:], raw[:], every(slope), ALU.mult).then_inc(gate_step, 1)
            dve.wait_ge(gate_step, 8)
            nc.vector.tensor_scalar(raw[:], raw[:], EXP_LIMIT, None, ALU.min).then_inc(z_ready, 1)
            dve.wait_ge(gate_exp, 1)
            nc.vector.tensor_scalar(gate[:], gate[:], 1.0, None, ALU.add).then_inc(gate_step, 1)
            dve.wait_ge(gate_step, 9)
            nc.vector.reciprocal(gate[:], gate[:]).then_inc(gate_step, 1)
            dve.wait_ge(gate_step, 10)
            nc.vector.tensor_reduce(best[:], gate[:], AX.X, ALU.max).then_inc(gate_step, 1)
            dve.wait_ge(gate_step, 11)
            nc.vector.tensor_tensor(gate[:], gate[:], across(best), ALU.is_ge).then_inc(gate_step, 1)
            nc.vector.tensor_scalar(keep[:], best[:], -1.0, 1.0, ALU.mult, ALU.add).then_inc(gate_step, 1)
            dve.wait_ge(gate_step, 13)
            nc.vector.tensor_tensor(gate[:], gate[:], every(first), ALU.mult).then_inc(gate_step, 1)
            nc.vector.tensor_tensor(keep[:], keep[:], ln.rstd[:], ALU.mult).then_inc(gate_step, 1)
            dve.wait_ge(gate_step, 15)
            nc.vector.tensor_reduce(pick[:], gate[:], AX.X, ALU.max).then_inc(gate_step, 1)
            nc.vector.scalar_tensor_tensor(move[:], ln.mean[:], -1.0, keep[:], ALU.mult, ALU.mult).then_inc(moves, 1)
            dve.wait_ge(gate_step, 16)
            dve.wait_ge(moves, 1)
            nc.vector.tensor_scalar(keep[:], keep[:], 1.0, None, ALU.add).then_inc(moves, 1)
            nc.vector.tensor_tensor(hot[:], gate[:], across(pick), ALU.is_equal).then_inc(gate_step, 1)
            dve.wait_ge(gate_step, 17)
            nc.vector.tensor_tensor(hot[:], hot[:], across(best), ALU.mult).then_inc(hot_ready, 1)
            dve.wait_ge(hot_ready, 1)
            dve.wait_ge(zeroed, 1)

            def turn(t, place, valid):
                if valid(t + 2):
                    if started(t, 0):
                        dve.wait_ge(turned, t + 1)
                    nc.vector.tensor_tensor(by_update(chosen[:, place(2), 0:F_UPD], F_H), by_update(proj[:, t + 2, F_UPD_AT:], F_H),
                                            hot[:, t + 2, :, None].to_broadcast([P, F_N, F_H]), ALU.mult).then_inc(chosen_ready, 1)
                if valid(t):
                    dve.wait_ge(back, t + 1)
                    dve.wait_ge(moved_ready, t + 1)
                    nc.vector.tensor_tensor(core.x[:, t, :], moved[:, place(0)], ps[:, 2 + place(0), 0:E], ALU.add).then_inc(x_ready, 1)
                    dve.wait_ge(x_ready, t + 1)
                    nc.vector.bn_stats(core.row_stats[:, t, :], core.x[:, t, :]).then_inc(stats_done, 1)

            pipeline(dve, turn, 2)
            dve.wait_ge(stats_done, TILES)

        @block.tensor
        def _(pe):

            def project(t, place, valid):
                if valid(t + 1):
                    pe.wait_ge(xn_ready, t + 2)
                    for c in range(KC):
                        done = nc.tensor.transpose(ps[:, place(1), c * P:(c + 1) * P], xn[:, place(1), c * P:(c + 1) * P], ident[:])
                    done.then_inc(xT_psum, 1)
                if isinstance(t, int) and t == -1:
                    pe.wait_ge(loaded, LOADS)
                    pe.wait_ge(shift_step, 1 + 3 * KC)
                    for c in range(KC):
                        done = nc.tensor.matmul(ps[:, 7, 0:F_IN], ones[:], shift_parts[:, c], start=(c == 0), stop=(c == KC - 1))
                    done.then_inc(shift_psum, 1)
                if valid(t):
                    pe.wait_ge(xT_ready, t + 1)
                    if started(t, 2):
                        pe.wait_ge(proj_ready, t - 1)
                    for c in range(KC):
                        done = nc.tensor.matmul(ps[:, 2 + place(0), 0:F_IN], xT[:, place(0), c * P:(c + 1) * P], w_in[:, c],
                                                start=(c == 0), stop=(c == KC - 1))
                    done.then_inc(projected, 1)

            pipeline(pe, project, 1)

            def turn(t, place, valid):
                if valid(t + 1):
                    pe.wait_ge(chosen_ready, t + 2)
                    pe.wait_ge(bias_ready, t + 2)
                    nc.tensor.transpose(ps[0:F_ROWS, place(1), 0:P], chosen[:, place(1)], ident[:]).then_inc(turned, 1)
                if valid(t):
                    pe.wait_ge(chosenT_ready, t + 1)
                    if started(t, 2):
                        pe.wait_ge(x_ready, t - 1)
                    nc.tensor.matmul(ps[:, 2 + place(0), 0:E], chosenT[0:F_ROWS, place(0)], w_back[0:F_ROWS], start=True, stop=True).then_inc(back, 1)

            pipeline(pe, turn, 1)

S_HEADS, S_STATE = 32, 64
S_HD = E // S_HEADS
LEVELS = SEQ.bit_length() - 1


def state_space(core, staged):
    nc, dram, ps, ident = core.nc, core.dram, core.psum, core.ident
    with ExitStack() as scope:
        sb = lambda name, shape, dt=F32: scope.enter_context(nc.sbuf_tensor(f"ss_{name}", shape, dt))
        sem = lambda name: core.sem(f"ss_{name}")
        ln = RowNorm(core, "ss", scope)
        w_bc = sb("w_bc", [P, KC, 2 * S_STATE])
        w_dt, w_out = sb("w_dt", [P, KC, S_HEADS]), sb("w_out", [P, KC, E])
        bias_bc = sb("bias_bc", [S_STATE, 2])
        bias_dt, skip, rate, bias_out = sb("bias_dt", [P, S_HEADS]), sb("skip", [P, S_HEADS]), sb("rate", [P, S_HEADS]), sb("bias_out", [P, E])
        spans = sb("spans", [P, LEVELS, P])
        pairs = sb("pairs", [P, LEVELS, P])
        xn, xn_kept = sb("xn", [P, 2, E]), sb("xn_kept", [P, TILES, E])
        xT, bcT = sb("xT", [P, 2, E]), sb("bcT", [S_STATE, 2, 2, P])
        dt, dt_tail, dA = (sb(name, [P, TILES, S_HEADS]) for name in ("dt", "dt_tail", "dA"))
        scoresT = sb("scoresT", [P, TILES, P])
        same, same_dot = sb("same", [P, TILES, P]), sb("same_dot", [P, TILES])
        own = sb("own", [P, TILES, S_HEADS])
        decay, decay_dt = (sb(name, [P, TILES, LEVELS, S_HEADS]) for name in ("decay", "decay_dt"))
        level_scores, inputs = sb("level_scores", [P, 2, LEVELS, P]), sb("inputs", [P, 2, LEVELS, E])
        outputs, own_rows = sb("outputs", [P, LEVELS, E]), sb("own_rows", [P, 2, E])
        sums = sb("sums", [P, 2, LEVELS // 2, E])
        yT = sb("yT", [P, 2, E])

        weights_loaded, loaded, next_weights = (sem(n) for n in ("weights_loaded", "loaded", "next_weights"))
        xn_ready, xn_kept_ready, xT_psum, xT_ready, projected, bc_ready, dt_raw, scored, scores_ready = (
            sem(n) for n in ("xn_ready", "xn_kept_ready", "xT_psum", "xT_ready", "projected", "bc_ready", "dt_raw", "scored", "scores_ready"))
        soft_step, tail_exp, tail_log, rate_ready, dA_ready, spans_psum, decay_ready, decay_dt_ready, own_step = (
            sem(n) for n in ("soft_step", "tail_exp", "tail_log", "rate_ready", "dA_ready", "spans_psum", "decay_ready", "decay_dt_ready", "own_step"))
        inputs_ready, own_ready, biased, level_ready, level_psum, outputs_ready, sums_ready, y_psum, yT_ready, out_psum, x_ready, stats_done = (
            sem(n) for n in ("inputs_ready", "own_ready", "biased", "level_ready", "level_psum", "outputs_ready", "sums_ready",
                             "y_psum", "yT_ready", "out_psum", "x_ready", "stats_done"))
        WEIGHT_LOADS, LOADS = 4 * 16, 6 * 16
        by_head = lambda a: a.rearrange("p (h d) -> p h d", d=S_HD)
        per_head = lambda a: a[:, :, None].to_broadcast([P, S_HEADS, S_HD])

        def pipeline(eng, turn, before):
            first = 3
            rounds = (TILES - before - first) // 2
            exists = lambda k: 0 <= k < TILES
            for t in range(-before, first):
                turn(t, lambda d: (t + d) % 2, exists)
            with eng.Fori(0, rounds) as i:
                for r in range(2):
                    turn(2 * i + (first + r), lambda d: (first + r + d) % 2, lambda k: True)
            for t in range(first + 2 * rounds, TILES + 1):
                turn(t, lambda d: (t + d) % 2, exists)

        def started(t, first):
            return not isinstance(t, int) or t >= first

        block = scope.enter_context(nc.Block())

        @block.sync
        def _(sp):
            for out, src in ((w_bc[:], chunked(dram["ss_w_bc"])), (w_dt[:], chunked(dram["ss_w_dt"])), (bias_bc[:], dram["ss_bias_bc"]),
                             (bias_dt[:], dram["ss_bias_dt"])):
                sp.dma_start(out, src).then_inc(weights_loaded, 16)
            for out, src in ((bias_out[:], dram["ss_bias_out"]), (rate[:], dram["ss_A_log"]), (skip[:], dram["ss_skip"]),
                             (spans[:], dram["ss_spans"]), (pairs[:], dram["ss_pairs"]), (w_out[:], chunked(dram["ss_w_out"]))):
                sp.dma_start(out, src).then_inc(loaded, 16)
            sp.dma_start(staged[:].rearrange("p (c q) -> p c q", c=KC), chunked(dram["ga_w_q"])).then_inc(next_weights, 16)
            sp.wait_ge(weights_loaded, WEIGHT_LOADS)
            sp.wait_ge(loaded, LOADS)
            sp.wait_ge(next_weights, 16)

        @block.gpsimd
        def _(pool):
            pool.wait_ge(loaded, LOADS)
            with pool.Fori(0, TILES) as t:
                pool.wait_ge(xn_kept_ready, t + 1)
                nc.gpsimd.tensor_tensor(core.x[:, t, :], core.x[:, t, :], bias_out[:], ALU.add).then_inc(biased, 1)
            pool.wait_ge(own_step, 4)
            pool.wait_ge(decay_dt_ready, LEVELS)

            def turn(t, place, valid):
                if valid(t + 2):
                    if started(t, 0):
                        pool.wait_ge(level_psum, t + 1)
                    nc.gpsimd.tensor_tensor(inputs[:, place(2)].rearrange("p m (h d) -> p m h d", d=S_HD),
                                            by_head(xn_kept[:, t + 2, :])[:, None].to_broadcast([P, LEVELS, S_HEADS, S_HD]),
                                            decay_dt[:, t + 2, :, :, None].to_broadcast([P, LEVELS, S_HEADS, S_HD]), ALU.mult).then_inc(inputs_ready, 1)
                if valid(t + 1):
                    if started(t, 1):
                        pool.wait_ge(y_psum, t)
                    nc.gpsimd.tensor_tensor(by_head(own_rows[:, place(1)]), by_head(xn_kept[:, t + 1, :]), per_head(own[:, t + 1, :]),
                                            ALU.mult).then_inc(own_ready, 1)

            pipeline(pool, turn, 2)

        @block.scalar
        def _(act):
            act.preload_act_table_set(EXP_LN)
            ln.on_scalar(act)

            def project(t, place, valid):
                if valid(t + 1):
                    act.wait_ge(xT_psum, t + 2)
                    nc.scalar.copy(xT[:, place(1)], ps[:, place(1), 0:E]).then_inc(xT_ready, 1)
                if isinstance(t, int) and t == 0:
                    act.wait_ge(weights_loaded, WEIGHT_LOADS)
                if valid(t):
                    act.wait_ge(projected, t + 1)
                    for k in range(2):
                        done = nc.scalar.activation(bcT[:, place(0), k], ps[0:S_STATE, 2 + place(0), k * P:(k + 1) * P],
                                                    ACT.Identity, bias=bias_bc[:, k:k + 1])
                    done.then_inc(bc_ready, 1)
                if valid(t - 1):
                    act.wait_ge(scored, t)
                    nc.scalar.copy(scoresT[:, t - 1, :], ps[:, 6 + place(-1), 0:P]).then_inc(scores_ready, 1)

            pipeline(act, project, 1)
            act.wait_ge(loaded, LOADS)
            nc.scalar.activation(rate[:], rate[:], ACT.Exp).then_inc(rate_ready, 1)
            act.wait_ge(soft_step, 1)
            nc.scalar.activation(dt_tail[:], dt_tail[:], ACT.Exp, scale=-1.0).then_inc(tail_exp, 1)
            act.wait_ge(tail_exp, 1)
            nc.scalar.activation(dt_tail[:], dt_tail[:], ACT.Ln, bias=1.0).then_inc(tail_log, 1)
            for m in range(LEVELS):
                act.wait_ge(spans_psum, m + 1)
                nc.scalar.activation(decay[:, :, m, :], ps[:, m, :].rearrange("p (t h) -> p t h", h=S_HEADS), ACT.Exp).then_inc(decay_ready, 1)

            def turn(t, place, valid):
                if valid(t):
                    act.wait_ge(y_psum, t + 1)
                    nc.scalar.copy(yT[:, place(0)], ps[:, 6, 0:E]).then_inc(yT_ready, 1)

            pipeline(act, turn, 2)

        @block.vector
        def _(dve):
            ln.on_vector(dve)
            dve.wait_ge(ln.ready, 1)

            def project(t, place, valid):
                if valid(t + 2):
                    if started(t, 0):
                        dve.wait_ge(xT_psum, t + 1)
                    ln.normalise(xn[:, place(2)], t + 2).then_inc(xn_ready, 1)
                    ln.normalise(xn_kept[:, t + 2, :], t + 2).then_inc(xn_kept_ready, 1)
                if isinstance(t, int) and t == 0:
                    dve.wait_ge(weights_loaded, WEIGHT_LOADS)
                if valid(t):
                    dve.wait_ge(projected, t + 1)
                    nc.vector.tensor_tensor(dt[:, t, :], ps[:, 4 + place(0), 0:S_HEADS], bias_dt[:], ALU.add).then_inc(dt_raw, 1)

            pipeline(dve, project, 2)
            dve.wait_ge(loaded, LOADS)
            every = lambda a: a[:, None, :].to_broadcast([P, TILES, S_HEADS])
            dve.wait_ge(dt_raw, TILES)
            nc.vector.scalar_tensor_tensor(dt_tail[:], dt[:], -1.0, dt[:], ALU.mult, ALU.max).then_inc(soft_step, 1)
            dve.wait_ge(tail_log, 1)
            nc.vector.scalar_tensor_tensor(dt[:], dt[:], 0.0, dt_tail[:], ALU.max, ALU.add).then_inc(soft_step, 1)
            dve.wait_ge(soft_step, 2)
            dve.wait_ge(rate_ready, 1)
            nc.vector.scalar_tensor_tensor(dA[:], dt[:], -1.0, every(rate), ALU.mult, ALU.mult).then_inc(dA_ready, 1)
            dve.wait_ge(scores_ready, TILES)
            nc.vector.tensor_tensor(same[:], scoresT[:], ident[:, None, :].to_broadcast([P, TILES, P]), ALU.mult).then_inc(own_step, 1)
            dve.wait_ge(own_step, 1)
            nc.vector.tensor_reduce(same_dot[:], same[:], AX.X, ALU.add).then_inc(own_step, 1)
            dve.wait_ge(own_step, 2)
            nc.vector.tensor_tensor(own[:], dt[:], same_dot[:, :, None].to_broadcast([P, TILES, S_HEADS]), ALU.mult).then_inc(own_step, 1)
            dve.wait_ge(own_step, 3)
            nc.vector.tensor_tensor(own[:], own[:], every(skip), ALU.add).then_inc(own_step, 1)
            for m in range(LEVELS):
                dve.wait_ge(decay_ready, m + 1)
                nc.vector.tensor_tensor(decay_dt[:, :, m, :], decay[:, :, m, :], dt[:], ALU.mult).then_inc(decay_dt_ready, 1)

            def turn(t, place, valid):
                if valid(t):
                    if started(t, 1):
                        dve.wait_ge(sums_ready, t)
                    dve.wait_ge(level_psum, t + 1)
                    nc.vector.tensor_tensor(outputs[:].rearrange("p m (h d) -> p m h d", d=S_HD),
                                            ps[:, 3 * place(0):3 * place(0) + 3, :].rearrange("p k (m h d) -> p (k m) h d", m=2, d=S_HD),
                                            decay[:, t, :, :, None].to_broadcast([P, LEVELS, S_HEADS, S_HD]), ALU.mult).then_inc(outputs_ready, 1)
                    dve.wait_ge(outputs_ready, t + 1)
                    nc.vector.tensor_tensor(sums[:, place(0)], outputs[:, 0:LEVELS // 2], outputs[:, LEVELS // 2:], ALU.add).then_inc(sums_ready, 1)
                if valid(t + 2):
                    nc.vector.tensor_tensor(level_scores[:, place(2)], pairs[:], scoresT[:, t + 2, None, :].to_broadcast([P, LEVELS, P]),
                                            ALU.mult).then_inc(level_ready, 1)
                if valid(t - 1):
                    dve.wait_ge(out_psum, t)
                    dve.wait_ge(biased, TILES)
                    nc.vector.tensor_tensor(core.x[:, t - 1, :], core.x[:, t - 1, :], ps[:, 7, 0:E],
                                            ALU.add).then_inc(x_ready, 1)
                    dve.wait_ge(x_ready, t)
                    nc.vector.bn_stats(core.row_stats[:, t - 1, :], core.x[:, t - 1, :]).then_inc(stats_done, 1)

            pipeline(dve, turn, 2)
            dve.wait_ge(stats_done, TILES)

        @block.tensor
        def _(pe):
            def project(t, place, valid):
                if valid(t + 1):
                    pe.wait_ge(xn_ready, t + 2)
                    for c in range(KC):
                        done = nc.tensor.transpose(ps[:, place(1), c * P:(c + 1) * P], xn[:, place(1), c * P:(c + 1) * P], ident[:])
                    done.then_inc(xT_psum, 1)
                if isinstance(t, int) and t == -1:
                    pe.wait_ge(weights_loaded, WEIGHT_LOADS)
                if valid(t):
                    pe.wait_ge(xT_ready, t + 1)
                    if started(t, 2):
                        pe.wait_ge(dt_raw, t - 1)
                    rows = lambda c: xT[:, place(0), c * P:(c + 1) * P]
                    for k in range(2):
                        for c in range(KC):
                            nc.tensor.matmul(ps[0:S_STATE, 2 + place(0), k * P:(k + 1) * P], w_bc[:, c, k * S_STATE:(k + 1) * S_STATE], rows(c),
                                             start=(c == 0), stop=(c == KC - 1))
                    for c in range(KC):
                        done = nc.tensor.matmul(ps[:, 4 + place(0), 0:S_HEADS], rows(c), w_dt[:, c], start=(c == 0), stop=(c == KC - 1))
                    done.then_inc(projected, 1)
                if valid(t - 1):
                    pe.wait_ge(bc_ready, t)
                    if started(t, 3):
                        pe.wait_ge(scores_ready, t - 2)
                    nc.tensor.matmul(ps[:, 6 + place(-1), 0:P], bcT[:, place(-1), 0], bcT[:, place(-1), 1], start=True, stop=True).then_inc(scored, 1)

            pipeline(pe, project, 1)
            pe.wait_ge(loaded, LOADS)
            pe.wait_ge(dA_ready, 1)
            for m in range(LEVELS):
                nc.tensor.matmul(ps[:, m, :], spans[:, m], dA[:].rearrange("p t h -> p (t h)"), start=True, stop=True).then_inc(spans_psum, 1)

            def turn(t, place, valid):
                if valid(t + 1):
                    pe.wait_ge(level_ready, t + 2)
                    pe.wait_ge(inputs_ready, t + 2)
                    if started(t, 1):
                        pe.wait_ge(outputs_ready, t)
                    for m in range(LEVELS):
                        done = nc.tensor.matmul(ps[:, 3 * place(1) + m // 2, (m % 2) * E:(m % 2 + 1) * E], level_scores[:, place(1), m],
                                                inputs[:, place(1), m], start=True, stop=True)
                    done.then_inc(level_psum, 1)
                if valid(t - 1):
                    pe.wait_ge(yT_ready, t)
                    if started(t, 2):
                        pe.wait_ge(x_ready, t - 1)
                    for c in range(KC):
                        done = nc.tensor.matmul(ps[:, 7, 0:E], yT[:, place(-1), c * P:(c + 1) * P], w_out[:, c],
                                                start=(c == 0), stop=(c == KC - 1))
                    done.then_inc(out_psum, 1)
                if valid(t):
                    pe.wait_ge(own_ready, t + 1)
                    pe.wait_ge(sums_ready, t + 1)
                    for c in range(KC):
                        columns = slice(c * P, (c + 1) * P)
                        y = ps[:, 6, columns]
                        nc.tensor.matmul(y, own_rows[:, place(0), columns], ident[:], start=True, stop=False)
                        for m in range(LEVELS // 2):
                            done = nc.tensor.matmul(y, sums[:, place(0), m, columns], ident[:], start=False, stop=(m == LEVELS // 2 - 1))
                    done.then_inc(y_psum, 1)

            pipeline(pe, turn, 2)

G_HEADS, G_KV, G_HD = 16, 4, 128
G_GROUP = G_HEADS // G_KV
Q_COLS, KV_COLS = G_HEADS * G_HD, G_KV * G_HD
G_CHUNK = Q_COLS // G_KV



def three_passes(nc, out, lhsT, rhs, start, stop):
    for k, (i, j) in enumerate(((0, 0), (1, 0), (0, 1))):
        done = nc.tensor.matmul(out, lhsT[i], rhs[j], start=start and k == 0, stop=stop and k == 2)
    return done


def grouped_attention(core, raw):
    nc, dram, ps, ident = core.nc, core.dram, core.psum, core.ident
    with ExitStack() as scope:
        sb = lambda name, shape, dt=F32: scope.enter_context(nc.sbuf_tensor(f"ga_{name}", shape, dt))
        sem = lambda name: core.sem(f"ga_{name}")
        ln = RowNorm(core, "ga", scope)
        w_q_high, w_q_low = sb("w_q_high", [P, KC, Q_COLS], F32R), sb("w_q_low", [P, KC, Q_COLS], F32R)
        w_o_high, w_o_low = sb("w_o_high", [P, G_HEADS, E], F32R), sb("w_o_low", [P, G_HEADS, E], F32R)
        w_k = sb("w_k", [P, KC, KV_COLS])
        w_v_high, w_v_low = sb("w_v_high", [P, KC, KV_COLS], F32R), sb("w_v_low", [P, KC, KV_COLS], F32R)
        bias_q, bias_v, bias_k = sb("bias_q", [P, Q_COLS]), sb("bias_v", [P, KV_COLS]), sb("bias_k", [P, G_KV])
        gain_q, gain_k, gain = sb("gain_q", [P, 1]), sb("gain_k", [P, 1]), sb("gain", [P, 1])
        mask = sb("mask", [P, SEQ])
        ones, rms_eps = sb("ones", [P, P], F32R), sb("rms_eps", [P, 1])
        xn, ctxT_k, ctxT_v = sb("xn", [P, E]), sb("ctxT_k", [P, KC, P]), sb("ctxT_v", [P, KC, P])
        ctxT_high, ctxT_low = sb("ctxT_high", [P, KC, P], F32R), sb("ctxT_low", [P, KC, P], F32R)
        xT_high, xT_low = sb("xT_high", [P, E], F32R), sb("xT_low", [P, E], F32R)
        q, q_scaled = sb("q", [P, Q_COLS]), sb("q_scaled", [P, Q_COLS])
        q_sum, q_log, q_inv = sb("q_sum", [P, G_HEADS]), sb("q_log", [P, G_HEADS]), sb("q_inv", [P, G_HEADS])
        qT = sb("qT", [P, G_HEADS, P])
        k_raw, k_squares, k_log, k_inv, kT = (sb(name, [P, KV_COLS]) for name in ("k_raw", "k_squares", "k_log", "k_inv", "kT"))
        k_high, k_low = sb("k_high", [P, KV_COLS], F32R), sb("k_low", [P, KV_COLS], F32R)
        values = sb("values", [P, KV_COLS])
        values_high, values_low = sb("values_high", [P, 2, KV_COLS], F32R), sb("values_low", [P, 2, KV_COLS], F32R)
        scoresT = sb("scoresT", [P, G_HEADS * SEQ])
        probs = sb("probs", [P, G_HEADS, SEQ])
        w_v = probs[:].rearrange("p (c h) s -> p c (h s)", c=KC)
        top, total, inv = sb("top", [P, G_HEADS]), sb("total", [P, G_HEADS]), sb("inv", [P, G_HEADS])
        probsT_high, probsT_low = sb("probsT_high", [P, G_HEADS * SEQ], F32R), sb("probsT_low", [P, G_HEADS * SEQ], F32R)
        mixedT_high, mixedT_low = sb("mixedT_high", [P, G_HEADS, P], F32R), sb("mixedT_low", [P, G_HEADS, P], F32R)

        loaded, w_o_loaded, consts_set, zeroed = (sem(n) for n in ("loaded", "w_o_loaded", "consts_set", "zeroed"))
        w_q_highs, w_q_split, w_o_highs, w_o_split = (sem(n) for n in ("w_q_highs", "w_q_split", "w_o_highs", "w_o_split"))
        ctx_k_ready, ctx_v_ready, xn_ready, xT_psum, xT_highs, xT_ready = (
            sem(n) for n in ("ctx_k_ready", "ctx_v_ready", "xn_ready", "xT_psum", "xT_highs", "xT_ready"))
        q_psum, q_ready, squares_ready, q_sums, q_logs, q_invs, q_scaled_ready, qT_psum, qT_ready = (
            sem(n) for n in ("q_psum", "q_ready", "squares_ready", "q_sums", "q_logs", "q_invs", "q_scaled_ready", "qT_psum", "qT_ready"))
        k_psum, k_ready, k_squared, k_highs, k_lows, k_sums, k_logs, k_invs, kT_ready = (
            sem(n) for n in ("k_psum", "k_ready", "k_squared", "k_highs", "k_lows", "k_sums", "k_logs", "k_invs", "kT_ready"))
        w_v_highs, w_v_split, ctx_highs, ctx_lows, v_psum, v_ready, v_highs, v_lows = (
            sem(n) for n in ("w_v_highs", "w_v_split", "ctx_highs", "ctx_lows", "v_psum", "v_ready", "v_highs", "v_lows"))
        scored, scoresT_ready, turned, masked, top_ready, shifted, exp_done, totals, inv_ready, probs_ready = (
            sem(n) for n in ("scored", "scoresT_ready", "turned", "masked", "top_ready", "shifted", "exp_done", "totals", "inv_ready", "probs_ready"))
        probsT_psum, probsT_highs, probsT_lows, mixed_psum, mixed_highs, mixed_lows, out_psum, x_ready, stats_done = (
            sem(n) for n in ("probsT_psum", "probsT_highs", "probsT_lows", "mixed_psum", "mixed_highs", "mixed_lows", "out_psum", "x_ready", "stats_done"))
        LOADS = 9 * 16
        HALF = G_HEADS // 2

        block = scope.enter_context(nc.Block())

        def pipeline(eng, turn):
            first, last = 1, TILES - 2
            for t in range(-2, first):
                turn(t, lambda k: 0 <= k < TILES)
            with eng.Fori(first, last) as t:
                turn(t, lambda k: True)
            for t in range(last, TILES + 1):
                turn(t, lambda k: 0 <= k < TILES)

        def started(t, first):
            return not isinstance(t, int) or t >= first

        @block.sync
        def _(sp):
            ctx_rows = chunked(dram["ctxT"])
            for out, src in ((bias_q[:], dram["ga_bias_q"].to_broadcast([P, Q_COLS])),
                             (w_k[:], chunked(dram["ga_w_k"])), (w_v, chunked(dram["ga_w_v"])),
                             (bias_v[:], dram["ga_bias_v"].to_broadcast([P, KV_COLS])), (bias_k[:], dram["ga_bias_k"]),
                             (gain_q[:], dram["ga_gain_q"]), (gain_k[:], dram["ga_gain_k"]),
                             (mask[0:SEQ], dram["mask"]), (mask[SEQ:P], dram["mask"])):
                sp.dma_start(out, src).then_inc(loaded, 16)

            def turn(t, valid):
                if valid(t + 1):
                    if started(t, 0):
                        sp.wait_ge(k_psum, t + 1)
                    sp.dma_start(ctxT_k[:], ctx_rows[:, :, bass.ts(t + 1, P)]).then_inc(ctx_k_ready, 16)
                if valid(t):
                    if started(t, 1):
                        sp.wait_ge(v_psum, t)
                    sp.dma_start(ctxT_v[:], ctx_rows[:, :, bass.ts(t, P)]).then_inc(ctx_v_ready, 16)
                if isinstance(t, int) and t == -1:
                    sp.wait_ge(w_q_split, KC + 1)
                    sp.dma_start(raw[:].rearrange("p (h e) -> p h e", e=E), chunked(dram["ga_w_o"])).then_inc(w_o_loaded, 16)

            pipeline(sp, turn)
            sp.wait_ge(ctx_v_ready, 16 * TILES)
            sp.wait_ge(loaded, LOADS)

        @block.gpsimd
        def _(pool):
            nc.gpsimd.memset(values_high[:].bitcast(F32), 0.0).then_inc(zeroed, 1)
            pool.wait_ge(zeroed, 1)
            nc.gpsimd.memset(values_low[:].bitcast(F32), 0.0).then_inc(zeroed, 1)
            pool.wait_ge(zeroed, 2)

            def turn(t, valid):
                def scale_queries(half):
                    heads = slice(HALF * half, HALF * (half + 1))
                    columns = slice(HALF * G_HD * half, HALF * G_HD * (half + 1))
                    pool.wait_ge(q_invs, 2 * t + (half + 3))
                    nc.gpsimd.tensor_tensor(q_scaled[:, columns].rearrange("p (h d) -> p h d", d=G_HD), q[:, columns].rearrange("p (h d) -> p h d", d=G_HD),
                                            q_inv[:, heads, None].to_broadcast([P, HALF, G_HD]), ALU.mult).then_inc(q_scaled_ready, 1)

                if valid(t):
                    pool.wait_ge(ctx_highs, t + 1)
                    nc.gpsimd.tensor_tensor(ctxT_low[:], ctxT_v[:], ctxT_high[:].bitcast(F32), ALU.subtract).then_inc(ctx_lows, 1)
                if valid(t + 1):
                    scale_queries(0)
                    pool.wait_ge(k_highs, t + 2)
                    nc.gpsimd.tensor_tensor(k_low[:], k_squares[:], k_high[:].bitcast(F32), ALU.subtract).then_inc(k_lows, 1)
                    scale_queries(1)
                if isinstance(t, int) and t == -2:
                    pool.wait_ge(w_q_highs, 2)
                    nc.gpsimd.tensor_tensor(w_q_low[:, 1, Q_COLS // 2:], raw[:, KC * Q_COLS - Q_COLS // 2:],
                                            w_q_high[:, 1, Q_COLS // 2:].bitcast(F32), ALU.subtract).then_inc(w_q_split, 1)
                if isinstance(t, int) and t == -1:
                    pool.wait_ge(w_v_highs, 1)
                    nc.gpsimd.tensor_tensor(w_v_low[:], w_v, w_v_high[:].bitcast(F32), ALU.subtract).then_inc(w_v_split, 1)
                    pool.wait_ge(w_o_highs, 1)
                    nc.gpsimd.tensor_tensor(w_o_low[:], raw[:].rearrange("p (h e) -> p h e", e=E), w_o_high[:].bitcast(F32), ALU.subtract).then_inc(w_o_split, 1)

            pipeline(pool, turn)

        @block.scalar
        def _(act):
            act.preload_act_table_set(EXP_LN)
            ln.on_scalar(act)
            act.wait_ge(w_q_highs, 1)
            nc.scalar.copy(w_q_high[:, 1], raw[:, Q_COLS:]).then_inc(w_q_highs, 1)

            def square(n, g):
                act.wait_ge(q_ready, 4 * n + (g + 1))
                nc.scalar.activation(q_scaled[:, g * G_CHUNK:(g + 1) * G_CHUNK], q[:, g * G_CHUNK:(g + 1) * G_CHUNK], ACT.Square).then_inc(squares_ready, 1)

            def query_rms(n, half):
                heads = slice(HALF * half, HALF * (half + 1))
                act.wait_ge(q_sums, 2 * n + (half + 1))
                nc.scalar.activation(q_log[:, heads], q_sum[:, heads], ACT.Ln, bias=rms_eps[:], scale=1.0 / G_HD).then_inc(q_logs, 1)
                act.wait_ge(q_logs, 2 * n + (half + 1))
                nc.scalar.activation(q_inv[:, heads], q_log[:, heads], ACT.Exp, scale=-0.5).then_inc(q_invs, 1)

            def take_mixed(n, j):
                act.wait_ge(mixed_psum, 4 * n + (j + 1))
                nc.scalar.copy(mixedT_high[:, 4 * j:4 * j + 4].rearrange("p h (b t) -> p b h t", b=2),
                               ps[:, 4 + j % 2, :].rearrange("p (b h t) -> p b h t", b=2, h=G_GROUP)).then_inc(mixed_highs, 1)

            def turn(t, valid):
                if isinstance(t, int) and t == -1:
                    act.wait_ge(loaded, LOADS)
                    act.wait_ge(consts_set, 1)
                    act.wait_ge(zeroed, 2)
                if valid(t):
                    act.wait_ge(scored, t + 1)
                    nc.scalar.copy(scoresT[:].rearrange("p (b c) -> p b c", b=2), ps[:, 4:6, :]).then_inc(scoresT_ready, 1)
                    act.wait_ge(ctx_v_ready, 16 * t + 16)
                    nc.scalar.copy(ctxT_high[:], ctxT_v[:]).then_inc(ctx_highs, 1)
                if valid(t + 1):
                    square(t + 1, 0)
                    square(t + 1, 1)
                if valid(t - 1):
                    take_mixed(t - 1, 0)
                    take_mixed(t - 1, 1)
                if valid(t):
                    act.wait_ge(shifted, t + 1)
                    nc.scalar.activation(probs[:], probs[:], ACT.Exp).then_inc(exp_done, 1)
                if valid(t + 1):
                    square(t + 1, 2)
                    square(t + 1, 3)
                if valid(t + 1):
                    query_rms(t + 1, 0)
                if valid(t - 1):
                    take_mixed(t - 1, 2)
                    take_mixed(t - 1, 3)
                if valid(t + 1):
                    act.wait_ge(k_psum, t + 2)
                    for j in range(G_KV):
                        done = nc.scalar.activation(k_raw[:, j * P:(j + 1) * P], ps[:, 2, j * P:(j + 1) * P], ACT.Identity, bias=bias_k[:, j:j + 1])
                    done.then_inc(k_ready, 1)
                    act.wait_ge(k_ready, t + 2)
                    nc.scalar.activation(k_squares[:], k_raw[:], ACT.Square).then_inc(k_squared, 1)
                    act.wait_ge(k_squared, t + 2)
                    nc.scalar.copy(k_high[:], k_squares[:]).then_inc(k_highs, 1)
                    query_rms(t + 1, 1)
                    act.wait_ge(k_sums, t + 2)
                    nc.scalar.activation(k_log[:], ps[:, 2, :], ACT.Ln, bias=rms_eps[:], scale=1.0 / G_HD).then_inc(k_logs, 1)
                    act.wait_ge(k_logs, t + 2)
                    nc.scalar.activation(k_inv[:], k_log[:], ACT.Exp, scale=-0.5).then_inc(k_invs, 1)
                if valid(t):
                    act.wait_ge(probsT_psum, t + 1)
                    nc.scalar.copy(probsT_high[:].rearrange("p (b c) -> p b c", b=2), ps[:, 4:6, :]).then_inc(probsT_highs, 1)

                def take_queries(g):
                    act.wait_ge(qT_psum, 4 * t + (g + 5))
                    nc.scalar.copy(qT[:, 4 * g:4 * g + 4].rearrange("p h t -> p (h t)"), ps[:, g % 2, :]).then_inc(qT_ready, 1)

                if valid(t + 1):
                    take_queries(0)
                    take_queries(1)
                if valid(t + 2):
                    act.wait_ge(xT_psum, t + 3)
                    nc.scalar.copy(xT_high[:], ps[:, 2, 0:E]).then_inc(xT_highs, 1)
                if valid(t + 1):
                    take_queries(2)
                    take_queries(3)
                if isinstance(t, int) and t == -1:
                    nc.scalar.copy(w_v_high[:], w_v).then_inc(w_v_highs, 1)
                if valid(t):
                    act.wait_ge(v_ready, t + 1)
                    for b in range(2):
                        half = slice(SEQ * b, SEQ * b + SEQ)
                        done = nc.scalar.copy(values_high[half, b, :], values[half])
                    done.then_inc(v_highs, 1)

            pipeline(act, turn)

        @block.vector
        def _(dve):
            ln.on_vector(dve)
            nc.vector.memset(ones[:].bitcast(F32), 1.0)
            nc.vector.memset(rms_eps[:], RMS_EPS).then_inc(consts_set, 1)
            nc.vector.tensor_copy(w_q_high[:, 0], raw[:, 0:Q_COLS]).then_inc(w_q_highs, 1)
            dve.wait_ge(w_q_highs, 1)
            nc.vector.tensor_tensor(w_q_low[:, 0], raw[:, 0:Q_COLS], w_q_high[:, 0].bitcast(F32), ALU.subtract).then_inc(w_q_split, 1)
            dve.wait_ge(zeroed, 2)
            dve.wait_ge(ln.ready, 1)
            dve.sem_inc(x_ready, 1)
            across = lambda a: a[:, :, None].to_broadcast([P, G_HEADS, SEQ])

            def biased(n, g):
                dve.wait_ge(q_psum, 4 * n + (g + 1))
                nc.vector.tensor_tensor(q[:, g * G_CHUNK:(g + 1) * G_CHUNK], ps[:, g % 2, :], bias_q[:, g * G_CHUNK:(g + 1) * G_CHUNK],
                                        ALU.add).then_inc(q_ready, 1)

            def query_sums(n, half):
                columns = slice(HALF * G_HD * half, HALF * G_HD * (half + 1))
                dve.wait_ge(squares_ready, 4 * n + (2 * half + 2))
                nc.vector.tensor_reduce(q_sum[:, HALF * half:HALF * (half + 1)], q_scaled[:, columns].rearrange("p (h d) -> p h d", d=G_HD),
                                        AX.X, ALU.add).then_inc(q_sums, 1)

            def mixed_low(n, j):
                dve.wait_ge(mixed_highs, 4 * n + (j + 1))
                halves = [half[:, G_GROUP * j:G_GROUP * (j + 1)].rearrange("p h (b t) -> p b h t", b=2) for half in (mixedT_high, mixedT_low)]
                nc.vector.tensor_tensor(halves[1], ps[:, 4 + j % 2, :].rearrange("p (b h t) -> p b h t", b=2, h=G_GROUP),
                                        halves[0].bitcast(F32), ALU.subtract).then_inc(mixed_lows, 1)

            def split_rest():
                dve.wait_ge(w_q_highs, 2)
                nc.vector.tensor_tensor(w_q_low[:, 1, 0:Q_COLS // 2], raw[:, Q_COLS:Q_COLS + Q_COLS // 2], w_q_high[:, 1, 0:Q_COLS // 2].bitcast(F32),
                                        ALU.subtract).then_inc(w_q_split, 1)

            def gains():
                dve.wait_ge(loaded, LOADS)
                nc.vector.scalar_tensor_tensor(gain[:], gain_q[:], float(np.float32(1.0) / np.sqrt(np.float32(G_HD))), gain_k[:],
                                               ALU.mult, ALU.mult).then_inc(consts_set, 1)
                dve.wait_ge(consts_set, 2)

            def turn(t, valid):
                if isinstance(t, int) and t == -1:
                    gains()
                if valid(t - 1):
                    dve.wait_ge(v_highs, t)
                    for b in range(2):
                        half = slice(SEQ * b, SEQ * b + SEQ)
                        done = nc.vector.tensor_tensor(values_low[half, b, :], values[half], values_high[half, b, :].bitcast(F32), ALU.subtract)
                    done.then_inc(v_lows, 1)
                if valid(t + 1):
                    biased(t + 1, 0)
                    biased(t + 1, 1)
                if valid(t + 2):
                    ln.normalise(xn[:], t + 2).then_inc(xn_ready, 1)
                if valid(t):
                    if isinstance(t, int) and t == 0:
                        dve.wait_ge(w_v_split, 1)
                    dve.wait_ge(turned, t + 1)
                    nc.vector.tensor_tensor(probs[:], ps[:, 6:8, :].rearrange("p k (h s) -> p (k h) s", s=SEQ),
                                            mask[:, None, :].to_broadcast([P, G_HEADS, SEQ]), ALU.add).then_inc(masked, 1)
                    dve.wait_ge(masked, t + 1)
                    nc.vector.tensor_reduce(top[:], probs[:], AX.X, ALU.max).then_inc(top_ready, 1)
                    dve.wait_ge(top_ready, t + 1)
                    nc.vector.tensor_tensor(probs[:], probs[:], across(top), ALU.subtract).then_inc(shifted, 1)
                if valid(t - 1):
                    mixed_low(t - 1, 0)
                    mixed_low(t - 1, 1)
                if valid(t + 1):
                    biased(t + 1, 2)
                    biased(t + 1, 3)
                    query_sums(t + 1, 0)
                if isinstance(t, int) and t == -1:
                    dve.wait_ge(w_o_loaded, 16)
                    nc.vector.tensor_copy(w_o_high[:], raw[:].rearrange("p (h e) -> p h e", e=E)).then_inc(w_o_highs, 1)
                if valid(t):
                    dve.wait_ge(exp_done, t + 1)
                    nc.vector.tensor_reduce(total[:], probs[:], AX.X, ALU.add).then_inc(totals, 1)
                    dve.wait_ge(totals, t + 1)
                    nc.vector.reciprocal(inv[:], total[:]).then_inc(inv_ready, 1)
                if valid(t - 1):
                    mixed_low(t - 1, 2)
                    mixed_low(t - 1, 3)
                if valid(t):
                    dve.wait_ge(inv_ready, t + 1)
                    nc.vector.tensor_tensor(probs[:], probs[:], across(inv), ALU.mult).then_inc(probs_ready, 1)
                if valid(t + 1):
                    query_sums(t + 1, 1)
                if valid(t - 1):
                    dve.wait_ge(out_psum, t)
                    nc.vector.tensor_tensor(core.x[:, t - 1, :], core.x[:, t - 1, :], ps[:, 6, 0:E], ALU.add).then_inc(x_ready, 1)
                if valid(t + 1):
                    dve.wait_ge(k_invs, t + 2)
                    nc.vector.scalar_tensor_tensor(kT[:], k_raw[:], gain[:], k_inv[:], ALU.mult, ALU.mult).then_inc(kT_ready, 1)
                if valid(t - 1):
                    dve.wait_ge(x_ready, t + 1)
                    nc.vector.bn_stats(core.row_stats[:, t - 1, :], core.x[:, t - 1, :]).then_inc(stats_done, 1)
                if valid(t):
                    dve.wait_ge(probsT_highs, t + 1)
                    nc.vector.tensor_tensor(probsT_low[:].rearrange("p (b c) -> p b c", b=2), ps[:, 4:6, :],
                                            probsT_high[:].rearrange("p (b c) -> p b c", b=2).bitcast(F32), ALU.subtract).then_inc(probsT_lows, 1)
                if valid(t + 2):
                    dve.wait_ge(xT_highs, t + 3)
                    nc.vector.tensor_tensor(xT_low[:], ps[:, 2, 0:E], xT_high[:].bitcast(F32), ALU.subtract).then_inc(xT_ready, 1)
                if isinstance(t, int) and t == -2:
                    split_rest()
                if valid(t):
                    dve.wait_ge(v_psum, t + 1)
                    if started(t, 1):
                        dve.wait_ge(v_lows, t)
                    nc.vector.tensor_tensor(values[:], ps[:, 3, :], bias_v[:], ALU.add).then_inc(v_ready, 1)

            pipeline(dve, turn)
            dve.wait_ge(stats_done, TILES)

        @block.tensor
        def _(pe):

            def query(n, g):
                if g >= 2:
                    pe.wait_ge(q_ready, 4 * n + (g - 1))
                for c in range(KC):
                    rows, columns = slice(c * P, (c + 1) * P), slice(g * G_CHUNK, (g + 1) * G_CHUNK)
                    done = three_passes(nc, ps[:, g % 2, :], (xT_high[:, rows], xT_low[:, rows]), (w_q_high[:, c, columns], w_q_low[:, c, columns]),
                                        start=(c == 0), stop=(c == KC - 1))
                done.then_inc(q_psum, 1)

            def mix(n, j):
                if j >= 2:
                    pe.wait_ge(mixed_lows, 4 * n + (j - 1))
                for b in range(2):
                    of, columns = slice(j * G_HD, (j + 1) * G_HD), slice(j * E, (j + 1) * E)
                    done = three_passes(nc, ps[:, 4 + j % 2, b * E:(b + 1) * E], (values_high[:, b, of], values_low[:, b, of]),
                                        (probsT_high[:, columns], probsT_low[:, columns]), start=True, stop=True)
                done.then_inc(mixed_psum, 1)

            def turn(t, valid):
                if valid(t):
                    pe.wait_ge(kT_ready, t + 1)
                    if started(t, 1):
                        pe.wait_ge(probsT_lows, t)
                    for j in range(G_KV):
                        pe.wait_ge(qT_ready, 4 * t + (j + 1))
                        for b in range(2):
                            half = slice(SEQ * b, SEQ * b + SEQ)
                            done = nc.tensor.matmul(ps[half, 4 + j // 2, (j % 2) * E:(j % 2 + 1) * E], kT[:, j * P + SEQ * b:j * P + SEQ * b + SEQ],
                                                    qT[:, 4 * j:4 * j + 4, SEQ * b:SEQ * b + SEQ], start=True, stop=True)
                    done.then_inc(scored, 1)
                if valid(t + 1):
                    if isinstance(t, int) and t == -1:
                        pe.wait_ge(w_q_split, KC + 1)
                    pe.wait_ge(xT_ready, t + 2)
                    query(t + 1, 0)
                    query(t + 1, 1)
                if valid(t):
                    pe.wait_ge(scoresT_ready, t + 1)
                    if started(t, 1):
                        pe.wait_ge(x_ready, t)
                    for j in range(G_HEADS // 2):
                        done = nc.tensor.transpose(ps[:, 6 + j // 4, (j % 4) * P:(j % 4 + 1) * P], scoresT[:, j * P:(j + 1) * P], ident[:])
                    done.then_inc(turned, 1)
                if valid(t + 1):
                    query(t + 1, 2)
                    query(t + 1, 3)
                if valid(t - 1):
                    pe.wait_ge(v_lows, t)
                    pe.wait_ge(probsT_lows, t)
                    if valid(t):
                        pe.wait_ge(scoresT_ready, t + 1)
                        pe.wait_ge(masked, t + 1)
                    mix(t - 1, 0)
                    mix(t - 1, 1)
                if valid(t + 1):
                    if isinstance(t, int) and t == -1:
                        pe.wait_ge(loaded, LOADS)
                        pe.wait_ge(consts_set, 2)
                    pe.wait_ge(ctx_k_ready, 16 * t + 32)
                    for j in range(G_KV):
                        for c in range(KC):
                            done = nc.tensor.matmul(ps[:, 2, j * P:(j + 1) * P], w_k[:, c, j * P:(j + 1) * P], ctxT_k[:, c],
                                                    start=(c == 0), stop=(c == KC - 1))
                    done.then_inc(k_psum, 1)
                if valid(t - 1):
                    mix(t - 1, 2)
                    mix(t - 1, 3)
                if valid(t - 1):
                    if isinstance(t, int) and t == 1 or not isinstance(t, int):
                        pe.wait_ge(w_o_split, 1)
                    for j in range(G_KV):
                        pe.wait_ge(mixed_highs, 4 * t + (j - 3))
                        for h in range(4 * j, 4 * j + 4):
                            for weight in (w_o_high, w_o_low):
                                nc.tensor.matmul(ps[:, 6, 0:E], mixedT_high[:, h], weight[:, h], start=(h == 0 and weight is w_o_high), stop=False)
                    for j in range(G_KV):
                        pe.wait_ge(mixed_lows, 4 * t + (j - 3))
                        for h in range(4 * j, 4 * j + 4):
                            done = nc.tensor.matmul(ps[:, 6, 0:E], mixedT_low[:, h], w_o_high[:, h], start=False, stop=(h == G_HEADS - 1))
                    done.then_inc(out_psum, 1)
                if valid(t):
                    pe.wait_ge(probs_ready, t + 1)
                    if started(t, 1):
                        pe.wait_ge(mixed_lows, 4 * t)
                    for j in range(G_HEADS // 2):
                        done = nc.tensor.transpose(ps[:, 4 + j // 4, (j % 4) * P:(j % 4 + 1) * P],
                                                   probs[:, 2 * j:2 * j + 2].rearrange("p b s -> p (b s)"), ident[:])
                    done.then_inc(probsT_psum, 1)

                if valid(t + 1):
                    pe.wait_ge(k_lows, t + 2)
                    nc.tensor.matmul(ps[:, 2, :], ones[:], k_high[:], start=True, stop=False)
                    nc.tensor.matmul(ps[:, 2, :], ones[:], k_low[:], start=False, stop=True).then_inc(k_sums, 1)

                def turn_queries(g):
                    if g >= 2:
                        pe.wait_ge(qT_ready, 4 * t + (g + 3))
                    else:
                        pe.wait_ge(q_ready, 4 * t + (g + 7))
                    pe.wait_ge(q_scaled_ready, 2 * t + (g // 2 + 3))
                    for h in range(4 * g, 4 * g + 4):
                        done = nc.tensor.transpose(ps[:, g % 2, (h % 4) * P:(h % 4 + 1) * P], q_scaled[:, h * G_HD:(h + 1) * G_HD], ident[:])
                    done.then_inc(qT_psum, 1)

                if valid(t + 1):
                    turn_queries(0)
                    turn_queries(1)
                if valid(t + 2):
                    pe.wait_ge(xn_ready, t + 3)
                    if valid(t + 1):
                        pe.wait_ge(k_logs, t + 2)
                    for c in range(KC):
                        done = nc.tensor.transpose(ps[:, 2, c * P:(c + 1) * P], xn[:, c * P:(c + 1) * P], ident[:])
                    done.then_inc(xT_psum, 1)
                if valid(t):
                    if isinstance(t, int) and t == 0:
                        pe.wait_ge(w_v_split, 1)
                    pe.wait_ge(ctx_lows, t + 1)
                    if started(t, 1):
                        pe.wait_ge(v_ready, t)
                    for c in range(KC):
                        done = three_passes(nc, ps[:, 3, :], (ctxT_high[:, c], ctxT_low[:, c]), (w_v_high[:, c], w_v_low[:, c]),
                                            start=(c == 0), stop=(c == KC - 1))
                    done.then_inc(v_psum, 1)
                if valid(t + 1):
                    turn_queries(2)
                    turn_queries(3)

            pipeline(pe, turn)

M_EXPERTS, M_FF = 8, 256
M_RANK, M_LORA = 64, 2
FT = M_FF // P
ZONE_CENTER, ZONE_LOW, ZONE_HIGH = 1.0 / math.e, 0.5 - math.log(4.0 / 3.0), 0.5
ZONE_WIDTH, FALLBACK_WIDTH, TINY = 0.1, 0.3, 1e-8
QUAD = 4


def mixture(core):
    nc, dram, ps, ident = core.nc, core.dram, core.psum, core.ident
    with ExitStack() as scope:
        sb = lambda name, shape, dt=F32: scope.enter_context(nc.sbuf_tensor(f"mo_{name}", shape, dt))
        sem = lambda name: core.sem(f"mo_{name}")
        ln = RowNorm(core, "mo", scope)
        RAW, LAG, MATRICES = 4, 2, 3
        GATE, UP, DOWN = range(MATRICES)
        raw = sb("raw", [P, RAW, MATRICES, KC, M_FF])
        w_high, w_low = (sb(name, [P, M_EXPERTS, MATRICES, KC, M_FF], F32R) for name in ("w_high", "w_low"))
        w_route = sb("w_route", [P, KC, M_EXPERTS])
        temperature, first = sb("temperature", [P, 1]), sb("first", [P, M_EXPERTS])
        xn, xT = sb("xn", [P, QUAD, E]), sb("xT", [P, QUAD, E])
        xT_high, xT_low = sb("xT_high", [P, KC, TILES * P], F32R), sb("xT_low", [P, KC, TILES * P], F32R)
        logits, gate, dist, zone, near, rank, hot1, hot2 = (
            sb(name, [P, TILES, M_EXPERTS]) for name in ("logits", "gate", "dist", "zone", "near", "rank", "hot1", "hot2"))
        total, nobody, best = (sb(name, [P, TILES]) for name in ("total", "nobody", "best"))
        silu, mid = sb("silu", [P, 4, 2 * P]), sb("mid", [P, 4, 2 * P])
        with ExitStack() as early:
            lora_a, lora_b = (early.enter_context(nc.sbuf_tensor(f"mo_{name}", [M_RANK, MATRICES, M_LORA, M_FF], F32))
                              for name in ("lora_a", "lora_b"))
        mid_high, mid_low = sb("mid_high", [P, 4, FT, 2 * P], F32R), sb("mid_low", [P, 4, FT, 2 * P], F32R)

        loaded, folded_psum, folded, xn_ready, xT_psum, xT_ready, xT_highs, xT_lows, routed, logits_ready, route_step, inverted = (
            sem(n) for n in ("loaded", "folded_psum", "folded", "xn_ready", "xT_psum", "xT_ready", "xT_highs", "xT_lows", "routed",
                             "logits_ready", "route_step", "inverted"))
        raw_loaded, w_highs, w_lows = core.sems("mo_raw_loaded", RAW), sem("w_highs"), sem("w_lows")
        gate_arg, gate_exp, dists, near_exp, zone_exp, mix_ready = (
            sem(n) for n in ("gate_arg", "gate_exp", "dists", "near_exp", "zone_exp", "mix_ready"))
        wide_psum, silu_ready, mid_ready, mid_highs, mid_lows, down_psum, added, stored = (
            sem(n) for n in ("wide_psum", "silu_ready", "mid_ready", "mid_highs", "mid_lows", "down_psum", "added", "stored"))
        LOADS = 5 * 16
        MIDS = M_EXPERTS * FT
        ADDS = 2 * M_EXPERTS
        EXPERT_LOADS = 16 * MATRICES

        def turns(eng, turn):
            turn(0, lambda k: k >= 0)
            with eng.Fori(1, PAIRS) as i:
                turn(i, lambda k: True)

        block = scope.enter_context(nc.Block())

        @block.sync
        def _(sp):
            for out, src in ((w_route[:], chunked(dram["mo_w_route"])), (temperature[:], dram["mo_temperature"].to_broadcast([P, 1])),
                             (first[:], dram["ff_first"]), (lora_a[:], dram["mo_lora_a"]), (lora_b[:], dram["mo_lora_b"])):
                sp.dma_start(out, src).then_inc(loaded, 16)
            for e in range(M_EXPERTS):
                if e >= RAW:
                    sp.wait_ge(w_lows, MATRICES * (e - RAW + 1))
                for k, name in enumerate(("gate", "up", "down")):
                    sp.dma_start(raw[:, e % RAW, k], chunked(dram[f"mo_w_{name}"][e])).then_inc(raw_loaded[e % RAW], 16)
            for e in range(M_EXPERTS - RAW, M_EXPERTS):
                sp.wait_ge(raw_loaded[e % RAW], EXPERT_LOADS * (e // RAW + 1))
            sp.wait_ge(loaded, LOADS)
            rows = dram["out"].rearrange("(t p) e -> p t e", p=P)
            with sp.Fori(0, PAIRS) as i:
                sp.wait_ge(added, ADDS * i + ADDS)
                sp.dma_start(rows[:, bass.ts(i, 2), :], core.x[:, bass.ts(i, 2), :]).then_inc(stored, 16)
            sp.wait_ge(stored, 16 * PAIRS)

        @block.gpsimd
        def _(pool):
            with pool.Fori(0, TILES // QUAD) as i:
                for u in range(QUAD):
                    t = QUAD * i + u
                    pool.wait_ge(xT_highs, t + 1)
                    nc.gpsimd.tensor_tensor(xT_low[:, :, bass.ts(t, P)], xT[:, u].rearrange("p (c t) -> p c t", c=KC),
                                            xT_high[:, :, bass.ts(t, P)].bitcast(F32), ALU.subtract).then_inc(xT_lows, 1)
            for e in range(M_EXPERTS):
                for k in range(MATRICES):
                    pool.wait_ge(w_highs, MATRICES * e + (k + 1))
                    nc.gpsimd.tensor_tensor(w_low[:, e, k], raw[:, e % RAW, k], w_high[:, e, k].bitcast(F32), ALU.subtract).then_inc(w_lows, 1)

        @block.scalar
        def _(act):
            act.preload_act_table_set(EXP_LN)
            ln.on_scalar(act)
            with act.Fori(0, TILES // QUAD) as i:
                for u in range(QUAD):
                    act.wait_ge(xT_psum, QUAD * i + (u + 1))
                    nc.scalar.copy(xT[:, u], ps[:, u, 0:E]).then_inc(xT_ready, 1)
                act.wait_ge(routed, QUAD * i + QUAD)
                nc.scalar.copy(logits[:, bass.ts(i, QUAD), :], ps[:, QUAD, 0:QUAD * M_EXPERTS].rearrange("p (t e) -> p t e", t=QUAD)).then_inc(logits_ready, 1)
                act.wait_ge(xT_lows, QUAD * i + QUAD)

            def split_high(e):
                if e < M_LORA:
                    act.wait_ge(folded, MATRICES * (e + 1))
                else:
                    act.wait_ge(raw_loaded[e % RAW], EXPERT_LOADS * (e // RAW + 1))
                for k in range(MATRICES):
                    nc.scalar.copy(w_high[:, e, k], raw[:, e % RAW, k]).then_inc(w_highs, 1)

            act.wait_ge(gate_arg, 1)
            nc.scalar.activation(gate[:], logits[:], ACT.Exp).then_inc(gate_exp, 1)
            act.wait_ge(dists, 1)
            nc.scalar.activation(near[:], dist[:], ACT.Exp, scale=-1.0 / FALLBACK_WIDTH).then_inc(near_exp, 1)
            nc.scalar.activation(dist[:], dist[:], ACT.Exp, scale=-1.0 / ZONE_WIDTH).then_inc(zone_exp, 1)
            act.preload_act_table_set("silu_and_others")
            for e in range(RAW):
                split_high(e)

            def middle_high(i, j):
                act.wait_ge(mid_ready, MIDS * i + (j + 1))
                nc.scalar.copy(mid_high[:, j // FT % 4, j % FT], mid[:, j % 4]).then_inc(mid_highs, 1)

            def turn(i, later):
                for e in range(M_EXPERTS):
                    for f in range(FT):
                        j = FT * e + f
                        act.wait_ge(wide_psum, MIDS * i + (j + 1))
                        nc.scalar.activation(silu[:, j % 4], ps[:, j % 4, 0:2 * P], ACT.Silu).then_inc(silu_ready, 1)
                        if later(j - 1):
                            middle_high(i, j - 1)
                    if isinstance(i, int) and e + RAW < M_EXPERTS:
                        split_high(e + RAW)

            turns(act, turn)
            middle_high(PAIRS, -1)

        @block.vector
        def _(dve):
            ln.on_vector(dve)
            dve.wait_ge(ln.ready, 1)
            with dve.Fori(0, TILES // QUAD) as i:
                for u in range(QUAD):
                    ln.normalise(xn[:, u], QUAD * i + u).then_inc(xn_ready, 1)
                for u in range(QUAD):
                    t = QUAD * i + u
                    dve.wait_ge(xT_psum, t + 1)
                    dve.wait_ge(xT_ready, t + 1)
                    nc.vector.tensor_copy(xT_high[:, :, bass.ts(t, P)], ps[:, u, 0:E].rearrange("p (c t) -> p c t", c=KC)).then_inc(xT_highs, 1)
            dve.wait_ge(loaded, LOADS)
            nc.vector.reciprocal(temperature[:], temperature[:]).then_inc(inverted, 1)
            dve.wait_ge(inverted, 1)
            def fold(j):
                e, k = j // MATRICES, j % MATRICES
                dve.wait_ge(raw_loaded[e], EXPERT_LOADS)
                dve.wait_ge(folded_psum, j + 1)
                nc.vector.tensor_tensor(raw[:, e, k], raw[:, e, k], ps[:, 4 + j % 4, :].rearrange("p (c f) -> p c f", c=KC),
                                        ALU.add).then_inc(folded, 1)

            across = lambda a: a[:, :, None].to_broadcast([P, TILES, M_EXPERTS])
            every = lambda a: a[:, None, :].to_broadcast([P, TILES, M_EXPERTS])
            dve.wait_ge(logits_ready, TILES // QUAD)
            nc.vector.tensor_scalar(logits[:], logits[:], temperature[:], -1.0, ALU.mult, ALU.mult).then_inc(route_step, 1)
            dve.wait_ge(route_step, 1)
            nc.vector.tensor_scalar(logits[:], logits[:], EXP_LIMIT, None, ALU.min).then_inc(gate_arg, 1)
            fold(0)
            dve.wait_ge(gate_exp, 1)
            nc.vector.tensor_scalar(gate[:], gate[:], 1.0, None, ALU.add).then_inc(route_step, 1)
            dve.wait_ge(route_step, 2)
            nc.vector.reciprocal(gate[:], gate[:]).then_inc(route_step, 1)
            dve.wait_ge(route_step, 3)
            nc.vector.tensor_scalar(dist[:], gate[:], ZONE_CENTER, None, ALU.subtract).then_inc(route_step, 1)
            dve.wait_ge(route_step, 4)
            nc.vector.scalar_tensor_tensor(dist[:], dist[:], -1.0, dist[:], ALU.mult, ALU.max).then_inc(dists, 1)
            nc.vector.tensor_scalar(zone[:], gate[:], ZONE_LOW, None, ALU.is_ge).then_inc(route_step, 1)
            dve.wait_ge(route_step, 5)
            nc.vector.scalar_tensor_tensor(zone[:], gate[:], ZONE_HIGH, zone[:], ALU.is_le, ALU.mult).then_inc(route_step, 1)
            fold(1)
            dve.wait_ge(route_step, 6)
            dve.wait_ge(zone_exp, 1)
            nc.vector.tensor_tensor(zone[:], zone[:], dist[:], ALU.mult).then_inc(route_step, 1)
            dve.wait_ge(route_step, 7)
            nc.vector.tensor_reduce(total[:], zone[:], AX.X, ALU.add).then_inc(route_step, 1)
            dve.wait_ge(route_step, 8)
            nc.vector.tensor_scalar(nobody[:], total[:], TINY, None, ALU.is_lt).then_inc(route_step, 1)
            dve.wait_ge(route_step, 9)
            nc.vector.tensor_reduce(best[:], near[:], AX.X, ALU.max).then_inc(route_step, 1)
            dve.wait_ge(route_step, 10)
            nc.vector.tensor_tensor(rank[:], near[:], across(best), ALU.is_ge).then_inc(route_step, 1)
            fold(2)
            dve.wait_ge(route_step, 11)
            nc.vector.tensor_tensor(rank[:], rank[:], every(first), ALU.mult).then_inc(route_step, 1)
            dve.wait_ge(route_step, 12)
            nc.vector.tensor_reduce(best[:], rank[:], AX.X, ALU.max).then_inc(route_step, 1)
            dve.wait_ge(route_step, 13)
            nc.vector.tensor_tensor(hot1[:], rank[:], across(best), ALU.is_equal).then_inc(route_step, 1)
            dve.wait_ge(route_step, 14)
            nc.vector.scalar_tensor_tensor(gate[:], hot1[:], -2.0, near[:], ALU.mult, ALU.add).then_inc(route_step, 1)
            dve.wait_ge(route_step, 15)
            nc.vector.tensor_reduce(best[:], gate[:], AX.X, ALU.max).then_inc(route_step, 1)
            fold(3)
            dve.wait_ge(route_step, 16)
            nc.vector.tensor_tensor(rank[:], gate[:], across(best), ALU.is_ge).then_inc(route_step, 1)
            dve.wait_ge(route_step, 17)
            nc.vector.tensor_tensor(rank[:], rank[:], every(first), ALU.mult).then_inc(route_step, 1)
            dve.wait_ge(route_step, 18)
            nc.vector.tensor_reduce(best[:], rank[:], AX.X, ALU.max).then_inc(route_step, 1)
            dve.wait_ge(route_step, 19)
            nc.vector.tensor_tensor(hot2[:], rank[:], across(best), ALU.is_equal).then_inc(route_step, 1)
            dve.wait_ge(route_step, 20)
            nc.vector.tensor_tensor(hot1[:], hot1[:], hot2[:], ALU.add).then_inc(route_step, 1)
            fold(4)
            dve.wait_ge(route_step, 21)
            nc.vector.tensor_tensor(near[:], near[:], hot1[:], ALU.mult).then_inc(route_step, 1)
            dve.wait_ge(route_step, 22)
            nc.vector.tensor_reduce(best[:], near[:], AX.X, ALU.add).then_inc(route_step, 1)
            dve.wait_ge(route_step, 23)
            nc.vector.tensor_scalar(best[:], best[:], TINY, None, ALU.max).then_inc(route_step, 1)
            dve.wait_ge(route_step, 24)
            nc.vector.reciprocal(best[:], best[:]).then_inc(route_step, 1)
            fold(5)
            dve.wait_ge(route_step, 25)
            nc.vector.tensor_tensor(best[:], best[:], nobody[:], ALU.mult).then_inc(route_step, 1)
            dve.wait_ge(route_step, 26)
            nc.vector.tensor_tensor(near[:], near[:], across(best), ALU.mult).then_inc(route_step, 1)
            dve.wait_ge(route_step, 27)
            nc.vector.tensor_scalar(nobody[:], nobody[:], -1.0, 1.0, ALU.mult, ALU.add).then_inc(route_step, 1)
            dve.wait_ge(route_step, 28)
            nc.vector.tensor_tensor(zone[:], zone[:], across(nobody), ALU.mult).then_inc(route_step, 1)
            dve.wait_ge(route_step, 29)
            nc.vector.tensor_tensor(zone[:], zone[:], near[:], ALU.add).then_inc(route_step, 1)
            dve.wait_ge(route_step, 30)
            nc.vector.tensor_reduce(total[:], zone[:], AX.X, ALU.add).then_inc(route_step, 1)
            dve.wait_ge(route_step, 31)
            nc.vector.tensor_scalar(total[:], total[:], TINY, None, ALU.max).then_inc(route_step, 1)
            dve.wait_ge(route_step, 32)
            nc.vector.reciprocal(total[:], total[:]).then_inc(route_step, 1)
            dve.wait_ge(route_step, 33)
            nc.vector.tensor_tensor(zone[:], zone[:], across(total), ALU.mult).then_inc(mix_ready, 1)
            dve.wait_ge(mix_ready, 1)

            def middle(i, j):
                dve.wait_ge(silu_ready, MIDS * i + (j + 1))
                nc.vector.tensor_tensor(mid[:, j % 4], silu[:, j % 4], ps[:, j % 4, 2 * P:4 * P], ALU.mult).then_inc(mid_ready, 1)

            def middle_low(i, j):
                place = (slice(None), j // FT % 4, j % FT)
                dve.wait_ge(mid_highs, MIDS * i + (j + 1))
                nc.vector.tensor_tensor(mid_low[place], mid[:, j % 4], mid_high[place].bitcast(F32), ALU.subtract).then_inc(mid_lows, 1)

            def add(i, e, later):
                dve.wait_ge(down_psum, M_EXPERTS * i + (e + 1))
                e, i = e % M_EXPERTS, i + e // M_EXPERTS
                for u in range(2):
                    t = 2 * i + u
                    if later(e - 1):
                        dve.wait_ge(added, ADDS * i + (2 * e + u - 1))
                    nc.vector.scalar_tensor_tensor(core.x[:, t, :], ps[:, 4 + e % 4, u * E:(u + 1) * E], zone[:, t, e:e + 1],
                                                   core.x[:, t, :], ALU.mult, ALU.add).then_inc(added, 1)

            def turn(i, later):
                for e in range(M_EXPERTS):
                    if later(e - LAG - 1):
                        add(i, e - LAG - 1, later)
                    for f in range(FT):
                        j = FT * e + f
                        middle(i, j)
                        if later(j - 1):
                            middle_low(i, j - 1)

            turns(dve, turn)
            middle_low(PAIRS, -1)
            for e in range(-LAG - 1, 0):
                add(PAIRS, e, lambda k: True)

        @block.tensor
        def _(pe):
            with pe.Fori(0, TILES // QUAD) as i:
                for u in range(QUAD):
                    pe.wait_ge(xn_ready, QUAD * i + (u + 1))
                    for c in range(KC):
                        done = nc.tensor.transpose(ps[:, u, c * P:(c + 1) * P], xn[:, u, c * P:(c + 1) * P], ident[:])
                    done.then_inc(xT_psum, 1)
                pe.wait_ge(loaded, LOADS)
                for u in range(QUAD):
                    pe.wait_ge(xT_ready, QUAD * i + (u + 1))
                    for c in range(KC):
                        done = nc.tensor.matmul(ps[:, QUAD, u * M_EXPERTS:(u + 1) * M_EXPERTS], xT[:, u, c * P:(c + 1) * P], w_route[:, c],
                                                start=(c == 0), stop=(c == KC - 1))
                done.then_inc(routed, QUAD)
                pe.wait_ge(xT_highs, QUAD * i + QUAD)
                pe.wait_ge(logits_ready, i + 1)
            for e in range(M_LORA):
                for k in range(MATRICES):
                    j = MATRICES * e + k
                    if j >= 4:
                        pe.wait_ge(folded, j - 3)
                    for c in range(KC):
                        done = nc.tensor.matmul(ps[:, 4 + j % 4, c * M_FF:(c + 1) * M_FF], lora_a[:, k, e, c * P:(c + 1) * P], lora_b[:, k, e],
                                                start=True, stop=True)
                    done.then_inc(folded_psum, 1)
            pe.wait_ge(xT_lows, TILES)

            def widen(i, e, later):
                if isinstance(i, int):
                    pe.wait_ge(w_lows, MATRICES * e + UP + 1)
                for f in range(FT):
                    j = FT * e + f
                    if later(j - 4):
                        pe.wait_ge(mid_ready, MIDS * i + (j - 3))
                    for k in (GATE, UP):
                        for c in range(KC):
                            columns, rows = slice(f * P, (f + 1) * P), bass.ts(i, 2 * P)
                            done = three_passes(nc, ps[:, j % 4, 2 * P * k:2 * P * (k + 1)], (w_high[:, e, k, c, columns], w_low[:, e, k, c, columns]),
                                                (xT_high[:, c, rows], xT_low[:, c, rows]), start=(c == 0), stop=(c == KC - 1))
                    done.then_inc(wide_psum, 1)

            def narrow(i, e, later):
                if isinstance(i, int) and i == 0:
                    pe.wait_ge(folded, M_LORA * MATRICES)
                    pe.wait_ge(w_lows, MATRICES * (e + 1))
                pe.wait_ge(mid_lows, MIDS * i + FT * (e + 1))
                if later(e - 4):
                    pe.wait_ge(added, ADDS * i + 2 * (e - 3))
                e = e % M_EXPERTS
                for u in range(2):
                    for f in range(FT):
                        tokens = slice(u * P, (u + 1) * P)
                        done = three_passes(nc, ps[:, 4 + e % 4, u * E:(u + 1) * E], (mid_high[:, e % 4, f, tokens], mid_low[:, e % 4, f, tokens]),
                                            (w_high[:, e, DOWN, f], w_low[:, e, DOWN, f]), start=(f == 0), stop=(f == FT - 1))
                done.then_inc(down_psum, 1)

            def turn(i, later):
                for e in range(M_EXPERTS):
                    widen(i, e, later)
                    if later(e - LAG):
                        narrow(i, e - LAG, later)
                if isinstance(i, int):
                    pe.wait_ge(w_lows, MATRICES * M_EXPERTS)

            turns(pe, turn)
            for e in range(-LAG, 0):
                narrow(PAIRS, e, lambda k: True)

def decoder(nc, dram):
    with ExitStack() as ctx:
        for name in ("q_parts", "k_parts"):
            dram[name] = nc.dram_tensor(name, (STACK, BATCH * C_HEADS, E), BF16, kind="Internal").ap()
        core = Core(nc, ctx, dram)
        for sublayer in (differential_attention, feature_attention, selected_update):
            sublayer(core)
            core.end_sublayer()
        with nc.sbuf_tensor("staged", [P, KC * Q_COLS], F32) as staged:
            for sublayer in (state_space, grouped_attention):
                sublayer(core, staged)
                core.end_sublayer()
        mixture(core)
        core.end_sublayer()


def rotary_tables():
    inv_freq = 1.0 / 10000.0 ** (np.arange(0, D_HD, 2, dtype=np.float32) / np.float32(D_HD))
    angle = np.arange(SEQ, dtype=np.float32)[None, :] * inv_freq.astype(np.float32)[:, None]
    cos = np.tile(np.cos(angle), (P // (D_HD // 2), 2))
    sin = np.tile(np.concatenate([np.sin(angle), -np.sin(angle)]), (P // D_HD, 2))
    scale = np.float32(D_HD ** -0.5)
    return np.stack([np.concatenate([t * scale, t * scale, t], axis=1) for t in (cos, sin)], axis=1).astype(np.float32)


def swapped(w):
    rows = w.shape[0]
    return w.reshape(rows, -1, 2, D_HD // 2)[:, :, ::-1].reshape(rows, -1)


def layout(inputs):
    a = {k: np.asarray(v) for k, v in inputs.items()}
    f32 = np.float32
    halves = a["L0_attn_Wq"].reshape(E, D_HEADS, 2, D_HD)
    q0, q1 = halves[:, :, 0].reshape(E, P), halves[:, :, 1].reshape(E, P)
    k = a["L0_attn_Wk"]
    rows = np.arange(P)
    tri = np.where(np.arange(SEQ)[None, :] <= np.arange(SEQ)[:, None], 0.0, MASKED).astype(f32)
    out = {
        "x": a["x"].reshape(BATCH * SEQ, E),
        "ctx": a["ctx_2048"].reshape(BATCH * SEQ, E),
        "ident": np.eye(P, dtype=f32),
        "ident_bf": np.eye(P, dtype=f32),
        "da_w_qk": np.concatenate([q0, q1, k, swapped(q0), swapped(q1), swapped(k)], axis=1),
        "da_w_v": a["L0_attn_Wv"],
        "da_w_o": a["L0_attn_Wo"],
        "da_gain": np.tile(a["L0_attn_g"], P // D_DV)[:, None],
        "rotary": rotary_tables(),
        "da_head_mask": (rows[:, None] // D_HD % (D_HEADS // 2) == np.arange(D_HEADS // 2)[None, :]).astype(f32),
        "causal": np.tile(tri, (2, 8)),
        "da_lam": np.broadcast_to(np.stack([a["L0_attn_lam_" + v] for v in ("q1", "q2", "k1", "k2")])[None], (P, 4, D_HD)),
    }
    w_out = np.zeros((2, SEQ, 2, SEQ), f32)
    for b in range(2):
        w_out[b, :, b] = a["L0_xattn_W"].T
    out["fa_w_out"] = w_out.reshape(P, P)
    out["fa_padding"] = np.repeat(np.arange(STACK_ROWS - PARTS * STACK) >= MAX_ROW - PARTS * STACK, 2 * C_HEADS * E).reshape(-1, 2 * C_HEADS * E).astype(f32)
    spread = lambda v: np.broadcast_to(v[None], (P, v.shape[0]))
    out["ff_w_in"] = np.concatenate([a["L0_ffn_select_weight"].transpose(1, 0, 2).reshape(E, F_SEL), a["L0_ffn_select_mean_diff"].T,
                                     a["L0_ffn_lora_update"].transpose(1, 0, 2).reshape(E, F_UPD)], axis=1)
    out["ff_debias"] = a["L0_ffn_debias_w"].T
    out["ff_w_back"] = np.concatenate([a["L0_ffn_lora_degen"].transpose(0, 2, 1).reshape(F_UPD, E), a["L0_ffn_bias_w"],
                                       np.zeros((F_ROWS - F_UPD - F_N, E), f32)], axis=0)
    out["ff_center"], out["ff_slope"] = spread(a["L0_ffn_imp_center"]), spread(a["L0_ffn_imp_slope"])
    out["ff_first"] = spread(np.arange(F_N, 0, -1).astype(f32))
    out["ss_w_bc"] = np.concatenate([a["L1_attn_B_w"].T, a["L1_attn_C_w"].T], axis=1)
    out["ss_bias_bc"] = np.stack([a["L1_attn_B_b"], a["L1_attn_C_b"]], axis=1)
    out["ss_w_dt"], out["ss_w_out"] = a["L1_attn_dt_w"].T, a["L1_attn_out_w"].T
    out["ss_bias_dt"], out["ss_skip"] = spread(a["L1_attn_dt_b"]), spread(a["L1_attn_D"])
    out["ss_A_log"], out["ss_bias_out"] = spread(a["L1_attn_A_log"]), spread(a["L1_attn_out_b"])
    row, col = rows[:, None], rows[None, :]
    spans, pairs = [], []
    for level in range(LEVELS):
        half = 1 << level
        pivot = col // (2 * half) * (2 * half) + half - 1
        spans.append(((col <= pivot) & (row > col) & (row <= pivot)) | ((col > pivot) & (row > pivot) & (row <= col)))
        pairs.append((row // (2 * half) == col // (2 * half)) & (row <= pivot) & (col > pivot))
    out["ss_spans"], out["ss_pairs"] = np.stack(spans, axis=1).astype(f32), np.stack(pairs, axis=1).astype(f32)
    out["ctxT"] = out["ctx"].T
    for name in ("q", "k", "v", "o"):
        out["ga_w_" + name] = a["L1_xattn_W" + name]
    out["ga_bias_q"], out["ga_bias_v"] = a["L1_xattn_bq"][None], a["L1_xattn_bv"][None]
    out["ga_bias_k"] = a["L1_xattn_bk"].reshape(G_KV, G_HD).T
    out["ga_gain_q"], out["ga_gain_k"] = a["L1_xattn_qn_w"][:, None], a["L1_xattn_kn_w"][:, None]
    out["mask"] = a["mask_1xSxS2_ff0"][0]
    out["mo_w_route"], out["mo_temperature"] = a["L1_ffn_Wr"], a["L1_ffn_temperature"][None]
    out["mo_w_gate"], out["mo_w_up"], out["mo_w_down"] = a["L1_ffn_Wg"], a["L1_ffn_Wu"], a["L1_ffn_Wd"]
    out["mo_lora_a"] = np.stack([a["L1_ffn_" + n].transpose(2, 0, 1) for n in ("Ga", "Ua", "Da")], axis=1)
    out["mo_lora_b"] = np.stack([a["L1_ffn_" + n].transpose(1, 0, 2) for n in ("Gb", "Ub", "Db")], axis=1)
    bf16 = mybir.dt.np(BF16)
    for name in ("ident_bf", "causal", "fa_padding"):
        out[name] = out[name].astype(bf16)
    return {n: np.ascontiguousarray(v) for n, v in out.items()}


def kernel(**inputs):
    import concourse.bacc as bacc
    from concourse.bass_utils import run_bass_kernel_spmd

    nc = bacc.Bacc("TRN2", target_bir_lowering=False, num_devices=1)
    arrays = layout(inputs)
    dram = {n: nc.dram_tensor(f"in_{n}", v.shape, mybir.dt.from_np(v.dtype), kind="ExternalInput").ap() for n, v in arrays.items()}
    dram["out"] = nc.dram_tensor("out", (BATCH * SEQ, E), F32, kind="ExternalOutput").ap()
    decoder(nc, dram)
    result = run_bass_kernel_spmd(nc, [{f"in_{n}": v for n, v in arrays.items()}], core_ids=[0])
    return result.results[0]["out"].reshape(BATCH, SEQ, E)
```
